# Optimizing a Trainium2 kernel written in Bass

```python
import numpy as np
import jax
import jax.numpy as jnp

def _softmax(x, axis=-1):
    return jax.nn.softmax(x, axis=axis)

def _gelu(x):
    return jax.nn.gelu(x, approximate=True)

def _silu(x):
    return jax.nn.silu(x)

def _sigmoid(x):
    return jax.nn.sigmoid(x)

def _layernorm(x, axis=-1, eps=1e-05):
    m = jnp.mean(x, axis=axis, keepdims=True)
    v = jnp.var(x, axis=axis, keepdims=True)
    return (x - m) / jnp.sqrt(v + eps)

def _scatter_add(tgt, idx, src, axis=0):
    return tgt.at[idx].add(src)

def _segment_sum(src, seg, n):
    return jax.ops.segment_sum(src, seg, n)
kernel_name = 'mk_xattn_ffn_d4_seqx_r4_557b29'

def setup_inputs(seed: int=0):
    np.random.seed(seed)
    _w = jnp.asarray

    def _rec_inputs():
        import jax
        import jax.numpy as jnp
        _rk = jax.random.key(seed)
        x = -0.0002928 + 1 * jax.random.normal(jax.random.fold_in(_rk, 1), (4, 512, 256), jnp.float32)
        _lenS = 512 - jax.random.randint(jax.random.fold_in(_rk, 7), (4,), 0, max(1, 512 // 4) + 1, jnp.int32)
        _lenS2 = 512 - jax.random.randint(jax.random.fold_in(_rk, 8), (4,), 0, max(1, 512 // 4) + 1, jnp.int32)
        _ctx_1024P = jax.random.normal(jax.random.fold_in(_rk, 11), (4, 16, 256), jnp.float32)
        _ctx_1024c = jax.random.dirichlet(jax.random.fold_in(_rk, 511), 0.3 * jnp.ones((16,), jnp.float32), (4, 512))
        _ctx_1024t = jnp.einsum('bsk,bkd->bsd', _ctx_1024c, _ctx_1024P)
        _ctx_1024t = _ctx_1024t * jax.lax.rsqrt(jnp.mean(jnp.square(_ctx_1024t)) + 1e-12) * 0.953939
        ctx_1024 = -1.39393e-06 + 0.999914 * (_ctx_1024t + 0.3 * jax.random.normal(jax.random.fold_in(_rk, 611), (4, 512, 256), jnp.float32))
        _validS = jnp.arange(512)[None, :] < _lenS[:, None]
        _validS2 = jnp.arange(512)[None, :] < _lenS2[:, None]
        _causal = jnp.tril(jnp.ones((512, 512), dtype=bool))
        mask_BxSxS2_ff0 = jnp.where(jnp.ones((4, 512, 512), dtype=bool), 0.0, -1000000000.0).astype(jnp.float32)
        return (x, ctx_1024, mask_BxSxS2_ff0)
    x, ctx_1024, mask_BxSxS2_ff0 = _rec_inputs()

    def _L0_xattn_setup():
        import jax, jax.numpy as jnp
        import numpy as np
        EMBED_DIM = 256
        NUM_HEADS = 16
        HEAD_DIM = EMBED_DIM // NUM_HEADS
        key = jax.random.key(seed)
        ks = jax.random.split(key, 7)
        B, S, E = (2, 512, EMBED_DIM)
        bound = float(np.sqrt(6.0 / (E + E)))
        mkw = lambda k: jax.random.uniform(k, (E, E), jnp.float32, -bound, bound)
        return {'query': jax.random.normal(ks[0], (B, S, E), jnp.float32), 'key': jax.random.normal(ks[1], (B, S, E), jnp.float32), 'value': jax.random.normal(ks[2], (B, S, E), jnp.float32), 'Wq': mkw(ks[3]), 'Wk': mkw(ks[4]), 'Wv': mkw(ks[5]), 'Wo': mkw(ks[6])}
    _L0_xattn_all = _L0_xattn_setup()
    _L0_xattn_in = {k: v for k, v in _L0_xattn_all.items() if k in ('Wq', 'Wk', 'Wv', 'Wo')}
    del _L0_xattn_all

    def _L0_ffn_setup():
        import jax, jax.numpy as jnp
        import numpy as np
        B, S, D, H, F = (4, 1024, 256, 16, 1024)
        CAP = 0.125
        ROPE_BASE = 10000.0

        def rmsnorm(x, g):
            return x * jax.lax.rsqrt(jnp.mean(x * x, -1, keepdims=True) + 1e-06) * g

        def rope(t, pos):
            hd = t.shape[-1]
            inv = 1.0 / ROPE_BASE ** (jnp.arange(0, hd, 2, dtype=jnp.float32) / hd)
            f = pos[:, None, :, None].astype(jnp.float32) * inv
            emb = jnp.concatenate([f, f], axis=-1)
            cos, sin = (jnp.cos(emb), jnp.sin(emb))
            rot = jnp.concatenate([-t[..., hd // 2:], t[..., :hd // 2]], axis=-1)
            return t * cos + rot * sin
        key = jax.random.key(seed)
        ks = jax.random.split(key, 9)
        scale = 0.02
        x = jax.random.normal(ks[0], (B, S, D), jnp.float32)
        causal = jnp.where(jnp.tril(jnp.ones((S, S), bool)), 0.0, -1000000000.0).astype(jnp.float32)
        attention_mask = jnp.broadcast_to(causal[None, None], (B, 1, S, S))
        position_ids = jnp.broadcast_to(jnp.arange(S, dtype=jnp.int32), (B, S))
        return {'x': x, 'attention_mask': attention_mask, 'position_ids': position_ids, 'router_w': jax.random.normal(ks[1], (D, 1), jnp.float32) * scale, 'router_b': jnp.zeros((1,), jnp.float32), 'wq': jax.random.normal(ks[2], (D, D), jnp.float32) * scale, 'wk': jax.random.normal(ks[3], (D, D), jnp.float32) * scale, 'wv': jax.random.normal(ks[4], (D, D), jnp.float32) * scale, 'wo': jax.random.normal(ks[5], (D, D), jnp.float32) * scale, 'w1': jax.random.normal(ks[6], (D, F), jnp.float32) * scale, 'w2': jax.random.normal(ks[7], (F, D), jnp.float32) * scale, 'ln1': jnp.ones((D,), jnp.float32), 'ln2': jnp.ones((D,), jnp.float32)}
    _L0_ffn_all = _L0_ffn_setup()
    _L0_ffn_in = {k: v for k, v in _L0_ffn_all.items() if k in ('attention_mask', 'position_ids', 'router_w', 'router_b', 'wq', 'wk', 'wv', 'wo', 'w1', 'w2', 'ln1', 'ln2')}
    del _L0_ffn_all

    def _L1_xattn_setup():
        import jax, jax.numpy as jnp
        import numpy as np
        B, T, D = (8, 512, 256)
        key = jax.random.key(seed)
        kq, kk, kv = jax.random.split(key, 3)
        return {'query': jax.random.normal(kq, (B, T, D), dtype=jnp.float32), 'key': jax.random.normal(kk, (B, T, D), dtype=jnp.float32), 'value': jax.random.normal(kv, (B, T, D), dtype=jnp.float32)}
    _L1_xattn_all = _L1_xattn_setup()
    _L1_xattn_in = {k: v for k, v in _L1_xattn_all.items() if k in ()}
    del _L1_xattn_all

    def _L1_ffn_setup():
        import jax, jax.numpy as jnp
        import numpy as np
        QMAX = 127.0

        def _ste_round(v):
            return v + jax.lax.stop_gradient(jnp.round(v) - v)

        def _act_fake_quant(x, clip_factor):
            scale = jax.nn.sigmoid(clip_factor) * jnp.max(jnp.abs(x)) / QMAX
            return jnp.clip(_ste_round(x / scale), -QMAX - 1.0, QMAX) * scale

        def _weight_fake_quant(w):
            scale = jnp.max(jnp.abs(w), axis=1, keepdims=True) / QMAX
            return jnp.clip(_ste_round(w / scale), -QMAX - 1.0, QMAX) * scale
        key = jax.random.key(seed)
        k1, k2, k3, k4 = jax.random.split(key, 4)
        B, S, H, I = (8, 2048, 256, 704)
        return {'x': jax.random.normal(k1, (B, S, H), dtype=jnp.float32), 'clip_x': jnp.full((1,), 4.0, dtype=jnp.float32), 'clip_down': jnp.full((1,), 4.0, dtype=jnp.float32), 'w_gate': jax.random.normal(k2, (I, H), dtype=jnp.float32) * 0.02, 'w_up': jax.random.normal(k3, (I, H), dtype=jnp.float32) * 0.02, 'w_down': jax.random.normal(k4, (H, I), dtype=jnp.float32) * 0.02}
    _L1_ffn_all = _L1_ffn_setup()
    _L1_ffn_in = {k: v for k, v in _L1_ffn_all.items() if k in ('clip_x', 'clip_down', 'w_gate', 'w_up', 'w_down')}
    del _L1_ffn_all

    def _L2_xattn_setup():
        import math
        import jax, jax.numpy as jnp
        import numpy as np
        H = 16
        D_MODEL = 256
        DK = D_MODEL // H
        K_FACTOR = 2

        def _time_delay_agg_inference(v, corr):
            B, _, _, L = v.shape
            top_k = min(int(K_FACTOR * math.log(L)), L)
            mean_value = jnp.mean(corr, axis=(1, 2))
            weights, delay = jax.lax.top_k(mean_value, top_k)
            tmp_corr = jax.nn.softmax(weights, axis=-1)
            idx = (delay[:, :, None] + jnp.arange(L)) % L
            gathered = jnp.take_along_axis(v[:, None], idx[:, :, None, None, :], axis=-1)
            return jnp.einsum('bk,bkhdl->bhdl', tmp_corr, gathered)
        key = jax.random.key(seed)
        ks = jax.random.split(key, 11)
        B, L, D = (4, 512, D_MODEL)
        s = 1.0 / math.sqrt(D)
        return {'queries': jax.random.normal(ks[0], (B, L, D), jnp.float32), 'keys': jax.random.normal(ks[1], (B, L, D), jnp.float32), 'values': jax.random.normal(ks[2], (B, L, D), jnp.float32), 'Wq': jax.random.normal(ks[3], (D, H * DK), jnp.float32) * s, 'bq': jnp.zeros((H * DK,), jnp.float32), 'Wk': jax.random.normal(ks[4], (D, H * DK), jnp.float32) * s, 'bk': jnp.zeros((H * DK,), jnp.float32), 'Wv': jax.random.normal(ks[5], (D, H * DK), jnp.float32) * s, 'bv': jnp.zeros((H * DK,), jnp.float32), 'Wo': jax.random.normal(ks[6], (H * DK, D), jnp.float32) * s, 'bo': jnp.zeros((D,), jnp.float32)}
    _L2_xattn_all = _L2_xattn_setup()
    _L2_xattn_in = {k: v for k, v in _L2_xattn_all.items() if k in ('Wq', 'bq', 'Wk', 'bk', 'Wv', 'bv', 'Wo', 'bo')}
    del _L2_xattn_all

    def _L2_ffn_setup():
        import jax, jax.numpy as jnp
        import numpy as np
        B, T, C = (2, 512, 256)
        E, F = (8, 256)
        FS = 512
        TOP_K = 2
        key = jax.random.key(seed)
        ks = jax.random.split(key, 6)
        s = lambda *d: 1.0 / np.sqrt(d[-1])
        return {'hidden_tensor': jax.random.normal(ks[0], (B, T, C), jnp.float32), 'w_router': jax.random.normal(ks[1], (E, C), jnp.float32) * s(C), 'w1_stack': jax.random.normal(ks[2], (E, F, C), jnp.float32) * s(C), 'w2_stack': jax.random.normal(ks[3], (E, C, F), jnp.float32) * s(F), 'ws1': jax.random.normal(ks[4], (FS, C), jnp.float32) * s(C), 'ws2': jax.random.normal(ks[5], (C, FS), jnp.float32) * s(FS)}
    _L2_ffn_all = _L2_ffn_setup()
    _L2_ffn_in = {k: v for k, v in _L2_ffn_all.items() if k in ('w_router', 'w1_stack', 'w2_stack', 'ws1', 'ws2')}
    del _L2_ffn_all

    def _L3_xattn_setup():
        import jax, jax.numpy as jnp
        import numpy as np
        DIM = 256
        CTX_DIM = 256
        HEADS = 16
        DIM_HEAD = 64
        INNER = HEADS * DIM_HEAD
        FF_INNER = 4 * DIM
        EPS = 1e-05

        def layer_norm(x, g, b):
            mu = jnp.mean(x, axis=-1, keepdims=True)
            var = jnp.var(x, axis=-1, keepdims=True)
            return (x - mu) * jax.lax.rsqrt(var + EPS) * g + b
        key = jax.random.key(seed)
        ks = jax.random.split(key, 10)
        b, n, j = (2, 512, 512)
        x = jax.random.normal(ks[0], (b, n, DIM), dtype=jnp.float32)
        context = jax.random.normal(ks[1], (b, j, CTX_DIM), dtype=jnp.float32)
        mask = jnp.zeros((b, n, j), dtype=jnp.float32)
        s = 0.02
        Wq = jax.random.normal(ks[2], (DIM, INNER), dtype=jnp.float32) * s
        Wkv = jax.random.normal(ks[3], (CTX_DIM, 2 * DIM_HEAD), dtype=jnp.float32) * s
        Wout = jax.random.normal(ks[4], (INNER, DIM), dtype=jnp.float32) * s
        W1 = jax.random.normal(ks[5], (DIM, 2 * FF_INNER), dtype=jnp.float32) * s
        W2 = jax.random.normal(ks[6], (FF_INNER, DIM), dtype=jnp.float32) * s
        ln_g = jnp.ones((DIM,), jnp.float32)
        ln_b = jnp.zeros((DIM,), jnp.float32)
        cln_g = jnp.ones((CTX_DIM,), jnp.float32)
        cln_b = jnp.zeros((CTX_DIM,), jnp.float32)
        return {'x': x, 'context': context, 'mask': mask, 'ln_g': ln_g, 'ln_b': ln_b, 'cln_g': cln_g, 'cln_b': cln_b, 'Wq': Wq, 'Wkv': Wkv, 'Wout': Wout, 'W1': W1, 'W2': W2}
    _L3_xattn_all = _L3_xattn_setup()
    _L3_xattn_in = {k: v for k, v in _L3_xattn_all.items() if k in ('ln_g', 'ln_b', 'cln_g', 'cln_b', 'Wq', 'Wkv', 'Wout', 'W1', 'W2')}
    del _L3_xattn_all

    def _L3_ffn_setup():
        import jax, jax.numpy as jnp
        import numpy as np
        TOP_K = 2

        def _route(x2d, gate_w, num_experts, top_k):
            scores = jax.nn.softmax((x2d @ gate_w.T).astype(jnp.float32), axis=1)
            top_scores, sel = jax.lax.top_k(scores, top_k)
            sel_flat = sel.reshape(-1)
            counts = jnp.bincount(sel_flat, length=num_experts)
            order = jnp.argsort(sel_flat, stable=True)
            top_scores_sorted = top_scores.reshape(-1)[order]
            token_idx = order // top_k
            return (top_scores_sorted, token_idx, counts)

        def _grouped_swiglu(xr, w1, w2, w3, eid):
            out = jnp.zeros((xr.shape[0], w2.shape[-1]), dtype=xr.dtype)
            for e in range(w1.shape[0]):
                xe = jnp.where((eid == e)[:, None], xr, 0.0)
                h = jax.nn.silu(xe @ w1[e]) * (xe @ w3[e])
                out = out + h @ w2[e]
            return out
        key = jax.random.key(seed)
        ks = jax.random.split(key, 5)
        bs, slen, dim, hidden, E = (2, 512, 256, 704, 8)
        x = jax.random.normal(ks[0], (bs, slen, dim), dtype=jnp.float32)
        gate_w = jax.random.normal(ks[1], (E, dim), dtype=jnp.float32) * 0.02
        w1 = jax.random.normal(ks[2], (E, dim, hidden), dtype=jnp.float32) * 0.02
        w2 = jax.random.normal(ks[3], (E, hidden, dim), dtype=jnp.float32) * 0.02
        w3 = jax.random.normal(ks[4], (E, dim, hidden), dtype=jnp.float32) * 0.02
        return {'x': x, 'gate_w': gate_w, 'w1': w1, 'w2': w2, 'w3': w3}
    _L3_ffn_all = _L3_ffn_setup()
    _L3_ffn_in = {k: v for k, v in _L3_ffn_all.items() if k in ('gate_w', 'w1', 'w2', 'w3')}
    del _L3_ffn_all
    return {'x': x, 'ctx_1024': ctx_1024, 'mask_BxSxS2_ff0': mask_BxSxS2_ff0, 'L0_xattn_Wq': _L0_xattn_in['Wq'], 'L0_xattn_Wk': _L0_xattn_in['Wk'], 'L0_xattn_Wv': _L0_xattn_in['Wv'], 'L0_xattn_Wo': _L0_xattn_in['Wo'], 'L0_ffn_attention_mask': _L0_ffn_in['attention_mask'], 'L0_ffn_position_ids': _L0_ffn_in['position_ids'], 'L0_ffn_router_w': _L0_ffn_in['router_w'], 'L0_ffn_router_b': _L0_ffn_in['router_b'], 'L0_ffn_wq': _L0_ffn_in['wq'], 'L0_ffn_wk': _L0_ffn_in['wk'], 'L0_ffn_wv': _L0_ffn_in['wv'], 'L0_ffn_wo': _L0_ffn_in['wo'], 'L0_ffn_w1': _L0_ffn_in['w1'], 'L0_ffn_w2': _L0_ffn_in['w2'], 'L0_ffn_ln1': _L0_ffn_in['ln1'], 'L0_ffn_ln2': _L0_ffn_in['ln2'], 'L1_ffn_clip_x': _L1_ffn_in['clip_x'], 'L1_ffn_clip_down': _L1_ffn_in['clip_down'], 'L1_ffn_w_gate': _L1_ffn_in['w_gate'], 'L1_ffn_w_up': _L1_ffn_in['w_up'], 'L1_ffn_w_down': _L1_ffn_in['w_down'], 'L2_xattn_Wq': _L2_xattn_in['Wq'], 'L2_xattn_bq': _L2_xattn_in['bq'], 'L2_xattn_Wk': _L2_xattn_in['Wk'], 'L2_xattn_bk': _L2_xattn_in['bk'], 'L2_xattn_Wv': _L2_xattn_in['Wv'], 'L2_xattn_bv': _L2_xattn_in['bv'], 'L2_xattn_Wo': _L2_xattn_in['Wo'], 'L2_xattn_bo': _L2_xattn_in['bo'], 'L2_ffn_w_router': _L2_ffn_in['w_router'], 'L2_ffn_w1_stack': _L2_ffn_in['w1_stack'], 'L2_ffn_w2_stack': _L2_ffn_in['w2_stack'], 'L2_ffn_ws1': _L2_ffn_in['ws1'], 'L2_ffn_ws2': _L2_ffn_in['ws2'], 'L3_xattn_ln_g': _L3_xattn_in['ln_g'], 'L3_xattn_ln_b': _L3_xattn_in['ln_b'], 'L3_xattn_cln_g': _L3_xattn_in['cln_g'], 'L3_xattn_cln_b': _L3_xattn_in['cln_b'], 'L3_xattn_Wq': _L3_xattn_in['Wq'], 'L3_xattn_Wkv': _L3_xattn_in['Wkv'], 'L3_xattn_Wout': _L3_xattn_in['Wout'], 'L3_xattn_W1': _L3_xattn_in['W1'], 'L3_xattn_W2': _L3_xattn_in['W2'], 'L3_ffn_gate_w': _L3_ffn_in['gate_w'], 'L3_ffn_w1': _L3_ffn_in['w1'], 'L3_ffn_w2': _L3_ffn_in['w2'], 'L3_ffn_w3': _L3_ffn_in['w3']}

def reference(x, ctx_1024, mask_BxSxS2_ff0, L0_xattn_Wq, L0_xattn_Wk, L0_xattn_Wv, L0_xattn_Wo, L0_ffn_attention_mask, L0_ffn_position_ids, L0_ffn_router_w, L0_ffn_router_b, L0_ffn_wq, L0_ffn_wk, L0_ffn_wv, L0_ffn_wo, L0_ffn_w1, L0_ffn_w2, L0_ffn_ln1, L0_ffn_ln2, L1_ffn_clip_x, L1_ffn_clip_down, L1_ffn_w_gate, L1_ffn_w_up, L1_ffn_w_down, L2_xattn_Wq, L2_xattn_bq, L2_xattn_Wk, L2_xattn_bk, L2_xattn_Wv, L2_xattn_bv, L2_xattn_Wo, L2_xattn_bo, L2_ffn_w_router, L2_ffn_w1_stack, L2_ffn_w2_stack, L2_ffn_ws1, L2_ffn_ws2, L3_xattn_ln_g, L3_xattn_ln_b, L3_xattn_cln_g, L3_xattn_cln_b, L3_xattn_Wq, L3_xattn_Wkv, L3_xattn_Wout, L3_xattn_W1, L3_xattn_W2, L3_ffn_gate_w, L3_ffn_w1, L3_ffn_w2, L3_ffn_w3):
    import jax
    import jax.numpy as jnp

    def _L0_xattn_ref(query, key, value, Wq, Wk, Wv, Wo):
        import jax, jax.numpy as jnp
        import numpy as np
        EMBED_DIM = 256
        NUM_HEADS = 16
        HEAD_DIM = EMBED_DIM // NUM_HEADS
        B, L, E = query.shape
        H, D = (NUM_HEADS, HEAD_DIM)
        scale = D ** (-0.5)
        q = (query @ Wq.T).reshape(B, L, H, D) * scale
        k = (key @ Wk.T).reshape(B, -1, H, D)
        v = (value @ Wv.T).reshape(B, -1, H, D)
        scores = jax.nn.sigmoid(jnp.einsum('blhd,bshd->bhls', q, k))
        o = jnp.einsum('bhls,bshd->blhd', scores, v).reshape(B, L, E)
        return o @ Wo.T

    def _L0_ffn_ref(x, attention_mask, position_ids, router_w, router_b, wq, wk, wv, wo, w1, w2, ln1, ln2):
        import jax, jax.numpy as jnp
        import numpy as np
        B, S, D, H, F = (4, 1024, 256, 16, 1024)
        CAP = 0.125
        ROPE_BASE = 10000.0

        def rmsnorm(x, g):
            return x * jax.lax.rsqrt(jnp.mean(x * x, -1, keepdims=True) + 1e-06) * g

        def rope(t, pos):
            hd = t.shape[-1]
            inv = 1.0 / ROPE_BASE ** (jnp.arange(0, hd, 2, dtype=jnp.float32) / hd)
            f = pos[:, None, :, None].astype(jnp.float32) * inv
            emb = jnp.concatenate([f, f], axis=-1)
            cos, sin = (jnp.cos(emb), jnp.sin(emb))
            rot = jnp.concatenate([-t[..., hd // 2:], t[..., :hd // 2]], axis=-1)
            return t * cos + rot * sin
        b, s, d = x.shape
        hd = d // H
        weights = (x @ router_w)[..., 0] + router_b[0]
        k = int(CAP * s)
        topv, topi = jax.lax.top_k(weights, k)
        thr = topv[:, -1]
        sel_mask = (weights > thr[:, None]).astype(x.dtype)
        kc = k - 1
        sel_idx = jnp.sort(topi[:, :kc], axis=1)
        bidx = jnp.arange(b)[:, None]
        x_sel = x[bidx, sel_idx]
        pos_sel = position_ids[bidx, sel_idx]
        w_sel = weights[bidx, sel_idx]
        m = attention_mask[:, 0]
        m_sel = m[bidx[:, :, None], sel_idx[:, :, None], sel_idx[:, None, :]]
        hn = rmsnorm(x_sel, ln1)

        def heads(t):
            return t.reshape(b, kc, H, hd).transpose(0, 2, 1, 3)
        q = rope(heads(hn @ wq), pos_sel)
        kk = rope(heads(hn @ wk), pos_sel)
        v = heads(hn @ wv)
        sc = jnp.einsum('bhqd,bhkd->bhqk', q, kk) / np.sqrt(hd).astype(np.float32)
        sc = sc + m_sel[:, None]
        a = jax.nn.softmax(sc, axis=-1)
        o = jnp.einsum('bhqk,bhkd->bhqd', a, v).transpose(0, 2, 1, 3).reshape(b, kc, d) @ wo
        x1 = x_sel + o
        x2 = x1 + jax.nn.gelu(rmsnorm(x1, ln2) @ w1) @ w2
        proc = x2 * w_sel[..., None]
        out = jnp.zeros_like(x).at[bidx, sel_idx].set(proc)
        return out + x * (1.0 - sel_mask)[..., None]

    def _L1_xattn_ref(query, key, value):
        import jax, jax.numpy as jnp
        import numpy as np
        B, T, D = (8, 512, 256)
        d = query.shape[-1]
        scores = jnp.einsum('bqd,bkd->bqk', query, key) * d ** (-0.5)
        tril = jnp.tril(jnp.ones((query.shape[1], key.shape[1]), dtype=bool))
        scores = jnp.where(tril, scores, -jnp.inf)
        attn = jax.nn.softmax(scores, axis=-1)
        return jnp.einsum('bqk,bkd->bqd', attn, value)

    def _L1_ffn_ref(x, clip_x, clip_down, w_gate, w_up, w_down):
        import jax, jax.numpy as jnp
        import numpy as np
        QMAX = 127.0

        def _ste_round(v):
            return v + jax.lax.stop_gradient(jnp.round(v) - v)

        def _act_fake_quant(x, clip_factor):
            scale = jax.nn.sigmoid(clip_factor) * jnp.max(jnp.abs(x)) / QMAX
            return jnp.clip(_ste_round(x / scale), -QMAX - 1.0, QMAX) * scale

        def _weight_fake_quant(w):
            scale = jnp.max(jnp.abs(w), axis=1, keepdims=True) / QMAX
            return jnp.clip(_ste_round(w / scale), -QMAX - 1.0, QMAX) * scale
        xq = _act_fake_quant(x, clip_x[0])
        gate = jnp.einsum('bsh,ih->bsi', xq, _weight_fake_quant(w_gate))
        up = jnp.einsum('bsh,ih->bsi', xq, _weight_fake_quant(w_up))
        h = _act_fake_quant(jax.nn.silu(gate) * up, clip_down[0])
        return jnp.einsum('bsi,hi->bsh', h, _weight_fake_quant(w_down))

    def _L2_xattn_ref(queries, keys, values, Wq, bq, Wk, bk, Wv, bv, Wo, bo):
        import math
        import jax, jax.numpy as jnp
        import numpy as np
        H = 16
        D_MODEL = 256
        DK = D_MODEL // H
        K_FACTOR = 2

        def _time_delay_agg_inference(v, corr):
            B, _, _, L = v.shape
            top_k = min(int(K_FACTOR * math.log(L)), L)
            mean_value = jnp.mean(corr, axis=(1, 2))
            weights, delay = jax.lax.top_k(mean_value, top_k)
            tmp_corr = jax.nn.softmax(weights, axis=-1)
            idx = (delay[:, :, None] + jnp.arange(L)) % L
            gathered = jnp.take_along_axis(v[:, None], idx[:, :, None, None, :], axis=-1)
            return jnp.einsum('bk,bkhdl->bhdl', tmp_corr, gathered)
        B, Lq, _ = queries.shape
        Lk = keys.shape[1]
        q = (queries @ Wq + bq).reshape(B, Lq, H, DK)
        k = (keys @ Wk + bk).reshape(B, Lk, H, DK)
        v = (values @ Wv + bv).reshape(B, Lk, H, DK)
        if Lq > Lk:
            pad = ((0, 0), (0, Lq - Lk), (0, 0), (0, 0))
            k = jnp.pad(k, pad)
            v = jnp.pad(v, pad)
        else:
            k = k[:, :Lq]
            v = v[:, :Lq]
        qt = jnp.transpose(q, (0, 2, 3, 1))
        kt = jnp.transpose(k, (0, 2, 3, 1))
        vt = jnp.transpose(v, (0, 2, 3, 1))
        qf = jnp.fft.rfft(qt)
        kf = jnp.fft.rfft(kt)
        c = qf.real * kf.real + 1j * -(qf.imag * kf.imag)
        corr = jnp.fft.irfft(c, n=Lq).astype(qt.dtype)
        agg = _time_delay_agg_inference(vt, corr)
        out = jnp.transpose(agg, (0, 3, 1, 2)).reshape(B, Lq, H * DK)
        return out @ Wo + bo

    def _L2_ffn_ref(hidden_tensor, w_router, w1_stack, w2_stack, ws1, ws2):
        import jax, jax.numpy as jnp
        import numpy as np
        B, T, C = (2, 512, 256)
        E, F = (8, 256)
        FS = 512
        TOP_K = 2
        Bb, Tt, Cc = hidden_tensor.shape
        x = hidden_tensor.reshape(-1, Cc)
        t = x.shape[0]
        logits = x @ w_router.T
        probs = jax.nn.softmax(logits, axis=-1)
        expert_weight, expert_idx = jax.lax.top_k(probs, TOP_K)
        expert_weight = expert_weight / jnp.sum(expert_weight, axis=-1, keepdims=True)
        flat_e = expert_idx.reshape(-1)
        order = jnp.argsort(flat_e, stable=True)
        sorted_e = flat_e[order]
        flat_tok = jnp.repeat(jnp.arange(t), TOP_K)
        sorted_tok = flat_tok[order]
        sorted_w = expert_weight.reshape(-1)[order]
        counts = jnp.bincount(sorted_e, length=E)
        offsets = jnp.concatenate([jnp.zeros((1,), counts.dtype), jnp.cumsum(counts)])
        local_pos = jnp.arange(t * TOP_K) - offsets[sorted_e]
        cap = t * TOP_K
        binned = jnp.zeros((E, cap, Cc), x.dtype).at[sorted_e, local_pos].set(x[sorted_tok])
        inter = jnp.einsum('ecd,efd->ecf', binned, w1_stack)
        inter = jnp.square(jax.nn.relu(inter))
        outb = jnp.einsum('ecf,edf->ecd', inter, w2_stack)
        flat_out = outb[sorted_e, local_pos] * sorted_w[:, None]
        moe_out = jnp.zeros((t, Cc), x.dtype).at[sorted_tok].add(flat_out)
        moe_out = moe_out.reshape(Bb, Tt, Cc)
        sh = jnp.square(jax.nn.relu(jnp.einsum('btc,fc->btf', hidden_tensor, ws1)))
        shared_out = jnp.einsum('btf,cf->btc', sh, ws2)
        return shared_out + moe_out

    def _L3_xattn_ref(x, context, mask, ln_g, ln_b, cln_g, cln_b, Wq, Wkv, Wout, W1, W2):
        import jax, jax.numpy as jnp
        import numpy as np
        DIM = 256
        CTX_DIM = 256
        HEADS = 16
        DIM_HEAD = 64
        INNER = HEADS * DIM_HEAD
        FF_INNER = 4 * DIM
        EPS = 1e-05

        def layer_norm(x, g, b):
            mu = jnp.mean(x, axis=-1, keepdims=True)
            var = jnp.var(x, axis=-1, keepdims=True)
            return (x - mu) * jax.lax.rsqrt(var + EPS) * g + b
        scale = DIM_HEAD ** (-0.5)
        xn = layer_norm(x, ln_g, ln_b)
        cn = layer_norm(context, cln_g, cln_b)
        b, n, _ = xn.shape
        q = (xn @ Wq).reshape(b, n, HEADS, DIM_HEAD).transpose(0, 2, 1, 3) * scale
        kv = cn @ Wkv
        k, v = jnp.split(kv, 2, axis=-1)
        sim = jnp.einsum('bhid,bjd->bhij', q, k) + mask[:, None, :, :]
        attn = jax.nn.softmax(sim, axis=-1)
        out = jnp.einsum('bhij,bjd->bhid', attn, v)
        out = out.transpose(0, 2, 1, 3).reshape(b, n, INNER) @ Wout
        h = xn @ W1
        val, gate = jnp.split(h, 2, axis=-1)
        out = out + jax.nn.silu(gate) * val @ W2
        return out

    def _L3_ffn_ref(x, gate_w, w1, w2, w3):
        import jax, jax.numpy as jnp
        import numpy as np
        TOP_K = 2

        def _route(x2d, gate_w, num_experts, top_k):
            scores = jax.nn.softmax((x2d @ gate_w.T).astype(jnp.float32), axis=1)
            top_scores, sel = jax.lax.top_k(scores, top_k)
            sel_flat = sel.reshape(-1)
            counts = jnp.bincount(sel_flat, length=num_experts)
            order = jnp.argsort(sel_flat, stable=True)
            top_scores_sorted = top_scores.reshape(-1)[order]
            token_idx = order // top_k
            return (top_scores_sorted, token_idx, counts)

        def _grouped_swiglu(xr, w1, w2, w3, eid):
            out = jnp.zeros((xr.shape[0], w2.shape[-1]), dtype=xr.dtype)
            for e in range(w1.shape[0]):
                xe = jnp.where((eid == e)[:, None], xr, 0.0)
                h = jax.nn.silu(xe @ w1[e]) * (xe @ w3[e])
                out = out + h @ w2[e]
            return out
        bs, slen, dim = x.shape
        E, top_k = (gate_w.shape[0], TOP_K)
        x2d = x.reshape(bs * slen, dim)
        top_scores, token_idx, counts = _route(x2d, gate_w, E, top_k)
        routed_in = (x2d[token_idx].astype(jnp.float32) * top_scores[:, None]).astype(x.dtype)
        Tr = bs * slen * top_k
        eid = jnp.repeat(jnp.arange(E), counts, total_repeat_length=Tr)
        routed_out = _grouped_swiglu(routed_in, w1, w2, w3, eid)
        out = jnp.zeros((bs * slen, dim), dtype=x.dtype).at[token_idx].add(routed_out)
        return out.reshape(bs, slen, dim)
    x = x + _L0_xattn_ref(_layernorm(x, axis=-1), ctx_1024, ctx_1024, L0_xattn_Wq, L0_xattn_Wk, L0_xattn_Wv, L0_xattn_Wo)
    x = x + _L0_ffn_ref(_layernorm(x, axis=-1), L0_ffn_attention_mask, L0_ffn_position_ids, L0_ffn_router_w, L0_ffn_router_b, L0_ffn_wq, L0_ffn_wk, L0_ffn_wv, L0_ffn_wo, L0_ffn_w1, L0_ffn_w2, L0_ffn_ln1, L0_ffn_ln2)
    x = x + _L1_xattn_ref(_layernorm(x, axis=-1), ctx_1024, ctx_1024)
    x = x + _L1_ffn_ref(_layernorm(x, axis=-1), L1_ffn_clip_x, L1_ffn_clip_down, L1_ffn_w_gate, L1_ffn_w_up, L1_ffn_w_down)
    x = x + _L2_xattn_ref(_layernorm(x, axis=-1), ctx_1024, ctx_1024, L2_xattn_Wq, L2_xattn_bq, L2_xattn_Wk, L2_xattn_bk, L2_xattn_Wv, L2_xattn_bv, L2_xattn_Wo, L2_xattn_bo)
    x = x + _L2_ffn_ref(_layernorm(x, axis=-1), L2_ffn_w_router, L2_ffn_w1_stack, L2_ffn_w2_stack, L2_ffn_ws1, L2_ffn_ws2)
    x = x + _L3_xattn_ref(_layernorm(x, axis=-1), ctx_1024, mask_BxSxS2_ff0, L3_xattn_ln_g, L3_xattn_ln_b, L3_xattn_cln_g, L3_xattn_cln_b, L3_xattn_Wq, L3_xattn_Wkv, L3_xattn_Wout, L3_xattn_W1, L3_xattn_W2)
    x = x + _L3_ffn_ref(_layernorm(x, axis=-1), L3_ffn_gate_w, L3_ffn_w1, L3_ffn_w2, L3_ffn_w3)
    return x

_drawn_inputs = setup_inputs


def setup_inputs(seed=0):
    import zlib

    import numpy as np

    out = dict(_drawn_inputs(seed))
    spreads = {'L0_ffn_ln1': (1.0, 0.6),
     'L0_ffn_ln2': (1.0, 0.6),
     'L2_xattn_bq': (0.0, 2.0),
     'L2_xattn_bk': (0.0, 2.0),
     'L2_xattn_bv': (0.0, 0.8),
     'L2_xattn_bo': (0.0, 2.0),
     'L3_xattn_ln_g': (1.0, 0.6),
     'L3_xattn_ln_b': (0.0, 0.8),
     'L3_xattn_cln_g': (1.0, 0.6),
     'L3_xattn_cln_b': (0.0, 2.0)}
    factors = {'L0_ffn_router_w': 8.0,
     'L0_ffn_wq': 8.0,
     'L0_ffn_wk': 8.0,
     'L0_ffn_wv': 8.0,
     'L0_ffn_wo': 8.0,
     'L0_ffn_w1': 8.0,
     'L0_ffn_w2': 8.0,
     'L1_ffn_w_gate': 8.0,
     'L1_ffn_w_up': 8.0,
     'L1_ffn_w_down': 8.0,
     'L2_xattn_Wq': 8.0,
     'L2_xattn_Wk': 8.0,
     'L2_xattn_Wv': 8.0,
     'L2_xattn_Wo': 8.0,
     'L2_ffn_w_router': 8.0,
     'L2_ffn_w1_stack': 8.0,
     'L2_ffn_w2_stack': 8.0,
     'L2_ffn_ws1': 6.924,
     'L2_ffn_ws2': 6.15,
     'L3_xattn_Wq': 8.0,
     'L3_xattn_Wkv': 8.0,
     'L3_xattn_Wout': 8.0,
     'L3_xattn_W1': 8.0,
     'L3_xattn_W2': 8.0,
     'L3_ffn_gate_w': 33.998,
     'L3_ffn_w1': 29.932,
     'L3_ffn_w2': 27.772,
     'L3_ffn_w3': 25.67}
    for name, (base, spread) in spreads.items():
        noise = np.random.default_rng([zlib.crc32(name.encode()), seed]).standard_normal(out[name].shape)
        drawn = base * np.exp(spread * noise) if base else spread * noise
        out[name] = jnp.asarray(drawn.astype(out[name].dtype))
    for name, factor in factors.items():
        out[name] = (out[name] * factor).astype(out[name].dtype)
    return out
```

```python
from contextlib import ExitStack

import concourse.bass as bass
from concourse import mybir

ALU = mybir.AluOpType
ACT = mybir.ActivationFunctionType
AX = mybir.AxisListType.X
F32 = mybir.dt.float32
F16 = mybir.dt.float16
BF16 = mybir.dt.bfloat16
I32 = mybir.dt.int32
P = 128
B = 4
S = 512
D = 256
TT = S // P
DC = D // P
NEG = -3.0e38
ROUND = 12582912.0


class Stage:

    def __init__(self, core, name):
        self.core, self.nc, self.name, self.ctx = core, core.nc, name, ExitStack()
        self.sems = []

    def __enter__(self):
        return self

    def __exit__(self, *exc):
        done = self.ctx.__exit__(*exc)
        self.nc.clear_and_free_semaphores(self.sems)
        self.nc.all_engine_barrier()
        return done

    def sb(self, name, shape, dt=F32):
        return self.ctx.enter_context(self.nc.sbuf_tensor(f"{self.name}_{name}", shape, dt))

    def sem(self, name):
        self.sems.append(self.nc.alloc_semaphore(f"{self.name}_{name}"))
        return self.sems[-1]

    def block(self):
        return self.ctx.enter_context(self.nc.Block())


class Chain:

    def __init__(self, eng, sem, base=0):
        self.eng, self.sem, self.base, self.n = eng, sem, base, 0

    def __call__(self, ins):
        self.n += 1
        ins.then_inc(self.sem, 1)
        self.eng.wait_ge(self.sem, self.base + self.n)


class Steps:

    def __init__(self, sem, names):
        assert len(set(names)) == len(names)
        self.sem, self.names, self.next = sem, names, 0

    def done(self, ins, name):
        assert self.names[self.next % len(self.names)] == name, (name, self.next)
        self.next += 1
        ins.then_inc(self.sem, 1)

    def wait(self, eng, name, it=0):
        eng.wait_ge(self.sem, it * len(self.names) + self.names.index(name) + 1)


class Norm:

    LINKS = 4

    def __init__(self, st, tag="", eps=1e-5):
        self.st, self.nc, self.core, self.eps = st, st.nc, st.core, eps
        self.bn = st.sb(f"bn{tag}", [P, TT, 6])
        self.mv = st.sb(f"mv{tag}", [P, TT, 2])
        self.var = st.sb(f"var{tag}", [P, TT])
        self.rstd = st.sb(f"rstd{tag}", [P, TT])
        self.stats = st.sem(f"norm{tag}_stats")
        self.rstd_ready = st.sem(f"norm{tag}_rstd")

    def vector(self, dve, it, src, dst, done):
        nc = self.nc
        link = Chain(dve, self.stats, it * self.LINKS)
        for j in range(TT):
            last = nc.vector.bn_stats(self.bn[:, j, :], src(j))
        link(last)
        dve.nop(nofuse=True)
        for j in range(TT):
            last = nc.vector.bn_aggr(self.mv[:, j, :], self.bn[:, j, :])
        link(last)
        link(nc.vector.tensor_scalar(self.var[:], self.mv[:, :, 1], self.eps, None, ALU.add))
        dve.wait_ge(self.rstd_ready, it + 1)
        for j in range(TT):
            last = nc.vector.tensor_scalar(dst(j), src(j), self.mv[:, j, 0:1], self.rstd[:, j:j + 1],
                                           ALU.subtract, ALU.mult)
        last.then_inc(done, 1)
        self.finish(dve, link)

    def finish(self, dve, link):
        link(self.nc.vector.tensor_copy(self.bn[:, 0, 0:1], self.mv[:, 0, 0:1]))

    def pool(self, pool, it):
        pool.wait_ge(self.stats, it * self.LINKS + 3)
        self.nc.gpsimd.tensor_tensor(self.rstd[:], self.var[:], self.core.neg_half[:, 0:TT],
                                     ALU.pow).then_inc(self.rstd_ready, 1)


class Core:

    def __init__(self, nc, ctx, dram):
        self.nc, self.dram = nc, dram
        self.x = ctx.enter_context(nc.sbuf_tensor("x_sb", [P, B * TT, D], F32))
        self.ident = ctx.enter_context(nc.sbuf_tensor("ident", [P, P], F32))
        self.neg_half = ctx.enter_context(nc.sbuf_tensor("neg_half", [P, 8], F32))
        self.ps = ctx.enter_context(nc.psum_tensor("ps", [P, 8, S], F32))


def load_stage(core):
    nc = core.nc
    with Stage(core, "load") as st:
        loaded, zeroed, made = st.sem("x_loaded"), st.sem("ident_zeroed"), st.sem("ident_made")
        block = st.block()

        @block.sync
        def _(sp):
            sp.dma_start(core.x[:], core.dram["x"].rearrange("b (j p) d -> p (b j) d", p=P)).then_inc(loaded, 16)
            sp.wait_ge(loaded, 16)

        @block.gpsimd
        def _(pool):
            nc.gpsimd.memset(core.neg_half[:], -0.5)
            nc.gpsimd.memset(core.ident[:], 0.0).then_inc(zeroed, 1)
            pool.wait_ge(zeroed, 1)
            nc.gpsimd.affine_select(out=core.ident[:], in_=core.ident[:], compare_op=ALU.not_equal, fill=1.0,
                                    base=0, pattern=[[-1, P]], channel_multiplier=1).then_inc(made, 1)


def store_stage(core, out):
    with Stage(core, "store") as st:
        stored = st.sem("x_stored")
        block = st.block()

        @block.sync
        def _(sp):
            sp.dma_start(out.rearrange("b (j p) d -> p (b j) d", p=P), core.x[:]).then_inc(stored, 16)
            sp.wait_ge(stored, 16)


def transpose_tokens(nc, core, src, bank, c, inc):
    for j in range(TT):
        last = nc.tensor.transpose(core.ps[:, bank, j * P:(j + 1) * P], src[:, j, c * P:(c + 1) * P], core.ident[:])
    last.then_inc(inc, 1)


def sigmoid_attention_stage(core):
    nc, dram = core.nc, core.dram
    HG = 4
    UNITS = HG * TT * 2
    SLOTS = 3
    LATE = 2
    RING = DC + 3 * HG + HG + TT
    HALF = 16
    with Stage(core, "l0x") as st:
        norm = Norm(st)
        wq, wk, wv = (st.sb(n, [P, DC, HG * P]) for n in ("wq", "wk", "wv"))
        wo = st.sb("wo", [P, HG, D])
        lo_rows = st.sb("lo_rows", [P, 1])
        xn = st.sb("xn", [P, TT, D])
        xnT = st.sb("xnT", [P, DC, S])
        ctxT = st.sb("ctxT", [P, DC, S])
        k_hi, k_lo, q_hi, q2 = (st.sb(n, [P, HG, S], F16) for n in ("k_hi", "k_lo", "q_hi", "q2"))
        oT = st.sb("oT", [P, HG, S])
        v = st.sb("v", [P, TT, 4 * HG, 2, HALF], F16)
        prob = st.sb("prob", [P, SLOTS, 2, S])
        p_hi, p_lo = (st.sb(n, [P, SLOTS, 2, S], F16) for n in ("p_hi", "p_lo"))
        weights_in, ctx_in, ctx_used = st.sem("weights_in"), st.sem("ctx_in"), st.sem("ctx_used")
        xn_ready, ring_full, ring_free = st.sem("xn_ready"), st.sem("ring_full"), st.sem("ring_free")
        hi_ready = st.sem("hi_ready")
        scores_ready, probs_ready, probs_used = st.sem("scores_ready"), st.sem("probs_ready"), st.sem("probs_used")
        p_hi_ready, p_lo_ready = st.sem("p_hi_ready"), st.sem("p_lo_ready")
        block = st.block()

        def ring_bank(n):
            return 6 + n % 2

        @block.sync
        def _(sp):
            for dst, name in ((wk, "l0x_wk"), (wq, "l0x_wq"), (wv, "l0x_wv")):
                sp.dma_start(dst[:], dram[name].rearrange("(c p) n -> p c n", p=P)).then_inc(weights_in, 16)
            sp.dma_start(wo[:], dram["l0x_wo"].rearrange("(g p) n -> p g n", p=P)).then_inc(weights_in, 16)
            sp.dma_start(lo_rows[:], dram["lo_rows"]).then_inc(weights_in, 16)
            with sp.Fori(0, B) as b:
                sp.wait_ge(ctx_used, b + 1)
                sp.dma_start(ctxT[:], dram["ctxT"][b].rearrange("(c p) s -> p c s", p=P)).then_inc(ctx_in, 16)

        @block.gpsimd
        def _(pool):
            with pool.Fori(0, B) as b:
                norm.pool(pool, b)

        @block.tensor
        def _(pe):
            pe.sem_inc(ctx_used, 1)
            pe.sem_inc(probs_used, SLOTS)
            pe.wait_ge(weights_in, 80)
            with pe.Fori(0, B) as b:
                base = b * RING
                ring = [0]

                def claim():
                    n = ring[0]
                    ring[0] += 1
                    pe.wait_ge(ring_free, base + n + 1)
                    return ring_bank(n)

                def emptied():
                    pe.wait_ge(ring_free, base + ring[0] + 2)

                def project(w, g, rhs):
                    bank = claim()
                    for c in range(DC):
                        last = nc.tensor.matmul(core.ps[:, bank, :], w[:, c, g * P:(g + 1) * P], rhs[:, c, :],
                                                start=(c == 0), stop=(c == DC - 1))
                    last.then_inc(ring_full, 1)

                pe.wait_ge(ctx_in, b * 16 + 16)
                for g in range(HG):
                    project(wk, g, ctxT)
                for j in range(TT):
                    bank = claim()
                    for c in range(DC):
                        last = nc.tensor.matmul(core.ps[:, bank, :], ctxT[:, c, j * P:(j + 1) * P], wv[:, c, :],
                                                start=(c == 0), stop=(c == DC - 1))
                    last.then_inc(ring_full, 1)
                pe.wait_ge(xn_ready, b + 1)
                for c in range(DC):
                    transpose_tokens(nc, core, xn, claim(), c, ring_full)
                emptied()
                pe.sem_inc(ctx_used, 1)
                for g in range(HG):
                    project(wq, g, xnT)
                emptied()

                units = [(g, j, h) for g in range(HG) for j in range(TT) for h in range(2)]

                def score(u):
                    g, j, h = units[u]
                    pe.wait_ge(probs_ready, b * UNITS + max(u + 1, SLOTS))
                    for i in range(2):
                        r = 32 * (2 * h + i)
                        for part, k in enumerate((k_hi, k_lo)):
                            last = nc.tensor.matmul(core.ps[:, 2 * (u % SLOTS) + i, :], k[r:r + 32, g, j * P:(j + 1) * P],
                                                    q2[r:r + 32, g, :], start=(part == 0), stop=(part == 1))
                    last.then_inc(scores_ready, 1)

                for u in range(SLOTS):
                    score(u)
                for u, (g, j, h) in enumerate(units):
                    if u + SLOTS < UNITS:
                        score(u + SLOTS)
                    if (j, h) == (0, 0):
                        bank = claim()
                    pe.wait_ge(p_lo_ready, b * UNITS + u + 1 + SLOTS)
                    for part, probs in enumerate((p_hi, p_lo)):
                        for i in range(2):
                            head = 2 * h + i
                            r = 32 * head
                            last = nc.tensor.matmul(core.ps[r:r + 32, bank, :], v[:, j, 4 * g + head, :, :],
                                                    probs[:, u % SLOTS, i, :], start=(j == 0 and part == 0),
                                                    stop=(j == TT - 1 and part == 1), tile_position=(0, r))
                    last.then_inc(probs_used, 1)
                emptied()
                for j in range(TT):
                    bank = claim()
                    for g in range(HG):
                        last = nc.tensor.matmul(core.ps[:, bank, 0:D], oT[:, g, j * P:(j + 1) * P], wo[:, g, :],
                                                start=(g == 0), stop=(g == HG - 1))
                    last.then_inc(ring_full, 1)
                assert ring[0] == RING

        @block.scalar
        def _(act):
            act.sem_inc(probs_ready, SLOTS)
            with act.Fori(0, B) as b:
                def hi(n, dst, src):
                    act.wait_ge(ring_full, b * (RING - HG) + n + 1)
                    nc.scalar.activation(dst, src(core.ps[:, ring_bank(n), :]), ACT.Copy).then_inc(hi_ready, 1)

                for g in range(HG):
                    hi(g, k_hi[:, g, :], lambda full: full)
                for j in range(TT):
                    hi(HG + j, v[:, j, :, 0, :], lambda full: full.rearrange("p (h a d) -> p h a d", a=2, d=HALF)[:, :, 0, :])
                for g in range(HG):
                    hi(HG + TT + DC + g, q_hi[:, g, :], lambda full: full)
                for u in range(UNITS):
                    act.wait_ge(scores_ready, b * UNITS + u + 1)
                    act.wait_ge(p_lo_ready, b * UNITS + max(u + 1, SLOTS))
                    nc.scalar.activation(prob[:, u % SLOTS, :, :], core.ps[:, 2 * (u % SLOTS):2 * (u % SLOTS) + 2, :],
                                         ACT.Sigmoid, scale=0.25).then_inc(probs_ready, 1)

        @block.vector
        def _(dve):
            V = nc.vector
            dve.sem_inc(ring_free, 2)
            dve.sem_inc(p_lo_ready, SLOTS)
            dve.wait_ge(weights_in, 80)
            with dve.Fori(0, B) as b:
                ring, full, his = [0], [0], [0]

                def take():
                    ring[0] += 1
                    full[0] += 1
                    dve.wait_ge(ring_full, b * (RING - HG) + full[0])
                    return ring_bank(ring[0] - 1)

                def take_split():
                    his[0] += 1
                    bank = take()
                    dve.wait_ge(hi_ready, b * (2 * HG + TT) + his[0])
                    return bank

                norm.vector(dve, b, lambda j: core.x[:, b * TT + j, :], lambda j: xn[:, j, :], xn_ready)
                for g in range(HG):
                    V.tensor_tensor(k_lo[:, g, :], core.ps[:, take_split(), :], k_hi[:, g, :], ALU.subtract
                                    ).then_inc(ring_free, 1)
                for j in range(TT):
                    own = core.ps[:, take_split(), :].rearrange("p (h a d) -> p h a d", a=2, d=HALF)[:, :, 1, :]
                    V.tensor_tensor(v[:, j, :, 1, :], own, v[:, j, :, 0, :], ALU.subtract).then_inc(ring_free, 1)
                for c in range(DC):
                    V.tensor_copy(xnT[:, c, :], core.ps[:, take(), :]).then_inc(ring_free, 1)
                for g in range(HG):
                    V.scalar_tensor_tensor(out=q2[:, g, :], in0=q_hi[:, g, :], scalar=lo_rows[:, 0:1],
                                           in1=core.ps[:, take_split(), :], op0=ALU.mult, op1=ALU.add).then_inc(ring_free, 1)

                def rows(g):
                    ring[0] += 1
                    dve.wait_ge(probs_used, b * UNITS + SLOTS + (g + 1) * UNITS // HG)
                    V.tensor_copy(oT[:, g, :], core.ps[:, ring_bank(ring[0] - 1), :]).then_inc(ring_free, 1)

                for u in range(UNITS + 1):
                    if u < UNITS:
                        dve.wait_ge(probs_ready, b * UNITS + u + 1 + SLOTS)
                        dve.wait_ge(probs_used, b * UNITS + max(u + 1, SLOTS))
                        V.tensor_copy(p_hi[:, u % SLOTS, :, :], prob[:, u % SLOTS, :, :]).then_inc(p_hi_ready, 1)
                    if u >= 1:
                        n = u - 1
                        dve.wait_ge(p_hi_ready, b * UNITS + n + 1)
                        V.tensor_tensor(p_lo[:, n % SLOTS, :, :], prob[:, n % SLOTS, :, :], p_hi[:, n % SLOTS, :, :],
                                        ALU.subtract).then_inc(p_lo_ready, 1)
                        if n % (UNITS // HG) == LATE and n > LATE:
                            rows(n // (UNITS // HG) - 1)
                rows(HG - 1)
                for j in range(TT):
                    V.tensor_tensor(core.x[:, b * TT + j, :], core.x[:, b * TT + j, :],
                                    core.ps[:, take(), 0:D], ALU.add).then_inc(ring_free, 1)


def mixture_of_depths_stage(core):
    nc, dram = core.nc, core.dram
    K = S // 8
    HALF = 64
    T2 = 2
    H, HD = 16, 16
    HG, STRIP = 4, 32
    F = 1024
    FT = F // P
    NA = D + 2
    with Stage(core, "l0f") as st:
        norm = Norm(st)
        xa = st.sb("xa", [P, B * TT, NA])
        rw, rb = st.sb("rw", [P, D]), st.sb("rb", [P, 1])
        junk = st.sb("junk", [P, TT, D])
        pos = st.sb("pos", [P, B * TT], I32)
        wcol = st.sb("wcol", [P, TT, B])
        wrow, work, chosen, above, ones = (st.sb(n, [B, S]) for n in ("wrow", "work", "chosen", "above", "ones"))
        top = st.sb("top", [B, K])
        last8 = st.sb("last8", [B, 8])
        base = st.sb("slot_base", [B, 1])
        slot, keep = st.sb("slot", [P, B, TT]), st.sb("keep", [P, B, TT])
        iota = st.sb("iota", [P, P])
        pick = st.sb("pick", [P, B * TT, P])
        pickT = st.sb("pickT", [P, B * TT, P])
        mask = st.sb("mask", [P, TT, S])
        half_mask = st.sb("half_mask", [P, B * TT, P])
        bar = st.sb("bar", [P, P])
        bias = st.sb("bias", [P, T2, P])
        xs = st.sb("xs", [P, T2, NA])
        ss, rms = st.sb("ss", [P, T2]), st.sb("rms", [P, T2])
        hn = st.sb("hn", [P, T2, D])
        hT = st.sb("hT", [P, DC, T2 * P])
        ln1, ln2 = st.sb("ln1", [P, DC]), st.sb("ln2", [P, DC])
        wq, wk, wv, wo = (st.sb(n, [P, DC, D]) for n in ("wq", "wk", "wv", "wo"))
        w1 = st.sb("w1", [P, DC, F])
        w2 = st.sb("w2", [P, FT, D])
        freq = st.sb("freq", [P, HD // 2])
        ang, turns, sin, cos = (st.sb(n, [P, T2, HD]) for n in ("ang", "turns", "sin", "cos"))
        q, k = (st.sb(n, [P, T2, H, STRIP]) for n in ("q", "k"))
        rot = st.sb("rot", [P, H, HD])
        v = st.sb("v", [P, T2, D])
        qT, kT = (st.sb(n, [P, HG, T2 * P]) for n in ("qT", "kT"))
        prob = st.sb("prob", [P, H, P])
        probT = st.sb("probT", [P, H, P])
        mx, total, inv = (st.sb(n, [P, H]) for n in ("mx", "total", "inv"))
        o = st.sb("o", [P, T2, D])
        oT = st.sb("oT", [P, DC, T2 * P])
        x1 = st.sb("x1", [P, T2, D])
        gT = st.sb("gT", [P, FT, T2 * P])
        y = st.sb("y", [P, T2, D])
        small_in, weights_in, mask_in = st.sem("small_in"), st.sem("weights_in"), st.sem("mask_in")
        mask_used, xn_ready, weighed = st.sem("mask_used"), st.sem("xn_ready"), st.sem("weighed")
        order = st.sem("vector_order")
        half_full, half_free = st.sem("half_mask_full"), st.sem("half_mask_free")
        pool_s = Steps(st.sem("pool_steps"), ["consts", "rms1", "rms2"])
        act_s = Steps(st.sem("act_steps"), ["sincos", "exp0", "exp1"] + [f"gelu{f}" for f in range(FT)])
        PE = (["w_rows", "slot_cols"] + [f"pickT{t}" for t in range(4)] + ["gather", "bias", "hT", "q", "k", "v", "qT", "kT"]
              + sum([[f"scores{t}", *[f"probT{t}{r}" for r in range(4)], f"av{t}"] for t in range(T2)], [])
              + ["oT", "proj", "h2T"] + [f"up{f}" for f in range(FT)] + ["down"] + [f"scatter{t}" for t in range(B * TT)])
        pe_s = Steps(st.sem("pe_steps"), PE)
        ve_s = Steps(st.sem("vector_steps"), [
            n for n in ["wcol", "wrow", "slots", "cols", "pick", *[f"pickT{t}" for t in range(4)], "xs", "bias",
                        "sq1", "hn", "hT", "angles", "q", "k", "v", "qT", "kT"]
            + sum([[f"biased{t}", f"probs{t}", *[f"probT{t}{r}" for r in range(4)], f"o{t}"] for t in range(T2)], [])
            + ["oT", "x1", "sq2", "h2", "h2T", "y"] + [f"row{t}" for t in range(B * TT)]])
        block = st.block()

        @block.sync
        def _(sp):
            sp.dma_start(rw[:], dram["l0f_rw"].to_broadcast([P, D])).then_inc(small_in, 16)
            sp.dma_start(rb[:], dram["l0f_rb"].to_broadcast([P, 1])).then_inc(small_in, 16)
            sp.dma_start(freq[:], dram["rope_freq"].to_broadcast([P, HD // 2])).then_inc(small_in, 16)
            sp.dma_start(pos[:], dram["pos"]).then_inc(small_in, 16)
            sp.dma_start(base[:], dram["slot_base"]).then_inc(small_in, 16)
            sp.dma_start(ln1[:], dram["l0f_ln1"]).then_inc(small_in, 16)
            sp.dma_start(ln2[:], dram["l0f_ln2"]).then_inc(small_in, 16)
            for dst, name in ((wq, "l0f_wq"), (wk, "l0f_wk"), (wv, "l0f_wv"), (wo, "l0f_wo"), (w1, "l0f_w1"), (w2, "l0f_w2")):
                sp.dma_start(dst[:], dram[name].rearrange("(c p) n -> p c n", p=P)).then_inc(weights_in, 16)
            with sp.Fori(0, B) as b:
                sp.wait_ge(mask_used, b + 1)
                sp.dma_start(mask[:], dram["attention_mask"][b].rearrange("(j p) s -> p j s", p=P)).then_inc(mask_in, 16)

        @block.gpsimd
        def _(pool):
            nc.gpsimd.memset(ones[:], 1.0)
            nc.gpsimd.iota(iota[:], [[1, P]], base=0, channel_multiplier=0, allow_small_or_imprecise_dtypes=True)
            nc.gpsimd.memset(q[:], 0.0)
            pool_s.done(nc.gpsimd.memset(k[:], 0.0), "consts")
            with pool.Fori(0, B) as b:
                norm.pool(pool, b)
            for n in (1, 2):
                ve_s.wait(pool, f"sq{n}")
                pool_s.done(nc.gpsimd.tensor_tensor(rms[:], ss[:], core.neg_half[:, 0:T2], ALU.pow), f"rms{n}")

        @block.scalar
        def _(act):
            ve_s.wait(act, "angles")
            nc.scalar.activation(sin[:], ang[:], ACT.Sin)
            act_s.done(nc.scalar.activation(cos[:], ang[:], ACT.Sin, scale=0.5), "sincos")
            for t in range(T2):
                ve_s.wait(act, f"biased{t}")
                act_s.done(nc.scalar.activation(prob[:], prob[:], ACT.Exp), f"exp{t}")
            for f in range(FT):
                pe_s.wait(act, f"up{f}")
                act_s.done(nc.scalar.activation(gT[:, f, :], core.ps[:, f % 4, 0:T2 * P], ACT.Gelu_apprx_tanh), f"gelu{f}")

        @block.tensor
        def _(pe):
            ident = core.ident
            ps = core.ps
            pe.sem_inc(mask_used, 1)
            ve_s.wait(pe, "wcol")
            for j in range(TT):
                last = nc.tensor.transpose(ps[0:B, 0, j * P:(j + 1) * P], wcol[:, j, :], ident[:])
            pe_s.done(last, "w_rows")
            ve_s.wait(pe, "slots")
            for n, rows in enumerate((work, above)):
                for j in range(TT):
                    last = nc.tensor.transpose(ps[:, 1, n * 16 + j * B:n * 16 + (j + 1) * B], rows[:, j * P:(j + 1) * P],
                                               ident[0:B, 0:B])
            pe_s.done(last, "slot_cols")
            ve_s.wait(pe, "pick")
            for b in range(B):
                for j in range(TT):
                    last = nc.tensor.transpose(ps[:, 2 + b, j * P:(j + 1) * P], pick[:, b * TT + j, :], ident[:])
                pe_s.done(last, f"pickT{b}")
            for t in range(T2):
                for n in range(2 * TT):
                    last = nc.tensor.matmul(ps[:, 6 + t, 0:NA], pick[:, t * 2 * TT + n, :], xa[:, t * 2 * TT + n, :],
                                            start=(n == 0), stop=(n == 2 * TT - 1))
            pe_s.done(last, "gather")
            with pe.Fori(0, B) as b:
                pe.wait_ge(mask_in, b * 16 + 16)
                pe.wait_ge(half_free, b + 1)
                for kt in range(TT):
                    for j in range(TT):
                        last = nc.tensor.matmul(ps[:, 0, kt * P:(kt + 1) * P], mask[:, j, kt * P:(kt + 1) * P],
                                                pick[:, b * TT + j, :], start=(j == 0), stop=(j == TT - 1))
                last.then_inc(half_full, 1)
                pe.wait_ge(half_free, b + 2)
                pe.sem_inc(mask_used, 1)
            for t in range(T2):
                for n in range(2 * TT):
                    last = nc.tensor.matmul(ps[:, 1, t * P:(t + 1) * P], half_mask[:, t * 2 * TT + n, :],
                                            pick[:, t * 2 * TT + n, :], start=(n == 0), stop=(n == 2 * TT - 1))
            pe_s.done(last, "bias")
            ve_s.wait(pe, "hn")

            def turn(src, bank, name):
                for c in range(DC):
                    for t in range(T2):
                        last = nc.tensor.transpose(ps[:, bank, (c * T2 + t) * P:(c * T2 + t + 1) * P],
                                                   src[:, t, c * P:(c + 1) * P], ident[:])
                pe_s.done(last, name)

            turn(hn, 2, "hT")
            ve_s.wait(pe, "hT")
            pe.wait_ge(weights_in, 16 * 6)
            for bank, w, name in ((3, wq, "q"), (4, wk, "k"), (5, wv, "v")):
                for t in range(T2):
                    for c in range(DC):
                        last = nc.tensor.matmul(ps[:, bank, t * D:(t + 1) * D], hT[:, c, t * P:(t + 1) * P], w[:, c, :],
                                                start=(c == 0), stop=(c == DC - 1))
                pe_s.done(last, name)
            for src, bank, name in ((q, 6, "q"), (k, 0, "k")):
                ve_s.wait(pe, name)
                if name == "k":
                    ve_s.wait(pe, "bias")
                    pe.wait_ge(half_free, B + 1)
                for t in range(T2):
                    for g in range(HG):
                        last = nc.tensor.transpose(ps[:, bank + t, g * P:(g + 1) * P],
                                                   src[:, t, g * HG:(g + 1) * HG, :], ident[:])
                pe_s.done(last, name + "T")
            ve_s.wait(pe, "v")
            for t in range(T2):
                ve_s.wait(pe, "kT")
                if t:
                    ve_s.wait(pe, "o0")
                for r in range(4):
                    for g in range(HG):
                        last = nc.tensor.matmul(ps[:, 2 + r, g * P:(g + 1) * P],
                                                qT[r * STRIP:(r + 1) * STRIP, g, t * P:(t + 1) * P],
                                                kT[r * STRIP:(r + 1) * STRIP, g, t * P:(t + 1) * P], start=True, stop=True,
                                                tile_position=(r * STRIP, 0))
                pe_s.done(last, f"scores{t}")
                ve_s.wait(pe, f"probs{t}")
                for r in range(4):
                    for n in range(4):
                        last = nc.tensor.transpose(ps[:, 2 + r, n * P:(n + 1) * P], prob[:, r * 4 + n, :], ident[:])
                    pe_s.done(last, f"probT{t}{r}")
                ve_s.wait(pe, f"probT{t}3")
                for h in range(H):
                    n = (h % HG) * 4 + h // HG
                    last = nc.tensor.matmul(ps[:, 6, h * HD:(h + 1) * HD], probT[:, n, :], v[:, t, h * HD:(h + 1) * HD],
                                            start=True, stop=True)
                pe_s.done(last, f"av{t}")
            ve_s.wait(pe, "o1")
            turn(o, 7, "oT")
            ve_s.wait(pe, "oT")
            for t in range(T2):
                for c in range(DC):
                    last = nc.tensor.matmul(ps[:, 0, t * D:(t + 1) * D], oT[:, c, t * P:(t + 1) * P], wo[:, c, :],
                                            start=(c == 0), stop=(c == DC - 1))
            pe_s.done(last, "proj")
            ve_s.wait(pe, "h2")
            turn(hn, 1, "h2T")
            ve_s.wait(pe, "h2T")
            for f in range(FT):
                if f >= 4:
                    act_s.wait(pe, f"gelu{f - 4}")
                for c in range(DC):
                    last = nc.tensor.matmul(ps[:, f % 4, 0:T2 * P], w1[:, c, f * P:(f + 1) * P], hT[:, c, :],
                                            start=(c == 0), stop=(c == DC - 1))
                pe_s.done(last, f"up{f}")
            act_s.wait(pe, f"gelu{FT - 1}")
            for t in range(T2):
                for f in range(FT):
                    last = nc.tensor.matmul(ps[:, 4, t * D:(t + 1) * D], gT[:, f, t * P:(t + 1) * P], w2[:, f, :],
                                            start=(f == 0), stop=(f == FT - 1))
            pe_s.done(last, "down")
            ve_s.wait(pe, "y")
            for t in range(B * TT):
                if t >= 4:
                    ve_s.wait(pe, f"row{t - 4}")
                pe_s.done(nc.tensor.matmul(ps[:, t % 4, 0:D], pickT[:, t, :], y[:, t // (2 * TT), :], start=True, stop=True),
                          f"scatter{t}")

        @block.vector
        def _(dve):
            ps = core.ps
            V = nc.vector
            dve.sem_inc(half_free, 1)
            V.memset(bar[0:HALF, 0:HALF - 1], 0.0)
            V.memset(bar[0:HALF, HALF - 1:P], NEG)
            V.memset(bar[HALF:P, 0:HALF], NEG)
            V.memset(bar[HALF:P, HALF:P - 1], 0.0)
            V.memset(bar[HALF:P, P - 1:P], NEG)
            dve.wait_ge(small_in, 16 * 7)
            with dve.Fori(0, B) as b:
                norm.vector(dve, b, lambda j: core.x[:, b * TT + j, :], lambda j: xa[:, b * TT + j, 0:D], xn_ready)
                dve.wait_ge(xn_ready, b + 1)
                for j in range(TT):
                    last = V.scalar_tensor_tensor(out=junk[:, j, :], in0=xa[:, b * TT + j, 0:D], scalar=1.0, in1=rw[:],
                                                  op0=ALU.mult, op1=ALU.mult, accum_out=xa[:, b * TT + j, D:D + 1])
                last.then_inc(weighed, 1)
                dve.wait_ge(weighed, b + 1)
            link = Chain(dve, order)
            link(V.tensor_copy(xa[:, :, D + 1], pos[:]))
            link(V.tensor_scalar(xa[:, :, D], xa[:, :, D], rb[:, 0:1], None, ALU.add))
            ve_s.done(V.tensor_copy(wcol[:].rearrange("p j b -> p b j"), xa[:, :, D].rearrange("p (b j) -> p b j", b=B)),
                      "wcol")
            pe_s.wait(dve, "w_rows")
            link(V.tensor_copy(wrow[:], ps[0:B, 0, :]))
            ve_s.done(V.tensor_copy(work[:], ps[0:B, 0, :]), "wrow")
            ve_s.wait(dve, "wrow")
            for n in range(K // 8 - 1):
                eight = top[:, n * 8:n * 8 + 8]
                link(V.max(eight, work[:]))
                link(V.match_replace(work[:], eight, work[:], NEG))
            link(V.max(top[:, K - 8:K], work[:]))
            link(V.tensor_copy(last8[:], top[:, K - 8:K]))
            link(V.memset(last8[:, 7:8], NEG))
            link(V.match_replace(work[:], last8[:], work[:], NEG))
            link(V.tensor_tensor(chosen[:], work[:], wrow[:], ALU.not_equal))
            link(V.tensor_scalar(above[:], wrow[:], top[:, K - 1:K], None, ALU.is_gt))
            pool_s.wait(dve, "consts")
            link(V.tensor_tensor_scan(work[:], ones[:], chosen[:], 0.0, ALU.mult, ALU.add))
            link(V.scalar_tensor_tensor(out=work[:], in0=work[:], scalar=base[:, 0:1], in1=chosen[:],
                                        op0=ALU.add, op1=ALU.mult))
            ve_s.done(V.tensor_scalar(work[:], work[:], -1.0, None, ALU.add), "slots")
            pe_s.wait(dve, "slot_cols")
            V.tensor_copy(slot[:].rearrange("p b j -> p j b"), ps[:, 1, 0:16].rearrange("p (j b) -> p j b", b=B))
            ve_s.done(V.tensor_scalar(keep[:].rearrange("p b j -> p j b"), ps[:, 1, 16:32].rearrange("p (j b) -> p j b", b=B),
                                      -1.0, 1.0, ALU.mult, ALU.add), "cols")
            ve_s.wait(dve, "cols")
            for t in range(B * TT):
                last = V.tensor_scalar(pick[:, t, :], iota[:], slot[:, t // TT, t % TT:t % TT + 1], None, ALU.is_equal)
            ve_s.done(last, "pick")
            for b in range(B):
                pe_s.wait(dve, f"pickT{b}")
                ve_s.done(V.tensor_copy(pickT[:, b * TT:(b + 1) * TT, :], ps[:, 2 + b, :]), f"pickT{b}")
            pe_s.wait(dve, "gather")
            ve_s.done(V.tensor_copy(xs[:], ps[:, 6:8, 0:NA]), "xs")
            with dve.Fori(0, B) as b:
                dve.wait_ge(half_full, b + 1)
                V.tensor_copy(half_mask[:, bass.ds(b * TT, TT), :], ps[:, 0, :].rearrange("p (k s) -> p k s", s=P)
                              ).then_inc(half_free, 1)
            pe_s.wait(dve, "bias")
            ve_s.done(V.tensor_tensor(bias[:], ps[:, 1, 0:T2 * P].rearrange("p (t s) -> p t s", s=P),
                                      bar[:].unsqueeze(1).to_broadcast([P, T2, P]), ALU.add), "bias")

            def rms_norm(src, n, name):
                for t in range(T2):
                    last = V.scalar_tensor_tensor(out=junk[:, t, :], in0=src[:, t, 0:D], scalar=1.0, in1=src[:, t, 0:D],
                                                  op0=ALU.mult, op1=ALU.mult, accum_out=ss[:, t:t + 1])
                link(last)
                ve_s.done(V.tensor_scalar(ss[:], ss[:], 1.0 / D, 1e-6, ALU.mult, ALU.add), f"sq{n}")
                pool_s.wait(dve, f"rms{n}")
                for t in range(T2):
                    last = V.tensor_scalar(hn[:, t, :], src[:, t, 0:D], rms[:, t:t + 1], None, ALU.mult)
                ve_s.done(last, name)

            def gained(bank, gain, name):
                for c in range(DC):
                    last = V.tensor_scalar(hT[:, c, :], ps[:, bank, c * T2 * P:(c + 1) * T2 * P], gain[:, c:c + 1],
                                           None, ALU.mult)
                ve_s.done(last, name)

            ve_s.wait(dve, "xs")
            rms_norm(xs, 1, "hn")
            pe_s.wait(dve, "hT")
            gained(2, ln1, "hT")
            for t in range(T2):
                last = V.tensor_scalar(ang[:, t, 0:8], freq[:], xs[:, t, D + 1:D + 2], None, ALU.mult)
            link(last)
            link(V.tensor_scalar(turns[:, :, 0:8], ang[:, :, 0:8], 0.15915494309189535, ROUND, ALU.mult, ALU.add))
            link(V.tensor_scalar(turns[:, :, 0:8], turns[:, :, 0:8], ROUND, None, ALU.subtract))
            for part in (6.28125, 0.0019350051879882812, 3.019916050e-07):
                link(V.scalar_tensor_tensor(out=ang[:, :, 0:8], in0=turns[:, :, 0:8], scalar=-part, in1=ang[:, :, 0:8],
                                            op0=ALU.mult, op1=ALU.add))
            link(V.tensor_scalar(ang[:, :, 0:8], ang[:, :, 0:8], 3.1415925, -3.1415925, ALU.min, ALU.max))
            ve_s.done(V.tensor_copy(ang[:, :, 8:16], ang[:, :, 0:8]), "angles")
            act_s.wait(dve, "sincos")
            link(V.tensor_scalar(sin[:, :, 0:8], sin[:, :, 0:8], -1.0, None, ALU.mult))
            link(V.tensor_tensor(cos[:], cos[:], cos[:], ALU.mult))
            link(V.tensor_scalar(cos[:], cos[:], -2.0, 1.0, ALU.mult, ALU.add))
            for bank, dst, name in ((3, q, "q"), (4, k, "k")):
                pe_s.wait(dve, name)
                for t in range(T2):
                    src = ps[:, bank, t * D:(t + 1) * D].rearrange("p (h d) -> p h d", h=H)
                    for lo, hi in ((0, 8), (8, 0)):
                        last = V.tensor_tensor(rot[:, :, lo:lo + 8], src[:, :, hi:hi + 8],
                                               sin[:, t, lo:lo + 8].unsqueeze(1).to_broadcast([P, H, 8]), ALU.mult)
                    last = V.tensor_tensor(dst[:, t, :, 0:HD], src, cos[:, t, :].unsqueeze(1).to_broadcast([P, H, HD]),
                                           ALU.mult)
                    link(last)
                    last = V.tensor_tensor(dst[:, t, :, 0:HD], dst[:, t, :, 0:HD], rot[:], ALU.add)
                    if t == 0:
                        link(last)
                ve_s.done(last, name)
                ve_s.wait(dve, name)
            pe_s.wait(dve, "v")
            ve_s.done(V.tensor_copy(v[:], ps[:, 5, :].rearrange("p (t d) -> p t d", t=T2)), "v")
            for bank, dst, name in ((6, qT, "qT"), (0, kT, "kT")):
                pe_s.wait(dve, name)
                for t in range(T2):
                    last = V.tensor_copy(dst[:, :, t * P:(t + 1) * P], ps[:, bank + t, :].rearrange("p (g s) -> p g s", g=HG))
                ve_s.done(last, name)
            for t in range(T2):
                pe_s.wait(dve, f"scores{t}")
                for r in range(4):
                    last = V.scalar_tensor_tensor(out=prob[:, r * 4:r * 4 + 4, :],
                                                  in0=ps[:, 2 + r, :].rearrange("p (g s) -> p g s", g=HG), scalar=HD ** -0.5,
                                                  in1=bias[:, t, :].unsqueeze(1).to_broadcast([P, HG, P]),
                                                  op0=ALU.mult, op1=ALU.add)
                link(last)
                link(V.tensor_reduce(mx[:], prob[:], AX, ALU.max))
                ve_s.done(V.tensor_tensor(prob[:], prob[:], mx[:].unsqueeze(2).to_broadcast([P, H, P]), ALU.subtract),
                          f"biased{t}")
                act_s.wait(dve, f"exp{t}")
                link(V.tensor_reduce(total[:], prob[:], AX, ALU.add))
                link(V.reciprocal(inv[:], total[:]))
                ve_s.done(V.tensor_tensor(prob[:], prob[:], inv[:].unsqueeze(2).to_broadcast([P, H, P]), ALU.mult),
                          f"probs{t}")
                for r in range(4):
                    pe_s.wait(dve, f"probT{t}{r}")
                    ve_s.done(V.tensor_copy(probT[:, r * 4:r * 4 + 4, :], ps[:, 2 + r, :].rearrange("p (g s) -> p g s", g=4)),
                              f"probT{t}{r}")
                pe_s.wait(dve, f"av{t}")
                ve_s.done(V.tensor_copy(o[:, t, :], ps[:, 6, 0:D]), f"o{t}")
            pe_s.wait(dve, "oT")
            ve_s.done(V.tensor_copy(oT[:], ps[:, 7, :].rearrange("p (c s) -> p c s", c=DC)), "oT")
            pe_s.wait(dve, "proj")
            ve_s.done(V.tensor_tensor(x1[:], xs[:, :, 0:D], ps[:, 0, :].rearrange("p (t d) -> p t d", t=T2), ALU.add), "x1")
            ve_s.wait(dve, "x1")
            rms_norm(x1, 2, "h2")
            pe_s.wait(dve, "h2T")
            gained(1, ln2, "h2T")
            pe_s.wait(dve, "down")
            link(V.tensor_tensor(x1[:], x1[:], ps[:, 4, :].rearrange("p (t d) -> p t d", t=T2), ALU.add))
            for t in range(T2):
                last = V.tensor_scalar(y[:, t, :], x1[:, t, :], xs[:, t, D:D + 1], None, ALU.mult)
            ve_s.done(last, "y")
            for t in range(B * TT):
                link(V.scalar_tensor_tensor(out=junk[:, t % TT, :], in0=xa[:, t, 0:D], scalar=keep[:, t // TT, t % TT:t % TT + 1],
                                            in1=core.x[:, t, :], op0=ALU.mult, op1=ALU.add))
                pe_s.wait(dve, f"scatter{t}")
                ve_s.done(V.tensor_tensor(core.x[:, t, :], junk[:, t % TT, :], ps[:, t % 4, 0:D], ALU.add), f"row{t}")


def causal_attention_stage(core):
    nc, dram = core.nc, core.dram
    SCALE = D ** -0.5
    with Stage(core, "l1x") as st:
        norm = Norm(st)
        xn = st.sb("xn", [P, TT, D])
        xnT = st.sb("xnT", [P, DC, S])
        ctx = st.sb("ctx", [P, 2, TT, D])
        ctxT = st.sb("ctxT", [P, 2, DC, S])
        future = st.sb("future", [P, P])
        prob = st.sb("prob", [P, TT, S])
        probT = st.sb("probT", [P, 2, S])
        top, shift, total, inv = (st.sb(n, [P, TT]) for n in ("top", "shift", "total", "inv"))
        ctx_in = [st.sem(f"ctx_in{i}") for i in range(2)]
        xn_ready, zeroed, future_made = st.sem("xn_ready"), st.sem("zeroed"), st.sem("future_made")
        row_used = st.sem("rows_done")
        pe_s = Steps(st.sem("pe_steps"), ["xT"] + [f"scores{q}" for q in range(TT)]
                     + sum([[f"turned{q}", f"out{q}"] for q in range(TT)], []))
        ve_s = Steps(st.sem("vector_steps"), ["xT"] + sum([[f"masked{q}", f"max{q}", f"shift{q}"] for q in range(TT)], [])
                     + sum([[f"probT{q}", f"inv{q}", f"row{q}"] for q in range(TT)], []))
        act_s = Steps(st.sem("act_steps"), [f"exp{q}" for q in range(TT)])
        block = st.block()

        @block.sync
        def _(sp):
            with sp.Fori(0, B // 2) as pair:
                for i in range(2):
                    sp.wait_ge(row_used, pair * 2 + i + 1)
                    sp.dma_start(ctx[:, i, :, :], dram["ctx"][pair * 2 + i].rearrange("(j p) d -> p j d", p=P)).then_inc(ctx_in[i], 16)
                    sp.dma_start(ctxT[:, i, :, :], dram["ctxT"][pair * 2 + i].rearrange("(c p) s -> p c s", p=P)).then_inc(ctx_in[i], 16)

        @block.gpsimd
        def _(pool):
            nc.gpsimd.memset(future[:], 0.0).then_inc(zeroed, 1)
            pool.wait_ge(zeroed, 1)
            nc.gpsimd.affine_select(out=future[:], in_=future[:], compare_op=ALU.is_ge, fill=NEG,
                                    base=0, pattern=[[-1, P]], channel_multiplier=1).then_inc(future_made, 1)
            with pool.Fori(0, B) as b:
                norm.pool(pool, b)

        @block.tensor
        def _(pe):
            ps = core.ps
            pe.sem_inc(row_used, 2)
            with pe.Fori(0, B // 2) as pair:
                for i in range(2):
                    b = pair * 2 + i
                    pe.wait_ge(xn_ready, b + 1)
                    for c in range(DC):
                        for j in range(TT):
                            last = nc.tensor.transpose(ps[:, 6 + c, j * P:(j + 1) * P], xn[:, j, c * P:(c + 1) * P], core.ident[:])
                    pe_s.done(last, "xT")
                    pe.wait_ge(ctx_in[i], pair * 32 + 32)
                    ve_s.wait(pe, "xT", b)
                    for q in range(TT):
                        for c in range(DC):
                            last = nc.tensor.matmul(ps[:, q, 0:(q + 1) * P], xnT[:, c, q * P:(q + 1) * P],
                                                    ctxT[:, i, c, 0:(q + 1) * P], start=(c == 0), stop=(c == DC - 1))
                        pe_s.done(last, f"scores{q}")
                    for q in range(TT):
                        act_s.wait(pe, f"exp{q}", b)
                        if q >= 2:
                            ve_s.wait(pe, f"probT{q - 2}", b)
                        for k in range(q + 1):
                            last = nc.tensor.transpose(ps[:, 4 + q % 2, k * P:(k + 1) * P], prob[:, q, k * P:(k + 1) * P],
                                                       core.ident[:])
                        pe_s.done(last, f"turned{q}")
                        ve_s.wait(pe, f"probT{q}", b)
                        if q >= 2:
                            ve_s.wait(pe, f"row{q - 2}", b)
                        for k in range(q + 1):
                            last = nc.tensor.matmul(ps[:, 6 + q % 2, 0:D], probT[:, q % 2, k * P:(k + 1) * P],
                                                    ctx[:, i, k, :], start=(k == 0), stop=(k == q))
                        pe_s.done(last, f"out{q}")
                    ve_s.wait(pe, f"row{TT - 1}", b)
                    pe.sem_inc(row_used, 1)

        @block.scalar
        def _(act):
            with act.Fori(0, B) as b:
                for q in range(TT):
                    ve_s.wait(act, f"shift{q}", b)
                    act_s.done(nc.scalar.activation(prob[:, q, 0:(q + 1) * P], core.ps[:, q, 0:(q + 1) * P], ACT.Exp,
                                                    bias=shift[:, q:q + 1], scale=SCALE, accum_out=total[:, q:q + 1]),
                               f"exp{q}")

        @block.vector
        def _(dve):
            ps, V = core.ps, nc.vector
            dve.wait_ge(future_made, 1)
            with dve.Fori(0, B) as b:
                norm.vector(dve, b, lambda j: core.x[:, b * TT + j, :], lambda j: xn[:, j, :], xn_ready)
                pe_s.wait(dve, "xT", b)
                ve_s.done(V.tensor_copy(xnT[:], ps[:, 6:8, :]), "xT")
                for q in range(TT):
                    pe_s.wait(dve, f"scores{q}", b)
                    own = ps[:, q, q * P:(q + 1) * P]
                    ve_s.done(V.tensor_tensor(own, own, future[:], ALU.add), f"masked{q}")
                    ve_s.wait(dve, f"masked{q}", b)
                    ve_s.done(V.tensor_reduce(top[:, q:q + 1], ps[:, q, 0:(q + 1) * P], AX, ALU.max), f"max{q}")
                    ve_s.wait(dve, f"max{q}", b)
                    ve_s.done(V.tensor_scalar(shift[:, q:q + 1], top[:, q:q + 1], -SCALE, None, ALU.mult), f"shift{q}")
                for q in range(TT):
                    pe_s.wait(dve, f"turned{q}", b)
                    ve_s.done(V.tensor_copy(probT[:, q % 2, 0:(q + 1) * P], ps[:, 4 + q % 2, 0:(q + 1) * P]), f"probT{q}")
                    act_s.wait(dve, f"exp{q}", b)
                    ve_s.done(V.reciprocal(inv[:, q:q + 1], total[:, q:q + 1]), f"inv{q}")
                    ve_s.wait(dve, f"inv{q}", b)
                    pe_s.wait(dve, f"out{q}", b)
                    row = core.x[:, b * TT + q, :]
                    ve_s.done(V.scalar_tensor_tensor(out=row, in0=ps[:, 6 + q % 2, 0:D], scalar=inv[:, q:q + 1], in1=row,
                                                     op0=ALU.mult, op1=ALU.add), f"row{q}")


def quantised_ffn_stage(core):
    nc, dram = core.nc, core.dram
    F = 704
    FT = -(-F // P)
    rows = [min(P, F - f * P) for f in range(FT)]
    QMAX = 127.0
    SLOTS = 3
    with Stage(core, "l1f") as st:
        norm = Norm(st)
        xn = st.sb("xn", [P, B * TT, D])
        hT = st.sb("hT", [P, FT, B * S])
        hq = st.sb("hq", [P, FT, S], BF16)
        silu = st.sb("silu", [P, SLOTS, S])
        xr = st.sb("xr", [P, TT, D])
        hr = st.sb("hr", [P, FT, S])
        xq = st.sb("xq", [P, TT, D], BF16)
        xqT = st.sb("xqT", [P, DC, S], BF16)
        ident = st.sb("ident16", [P, P], BF16)
        ones = st.sb("ones", [P, P])
        wraw = {n: st.sb(f"{n}_raw", [P, FT, D]) for n in ("gate", "up")}
        wraw["down"] = st.sb("down_raw", [P, DC, F])
        wmax = {n: st.sb(f"{n}_max", [P, DC if n == "down" else FT]) for n in wraw}
        winv = {n: st.sb(f"{n}_inv", [P, DC if n == "down" else FT]) for n in wraw}
        wlev = {n: st.sb(f"{n}_levels", list(wraw[n].shape), BF16) for n in wraw}
        wT = {n: st.sb(f"{n}T", [P, DC, F] if n != "down" else [P, FT, D], BF16) for n in wraw}
        gate_scale, up_scale = st.sb("gate_scale", [P, FT]), st.sb("up_scale", [P, FT])
        diag = st.sb("diag", [P, D])
        down_row, out_row = st.sb("down_row", [P, D]), st.sb("out_row", [P, D])
        clip = st.sb("clip", [P, 2])
        ratio = st.sb("ratio", [P, 2])
        xmax, hmax = st.sb("xmax", [P, B * TT]), st.sb("hmax", [P, B])
        own, whole, scale, inv = (st.sb(n, [P, 2]) for n in ("own", "whole", "scale", "inv"))
        part = st.sb("part", [P, TT, D])
        small_in, weights_in = st.sem("small_in"), st.sem("weights_in")
        xn_ready, max_ready, order = st.sem("xn_ready"), st.sem("max_ready"), st.sem("vector_order")
        act_ratio, ident_made, pool_max = st.sem("act_ratio"), st.sem("ident_made"), st.sem("pool_max")
        own_ready = st.sem("own_max_ready")
        pe_w = Steps(st.sem("pe_weight_steps"), ["gate0", "gate1", "up0", "up1", "down0", "down1", "down_row"])
        ve_w = Steps(st.sem("vector_weight_steps"), ["gate", "up", "down", "gate0", "gate1", "up0", "up1", "down0", "down1",
                                                     "diag", "down_row"])
        xq_ready, xT_full, xT_ready = st.sem("xq_ready"), st.sem("xT_full"), st.sem("xT_ready")
        both_full, silu_ready, hidden_ready = st.sem("gate_up_full"), st.sem("silu_ready"), st.sem("hidden_ready")
        hq_ready, down_full, rows_out = st.sem("hq_ready"), st.sem("down_full"), st.sem("rows_out")
        ve_x = st.sem("quantise_x_order")
        ve_h = st.sem("quantise_h_order")
        ve_r = st.sem("row_order")
        block = st.block()

        @block.sync
        def _(sp):
            for n in ("gate", "up"):
                sp.dma_start(wraw[n][:, 0:FT - 1, :], dram[f"l1f_{n}"][0:(FT - 1) * P, :].rearrange("(f p) d -> p f d", p=P)
                             ).then_inc(weights_in, 16)
                sp.dma_start(wraw[n][0:rows[-1], FT - 1, :], dram[f"l1f_{n}"][(FT - 1) * P:F, :]).then_inc(weights_in, 16)
            sp.dma_start(wraw["down"][:], dram["l1f_down"].rearrange("(c p) n -> p c n", p=P)).then_inc(weights_in, 16)
            for i, n in enumerate(("l1f_clip_x", "l1f_clip_down")):
                sp.dma_start(clip[:, i:i + 1], dram[n].to_broadcast([P, 1])).then_inc(small_in, 16)

        @block.gpsimd
        def _(pool):
            nc.gpsimd.memset(ones[:], 1.0)
            nc.gpsimd.tensor_copy(ident[:], core.ident[:]).then_inc(ident_made, 1)
            with pool.Fori(0, B) as b:
                norm.pool(pool, b)
            for i in range(2):
                pool.wait_ge(own_ready, i + 1)
                nc.gpsimd.partition_all_reduce(whole[:, i:i + 1], own[:, i:i + 1], P, bass.bass_isa.ReduceOp.max
                                               ).then_inc(pool_max, 1)

        @block.scalar
        def _(act):
            act.wait_ge(small_in, 32)
            nc.scalar.activation(ratio[:], clip[:], ACT.Sigmoid).then_inc(act_ratio, 1)
            with act.Fori(0, B) as b:
                for f, m in enumerate(rows):
                    act.wait_ge(both_full, b * FT + f + 1)
                    act.wait_ge(hidden_ready, b * FT + max(f + 1, SLOTS))
                    nc.scalar.activation(silu[0:m, f % SLOTS, :], core.ps[0:m, 2 * (f % SLOTS), :], ACT.Silu,
                                         scale=gate_scale[0:m, f:f + 1]).then_inc(silu_ready, 1)

        @block.tensor
        def _(pe):
            ps = core.ps
            pe.wait_ge(ident_made, 1)
            for n in ("gate", "up"):
                ve_w.wait(pe, n)
                for c in range(DC):
                    for f, m in enumerate(rows):
                        last = nc.tensor.transpose(ps[:, c, :].bitcast(BF16)[:, f * P:f * P + m],
                                                   wlev[n][0:m, f, c * P:(c + 1) * P], ident[0:m, 0:m])
                    pe_w.done(last, f"{n}{c}")
                    ve_w.wait(pe, f"{n}{c}")
            ve_w.wait(pe, "down")
            for c in range(DC):
                for f, m in enumerate(rows):
                    last = nc.tensor.transpose(ps[0:m, c, :].bitcast(BF16)[:, f * P:(f + 1) * P],
                                               wlev["down"][:, c, f * P:f * P + m], ident[:])
                pe_w.done(last, f"down{c}")
            ve_w.wait(pe, "diag")
            pe_w.done(nc.tensor.matmul(ps[:, 2, 0:D], ones[:], diag[:], start=True, stop=True), "down_row")
            ve_w.wait(pe, "down_row")
            with pe.Fori(0, B) as b:
                pe.wait_ge(xq_ready, b + 1)
                for c in range(DC):
                    for j in range(TT):
                        last = nc.tensor.transpose(ps[:, 6, :].bitcast(BF16)[:, (c * TT + j) * P:(c * TT + j + 1) * P],
                                                   xq[:, j, c * P:(c + 1) * P], ident[:])
                last.then_inc(xT_full, 1)
                pe.wait_ge(xT_ready, b + 1)
                for f, m in enumerate(rows):
                    pe.wait_ge(hidden_ready, b * FT + max(f + 1, SLOTS))
                    for i, n in enumerate(("gate", "up")):
                        for c in range(DC):
                            last = nc.tensor.matmul(ps[0:m, 2 * (f % SLOTS) + i, :], wT[n][:, c, f * P:f * P + m],
                                                    xqT[:, c, :], start=(c == 0), stop=(c == DC - 1))
                    last.then_inc(both_full, 1)
            with pe.Fori(0, B) as b:
                pe.wait_ge(hq_ready, b + 1)
                for j in range(TT):
                    pe.wait_ge(rows_out, b * TT + max(j + 1, 2))
                    for f, m in enumerate(rows):
                        last = nc.tensor.matmul(ps[:, 6 + j % 2, 0:D], hq[0:m, f, j * P:(j + 1) * P], wT["down"][0:m, f, :],
                                                start=(f == 0), stop=(f == FT - 1))
                    last.then_inc(down_full, 1)

        @block.vector
        def _(dve):
            ps, V = core.ps, nc.vector
            dve.sem_inc(hidden_ready, SLOTS)
            dve.sem_inc(rows_out, 2)
            with dve.Fori(0, B) as b:
                norm.vector(dve, b, lambda j: core.x[:, b * TT + j, :], lambda j: xn[:, b * TT + j, :], xn_ready)
                dve.wait_ge(xn_ready, b + 1)
                V.tensor_reduce(xmax[:, bass.ds(b * TT, TT)], xn[:, bass.ds(b * TT, TT), :], AX, ALU.max,
                                apply_absolute_value=True).then_inc(max_ready, 1)
            link = Chain(dve, order)

            def levels(link, dst, src, inv, tmp):
                link(V.tensor_scalar(tmp, src, inv, QMAX, ALU.mult, ALU.min))
                link(V.tensor_scalar(tmp, tmp, -QMAX - 1.0, ROUND, ALU.max, ALU.add))
                return V.tensor_scalar(dst, tmp, ROUND, None, ALU.subtract)

            def global_scale(i, maxima):
                link(V.tensor_reduce(own[:, i:i + 1], maxima, AX, ALU.max))
                V.tensor_copy(own[:, i:i + 1], own[:, i:i + 1]).then_inc(own_ready, 1)
                dve.wait_ge(pool_max, i + 1)
                link(V.tensor_tensor(scale[:, i:i + 1], whole[:, i:i + 1], ratio[:, i:i + 1], ALU.mult))
                link(V.tensor_scalar(scale[:, i:i + 1], scale[:, i:i + 1], 1.0 / QMAX, None, ALU.mult))
                link(V.reciprocal(inv[:, i:i + 1], scale[:, i:i + 1]))

            dve.wait_ge(max_ready, B)
            dve.wait_ge(act_ratio, 1)
            global_scale(0, xmax[:])
            dve.wait_ge(weights_in, 16 * 5)
            for n in ("gate", "up", "down"):
                tiles = [(c, P) for c in range(DC)] if n == "down" else list(enumerate(rows))
                for f, m in tiles:
                    link(V.tensor_reduce(wmax[n][0:m, f:f + 1], wraw[n][0:m, f, :], AX, ALU.max, apply_absolute_value=True))
                    link(V.tensor_scalar(wmax[n][0:m, f:f + 1], wmax[n][0:m, f:f + 1], 1.0 / QMAX, None, ALU.mult))
                    link(V.reciprocal(winv[n][0:m, f:f + 1], wmax[n][0:m, f:f + 1]))
                    last = levels(link, wlev[n][0:m, f, :], wraw[n][0:m, f, :], winv[n][0:m, f:f + 1], wraw[n][0:m, f, :])
                    if n != "down":
                        dst = gate_scale if n == "gate" else up_scale
                        V.tensor_scalar(dst[0:m, f:f + 1], wmax[n][0:m, f:f + 1], scale[0:m, 0:1], None, ALU.mult)
                ve_w.done(last, n)
            for n in ("gate", "up"):
                for c in range(DC):
                    pe_w.wait(dve, f"{n}{c}")
                    ve_w.done(V.tensor_copy(wT[n][:, c, :], ps[:, c, :].bitcast(BF16)[:, 0:F]), f"{n}{c}")
            for c in range(DC):
                pe_w.wait(dve, f"down{c}")
                turned = ps[:, c, :].bitcast(BF16)
                V.tensor_copy(wT["down"][:, 0:FT - 1, c * P:(c + 1) * P], turned[:, 0:(FT - 1) * P].rearrange("p (f n) -> p f n", n=P))
                ve_w.done(V.tensor_copy(wT["down"][0:rows[-1], FT - 1, c * P:(c + 1) * P], turned[0:rows[-1], (FT - 1) * P:FT * P]),
                          f"down{c}")
            for c in range(DC):
                last = V.tensor_scalar(diag[:, c * P:(c + 1) * P], core.ident[:], wmax["down"][:, c:c + 1], None, ALU.mult)
            ve_w.done(last, "diag")
            pe_w.wait(dve, "down_row")
            ve_w.done(V.tensor_copy(down_row[:], ps[:, 2, 0:D]), "down_row")
            V.memset(hT[rows[-1]:P, FT - 1, :], 0.0)
            with dve.Fori(0, B) as b:
                chain = Chain(dve, ve_x, b * 2)
                levels(chain, xq[:], xn[:, bass.ds(b * TT, TT), :], inv[:, 0:1], xr[:]).then_inc(xq_ready, 1)
                dve.wait_ge(xT_full, b + 1)
                V.tensor_copy(xqT[:], ps[:, 6, :].bitcast(BF16).rearrange("p (c s) -> p c s", c=DC)).then_inc(xT_ready, 1)
                for f, m in enumerate(rows):
                    dve.wait_ge(silu_ready, b * FT + f + 1)
                    V.scalar_tensor_tensor(out=hT[0:m, f, bass.ds(b * S, S)], in0=ps[0:m, 2 * (f % SLOTS) + 1, :],
                                           scalar=up_scale[0:m, f:f + 1], in1=silu[0:m, f % SLOTS, :],
                                           op0=ALU.mult, op1=ALU.mult).then_inc(hidden_ready, 1)
                dve.wait_ge(hidden_ready, (b + 1) * FT + SLOTS)
                V.tensor_reduce(hmax[:, bass.ds(b, 1)], hT[:, :, bass.ds(b * S, S)], mybir.AxisListType.XY, ALU.max,
                                apply_absolute_value=True).then_inc(max_ready, 1)
            dve.wait_ge(max_ready, 2 * B)
            global_scale(1, hmax[:])
            link(V.tensor_scalar(out_row[:], down_row[:], scale[:, 1:2], None, ALU.mult))
            with dve.Fori(0, B) as b:
                chain = Chain(dve, ve_h, b * 2)
                levels(chain, hq[:], hT[:, :, bass.ds(b * S, S)], inv[:, 1:2], hr[:]).then_inc(hq_ready, 1)
                for j in range(TT):
                    dve.wait_ge(down_full, b * TT + j + 1)
                    V.tensor_tensor(part[:, j, :], ps[:, 6 + j % 2, 0:D], out_row[:], ALU.mult).then_inc(rows_out, 1)
                    dve.wait_ge(rows_out, b * TT + j + 3)
                    row = core.x[:, b * TT + j, :]
                    last = V.tensor_tensor(row, row, part[:, j, :], ALU.add)
                last.then_inc(ve_r, 1)
                dve.wait_ge(ve_r, b + 1)


def autocorrelation_stage(core):
    nc, dram = core.nc, core.dram
    BEST = 12
    with Stage(core, "l2x") as st:
        norm = Norm(st)
        xn = st.sb("xn", [P, TT, D])
        xnT = st.sb("xnT", [P, DC, S])
        ctxT = st.sb("ctxT", [P, DC, S])
        wq, wk, wv, wo = (st.sb(n, [P, DC, D]) for n in ("wq", "wk", "wv", "wo"))
        bq, bk, bv, bo = (st.sb(n, [P, D]) for n in ("bq", "bk", "bv", "bo"))
        basis, inverse = st.sb("basis", [P, TT, S]), st.sb("inverse", [P, TT, S])
        qk = st.sb("qk", [P, TT, 2, D])
        qhat, junk = st.sb("qhat", [P, TT, D]), st.sb("junk", [P, TT, D])
        power = st.sb("power", [P, B, TT])
        power_b = st.sb("power_b", [P, TT, B])
        mean, work, chosen, gain = (st.sb(n, [B, S]) for n in ("mean", "work", "chosen", "gain"))
        eight, four = st.sb("eight", [B, 8]), st.sb("four", [B, 8])
        shift, total, inv = (st.sb(n, [B, 1]) for n in ("shift", "total", "inv"))
        circulant = st.sb("circulant", [P, B, TT, S])
        v = st.sb("v", [P, TT, D])
        aggT = st.sb("aggT", [P, DC, S])
        part = st.sb("part", [P, TT, D])
        rows = dram["delay_rows"]
        weights_in, bias_in, ctx_in, ctx_used = (st.sem(n) for n in ("weights_in", "bias_in", "ctx_in", "ctx_used"))
        xn_ready, order, rows_out, circulant_in = (st.sem(n) for n in ("xn_ready", "order", "rows_out", "circulant_in"))
        exp_done, summed = st.sem("exp_done"), st.sem("rows_summed")
        pe_a = Steps(st.sem("pe_spectrum_steps"), ["xT"] + [f"q{j}" for j in range(TT)] + [f"k{j}" for j in range(TT)]
                     + [f"hat{r}" for r in range(TT)])
        ve_a = Steps(st.sem("vector_spectrum_steps"), ["xT"] + [f"q{j}" for j in range(TT)] + [f"k{j}" for j in range(TT)]
                     + [f"power{r}" for r in range(TT)])
        act_a = Steps(st.sem("act_spectrum_steps"), [f"qhat{r}" for r in range(TT)])
        one = Steps(st.sem("pe_mean"), ["mean"])
        ve_m = Steps(st.sem("vector_mean_steps"), ["power", "shift", "gain"])
        pe_b = Steps(st.sem("pe_shift_steps"), [f"v{j}" for j in range(TT)] + [f"agg{c}" for c in range(DC)]
                     + [f"out{j}" for j in range(TT)])
        ve_b = Steps(st.sem("vector_shift_steps"), [f"v{j}" for j in range(TT)] + [f"agg{c}" for c in range(DC)]
                     + [f"out{j}" for j in range(TT)])
        block = st.block()

        @block.sync
        def _(sp):
            for dst, name in ((wq, "l2x_Wq"), (wk, "l2x_Wk"), (wv, "l2x_Wv"), (wo, "l2x_Wo"),
                              (basis, "dft_basis"), (inverse, "dft_inverse")):
                sp.dma_start(dst[:], dram[name].rearrange("(c p) n -> p c n", p=P)).then_inc(weights_in, 16)
            for dst, name in ((bq, "l2x_bq"), (bk, "l2x_bk"), (bv, "l2x_bv"), (bo, "l2x_bo")):
                sp.dma_start(dst[:], dram[name].to_broadcast([P, D])).then_inc(bias_in, 16)
            with sp.Fori(0, B) as b:
                sp.wait_ge(ctx_used, b + 1)
                sp.dma_start(ctxT[:], dram["ctxT"][b].rearrange("(c p) s -> p c s", p=P)).then_inc(ctx_in, 16)
            ve_m.wait(sp, "gain")
            for i in range(2):
                sp.dma_start(rows[:, i * S:(i + 1) * S], gain[:]).then_inc(rows_out, 16)
            sp.wait_ge(rows_out, 32)
            for b in range(B):
                for j in range(TT):
                    src = bass.AP(tensor=rows.tensor, offset=b * 2 * S + S - j * P - (P - 1), ap=[[1, P], [1, S]])
                    sp.dma_start(circulant[:, b, j, :], src).then_inc(circulant_in, 16)
            with sp.Fori(0, B) as b:
                sp.wait_ge(ctx_used, b + 1 + B)
                sp.dma_start(ctxT[:], dram["ctxT_back"][b].rearrange("(c p) s -> p c s", p=P)).then_inc(ctx_in, 16)

        @block.gpsimd
        def _(pool):
            with pool.Fori(0, B) as b:
                norm.pool(pool, b)

        @block.scalar
        def _(act):
            with act.Fori(0, B) as b:
                for r in range(TT):
                    pe_a.wait(act, f"hat{r}", b)
                    act_a.done(nc.scalar.activation(qhat[:, r, :], core.ps[:, r, 0:D], ACT.Copy), f"qhat{r}")
            ve_m.wait(act, "shift")
            nc.scalar.activation(gain[:], mean[:], ACT.Exp, bias=shift[:, 0:1]).then_inc(exp_done, 1)

        @block.tensor
        def _(pe):
            ps = core.ps
            pe.sem_inc(ctx_used, 1)
            pe.wait_ge(weights_in, 16 * 6)
            with pe.Fori(0, B) as b:
                pe.wait_ge(xn_ready, b + 1)
                for c in range(DC):
                    for j in range(TT):
                        last = nc.tensor.transpose(ps[:, 4 + c, j * P:(j + 1) * P], xn[:, j, c * P:(c + 1) * P], core.ident[:])
                pe_a.done(last, "xT")
                pe.wait_ge(ctx_in, b * 16 + 16)
                ve_a.wait(pe, "xT", b)
                for i, (src, w, name) in enumerate(((xnT, wq, "q"), (ctxT, wk, "k"))):
                    for j in range(TT):
                        n = i * TT + j
                        if n >= 2:
                            ve_a.wait(pe, f"{'qk'[(n - 2) // TT]}{(n - 2) % TT}", b)
                        for c in range(DC):
                            last = nc.tensor.matmul(ps[:, 6 + n % 2, 0:D], src[:, c, j * P:(j + 1) * P], w[:, c, :],
                                                    start=(c == 0), stop=(c == DC - 1))
                        pe_a.done(last, f"{name}{j}")
                ve_a.wait(pe, f"k{TT - 1}", b)
                pe.sem_inc(ctx_used, 1)
                for r in range(TT):
                    for j in range(TT):
                        last = nc.tensor.matmul(ps[:, r, :], basis[:, j, r * P:(r + 1) * P], qk[:, j, :, :],
                                                start=(j == 0), stop=(j == TT - 1))
                    pe_a.done(last, f"hat{r}")
                ve_a.wait(pe, f"power{TT - 1}", b)
            ve_m.wait(pe, "power")
            for r in range(TT):
                last = nc.tensor.matmul(ps[0:B, 0, :], power_b[:, r, :], inverse[:, r, :], start=(r == 0), stop=(r == TT - 1))
            one.done(last, "mean")
            pe.wait_ge(circulant_in, 16 * B * TT)
            with pe.Fori(0, B) as b:
                pe.wait_ge(ctx_in, b * 16 + 16 + B * 16)
                for j in range(TT):
                    if j >= 2:
                        ve_b.wait(pe, f"v{j - 2}", b)
                    for c in range(DC):
                        last = nc.tensor.matmul(ps[:, 6 + j % 2, 0:D], ctxT[:, c, j * P:(j + 1) * P], wv[:, c, :],
                                                start=(c == 0), stop=(c == DC - 1))
                    pe_b.done(last, f"v{j}")
                ve_b.wait(pe, f"v{TT - 1}", b)
                pe.sem_inc(ctx_used, 1)
                for c in range(DC):
                    for j in range(TT):
                        last = nc.tensor.matmul(ps[:, 4 + c, :], v[:, j, c * P:(c + 1) * P], circulant[:, b, j, :],
                                                start=(j == 0), stop=(j == TT - 1))
                    pe_b.done(last, f"agg{c}")
                ve_b.wait(pe, f"agg{DC - 1}", b)
                for j in range(TT):
                    for c in range(DC):
                        last = nc.tensor.matmul(ps[:, j, 0:D], aggT[:, c, j * P:(j + 1) * P], wo[:, c, :],
                                                start=(c == 0), stop=(c == DC - 1))
                    pe_b.done(last, f"out{j}")
                ve_b.wait(pe, f"out{TT - 1}", b)

        @block.vector
        def _(dve):
            ps, V = core.ps, nc.vector
            dve.wait_ge(bias_in, 16 * 4)
            with dve.Fori(0, B) as b:
                norm.vector(dve, b, lambda j: core.x[:, b * TT + j, :], lambda j: xn[:, j, :], xn_ready)
                pe_a.wait(dve, "xT", b)
                ve_a.done(V.tensor_copy(xnT[:], ps[:, 4:6, :]), "xT")
                for i, (name, bias) in enumerate((("q", bq), ("k", bk))):
                    for j in range(TT):
                        pe_a.wait(dve, f"{name}{j}", b)
                        ve_a.done(V.tensor_tensor(qk[:, j, i, :], ps[:, 6 + j % 2, 0:D], bias[:], ALU.add), f"{name}{j}")
                for r in range(TT):
                    act_a.wait(dve, f"qhat{r}", b)
                    ve_a.done(V.scalar_tensor_tensor(out=junk[:, r, :], in0=ps[:, r, D:2 * D], scalar=1.0, in1=qhat[:, r, :],
                                                     op0=ALU.mult, op1=ALU.mult, accum_out=power[:, b, r:r + 1]), f"power{r}")
                ve_a.wait(dve, f"power{TT - 1}", b)
            ve_m.done(V.tensor_copy(power_b[:].rearrange("p r b -> p b r"), power[:]), "power")
            one.wait(dve, "mean")
            link = Chain(dve, order)
            link(V.tensor_copy(mean[:], ps[0:B, 0, :]))
            link(V.max(eight[:], mean[:]))
            ve_m.done(V.tensor_scalar(shift[:], eight[:, 0:1], -1.0, None, ALU.mult), "shift")
            link(V.match_replace(work[:], eight[:], mean[:], NEG))
            link(V.max(four[:], work[:]))
            link(V.memset(four[:, BEST - 8:8], NEG))
            link(V.match_replace(work[:], four[:], work[:], NEG))
            link(V.tensor_tensor(chosen[:], work[:], mean[:], ALU.not_equal))
            dve.wait_ge(exp_done, 1)
            link(V.tensor_tensor(gain[:], gain[:], chosen[:], ALU.mult))
            link(V.tensor_reduce(total[:], gain[:], AX, ALU.add))
            link(V.reciprocal(inv[:], total[:]))
            ve_m.done(V.tensor_scalar(gain[:], gain[:], inv[:, 0:1], None, ALU.mult), "gain")
            with dve.Fori(0, B) as b:
                for j in range(TT):
                    pe_b.wait(dve, f"v{j}", b)
                    ve_b.done(V.tensor_tensor(v[:, j, :], ps[:, 6 + j % 2, 0:D], bv[:], ALU.add), f"v{j}")
                for c in range(DC):
                    pe_b.wait(dve, f"agg{c}", b)
                    ve_b.done(V.tensor_copy(aggT[:, c, :], ps[:, 4 + c, :]), f"agg{c}")
                for j in range(TT):
                    pe_b.wait(dve, f"out{j}", b)
                    ve_b.done(V.tensor_tensor(part[:, j, :], ps[:, j, 0:D], bo[:], ALU.add), f"out{j}")
                ve_b.wait(dve, f"out{TT - 1}", b)
                rows_now = core.x[:, bass.ds(b * TT, TT), :]
                V.tensor_tensor(rows_now, rows_now, part[:], ALU.add).then_inc(summed, 1)
                dve.wait_ge(summed, b + 1)


class Router:

    def __init__(self, st, name):
        self.st, self.nc, self.core, self.w_name = st, st.nc, st.core, name
        self.norm = Norm(st)
        self.xn = st.sb("xn", [P, TT, D])
        self.xnT = st.sb("xnT", [P, DC, S])
        self.xT = st.sb("xT", [P, B, DC, S])
        self.w = st.sb("w_router", [P, DC, 8])
        self.logits = st.sb("logits", [P, B * TT, 8])
        self.probs = st.sb("probs", [P, B * TT, 16])
        self.marked = st.sb("marked", [P, B * TT, 16])
        self.best = st.sb("best", [P, B * TT, 8])
        self.chosen = st.sb("chosen", [P, B * TT, 8])
        self.top, self.total, self.inv = (st.sb(n, [P, B * TT]) for n in ("top", "total", "inv"))
        self.w_in, self.xn_ready, self.order = st.sem("router_in"), st.sem("xn_ready"), st.sem("router_order")
        self.pe = Steps(st.sem("pe_router_steps"), ["xT", "logits"])
        self.ve = Steps(st.sem("vector_router_steps"), ["xT", "logits"])
        self.kept = st.sem("xT_kept")
        self.centred, self.exp_done = st.sem("centred"), st.sem("exp_done")

    def sync(self, sp):
        sp.dma_start(self.w[:], self.core.dram[self.w_name].rearrange("(c p) n -> p c n", p=P)).then_inc(self.w_in, 16)

    def pool(self, pool):
        with pool.Fori(0, B) as b:
            self.norm.pool(pool, b)

    def tensor(self, pe):
        nc, ps = self.nc, self.core.ps
        pe.wait_ge(self.w_in, 16)
        with pe.Fori(0, B) as b:
            pe.wait_ge(self.xn_ready, b + 1)
            for c in range(DC):
                for j in range(TT):
                    last = nc.tensor.transpose(ps[:, c, j * P:(j + 1) * P], self.xn[:, j, c * P:(c + 1) * P], self.core.ident[:])
            self.pe.done(last, "xT")
            self.ve.wait(pe, "xT", b)
            for j in range(TT):
                for c in range(DC):
                    last = nc.tensor.matmul(ps[:, 2, j * 8:(j + 1) * 8], self.xnT[:, c, j * P:(j + 1) * P], self.w[:, c, :],
                                            start=(c == 0), stop=(c == DC - 1))
            self.pe.done(last, "logits")
            self.ve.wait(pe, "logits", b)

    def scalar(self, act):
        nc = self.nc
        with act.Fori(0, B) as b:
            self.ve.wait(act, "xT", b)
            nc.scalar.activation(self.xT[:, b, :, :], self.xnT[:], ACT.Copy).then_inc(self.kept, 1)
        act.wait_ge(self.centred, 1)
        nc.scalar.activation(self.logits[:], self.logits[:], ACT.Exp).then_inc(self.exp_done, 1)

    def vector(self, dve):
        V, ps = self.nc.vector, self.core.ps
        with dve.Fori(0, B) as b:
            self.norm.vector(dve, b, lambda j: self.core.x[:, b * TT + j, :], lambda j: self.xn[:, j, :], self.xn_ready)
            self.pe.wait(dve, "xT", b)
            dve.wait_ge(self.xn_ready, b + 1)
            self.ve.done(V.tensor_copy(self.xnT[:], ps[:, 0:2, :]), "xT")
            self.pe.wait(dve, "logits", b)
            dve.wait_ge(self.kept, b + 1)
            self.ve.done(V.tensor_copy(self.logits[:, bass.ds(b * TT, TT), :],
                                       ps[:, 2, 0:TT * 8].rearrange("p (j e) -> p j e", e=8)), "logits")
        self.ve.wait(dve, "logits", B - 1)
        link = Chain(dve, self.order)
        shape = [P, B * TT, 8]
        link(V.tensor_reduce(self.top[:], self.logits[:], AX, ALU.max))
        V.tensor_tensor(self.logits[:], self.logits[:], self.top[:].unsqueeze(2).to_broadcast(shape), ALU.subtract
                        ).then_inc(self.centred, 1)
        dve.wait_ge(self.exp_done, 1)
        link(V.tensor_reduce(self.total[:], self.logits[:], AX, ALU.add))
        link(V.reciprocal(self.inv[:], self.total[:]))
        link(V.memset(self.probs[:, :, 8:16], -1.0))
        link(V.tensor_tensor(self.probs[:, :, 0:8], self.logits[:], self.inv[:].unsqueeze(2).to_broadcast(shape), ALU.mult))
        for t in range(B * TT):
            last = V.max(self.best[:, t, :], self.probs[:, t, :])
        link(last)
        link(V.tensor_tensor(self.total[:], self.best[:, :, 0], self.best[:, :, 1], ALU.add))
        link(V.memset(self.best[:, :, 2:8], -1.0))
        for t in range(B * TT):
            last = V.match_replace(self.marked[:, t, :], self.best[:, t, :], self.probs[:, t, :], 2.0)
        link(last)
        link(V.tensor_tensor(self.chosen[:], self.marked[:, :, 0:8], self.probs[:, :, 0:8], ALU.not_equal))
        return link


def relu_experts_stage(core):
    nc, dram = core.nc, core.dram
    E, FT = 10, 2
    ROUND_E = 2
    UNITS = ROUND_E * B
    with Stage(core, "l2f") as st:
        router = Router(st, "l2f_router")
        w1 = st.sb("w1", [P, ROUND_E, DC, FT * P])
        w2 = st.sb("w2", [P, ROUND_E, FT, D])
        weight = st.sb("weight", [P, B * TT, E])
        relu = st.sb("relu", [P, 2, FT, S])
        hT = st.sb("hT", [P, 2, FT, S])
        weights_in = [st.sem(f"weights_in{i}") for i in range(ROUND_E)]
        weights_used = [st.sem(f"weights_used{i}") for i in range(ROUND_E)]
        up_full, relu_ready, hidden_ready = st.sem("up_full"), st.sem("relu_ready"), st.sem("hidden_ready")
        down_full, rows_done, weighed = st.sem("down_full"), st.sem("rows_done"), st.sem("weighed")
        block = st.block()

        @block.sync
        def _(sp):
            router.sync(sp)
            with sp.Fori(0, E // ROUND_E) as r:
                for i in range(ROUND_E):
                    sp.wait_ge(weights_used[i], r + 1)
                    sp.dma_start(w1[:, i, :, :], dram["l2f_w1"][r * ROUND_E + i].rearrange("(c p) f -> p c f", p=P)
                                 ).then_inc(weights_in[i], 16)
                    sp.dma_start(w2[:, i, :, :], dram["l2f_w2"][r * ROUND_E + i].rearrange("(c p) f -> p c f", p=P)
                                 ).then_inc(weights_in[i], 16)

        @block.gpsimd
        def _(pool):
            router.pool(pool)

        @block.tensor
        def _(pe):
            ps = core.ps
            for i in range(ROUND_E):
                pe.sem_inc(weights_used[i], 1)
            router.tensor(pe)
            with pe.Fori(0, E // ROUND_E) as r:
                def up(u):
                    i, b = divmod(u, B)
                    if b == 0:
                        pe.wait_ge(weights_in[i], r * 32 + 32)
                    for f in range(FT):
                        n = u * FT + f
                        pe.wait_ge(relu_ready, (r * UNITS) * FT + n + 1)
                        for c in range(DC):
                            last = nc.tensor.matmul(ps[:, n % 4, :], w1[:, i, c, f * P:(f + 1) * P], router.xT[:, b, c, :],
                                                    start=(c == 0), stop=(c == DC - 1))
                        last.then_inc(up_full, 1)

                def down(u):
                    i, b = divmod(u, B)
                    pe.wait_ge(hidden_ready, (r * UNITS + u + 1) * FT + 4)
                    for j in range(TT):
                        pe.wait_ge(rows_done, (r * UNITS + u) * TT + j + 1)
                        for f in range(FT):
                            last = nc.tensor.matmul(ps[:, 4 + j, 0:D], hT[:, u % 2, f, j * P:(j + 1) * P], w2[:, i, f, :],
                                                    start=(f == 0), stop=(f == FT - 1))
                        last.then_inc(down_full, 1)
                    if b == B - 1:
                        pe.wait_ge(rows_done, (r * UNITS + u) * TT + TT + 4)
                        pe.sem_inc(weights_used[i], 1)

                up(0)
                for u in range(UNITS):
                    if u + 1 < UNITS:
                        up(u + 1)
                    down(u)

        @block.scalar
        def _(act):
            act.sem_inc(relu_ready, 4)
            router.scalar(act)
            with act.Fori(0, E // ROUND_E) as r:
                for u in range(UNITS):
                    for f in range(FT):
                        n = u * FT + f
                        act.wait_ge(up_full, r * UNITS * FT + n + 1)
                        act.wait_ge(hidden_ready, r * UNITS * FT + n + 1)
                        nc.scalar.activation(relu[:, u % 2, f, :], core.ps[:, n % 4, :], ACT.Relu).then_inc(relu_ready, 1)

        @block.vector
        def _(dve):
            ps, V = core.ps, nc.vector
            dve.sem_inc(hidden_ready, 4)
            dve.sem_inc(rows_done, 4)
            link = router.vector(dve)
            link(V.reciprocal(router.inv[:], router.total[:]))
            link(V.tensor_tensor(router.chosen[:], router.chosen[:], router.probs[:, :, 0:8], ALU.mult))
            link(V.memset(weight[:, :, 8:E], 1.0))
            link(V.tensor_tensor(weight[:, :, 0:8], router.chosen[:],
                                 router.inv[:].unsqueeze(2).to_broadcast([P, B * TT, 8]), ALU.mult))
            with dve.Fori(0, E // ROUND_E) as r:
                def square(u):
                    for f in range(FT):
                        n = u * FT + f
                        dve.wait_ge(relu_ready, r * UNITS * FT + n + 1 + 4)
                        if u >= 2:
                            dve.wait_ge(down_full, (r * UNITS + u - 1) * TT)
                        V.tensor_tensor(hT[:, u % 2, f, :], relu[:, u % 2, f, :], relu[:, u % 2, f, :], ALU.mult
                                        ).then_inc(hidden_ready, 1)

                def add(u):
                    i, b = divmod(u, B)
                    for j in range(TT):
                        t = b * TT + j
                        dve.wait_ge(down_full, (r * UNITS + u) * TT + j + 1)
                        dve.wait_ge(rows_done, (r * UNITS + u) * TT + j + 1)
                        V.scalar_tensor_tensor(out=core.x[:, t, :], in0=ps[:, 4 + j, 0:D],
                                               scalar=weight[:, t, bass.ds(r * ROUND_E + i, 1)], in1=core.x[:, t, :],
                                               op0=ALU.mult, op1=ALU.add).then_inc(rows_done, 1)

                square(0)
                for u in range(UNITS):
                    if u + 1 < UNITS:
                        square(u + 1)
                    add(u)


def gated_experts_stage(core):
    nc, dram = core.nc, core.dram
    E, F = 8, 704
    FT = -(-F // P)
    rows = [min(P, F - f * P) for f in range(FT)]
    ROUND_E = 2
    UNITS = ROUND_E * B
    with Stage(core, "l3f") as st:
        router = Router(st, "l3f_router")
        w1, w3 = (st.sb(n, [P, ROUND_E, DC, F]) for n in ("w1", "w3"))
        w2 = st.sb("w2", [P, ROUND_E, FT, D])
        score = st.sb("score", [P, E, B * TT])
        scoreT = st.sb("scoreT", [P, P])
        scores = st.sb("scores", [P, ROUND_E, B, S])
        xe = st.sb("xe", [P, 2, DC, S])
        silu = st.sb("silu", [P, 2, S])
        hT = st.sb("hT", [P, 2, FT, S])
        weights_in = [st.sem(f"weights_in{i}") for i in range(ROUND_E)]
        weights_used = [st.sem(f"weights_used{i}") for i in range(ROUND_E)]
        scores_ready, scoreT_full, scoreT_ready, scores_out = (
            st.sem(n) for n in ("scores_ready", "scoreT_full", "scoreT_ready", "scores_out"))
        xe_ready, both_full, silu_ready, hidden_ready = (
            st.sem(n) for n in ("xe_ready", "both_full", "silu_ready", "hidden_ready"))
        down_full, rows_done = st.sem("down_full"), st.sem("rows_done")
        block = st.block()

        @block.sync
        def _(sp):
            router.sync(sp)
            sp.wait_ge(scoreT_ready, 1)
            sp.dma_start(dram["score_rows"].rearrange("e (t p) -> (e t) p", p=P), scoreT[:]).then_inc(scores_out, 16)
            sp.wait_ge(scores_out, 16)
            with sp.Fori(0, E // ROUND_E) as r:
                for i in range(ROUND_E):
                    e = r * ROUND_E + i
                    sp.wait_ge(weights_used[i], r + 1)
                    for dst, name in ((w1, "l3f_w1"), (w3, "l3f_w3")):
                        sp.dma_start(dst[:, i, :, :], dram[name][e].rearrange("(c p) f -> p c f", p=P)
                                     ).then_inc(weights_in[i], 16)
                    sp.dma_start(scores[:, i, :, :], dram["score_rows"][bass.ds(e, 1), :].to_broadcast([P, B * S])
                                 ).then_inc(weights_in[i], 16)
                    sp.dma_start(w2[:, i, 0:FT - 1, :], dram["l3f_w2"][e, 0:(FT - 1) * P, :].rearrange("(f p) d -> p f d", p=P)
                                 ).then_inc(weights_in[i], 16)
                    sp.dma_start(w2[0:rows[-1], i, FT - 1, :], dram["l3f_w2"][e, (FT - 1) * P:F, :]).then_inc(weights_in[i], 16)

        @block.gpsimd
        def _(pool):
            router.pool(pool)

        @block.tensor
        def _(pe):
            ps = core.ps
            for i in range(ROUND_E):
                pe.sem_inc(weights_used[i], 1)
            router.tensor(pe)
            pe.wait_ge(scores_ready, 1)
            nc.tensor.transpose(ps[:, 3, 0:P], score[:].rearrange("p e t -> p (e t)"), core.ident[:]).then_inc(scoreT_full, 1)
            pe.wait_ge(scoreT_ready, 1)
            with pe.Fori(0, E // ROUND_E) as r:
                def up(u):
                    i, b = divmod(u, B)
                    if b == 0:
                        pe.wait_ge(weights_in[i], r * 80 + 80)
                    pe.wait_ge(xe_ready, r * UNITS + u + 1)
                    for f, m in enumerate(rows):
                        n = u * FT + f
                        pe.wait_ge(hidden_ready, r * UNITS * FT + n + 1)
                        for k, w in enumerate((w1, w3)):
                            for c in range(DC):
                                last = nc.tensor.matmul(ps[0:m, 2 * (n % 2) + k, :], w[:, i, c, f * P:f * P + m],
                                                        xe[:, u % 2, c, :], start=(c == 0), stop=(c == DC - 1))
                        last.then_inc(both_full, 1)

                def down(u):
                    i, b = divmod(u, B)
                    pe.wait_ge(hidden_ready, (r * UNITS + u + 1) * FT + 2)
                    for j in range(TT):
                        pe.wait_ge(rows_done, (r * UNITS + u) * TT + j + 1)
                        for f, m in enumerate(rows):
                            last = nc.tensor.matmul(ps[:, 4 + j, 0:D], hT[0:m, u % 2, f, j * P:(j + 1) * P], w2[0:m, i, f, :],
                                                    start=(f == 0), stop=(f == FT - 1))
                        last.then_inc(down_full, 1)
                    if b == B - 1:
                        pe.wait_ge(rows_done, (r * UNITS + u) * TT + TT + 4)
                        pe.sem_inc(weights_used[i], 1)

                up(0)
                for u in range(UNITS):
                    if u + 1 < UNITS:
                        up(u + 1)
                    down(u)

        @block.scalar
        def _(act):
            router.scalar(act)
            with act.Fori(0, E // ROUND_E) as r:
                for u in range(UNITS):
                    for f, m in enumerate(rows):
                        n = u * FT + f
                        act.wait_ge(both_full, r * UNITS * FT + n + 1)
                        act.wait_ge(hidden_ready, r * UNITS * FT + n + 1)
                        nc.scalar.activation(silu[0:m, n % 2, :], core.ps[0:m, 2 * (n % 2), :], ACT.Silu).then_inc(silu_ready, 1)

        @block.vector
        def _(dve):
            ps, V = core.ps, nc.vector
            dve.sem_inc(hidden_ready, 2)
            dve.sem_inc(rows_done, 4)
            link = router.vector(dve)
            V.tensor_tensor(score[:].rearrange("p e t -> p t e"), router.chosen[:], router.probs[:, :, 0:8], ALU.mult
                            ).then_inc(scores_ready, 1)
            dve.wait_ge(scoreT_full, 1)
            V.tensor_copy(scoreT[:], ps[:, 3, 0:P]).then_inc(scoreT_ready, 1)
            with dve.Fori(0, E // ROUND_E) as r:
                def scale(u):
                    i, b = divmod(u, B)
                    if b == 0:
                        dve.wait_ge(weights_in[i], r * 80 + 80)
                    if u >= 2:
                        dve.wait_ge(both_full, (r * UNITS + u - 1) * FT)
                    V.tensor_tensor(xe[:, u % 2, :, :], router.xT[:, b, :, :],
                                    scores[:, i, b, :].unsqueeze(1).to_broadcast([P, DC, S]), ALU.mult).then_inc(xe_ready, 1)

                def gate(u):
                    for f, m in enumerate(rows):
                        n = u * FT + f
                        dve.wait_ge(silu_ready, r * UNITS * FT + n + 1)
                        if u >= 2 and f == 0:
                            dve.wait_ge(down_full, (r * UNITS + u - 1) * TT)
                        V.tensor_tensor(hT[0:m, u % 2, f, :], silu[0:m, n % 2, :], ps[0:m, 2 * (n % 2) + 1, :], ALU.mult
                                        ).then_inc(hidden_ready, 1)

                def add(u):
                    i, b = divmod(u, B)
                    for j in range(TT):
                        dve.wait_ge(down_full, (r * UNITS + u) * TT + j + 1)
                        dve.wait_ge(rows_done, (r * UNITS + u) * TT + j + 1)
                        V.tensor_tensor(core.x[:, b * TT + j, :], core.x[:, b * TT + j, :], ps[:, 4 + j, 0:D], ALU.add
                                        ).then_inc(rows_done, 1)

                scale(0)
                for u in range(UNITS):
                    if u + 1 < UNITS:
                        scale(u + 1)
                    if u == 0:
                        gate(0)
                    if u + 1 < UNITS:
                        gate(u + 1)
                    add(u)


def parallel_attention_stage(core):
    nc, dram = core.nc, core.dram
    H, HD = 16, 64
    HP = H // 2
    FT = 8
    UNITS = H * TT
    LAG_T, LAG_O = 3, 4
    RING = 2 * DC + 2 + HP + HP + HP + TT
    with Stage(core, "l3x") as st:
        norm1, norm2, normc = Norm(st), Norm(st, "_again"), Norm(st, "_ctx")
        wq, w1 = st.sb("wq", [P, DC, H * HD]), st.sb("w1", [P, DC, 2 * FT * P])
        wk, wv = st.sb("wk", [P, DC, P]), st.sb("wv", [P, DC, HD])
        wout, w2 = st.sb("wout", [P, HP, D]), st.sb("w2", [P, FT, D])
        gains = st.sb("gains", [P, 4, DC])
        xn = st.sb("xn", [P, TT, D])
        xn2 = st.sb("xn2", [P, TT, D])
        xnT, cnT = st.sb("xnT", [P, DC, S]), st.sb("cnT", [P, DC, S])
        ctx, mask = st.sb("ctx", [P, TT, D]), st.sb("mask", [P, TT, S])
        k_hi, k_lo = st.sb("k_hi", [P, S], F16), st.sb("k_lo", [P, S], F16)
        v = st.sb("v", [P, TT, HD])
        q2 = st.sb("q2", [P, H, S], F16)
        oT = st.sb("oT", [P, HP, S])
        silu = st.sb("silu", [P, 3, S])
        hT = st.sb("hT", [P, FT, S])
        biased = st.sb("biased", [P, 4, S])
        prob, probT = st.sb("prob", [P, 4, S]), st.sb("probT", [P, 4, S])
        neg_max, total, inv = (st.sb(n, [P, H, TT]) for n in ("neg_max", "total", "inv"))
        o = st.sb("o", [P, TT, H, HD])
        weights_in, small_in, ctx_in, mask_in = (st.sem(n) for n in ("weights_in", "small_in", "ctx_in", "mask_in"))
        batch_done = st.sem("batch_done")
        xn_ready, xn2_ready, cn_ready = st.sem("xn_ready"), st.sem("xn2_ready"), st.sem("cn_ready")
        ring_full, ring_free, hi_ready = st.sem("ring_full"), st.sem("ring_free"), st.sem("hi_ready")
        both_full, silu_ready, hidden_ready = st.sem("both_full"), st.sem("silu_ready"), st.sem("hidden_ready")
        scores_full, biased_ready, exp_done = st.sem("scores_full"), st.sem("biased_ready"), st.sem("exp_done")
        turned, out_done, inv_ready = st.sem("turned"), st.sem("out_done"), st.sem("inv_ready")
        copied = [st.sem("probT_by_act"), st.sem("probT_by_vector")]
        block = st.block()

        @block.sync
        def _(sp):
            for dst, name in ((wq, "l3x_wq"), (wk, "l3x_wk"), (wv, "l3x_wv"), (w1, "l3x_w1"), (wout, "l3x_wout"), (w2, "l3x_w2")):
                sp.dma_start(dst[:], dram[name].rearrange("(c p) n -> p c n", p=P)).then_inc(weights_in, 16)
            sp.dma_start(gains[:], dram["l3x_gains"]).then_inc(small_in, 16)
            with sp.Fori(0, B) as b:
                sp.wait_ge(batch_done, b + 1)
                sp.dma_start(ctx[:], dram["ctx"][b].rearrange("(j p) d -> p j d", p=P)).then_inc(ctx_in, 16)
                sp.dma_start(mask[:], dram["mask"][b].rearrange("(j p) s -> p j s", p=P)).then_inc(mask_in, 16)

        @block.gpsimd
        def _(pool):
            with pool.Fori(0, B) as b:
                norm1.pool(pool, b)
                norm2.pool(pool, b)
                normc.pool(pool, b)

        @block.tensor
        def _(pe):
            ps = core.ps
            pe.sem_inc(batch_done, 1)
            pe.sem_inc(turned, 4)
            pe.sem_inc(out_done, 4)
            pe.wait_ge(weights_in, 16 * 6)
            with pe.Fori(0, B) as b:
                ring = [0]

                def claim():
                    n = ring[0]
                    ring[0] += 1
                    pe.wait_ge(ring_free, b * RING + n + 1)
                    return 6 + n % 2

                def emptied():
                    pe.wait_ge(ring_free, b * RING + ring[0] + 2)

                for src, ready in ((xn2, xn2_ready), (ctx, cn_ready)):
                    pe.wait_ge(ready, b + 1)
                    for c in range(DC):
                        transpose_tokens(nc, core, src, claim(), c, ring_full)
                emptied()
                bank = claim()
                for c in range(DC):
                    last = nc.tensor.matmul(ps[:, bank, :], wk[:, c, :], cnT[:, c, :], start=(c == 0), stop=(c == DC - 1))
                last.then_inc(ring_full, 1)
                bank = claim()
                for j in range(TT):
                    for c in range(DC):
                        last = nc.tensor.matmul(ps[:, bank, j * HD:(j + 1) * HD], cnT[:, c, j * P:(j + 1) * P], wv[:, c, :],
                                                start=(c == 0), stop=(c == DC - 1))
                last.then_inc(ring_full, 1)
                for g in range(HP):
                    bank = claim()
                    for c in range(DC):
                        last = nc.tensor.matmul(ps[:, bank, :], wq[:, c, g * P:(g + 1) * P], xnT[:, c, :],
                                                start=(c == 0), stop=(c == DC - 1))
                    last.then_inc(ring_full, 1)
                for f in range(FT):
                    pe.wait_ge(hidden_ready, b * FT + max(f + 1, 3))
                    for i in range(2):
                        for c in range(DC):
                            last = nc.tensor.matmul(ps[:, 2 * (f % 3) + i, :], w1[:, c, (i * FT + f) * P:(i * FT + f + 1) * P],
                                                    xnT[:, c, :], start=(c == 0), stop=(c == DC - 1))
                    last.then_inc(both_full, 1)
                emptied()
                pe.wait_ge(hidden_ready, (b + 1) * FT + 3)

                for u in range(UNITS + LAG_O):
                    if u < UNITS:
                        h, j = divmod(u, TT)
                        pe.wait_ge(biased_ready, b * UNITS + u + 1)
                        for part, k in enumerate((k_hi, k_lo)):
                            last = nc.tensor.matmul(ps[:, u % 2, :], q2[:, h, j * P:(j + 1) * P], k[:],
                                                    start=(part == 0), stop=(part == 1))
                        last.then_inc(scores_full, 1)
                    t = u - LAG_T
                    if 0 <= t < UNITS:
                        pe.wait_ge(exp_done, b * UNITS + t + 1 + 4)
                        pe.wait_ge(copied[t % 2], b * (UNITS // 2) + t // 2 + 1)
                        for s in range(TT):
                            last = nc.tensor.transpose(ps[:, 2 + t % 4, s * P:(s + 1) * P], prob[:, t % 4, s * P:(s + 1) * P],
                                                       core.ident[:])
                        last.then_inc(turned, 1)
                    n = u - LAG_O
                    if n >= 0:
                        h, j = divmod(n, TT)
                        if n % (2 * TT) == 0:
                            bank = claim()
                        pe.wait_ge(copied[n % 2], b * (UNITS // 2) + n // 2 + 1 + 2)
                        at = ((h % 2) * TT + j) * HD
                        for s in range(TT):
                            last = nc.tensor.matmul(ps[:, bank, at:at + HD], probT[:, n % 4, s * P:(s + 1) * P], v[:, s, :],
                                                    start=(s == 0), stop=(s == TT - 1))
                        last.then_inc(out_done, 1)
                emptied()
                for g in range(HP):
                    bank = claim()
                    for j in range(TT):
                        last = nc.tensor.transpose(ps[:, bank, j * P:(j + 1) * P], o[:, j, 2 * g:2 * g + 2, :], core.ident[:])
                    last.then_inc(ring_full, 1)
                emptied()
                for j in range(TT):
                    bank = claim()
                    for g in range(HP):
                        nc.tensor.matmul(ps[:, bank, 0:D], oT[:, g, j * P:(j + 1) * P], wout[:, g, :], start=(g == 0), stop=False)
                    for f in range(FT):
                        last = nc.tensor.matmul(ps[:, bank, 0:D], hT[:, f, j * P:(j + 1) * P], w2[:, f, :],
                                                start=False, stop=(f == FT - 1))
                    last.then_inc(ring_full, 1)
                emptied()
                pe.sem_inc(batch_done, 1)
                assert ring[0] == RING

        @block.scalar
        def _(act):
            ps = core.ps
            act.sem_inc(exp_done, 4)
            act.sem_inc(copied[0], 2)
            with act.Fori(0, B) as b:
                act.wait_ge(ring_full, b * (RING - HP) + 2 * DC + 1)
                nc.scalar.activation(k_hi[:], ps[:, 6 + 2 * DC % 2, :], ACT.Copy).then_inc(hi_ready, 1)
                for g in range(HP):
                    n = 2 * DC + 2 + g
                    act.wait_ge(ring_full, b * (RING - HP) + n + 1)
                    for i in range(2):
                        last = nc.scalar.activation(q2[0:HD, 2 * g + i, :], ps[i * HD:(i + 1) * HD, 6 + n % 2, :], ACT.Copy,
                                                    scale=HD ** -0.5)
                    last.then_inc(hi_ready, 1)
                for f in range(FT):
                    act.wait_ge(both_full, b * FT + f + 1)
                    act.wait_ge(hidden_ready, b * FT + max(f + 1, 3))
                    nc.scalar.activation(silu[:, f % 3, :], ps[:, 2 * (f % 3) + 1, :], ACT.Silu).then_inc(silu_ready, 1)
                for u in range(UNITS + LAG_T):
                    if u < UNITS:
                        act.wait_ge(biased_ready, b * UNITS + u + 1 + 2)
                        act.wait_ge(turned, b * UNITS + u + 1)
                        nc.scalar.activation(prob[:, u % 4, :], biased[:, u % 4, :], ACT.Exp, scale=-1.0,
                                             bias=neg_max[:, u // TT, u % TT:u % TT + 1],
                                             accum_out=total[:, u // TT, u % TT:u % TT + 1]).then_inc(exp_done, 1)
                    t = u - LAG_T
                    if t >= 0 and t % 2 == 0:
                        act.wait_ge(turned, b * UNITS + t + 1 + 4)
                        act.wait_ge(out_done, b * UNITS + t + 1)
                        nc.scalar.activation(probT[:, t % 4, :], ps[:, 2 + t % 4, :], ACT.Copy).then_inc(copied[0], 1)

        @block.vector
        def _(dve):
            ps, V = core.ps, nc.vector
            dve.sem_inc(ring_free, 2)
            dve.sem_inc(hidden_ready, 3)
            dve.sem_inc(biased_ready, 2)
            dve.sem_inc(copied[1], 2)
            dve.wait_ge(small_in, 16)
            with dve.Fori(0, B) as b:
                ring, full = [0], [0]

                def take():
                    ring[0] += 1
                    full[0] += 1
                    dve.wait_ge(ring_full, b * (RING - HP) + full[0])
                    return 6 + (ring[0] - 1) % 2

                norm1.vector(dve, b, lambda j: core.x[:, b * TT + j, :], lambda j: xn[:, j, :], xn_ready)
                dve.wait_ge(xn_ready, b + 1)
                norm2.vector(dve, b, lambda j: xn[:, j, :], lambda j: xn2[:, j, :], xn2_ready)
                dve.wait_ge(ctx_in, b * 16 + 16)
                normc.vector(dve, b, lambda j: ctx[:, j, :], lambda j: ctx[:, j, :], cn_ready)
                for k, dst in enumerate((xnT, cnT)):
                    for c in range(DC):
                        V.tensor_scalar(dst[:, c, :], ps[:, take(), :], gains[:, 2 * k, c:c + 1], gains[:, 2 * k + 1, c:c + 1],
                                        ALU.mult, ALU.add).then_inc(ring_free, 1)
                bank = take()
                dve.wait_ge(hi_ready, b * (HP + 1) + 1)
                V.tensor_tensor(k_lo[:], ps[:, bank, :], k_hi[:], ALU.subtract).then_inc(ring_free, 1)
                V.tensor_copy(v[:], ps[:, take(), 0:TT * HD].rearrange("p (j d) -> p j d", j=TT)).then_inc(ring_free, 1)
                for g in range(HP):
                    bank = take()
                    dve.wait_ge(hi_ready, b * (HP + 1) + g + 2)
                    for i in range(2):
                        last = V.scalar_tensor_tensor(out=q2[HD:P, 2 * g + i, :], in0=ps[i * HD:(i + 1) * HD, bank, :],
                                                      scalar=HD ** -0.5, in1=q2[0:HD, 2 * g + i, :],
                                                      op0=ALU.mult, op1=ALU.subtract)
                    last.then_inc(ring_free, 1)
                for f in range(FT):
                    dve.wait_ge(silu_ready, b * FT + f + 1)
                    V.tensor_tensor(hT[:, f, :], silu[:, f % 3, :], ps[:, 2 * (f % 3), :], ALU.mult).then_inc(hidden_ready, 1)
                dve.wait_ge(mask_in, b * 16 + 16)

                def rows(g):
                    ring[0] += 1
                    bank = 6 + (ring[0] - 1) % 2
                    dve.wait_ge(out_done, b * UNITS + 2 * TT * (g + 1) + 4)
                    V.reciprocal(inv[:, 2 * g:2 * g + 2, :], total[:, 2 * g:2 * g + 2, :]).then_inc(inv_ready, 1)
                    dve.wait_ge(inv_ready, b * HP + g + 1)
                    for i in range(2):
                        last = V.tensor_tensor(o[:, :, 2 * g + i, :],
                                               ps[:, bank, i * TT * HD:(i + 1) * TT * HD].rearrange("p (j d) -> p j d", d=HD),
                                               inv[:, 2 * g + i, :].unsqueeze(2).to_broadcast([P, TT, HD]), ALU.mult)
                    last.then_inc(ring_free, 1)

                for u in range(UNITS + LAG_T):
                    if u < UNITS:
                        h, j = divmod(u, TT)
                        dve.wait_ge(scores_full, b * UNITS + u + 1)
                        dve.wait_ge(exp_done, b * UNITS + u + 1)
                        dve.nop(nofuse=True)
                        V.tensor_tensor_reduce(out=biased[:, u % 4, :], in0=ps[:, u % 2, :], in1=mask[:, j, :], scale=-1.0,
                                               scalar=3.0e38, op0=ALU.add, op1=ALU.min,
                                               accum_out=neg_max[:, h, j:j + 1]).then_inc(biased_ready, 1)
                    t = u - LAG_T
                    if t >= 0 and t % 2 == 1:
                        dve.wait_ge(turned, b * UNITS + t + 1 + 4)
                        dve.wait_ge(out_done, b * UNITS + t + 1)
                        V.tensor_copy(probT[:, t % 4, :], ps[:, 2 + t % 4, :]).then_inc(copied[1], 1)
                    n = u - LAG_T - 3
                    if n >= 0 and n % (2 * TT) == 2 * TT - 1:
                        rows(n // (2 * TT))
                rows(HP - 1)
                for g in range(HP):
                    V.tensor_copy(oT[:, g, :], ps[:, take(), :]).then_inc(ring_free, 1)
                for j in range(TT):
                    V.tensor_tensor(core.x[:, b * TT + j, :], core.x[:, b * TT + j, :], ps[:, take(), 0:D], ALU.add
                                    ).then_inc(ring_free, 1)


def build(nc, dram, out):
    with ExitStack() as ctx:
        core = Core(nc, ctx, dram)
        load_stage(core)
        sigmoid_attention_stage(core)
        mixture_of_depths_stage(core)
        causal_attention_stage(core)
        quantised_ffn_stage(core)
        autocorrelation_stage(core)
        relu_experts_stage(core)
        parallel_attention_stage(core)
        gated_experts_stage(core)
        store_stage(core, out)


def lay_out(inputs):
    import numpy as np
    a = {k: np.asarray(v) for k, v in inputs.items()}

    def strips(w):
        return np.repeat(w.reshape(D, 16, 1, 16), 2, 2).reshape(D, 512)

    arrays = {
        "x": a["x"],
        "ctx": a["ctx_1024"],
        "ctxT": a["ctx_1024"].transpose(0, 2, 1),
        "ctxT_back": a["ctx_1024"].transpose(0, 2, 1).reshape(B, D, TT, P)[:, :, :, ::-1].reshape(B, D, S),
        "lo_rows": np.where(np.arange(P) % 32 < 16, 0.0, -1.0).astype(np.float32)[:, None],
        "l0x_wq": strips(a["L0_xattn_Wq"].T),
        "l0x_wk": strips(a["L0_xattn_Wk"].T),
        "l0x_wv": strips(a["L0_xattn_Wv"].T),
        "l0x_wo": strips(a["L0_xattn_Wo"]).T,
    }
    arrays |= {
        "pos": a["L0_ffn_position_ids"][:, 0:S].reshape(B, TT, P).transpose(2, 0, 1).reshape(P, B * TT),
        "attention_mask": a["L0_ffn_attention_mask"][:, 0, 0:S, 0:S],
        "slot_base": np.array([[0], [64], [0], [64]], np.float32),
        "rope_freq": (np.float32(1) / np.float32(10000) ** (np.arange(0, 16, 2, dtype=np.float32) / np.float32(16)))[None],
        "l0f_rw": a["L0_ffn_router_w"].T,
        "l0f_rb": a["L0_ffn_router_b"][None],
        "l0f_ln1": a["L0_ffn_ln1"].reshape(DC, P).T,
        "l0f_ln2": a["L0_ffn_ln2"].reshape(DC, P).T,
        **{f"l0f_{n}": a[f"L0_ffn_{n}"] for n in ("wq", "wk", "wv", "wo", "w1", "w2")},
    }
    arrays |= {
        "l1f_gate": a["L1_ffn_w_gate"],
        "l1f_up": a["L1_ffn_w_up"],
        "l1f_down": a["L1_ffn_w_down"],
        "l1f_clip_x": a["L1_ffn_clip_x"][None],
        "l1f_clip_down": a["L1_ffn_clip_down"][None],
    }
    t, f = np.arange(S), np.arange(S // 2)
    angle = 2 * np.pi / S * ((t[:, None] * f[None, :]) % S)
    basis = np.concatenate([np.cos(angle), np.sin(angle)], 1)
    basis[:, S // 2] = np.where(t % 2, -1.0, 1.0)
    share = np.full(S, 2.0 / (S * D))
    share[0] = share[S // 2] = 1.0 / (S * D)
    inverse = (basis * share)[(-t) % S].T
    arrays |= {
        **{f"l2x_{n}": a[f"L2_xattn_{n}"] for n in ("Wq", "Wk", "Wv", "Wo")},
        **{f"l2x_{n}": a[f"L2_xattn_{n}"][None] for n in ("bq", "bk", "bv", "bo")},
        "dft_basis": basis.astype(np.float32),
        "dft_inverse": inverse.astype(np.float32),
        "l2f_router": a["L2_ffn_w_router"].T,
        "l2f_w1": np.concatenate([a["L2_ffn_w1_stack"], a["L2_ffn_ws1"].reshape(2, D, D)]).transpose(0, 2, 1),
        "l2f_w2": np.concatenate([a["L2_ffn_w2_stack"].transpose(0, 2, 1), a["L2_ffn_ws2"].T.reshape(2, D, D)]),
        "l3f_router": a["L3_ffn_gate_w"].T,
        **{f"l3f_{n}": a[f"L3_ffn_{n}"] for n in ("w1", "w2", "w3")},
    }
    kv = a["L3_xattn_Wkv"]
    arrays |= {
        "mask": a["mask_BxSxS2_ff0"],
        "l3x_wq": a["L3_xattn_Wq"],
        "l3x_wk": np.concatenate([kv[:, 0:64], kv[:, 0:64]], 1),
        "l3x_wv": kv[:, 64:128],
        "l3x_w1": a["L3_xattn_W1"],
        "l3x_wout": a["L3_xattn_Wout"],
        "l3x_w2": a["L3_xattn_W2"],
        "l3x_gains": np.stack([a[f"L3_xattn_{n}"].reshape(DC, P) for n in ("ln_g", "ln_b", "cln_g", "cln_b")]
                              ).transpose(2, 0, 1),
    }
    return {k: np.ascontiguousarray(v) for k, v in arrays.items()}


def kernel(**inputs):
    import concourse.bacc as bacc
    from concourse.bass_utils import run_bass_kernel_spmd

    nc = bacc.Bacc("TRN2", target_bir_lowering=False, num_devices=1)
    arrays = lay_out(inputs)
    dram = {k: nc.dram_tensor(f"in_{k}", v.shape, mybir.dt.from_np(v.dtype), kind="ExternalInput").ap()
            for k, v in arrays.items()}
    out = nc.dram_tensor("out_x", (B, S, D), F32, kind="ExternalOutput").ap()
    dram["delay_rows"] = nc.dram_tensor("delay_rows", (B, 2 * S), F32).ap()
    dram["score_rows"] = nc.dram_tensor("score_rows", (8, B * S), F32).ap()
    build(nc, dram, out)
    result = run_bass_kernel_spmd(nc, [{f"in_{k}": v for k, v in arrays.items()}], core_ids=[0])
    return result.results[0]["out_x"]
```

```python
from contextlib import ExitStack

import concourse.bass as bass
from concourse import mybir

ALU = mybir.AluOpType
ACT = mybir.ActivationFunctionType
AX = mybir.AxisListType.X
F32 = mybir.dt.float32
F16 = mybir.dt.float16
BF16 = mybir.dt.bfloat16
I32 = mybir.dt.int32
P = 128
B = 4
S = 512
D = 256
TT = S // P
DC = D // P
NEG = -3.0e38
ROUND = 12582912.0


class Stage:

    def __init__(self, core, name):
        self.core, self.nc, self.name, self.ctx = core, core.nc, name, ExitStack()
        self.sems = []

    def __enter__(self):
        return self

    def __exit__(self, *exc):
        done = self.ctx.__exit__(*exc)
        self.nc.clear_and_free_semaphores(self.sems)
        self.nc.all_engine_barrier()
        return done

    def sb(self, name, shape, dt=F32):
        return self.ctx.enter_context(self.nc.sbuf_tensor(f"{self.name}_{name}", shape, dt))

    def sem(self, name):
        self.sems.append(self.nc.alloc_semaphore(f"{self.name}_{name}"))
        return self.sems[-1]

    def block(self):
        return self.ctx.enter_context(self.nc.Block())


class Chain:

    def __init__(self, eng, sem, base=0):
        self.eng, self.sem, self.base, self.n = eng, sem, base, 0

    def __call__(self, ins):
        self.n += 1
        ins.then_inc(self.sem, 1)
        self.eng.wait_ge(self.sem, self.base + self.n)


class Steps:

    def __init__(self, sem, names):
        assert len(set(names)) == len(names)
        self.sem, self.names, self.next = sem, names, 0

    def done(self, ins, name):
        assert self.names[self.next % len(self.names)] == name, (name, self.next)
        self.next += 1
        ins.then_inc(self.sem, 1)

    def wait(self, eng, name, it=0):
        eng.wait_ge(self.sem, it * len(self.names) + self.names.index(name) + 1)


class Norm:

    LINKS = 4

    def __init__(self, st, tag="", eps=1e-5):
        self.st, self.nc, self.core, self.eps = st, st.nc, st.core, eps
        self.bn = st.sb(f"bn{tag}", [P, TT, 6])
        self.mv = st.sb(f"mv{tag}", [P, TT, 2])
        self.var = st.sb(f"var{tag}", [P, TT])
        self.rstd = st.sb(f"rstd{tag}", [P, TT])
        self.stats = st.sem(f"norm{tag}_stats")
        self.rstd_ready = st.sem(f"norm{tag}_rstd")

    def vector(self, dve, it, src, dst, done):
        nc = self.nc
        link = Chain(dve, self.stats, it * self.LINKS)
        for j in range(TT):
            last = nc.vector.bn_stats(self.bn[:, j, :], src(j))
        link(last)
        dve.nop(nofuse=True)
        for j in range(TT):
            last = nc.vector.bn_aggr(self.mv[:, j, :], self.bn[:, j, :])
        link(last)
        link(nc.vector.tensor_scalar(self.var[:], self.mv[:, :, 1], self.eps, None, ALU.add))
        dve.wait_ge(self.rstd_ready, it + 1)
        for j in range(TT):
            last = nc.vector.tensor_scalar(dst(j), src(j), self.mv[:, j, 0:1], self.rstd[:, j:j + 1],
                                           ALU.subtract, ALU.mult)
        last.then_inc(done, 1)
        self.finish(dve, link)

    def finish(self, dve, link):
        link(self.nc.vector.tensor_copy(self.bn[:, 0, 0:1], self.mv[:, 0, 0:1]))

    def pool(self, pool, it):
        pool.wait_ge(self.stats, it * self.LINKS + 3)
        self.nc.gpsimd.tensor_tensor(self.rstd[:], self.var[:], self.core.neg_half[:, 0:TT],
                                     ALU.pow).then_inc(self.rstd_ready, 1)


class Core:

    def __init__(self, nc, ctx, dram):
        self.nc, self.dram = nc, dram
        self.x = ctx.enter_context(nc.sbuf_tensor("x_sb", [P, B * TT, D], F32))
        self.ident = ctx.enter_context(nc.sbuf_tensor("ident", [P, P], F32))
        self.neg_half = ctx.enter_context(nc.sbuf_tensor("neg_half", [P, 8], F32))
        self.ps = ctx.enter_context(nc.psum_tensor("ps", [P, 8, S], F32))


def load_stage(core):
    nc = core.nc
    with Stage(core, "load") as st:
        loaded, zeroed, made = st.sem("x_loaded"), st.sem("ident_zeroed"), st.sem("ident_made")
        block = st.block()

        @block.sync
        def _(sp):
            sp.dma_start(core.x[:], core.dram["x"].rearrange("b (j p) d -> p (b j) d", p=P)).then_inc(loaded, 16)
            sp.wait_ge(loaded, 16)

        @block.gpsimd
        def _(pool):
            nc.gpsimd.memset(core.neg_half[:], -0.5)
            nc.gpsimd.memset(core.ident[:], 0.0).then_inc(zeroed, 1)
            pool.wait_ge(zeroed, 1)
            nc.gpsimd.affine_select(out=core.ident[:], in_=core.ident[:], compare_op=ALU.not_equal, fill=1.0,
                                    base=0, pattern=[[-1, P]], channel_multiplier=1).then_inc(made, 1)


def store_stage(core, out):
    with Stage(core, "store") as st:
        stored = st.sem("x_stored")
        block = st.block()

        @block.sync
        def _(sp):
            sp.dma_start(out.rearrange("b (j p) d -> p (b j) d", p=P), core.x[:]).then_inc(stored, 16)
            sp.wait_ge(stored, 16)


def transpose_tokens(nc, core, src, bank, c, inc):
    for j in range(TT):
        last = nc.tensor.transpose(core.ps[:, bank, j * P:(j + 1) * P], src[:, j, c * P:(c + 1) * P], core.ident[:])
    last.then_inc(inc, 1)


def sigmoid_attention_stage(core):
    nc, dram = core.nc, core.dram
    HG = 4
    UNITS = HG * TT * 2
    SLOTS = 3
    LATE = 2
    RING = DC + 3 * HG + HG + TT
    HALF = 16
    with Stage(core, "l0x") as st:
        norm = Norm(st)
        wq, wk, wv = (st.sb(n, [P, DC, HG * P]) for n in ("wq", "wk", "wv"))
        wo = st.sb("wo", [P, HG, D])
        lo_rows = st.sb("lo_rows", [P, 1])
        xn = st.sb("xn", [P, TT, D])
        xnT = st.sb("xnT", [P, DC, S])
        ctxT = st.sb("ctxT", [P, DC, S])
        k_hi, k_lo, q_hi, q2 = (st.sb(n, [P, HG, S], F16) for n in ("k_hi", "k_lo", "q_hi", "q2"))
        oT = st.sb("oT", [P, HG, S])
        v = st.sb("v", [P, TT, 4 * HG, 2, HALF], F16)
        prob = st.sb("prob", [P, SLOTS, 2, S])
        p_hi, p_lo = (st.sb(n, [P, SLOTS, 2, S], F16) for n in ("p_hi", "p_lo"))
        weights_in, ctx_in, ctx_used = st.sem("weights_in"), st.sem("ctx_in"), st.sem("ctx_used")
        xn_ready, ring_full, ring_free = st.sem("xn_ready"), st.sem("ring_full"), st.sem("ring_free")
        hi_ready = st.sem("hi_ready")
        scores_ready, probs_ready, probs_used = st.sem("scores_ready"), st.sem("probs_ready"), st.sem("probs_used")
        p_hi_ready, p_lo_ready = st.sem("p_hi_ready"), st.sem("p_lo_ready")
        block = st.block()

        def ring_bank(n):
            return 6 + n % 2

        @block.sync
        def _(sp):
            for dst, name in ((wk, "l0x_wk"), (wq, "l0x_wq"), (wv, "l0x_wv")):
                sp.dma_start(dst[:], dram[name].rearrange("(c p) n -> p c n", p=P)).then_inc(weights_in, 16)
            sp.dma_start(wo[:], dram["l0x_wo"].rearrange("(g p) n -> p g n", p=P)).then_inc(weights_in, 16)
            sp.dma_start(lo_rows[:], dram["lo_rows"]).then_inc(weights_in, 16)
            with sp.Fori(0, B) as b:
                sp.wait_ge(ctx_used, b + 1)
                sp.dma_start(ctxT[:], dram["ctxT"][b].rearrange("(c p) s -> p c s", p=P)).then_inc(ctx_in, 16)

        @block.gpsimd
        def _(pool):
            with pool.Fori(0, B) as b:
                norm.pool(pool, b)

        @block.tensor
        def _(pe):
            pe.sem_inc(ctx_used, 1)
            pe.sem_inc(probs_used, SLOTS)
            pe.wait_ge(weights_in, 80)
            with pe.Fori(0, B) as b:
                base = b * RING
                ring = [0]

                def claim():
                    n = ring[0]
                    ring[0] += 1
                    pe.wait_ge(ring_free, base + n + 1)
                    return ring_bank(n)

                def emptied():
                    pe.wait_ge(ring_free, base + ring[0] + 2)

                def project(w, g, rhs):
                    bank = claim()
                    for c in range(DC):
                        last = nc.tensor.matmul(core.ps[:, bank, :], w[:, c, g * P:(g + 1) * P], rhs[:, c, :],
                                                start=(c == 0), stop=(c == DC - 1))
                    last.then_inc(ring_full, 1)

                pe.wait_ge(ctx_in, b * 16 + 16)
                for g in range(HG):
                    project(wk, g, ctxT)
                for j in range(TT):
                    bank = claim()
                    for c in range(DC):
                        last = nc.tensor.matmul(core.ps[:, bank, :], ctxT[:, c, j * P:(j + 1) * P], wv[:, c, :],
                                                start=(c == 0), stop=(c == DC - 1))
                    last.then_inc(ring_full, 1)
                pe.wait_ge(xn_ready, b + 1)
                for c in range(DC):
                    transpose_tokens(nc, core, xn, claim(), c, ring_full)
                emptied()
                pe.sem_inc(ctx_used, 1)
                for g in range(HG):
                    project(wq, g, xnT)
                emptied()

                units = [(g, j, h) for g in range(HG) for j in range(TT) for h in range(2)]

                def score(u):
                    g, j, h = units[u]
                    pe.wait_ge(probs_ready, b * UNITS + max(u + 1, SLOTS))
                    for i in range(2):
                        r = 32 * (2 * h + i)
                        for part, k in enumerate((k_hi, k_lo)):
                            last = nc.tensor.matmul(core.ps[:, 2 * (u % SLOTS) + i, :], k[r:r + 32, g, j * P:(j + 1) * P],
                                                    q2[r:r + 32, g, :], start=(part == 0), stop=(part == 1))
                    last.then_inc(scores_ready, 1)

                for u in range(SLOTS):
                    score(u)
                for u, (g, j, h) in enumerate(units):
                    if u + SLOTS < UNITS:
                        score(u + SLOTS)
                    if (j, h) == (0, 0):
                        bank = claim()
                    pe.wait_ge(p_lo_ready, b * UNITS + u + 1 + SLOTS)
                    for part, probs in enumerate((p_hi, p_lo)):
                        for i in range(2):
                            head = 2 * h + i
                            r = 32 * head
                            last = nc.tensor.matmul(core.ps[r:r + 32, bank, :], v[:, j, 4 * g + head, :, :],
                                                    probs[:, u % SLOTS, i, :], start=(j == 0 and part == 0),
                                                    stop=(j == TT - 1 and part == 1), tile_position=(0, r))
                    last.then_inc(probs_used, 1)
                emptied()
                for j in range(TT):
                    bank = claim()
                    for g in range(HG):
                        last = nc.tensor.matmul(core.ps[:, bank, 0:D], oT[:, g, j * P:(j + 1) * P], wo[:, g, :],
                                                start=(g == 0), stop=(g == HG - 1))
                    last.then_inc(ring_full, 1)
                assert ring[0] == RING

        @block.scalar
        def _(act):
            act.sem_inc(probs_ready, SLOTS)
            with act.Fori(0, B) as b:
                def hi(n, dst, src):
                    act.wait_ge(ring_full, b * (RING - HG) + n + 1)
                    nc.scalar.activation(dst, src(core.ps[:, ring_bank(n), :]), ACT.Copy).then_inc(hi_ready, 1)

                for g in range(HG):
                    hi(g, k_hi[:, g, :], lambda full: full)
                for j in range(TT):
                    hi(HG + j, v[:, j, :, 0, :], lambda full: full.rearrange("p (h a d) -> p h a d", a=2, d=HALF)[:, :, 0, :])
                for g in range(HG):
                    hi(HG + TT + DC + g, q_hi[:, g, :], lambda full: full)
                for u in range(UNITS):
                    act.wait_ge(scores_ready, b * UNITS + u + 1)
                    act.wait_ge(p_lo_ready, b * UNITS + max(u + 1, SLOTS))
                    nc.scalar.activation(prob[:, u % SLOTS, :, :], core.ps[:, 2 * (u % SLOTS):2 * (u % SLOTS) + 2, :],
                                         ACT.Sigmoid, scale=0.25).then_inc(probs_ready, 1)

        @block.vector
        def _(dve):
            V = nc.vector
            dve.sem_inc(ring_free, 2)
            dve.sem_inc(p_lo_ready, SLOTS)
            dve.wait_ge(weights_in, 80)
            with dve.Fori(0, B) as b:
                ring, full, his = [0], [0], [0]

                def take():
                    ring[0] += 1
                    full[0] += 1
                    dve.wait_ge(ring_full, b * (RING - HG) + full[0])
                    return ring_bank(ring[0] - 1)

                def take_split():
                    his[0] += 1
                    bank = take()
                    dve.wait_ge(hi_ready, b * (2 * HG + TT) + his[0])
                    return bank

                norm.vector(dve, b, lambda j: core.x[:, b * TT + j, :], lambda j: xn[:, j, :], xn_ready)
                for g in range(HG):
                    V.tensor_tensor(k_lo[:, g, :], core.ps[:, take_split(), :], k_hi[:, g, :], ALU.subtract
                                    ).then_inc(ring_free, 1)
                for j in range(TT):
                    own = core.ps[:, take_split(), :].rearrange("p (h a d) -> p h a d", a=2, d=HALF)[:, :, 1, :]
                    V.tensor_tensor(v[:, j, :, 1, :], own, v[:, j, :, 0, :], ALU.subtract).then_inc(ring_free, 1)
                for c in range(DC):
                    V.tensor_copy(xnT[:, c, :], core.ps[:, take(), :]).then_inc(ring_free, 1)
                for g in range(HG):
                    V.scalar_tensor_tensor(out=q2[:, g, :], in0=q_hi[:, g, :], scalar=lo_rows[:, 0:1],
                                           in1=core.ps[:, take_split(), :], op0=ALU.mult, op1=ALU.add).then_inc(ring_free, 1)

                def rows(g):
                    ring[0] += 1
                    dve.wait_ge(probs_used, b * UNITS + SLOTS + (g + 1) * UNITS // HG)
                    V.tensor_copy(oT[:, g, :], core.ps[:, ring_bank(ring[0] - 1), :]).then_inc(ring_free, 1)

                for u in range(UNITS + 1):
                    if u < UNITS:
                        dve.wait_ge(probs_ready, b * UNITS + u + 1 + SLOTS)
                        dve.wait_ge(probs_used, b * UNITS + max(u + 1, SLOTS))
                        V.tensor_copy(p_hi[:, u % SLOTS, :, :], prob[:, u % SLOTS, :, :]).then_inc(p_hi_ready, 1)
                    if u >= 1:
                        n = u - 1
                        dve.wait_ge(p_hi_ready, b * UNITS + n + 1)
                        V.tensor_tensor(p_lo[:, n % SLOTS, :, :], prob[:, n % SLOTS, :, :], p_hi[:, n % SLOTS, :, :],
                                        ALU.subtract).then_inc(p_lo_ready, 1)
                        if n % (UNITS // HG) == LATE and n > LATE:
                            rows(n // (UNITS // HG) - 1)
                rows(HG - 1)
                for j in range(TT):
                    V.tensor_tensor(core.x[:, b * TT + j, :], core.x[:, b * TT + j, :],
                                    core.ps[:, take(), 0:D], ALU.add).then_inc(ring_free, 1)


def mixture_of_depths_stage(core):
    nc, dram = core.nc, core.dram
    K = S // 8
    HALF = 64
    T2 = 2
    H, HD = 16, 16
    HG, STRIP = 4, 32
    F = 1024
    FT = F // P
    NA = D + 2
    with Stage(core, "l0f") as st:
        norm = Norm(st)
        xa = st.sb("xa", [P, B * TT, NA])
        rw, rb = st.sb("rw", [P, D]), st.sb("rb", [P, 1])
        junk = st.sb("junk", [P, TT, D])
        pos = st.sb("pos", [P, B * TT], I32)
        wcol = st.sb("wcol", [P, TT, B])
        wrow, work, chosen, above, ones = (st.sb(n, [B, S]) for n in ("wrow", "work", "chosen", "above", "ones"))
        top = st.sb("top", [B, K])
        last8 = st.sb("last8", [B, 8])
        base = st.sb("slot_base", [B, 1])
        slot, keep = st.sb("slot", [P, B, TT]), st.sb("keep", [P, B, TT])
        iota = st.sb("iota", [P, P])
        pick = st.sb("pick", [P, B * TT, P])
        pickT = st.sb("pickT", [P, B * TT, P])
        mask = st.sb("mask", [P, TT, S])
        half_mask = st.sb("half_mask", [P, B * TT, P])
        bar = st.sb("bar", [P, P])
        bias = st.sb("bias", [P, T2, P])
        xs = st.sb("xs", [P, T2, NA])
        ss, rms = st.sb("ss", [P, T2]), st.sb("rms", [P, T2])
        hn = st.sb("hn", [P, T2, D])
        hT = st.sb("hT", [P, DC, T2 * P])
        ln1, ln2 = st.sb("ln1", [P, DC]), st.sb("ln2", [P, DC])
        wq, wk, wv, wo = (st.sb(n, [P, DC, D]) for n in ("wq", "wk", "wv", "wo"))
        w1 = st.sb("w1", [P, DC, F])
        w2 = st.sb("w2", [P, FT, D])
        freq = st.sb("freq", [P, HD // 2])
        ang, turns, sin, cos = (st.sb(n, [P, T2, HD]) for n in ("ang", "turns", "sin", "cos"))
        q, k = (st.sb(n, [P, T2, H, STRIP]) for n in ("q", "k"))
        rot = st.sb("rot", [P, H, HD])
        v = st.sb("v", [P, T2, D])
        qT, kT = (st.sb(n, [P, HG, T2 * P]) for n in ("qT", "kT"))
        prob = st.sb("prob", [P, H, P])
        probT = st.sb("probT", [P, H, P])
        mx, total, inv = (st.sb(n, [P, H]) for n in ("mx", "total", "inv"))
        o = st.sb("o", [P, T2, D])
        oT = st.sb("oT", [P, DC, T2 * P])
        x1 = st.sb("x1", [P, T2, D])
        gT = st.sb("gT", [P, FT, T2 * P])
        y = st.sb("y", [P, T2, D])
        small_in, weights_in, mask_in = st.sem("small_in"), st.sem("weights_in"), st.sem("mask_in")
        mask_used, xn_ready, weighed = st.sem("mask_used"), st.sem("xn_ready"), st.sem("weighed")
        order = st.sem("vector_order")
        half_full, half_free = st.sem("half_mask_full"), st.sem("half_mask_free")
        pool_s = Steps(st.sem("pool_steps"), ["consts", "rms1", "rms2"])
        act_s = Steps(st.sem("act_steps"), ["sincos", "exp0", "exp1"] + [f"gelu{f}" for f in range(FT)])
        PE = (["w_rows", "slot_cols"] + [f"pickT{t}" for t in range(4)] + ["gather", "bias", "hT", "q", "k", "v", "qT", "kT"]
              + sum([[f"scores{t}", *[f"probT{t}{r}" for r in range(4)], f"av{t}"] for t in range(T2)], [])
              + ["oT", "proj", "h2T"] + [f"up{f}" for f in range(FT)] + ["down"] + [f"scatter{t}" for t in range(B * TT)])
        pe_s = Steps(st.sem("pe_steps"), PE)
        ve_s = Steps(st.sem("vector_steps"), [
            n for n in ["wcol", "wrow", "slots", "cols", "pick", *[f"pickT{t}" for t in range(4)], "xs", "bias",
                        "sq1", "hn", "hT", "angles", "q", "k", "v", "qT", "kT"]
            + sum([[f"biased{t}", f"probs{t}", *[f"probT{t}{r}" for r in range(4)], f"o{t}"] for t in range(T2)], [])
            + ["oT", "x1", "sq2", "h2", "h2T", "y"] + [f"row{t}" for t in range(B * TT)]])
        block = st.block()

        @block.sync
        def _(sp):
            sp.dma_start(rw[:], dram["l0f_rw"].to_broadcast([P, D])).then_inc(small_in, 16)
            sp.dma_start(rb[:], dram["l0f_rb"].to_broadcast([P, 1])).then_inc(small_in, 16)
            sp.dma_start(freq[:], dram["rope_freq"].to_broadcast([P, HD // 2])).then_inc(small_in, 16)
            sp.dma_start(pos[:], dram["pos"]).then_inc(small_in, 16)
            sp.dma_start(base[:], dram["slot_base"]).then_inc(small_in, 16)
            sp.dma_start(ln1[:], dram["l0f_ln1"]).then_inc(small_in, 16)
            sp.dma_start(ln2[:], dram["l0f_ln2"]).then_inc(small_in, 16)
            for dst, name in ((wq, "l0f_wq"), (wk, "l0f_wk"), (wv, "l0f_wv"), (wo, "l0f_wo"), (w1, "l0f_w1"), (w2, "l0f_w2")):
                sp.dma_start(dst[:], dram[name].rearrange("(c p) n -> p c n", p=P)).then_inc(weights_in, 16)
            with sp.Fori(0, B) as b:
                sp.wait_ge(mask_used, b + 1)
                sp.dma_start(mask[:], dram["attention_mask"][b].rearrange("(j p) s -> p j s", p=P)).then_inc(mask_in, 16)

        @block.gpsimd
        def _(pool):
            nc.gpsimd.memset(ones[:], 1.0)
            nc.gpsimd.iota(iota[:], [[1, P]], base=0, channel_multiplier=0, allow_small_or_imprecise_dtypes=True)
            nc.gpsimd.memset(q[:], 0.0)
            pool_s.done(nc.gpsimd.memset(k[:], 0.0), "consts")
            with pool.Fori(0, B) as b:
                norm.pool(pool, b)
            for n in (1, 2):
                ve_s.wait(pool, f"sq{n}")
                pool_s.done(nc.gpsimd.tensor_tensor(rms[:], ss[:], core.neg_half[:, 0:T2], ALU.pow), f"rms{n}")

        @block.scalar
        def _(act):
            ve_s.wait(act, "angles")
            nc.scalar.activation(sin[:], ang[:], ACT.Sin)
            act_s.done(nc.scalar.activation(cos[:], ang[:], ACT.Sin, scale=0.5), "sincos")
            for t in range(T2):
                ve_s.wait(act, f"biased{t}")
                act_s.done(nc.scalar.activation(prob[:], prob[:], ACT.Exp), f"exp{t}")
            for f in range(FT):
                pe_s.wait(act, f"up{f}")
                act_s.done(nc.scalar.activation(gT[:, f, :], core.ps[:, f % 4, 0:T2 * P], ACT.Gelu_apprx_tanh), f"gelu{f}")

        @block.tensor
        def _(pe):
            ident = core.ident
            ps = core.ps
            pe.sem_inc(mask_used, 1)
            ve_s.wait(pe, "wcol")
            for j in range(TT):
                last = nc.tensor.transpose(ps[0:B, 0, j * P:(j + 1) * P], wcol[:, j, :], ident[:])
            pe_s.done(last, "w_rows")
            ve_s.wait(pe, "slots")
            for n, rows in enumerate((work, above)):
                for j in range(TT):
                    last = nc.tensor.transpose(ps[:, 1, n * 16 + j * B:n * 16 + (j + 1) * B], rows[:, j * P:(j + 1) * P],
                                               ident[0:B, 0:B])
            pe_s.done(last, "slot_cols")
            ve_s.wait(pe, "pick")
            for b in range(B):
                for j in range(TT):
                    last = nc.tensor.transpose(ps[:, 2 + b, j * P:(j + 1) * P], pick[:, b * TT + j, :], ident[:])
                pe_s.done(last, f"pickT{b}")
            for t in range(T2):
                for n in range(2 * TT):
                    last = nc.tensor.matmul(ps[:, 6 + t, 0:NA], pick[:, t * 2 * TT + n, :], xa[:, t * 2 * TT + n, :],
                                            start=(n == 0), stop=(n == 2 * TT - 1))
            pe_s.done(last, "gather")
            with pe.Fori(0, B) as b:
                pe.wait_ge(mask_in, b * 16 + 16)
                pe.wait_ge(half_free, b + 1)
                for kt in range(TT):
                    for j in range(TT):
                        last = nc.tensor.matmul(ps[:, 0, kt * P:(kt + 1) * P], mask[:, j, kt * P:(kt + 1) * P],
                                                pick[:, b * TT + j, :], start=(j == 0), stop=(j == TT - 1))
                last.then_inc(half_full, 1)
                pe.wait_ge(half_free, b + 2)
                pe.sem_inc(mask_used, 1)
            for t in range(T2):
                for n in range(2 * TT):
                    last = nc.tensor.matmul(ps[:, 1, t * P:(t + 1) * P], half_mask[:, t * 2 * TT + n, :],
                                            pick[:, t * 2 * TT + n, :], start=(n == 0), stop=(n == 2 * TT - 1))
            pe_s.done(last, "bias")
            ve_s.wait(pe, "hn")

            def turn(src, bank, name):
                for c in range(DC):
                    for t in range(T2):
                        last = nc.tensor.transpose(ps[:, bank, (c * T2 + t) * P:(c * T2 + t + 1) * P],
                                                   src[:, t, c * P:(c + 1) * P], ident[:])
                pe_s.done(last, name)

            turn(hn, 2, "hT")
            ve_s.wait(pe, "hT")
            pe.wait_ge(weights_in, 16 * 6)
            for bank, w, name in ((3, wq, "q"), (4, wk, "k"), (5, wv, "v")):
                for t in range(T2):
                    for c in range(DC):
                        last = nc.tensor.matmul(ps[:, bank, t * D:(t + 1) * D], hT[:, c, t * P:(t + 1) * P], w[:, c, :],
                                                start=(c == 0), stop=(c == DC - 1))
                pe_s.done(last, name)
            for src, bank, name in ((q, 6, "q"), (k, 0, "k")):
                ve_s.wait(pe, name)
                if name == "k":
                    ve_s.wait(pe, "bias")
                    pe.wait_ge(half_free, B + 1)
                for t in range(T2):
                    for g in range(HG):
                        last = nc.tensor.transpose(ps[:, bank + t, g * P:(g + 1) * P],
                                                   src[:, t, g * HG:(g + 1) * HG, :], ident[:])
                pe_s.done(last, name + "T")
            ve_s.wait(pe, "v")
            for t in range(T2):
                ve_s.wait(pe, "kT")
                if t:
                    ve_s.wait(pe, "o0")
                for r in range(4):
                    for g in range(HG):
                        last = nc.tensor.matmul(ps[:, 2 + r, g * P:(g + 1) * P],
                                                qT[r * STRIP:(r + 1) * STRIP, g, t * P:(t + 1) * P],
                                                kT[r * STRIP:(r + 1) * STRIP, g, t * P:(t + 1) * P], start=True, stop=True,
                                                tile_position=(r * STRIP, 0))
                pe_s.done(last, f"scores{t}")
                ve_s.wait(pe, f"probs{t}")
                for r in range(4):
                    for n in range(4):
                        last = nc.tensor.transpose(ps[:, 2 + r, n * P:(n + 1) * P], prob[:, r * 4 + n, :], ident[:])
                    pe_s.done(last, f"probT{t}{r}")
                ve_s.wait(pe, f"probT{t}3")
                for h in range(H):
                    n = (h % HG) * 4 + h // HG
                    last = nc.tensor.matmul(ps[:, 6, h * HD:(h + 1) * HD], probT[:, n, :], v[:, t, h * HD:(h + 1) * HD],
                                            start=True, stop=True)
                pe_s.done(last, f"av{t}")
            ve_s.wait(pe, "o1")
            turn(o, 7, "oT")
            ve_s.wait(pe, "oT")
            for t in range(T2):
                for c in range(DC):
                    last = nc.tensor.matmul(ps[:, 0, t * D:(t + 1) * D], oT[:, c, t * P:(t + 1) * P], wo[:, c, :],
                                            start=(c == 0), stop=(c == DC - 1))
            pe_s.done(last, "proj")
            ve_s.wait(pe, "h2")
            turn(hn, 1, "h2T")
            ve_s.wait(pe, "h2T")
            for f in range(FT):
                if f >= 4:
                    act_s.wait(pe, f"gelu{f - 4}")
                for c in range(DC):
                    last = nc.tensor.matmul(ps[:, f % 4, 0:T2 * P], w1[:, c, f * P:(f + 1) * P], hT[:, c, :],
                                            start=(c == 0), stop=(c == DC - 1))
                pe_s.done(last, f"up{f}")
            act_s.wait(pe, f"gelu{FT - 1}")
            for t in range(T2):
                for f in range(FT):
                    last = nc.tensor.matmul(ps[:, 4, t * D:(t + 1) * D], gT[:, f, t * P:(t + 1) * P], w2[:, f, :],
                                            start=(f == 0), stop=(f == FT - 1))
            pe_s.done(last, "down")
            ve_s.wait(pe, "y")
            for t in range(B * TT):
                if t >= 4:
                    ve_s.wait(pe, f"row{t - 4}")
                pe_s.done(nc.tensor.matmul(ps[:, t % 4, 0:D], pickT[:, t, :], y[:, t // (2 * TT), :], start=True, stop=True),
                          f"scatter{t}")

        @block.vector
        def _(dve):
            ps = core.ps
            V = nc.vector
            dve.sem_inc(half_free, 1)
            V.memset(bar[0:HALF, 0:HALF - 1], 0.0)
            V.memset(bar[0:HALF, HALF - 1:P], NEG)
            V.memset(bar[HALF:P, 0:HALF], NEG)
            V.memset(bar[HALF:P, HALF:P - 1], 0.0)
            V.memset(bar[HALF:P, P - 1:P], NEG)
            dve.wait_ge(small_in, 16 * 7)
            with dve.Fori(0, B) as b:
                norm.vector(dve, b, lambda j: core.x[:, b * TT + j, :], lambda j: xa[:, b * TT + j, 0:D], xn_ready)
                dve.wait_ge(xn_ready, b + 1)
                for j in range(TT):
                    last = V.scalar_tensor_tensor(out=junk[:, j, :], in0=xa[:, b * TT + j, 0:D], scalar=1.0, in1=rw[:],
                                                  op0=ALU.mult, op1=ALU.mult, accum_out=xa[:, b * TT + j, D:D + 1])
                last.then_inc(weighed, 1)
                dve.wait_ge(weighed, b + 1)
            link = Chain(dve, order)
            link(V.tensor_copy(xa[:, :, D + 1], pos[:]))
            link(V.tensor_scalar(xa[:, :, D], xa[:, :, D], rb[:, 0:1], None, ALU.add))
            ve_s.done(V.tensor_copy(wcol[:].rearrange("p j b -> p b j"), xa[:, :, D].rearrange("p (b j) -> p b j", b=B)),
                      "wcol")
            pe_s.wait(dve, "w_rows")
            link(V.tensor_copy(wrow[:], ps[0:B, 0, :]))
            ve_s.done(V.tensor_copy(work[:], ps[0:B, 0, :]), "wrow")
            ve_s.wait(dve, "wrow")
            for n in range(K // 8 - 1):
                eight = top[:, n * 8:n * 8 + 8]
                link(V.max(eight, work[:]))
                link(V.match_replace(work[:], eight, work[:], NEG))
            link(V.max(top[:, K - 8:K], work[:]))
            link(V.tensor_copy(last8[:], top[:, K - 8:K]))
            link(V.memset(last8[:, 7:8], NEG))
            link(V.match_replace(work[:], last8[:], work[:], NEG))
            link(V.tensor_tensor(chosen[:], work[:], wrow[:], ALU.not_equal))
            link(V.tensor_scalar(above[:], wrow[:], top[:, K - 1:K], None, ALU.is_gt))
            pool_s.wait(dve, "consts")
            link(V.tensor_tensor_scan(work[:], ones[:], chosen[:], 0.0, ALU.mult, ALU.add))
            link(V.scalar_tensor_tensor(out=work[:], in0=work[:], scalar=base[:, 0:1], in1=chosen[:],
                                        op0=ALU.add, op1=ALU.mult))
            ve_s.done(V.tensor_scalar(work[:], work[:], -1.0, None, ALU.add), "slots")
            pe_s.wait(dve, "slot_cols")
            V.tensor_copy(slot[:].rearrange("p b j -> p j b"), ps[:, 1, 0:16].rearrange("p (j b) -> p j b", b=B))
            ve_s.done(V.tensor_scalar(keep[:].rearrange("p b j -> p j b"), ps[:, 1, 16:32].rearrange("p (j b) -> p j b", b=B),
                                      -1.0, 1.0, ALU.mult, ALU.add), "cols")
            ve_s.wait(dve, "cols")
            for t in range(B * TT):
                last = V.tensor_scalar(pick[:, t, :], iota[:], slot[:, t // TT, t % TT:t % TT + 1], None, ALU.is_equal)
            ve_s.done(last, "pick")
            for b in range(B):
                pe_s.wait(dve, f"pickT{b}")
                ve_s.done(V.tensor_copy(pickT[:, b * TT:(b + 1) * TT, :], ps[:, 2 + b, :]), f"pickT{b}")
            pe_s.wait(dve, "gather")
            ve_s.done(V.tensor_copy(xs[:], ps[:, 6:8, 0:NA]), "xs")
            with dve.Fori(0, B) as b:
                dve.wait_ge(half_full, b + 1)
                V.tensor_copy(half_mask[:, bass.ds(b * TT, TT), :], ps[:, 0, :].rearrange("p (k s) -> p k s", s=P)
                              ).then_inc(half_free, 1)
            pe_s.wait(dve, "bias")
            ve_s.done(V.tensor_tensor(bias[:], ps[:, 1, 0:T2 * P].rearrange("p (t s) -> p t s", s=P),
                                      bar[:].unsqueeze(1).to_broadcast([P, T2, P]), ALU.add), "bias")

            def rms_norm(src, n, name):
                for t in range(T2):
                    last = V.scalar_tensor_tensor(out=junk[:, t, :], in0=src[:, t, 0:D], scalar=1.0, in1=src[:, t, 0:D],
                                                  op0=ALU.mult, op1=ALU.mult, accum_out=ss[:, t:t + 1])
                link(last)
                ve_s.done(V.tensor_scalar(ss[:], ss[:], 1.0 / D, 1e-6, ALU.mult, ALU.add), f"sq{n}")
                pool_s.wait(dve, f"rms{n}")
                for t in range(T2):
                    last = V.tensor_scalar(hn[:, t, :], src[:, t, 0:D], rms[:, t:t + 1], None, ALU.mult)
                ve_s.done(last, name)

            def gained(bank, gain, name):
                for c in range(DC):
                    last = V.tensor_scalar(hT[:, c, :], ps[:, bank, c * T2 * P:(c + 1) * T2 * P], gain[:, c:c + 1],
                                           None, ALU.mult)
                ve_s.done(last, name)

            ve_s.wait(dve, "xs")
            rms_norm(xs, 1, "hn")
            pe_s.wait(dve, "hT")
            gained(2, ln1, "hT")
            for t in range(T2):
                last = V.tensor_scalar(ang[:, t, 0:8], freq[:], xs[:, t, D + 1:D + 2], None, ALU.mult)
            link(last)
            link(V.tensor_scalar(turns[:, :, 0:8], ang[:, :, 0:8], 0.15915494309189535, ROUND, ALU.mult, ALU.add))
            link(V.tensor_scalar(turns[:, :, 0:8], turns[:, :, 0:8], ROUND, None, ALU.subtract))
            for part in (6.28125, 0.0019350051879882812, 3.019916050e-07):
                link(V.scalar_tensor_tensor(out=ang[:, :, 0:8], in0=turns[:, :, 0:8], scalar=-part, in1=ang[:, :, 0:8],
                                            op0=ALU.mult, op1=ALU.add))
            link(V.tensor_scalar(ang[:, :, 0:8], ang[:, :, 0:8], 3.1415925, -3.1415925, ALU.min, ALU.max))
            ve_s.done(V.tensor_copy(ang[:, :, 8:16], ang[:, :, 0:8]), "angles")
            act_s.wait(dve, "sincos")
            link(V.tensor_scalar(sin[:, :, 0:8], sin[:, :, 0:8], -1.0, None, ALU.mult))
            link(V.tensor_tensor(cos[:], cos[:], cos[:], ALU.mult))
            link(V.tensor_scalar(cos[:], cos[:], -2.0, 1.0, ALU.mult, ALU.add))
            for bank, dst, name in ((3, q, "q"), (4, k, "k")):
                pe_s.wait(dve, name)
                for t in range(T2):
                    src = ps[:, bank, t * D:(t + 1) * D].rearrange("p (h d) -> p h d", h=H)
                    for lo, hi in ((0, 8), (8, 0)):
                        last = V.tensor_tensor(rot[:, :, lo:lo + 8], src[:, :, hi:hi + 8],
                                               sin[:, t, lo:lo + 8].unsqueeze(1).to_broadcast([P, H, 8]), ALU.mult)
                    last = V.tensor_tensor(dst[:, t, :, 0:HD], src, cos[:, t, :].unsqueeze(1).to_broadcast([P, H, HD]),
                                           ALU.mult)
                    link(last)
                    last = V.tensor_tensor(dst[:, t, :, 0:HD], dst[:, t, :, 0:HD], rot[:], ALU.add)
                    if t == 0:
                        link(last)
                ve_s.done(last, name)
                ve_s.wait(dve, name)
            pe_s.wait(dve, "v")
            ve_s.done(V.tensor_copy(v[:], ps[:, 5, :].rearrange("p (t d) -> p t d", t=T2)), "v")
            for bank, dst, name in ((6, qT, "qT"), (0, kT, "kT")):
                pe_s.wait(dve, name)
                for t in range(T2):
                    last = V.tensor_copy(dst[:, :, t * P:(t + 1) * P], ps[:, bank + t, :].rearrange("p (g s) -> p g s", g=HG))
                ve_s.done(last, name)
            for t in range(T2):
                pe_s.wait(dve, f"scores{t}")
                for r in range(4):
                    last = V.scalar_tensor_tensor(out=prob[:, r * 4:r * 4 + 4, :],
                                                  in0=ps[:, 2 + r, :].rearrange("p (g s) -> p g s", g=HG), scalar=HD ** -0.5,
                                                  in1=bias[:, t, :].unsqueeze(1).to_broadcast([P, HG, P]),
                                                  op0=ALU.mult, op1=ALU.add)
                link(last)
                link(V.tensor_reduce(mx[:], prob[:], AX, ALU.max))
                ve_s.done(V.tensor_tensor(prob[:], prob[:], mx[:].unsqueeze(2).to_broadcast([P, H, P]), ALU.subtract),
                          f"biased{t}")
                act_s.wait(dve, f"exp{t}")
                link(V.tensor_reduce(total[:], prob[:], AX, ALU.add))
                link(V.reciprocal(inv[:], total[:]))
                ve_s.done(V.tensor_tensor(prob[:], prob[:], inv[:].unsqueeze(2).to_broadcast([P, H, P]), ALU.mult),
                          f"probs{t}")
                for r in range(4):
                    pe_s.wait(dve, f"probT{t}{r}")
                    ve_s.done(V.tensor_copy(probT[:, r * 4:r * 4 + 4, :], ps[:, 2 + r, :].rearrange("p (g s) -> p g s", g=4)),
                              f"probT{t}{r}")
                pe_s.wait(dve, f"av{t}")
                ve_s.done(V.tensor_copy(o[:, t, :], ps[:, 6, 0:D]), f"o{t}")
            pe_s.wait(dve, "oT")
            ve_s.done(V.tensor_copy(oT[:], ps[:, 7, :].rearrange("p (c s) -> p c s", c=DC)), "oT")
            pe_s.wait(dve, "proj")
            ve_s.done(V.tensor_tensor(x1[:], xs[:, :, 0:D], ps[:, 0, :].rearrange("p (t d) -> p t d", t=T2), ALU.add), "x1")
            ve_s.wait(dve, "x1")
            rms_norm(x1, 2, "h2")
            pe_s.wait(dve, "h2T")
            gained(1, ln2, "h2T")
            pe_s.wait(dve, "down")
            link(V.tensor_tensor(x1[:], x1[:], ps[:, 4, :].rearrange("p (t d) -> p t d", t=T2), ALU.add))
            for t in range(T2):
                last = V.tensor_scalar(y[:, t, :], x1[:, t, :], xs[:, t, D:D + 1], None, ALU.mult)
            ve_s.done(last, "y")
            for t in range(B * TT):
                link(V.scalar_tensor_tensor(out=junk[:, t % TT, :], in0=xa[:, t, 0:D], scalar=keep[:, t // TT, t % TT:t % TT + 1],
                                            in1=core.x[:, t, :], op0=ALU.mult, op1=ALU.add))
                pe_s.wait(dve, f"scatter{t}")
                ve_s.done(V.tensor_tensor(core.x[:, t, :], junk[:, t % TT, :], ps[:, t % 4, 0:D], ALU.add), f"row{t}")


def causal_attention_stage(core):
    nc, dram = core.nc, core.dram
    SCALE = D ** -0.5
    with Stage(core, "l1x") as st:
        norm = Norm(st)
        xn = st.sb("xn", [P, TT, D])
        xnT = st.sb("xnT", [P, DC, S])
        ctx = st.sb("ctx", [P, 2, TT, D])
        ctxT = st.sb("ctxT", [P, 2, DC, S])
        future = st.sb("future", [P, P])
        prob = st.sb("prob", [P, TT, S])
        probT = st.sb("probT", [P, 2, S])
        top, shift, total, inv = (st.sb(n, [P, TT]) for n in ("top", "shift", "total", "inv"))
        ctx_in = [st.sem(f"ctx_in{i}") for i in range(2)]
        xn_ready, zeroed, future_made = st.sem("xn_ready"), st.sem("zeroed"), st.sem("future_made")
        row_used = st.sem("rows_done")
        pe_s = Steps(st.sem("pe_steps"), ["xT"] + [f"scores{q}" for q in range(TT)]
                     + sum([[f"turned{q}", f"out{q}"] for q in range(TT)], []))
        ve_s = Steps(st.sem("vector_steps"), ["xT"] + sum([[f"masked{q}", f"max{q}", f"shift{q}"] for q in range(TT)], [])
                     + sum([[f"probT{q}", f"inv{q}", f"row{q}"] for q in range(TT)], []))
        act_s = Steps(st.sem("act_steps"), [f"exp{q}" for q in range(TT)])
        block = st.block()

        @block.sync
        def _(sp):
            with sp.Fori(0, B // 2) as pair:
                for i in range(2):
                    sp.wait_ge(row_used, pair * 2 + i + 1)
                    sp.dma_start(ctx[:, i, :, :], dram["ctx"][pair * 2 + i].rearrange("(j p) d -> p j d", p=P)).then_inc(ctx_in[i], 16)
                    sp.dma_start(ctxT[:, i, :, :], dram["ctxT"][pair * 2 + i].rearrange("(c p) s -> p c s", p=P)).then_inc(ctx_in[i], 16)

        @block.gpsimd
        def _(pool):
            nc.gpsimd.memset(future[:], 0.0).then_inc(zeroed, 1)
            pool.wait_ge(zeroed, 1)
            nc.gpsimd.affine_select(out=future[:], in_=future[:], compare_op=ALU.is_ge, fill=NEG,
                                    base=0, pattern=[[-1, P]], channel_multiplier=1).then_inc(future_made, 1)
            with pool.Fori(0, B) as b:
                norm.pool(pool, b)

        @block.tensor
        def _(pe):
            ps = core.ps
            pe.sem_inc(row_used, 2)
            with pe.Fori(0, B // 2) as pair:
                for i in range(2):
                    b = pair * 2 + i
                    pe.wait_ge(xn_ready, b + 1)
                    for c in range(DC):
                        for j in range(TT):
                            last = nc.tensor.transpose(ps[:, 6 + c, j * P:(j + 1) * P], xn[:, j, c * P:(c + 1) * P], core.ident[:])
                    pe_s.done(last, "xT")
                    pe.wait_ge(ctx_in[i], pair * 32 + 32)
                    ve_s.wait(pe, "xT", b)
                    for q in range(TT):
                        for c in range(DC):
                            last = nc.tensor.matmul(ps[:, q, 0:(q + 1) * P], xnT[:, c, q * P:(q + 1) * P],
                                                    ctxT[:, i, c, 0:(q + 1) * P], start=(c == 0), stop=(c == DC - 1))
                        pe_s.done(last, f"scores{q}")
                    for q in range(TT):
                        act_s.wait(pe, f"exp{q}", b)
                        if q >= 2:
                            ve_s.wait(pe, f"probT{q - 2}", b)
                        for k in range(q + 1):
                            last = nc.tensor.transpose(ps[:, 4 + q % 2, k * P:(k + 1) * P], prob[:, q, k * P:(k + 1) * P],
                                                       core.ident[:])
                        pe_s.done(last, f"turned{q}")
                        ve_s.wait(pe, f"probT{q}", b)
                        if q >= 2:
                            ve_s.wait(pe, f"row{q - 2}", b)
                        for k in range(q + 1):
                            last = nc.tensor.matmul(ps[:, 6 + q % 2, 0:D], probT[:, q % 2, k * P:(k + 1) * P],
                                                    ctx[:, i, k, :], start=(k == 0), stop=(k == q))
                        pe_s.done(last, f"out{q}")
                    ve_s.wait(pe, f"row{TT - 1}", b)
                    pe.sem_inc(row_used, 1)

        @block.scalar
        def _(act):
            with act.Fori(0, B) as b:
                for q in range(TT):
                    ve_s.wait(act, f"shift{q}", b)
                    act_s.done(nc.scalar.activation(prob[:, q, 0:(q + 1) * P], core.ps[:, q, 0:(q + 1) * P], ACT.Exp,
                                                    bias=shift[:, q:q + 1], scale=SCALE, accum_out=total[:, q:q + 1]),
                               f"exp{q}")

        @block.vector
        def _(dve):
            ps, V = core.ps, nc.vector
            dve.wait_ge(future_made, 1)
            with dve.Fori(0, B) as b:
                norm.vector(dve, b, lambda j: core.x[:, b * TT + j, :], lambda j: xn[:, j, :], xn_ready)
                pe_s.wait(dve, "xT", b)
                ve_s.done(V.tensor_copy(xnT[:], ps[:, 6:8, :]), "xT")
                for q in range(TT):
                    pe_s.wait(dve, f"scores{q}", b)
                    own = ps[:, q, q * P:(q + 1) * P]
                    ve_s.done(V.tensor_tensor(own, own, future[:], ALU.add), f"masked{q}")
                    ve_s.wait(dve, f"masked{q}", b)
                    ve_s.done(V.tensor_reduce(top[:, q:q + 1], ps[:, q, 0:(q + 1) * P], AX, ALU.max), f"max{q}")
                    ve_s.wait(dve, f"max{q}", b)
                    ve_s.done(V.tensor_scalar(shift[:, q:q + 1], top[:, q:q + 1], -SCALE, None, ALU.mult), f"shift{q}")
                for q in range(TT):
                    pe_s.wait(dve, f"turned{q}", b)
                    ve_s.done(V.tensor_copy(probT[:, q % 2, 0:(q + 1) * P], ps[:, 4 + q % 2, 0:(q + 1) * P]), f"probT{q}")
                    act_s.wait(dve, f"exp{q}", b)
                    ve_s.done(V.reciprocal(inv[:, q:q + 1], total[:, q:q + 1]), f"inv{q}")
                    ve_s.wait(dve, f"inv{q}", b)
                    pe_s.wait(dve, f"out{q}", b)
                    row = core.x[:, b * TT + q, :]
                    ve_s.done(V.scalar_tensor_tensor(out=row, in0=ps[:, 6 + q % 2, 0:D], scalar=inv[:, q:q + 1], in1=row,
                                                     op0=ALU.mult, op1=ALU.add), f"row{q}")


def quantised_ffn_stage(core):
    nc, dram = core.nc, core.dram
    F = 704
    FT = -(-F // P)
    rows = [min(P, F - f * P) for f in range(FT)]
    QMAX = 127.0
    SLOTS = 3
    with Stage(core, "l1f") as st:
        norm = Norm(st)
        xn = st.sb("xn", [P, B * TT, D])
        hT = st.sb("hT", [P, FT, B * S])
        hq = st.sb("hq", [P, FT, S], BF16)
        silu = st.sb("silu", [P, SLOTS, S])
        xr = st.sb("xr", [P, TT, D])
        hr = st.sb("hr", [P, FT, S])
        xq = st.sb("xq", [P, TT, D], BF16)
        xqT = st.sb("xqT", [P, DC, S], BF16)
        ident = st.sb("ident16", [P, P], BF16)
        ones = st.sb("ones", [P, P])
        wraw = {n: st.sb(f"{n}_raw", [P, FT, D]) for n in ("gate", "up")}
        wraw["down"] = st.sb("down_raw", [P, DC, F])
        wmax = {n: st.sb(f"{n}_max", [P, DC if n == "down" else FT]) for n in wraw}
        winv = {n: st.sb(f"{n}_inv", [P, DC if n == "down" else FT]) for n in wraw}
        wlev = {n: st.sb(f"{n}_levels", list(wraw[n].shape), BF16) for n in wraw}
        wT = {n: st.sb(f"{n}T", [P, DC, F] if n != "down" else [P, FT, D], BF16) for n in wraw}
        gate_scale, up_scale = st.sb("gate_scale", [P, FT]), st.sb("up_scale", [P, FT])
        diag = st.sb("diag", [P, D])
        down_row, out_row = st.sb("down_row", [P, D]), st.sb("out_row", [P, D])
        clip = st.sb("clip", [P, 2])
        ratio = st.sb("ratio", [P, 2])
        xmax, hmax = st.sb("xmax", [P, B * TT]), st.sb("hmax", [P, B])
        own, whole, scale, inv = (st.sb(n, [P, 2]) for n in ("own", "whole", "scale", "inv"))
        part = st.sb("part", [P, TT, D])
        small_in, weights_in = st.sem("small_in"), st.sem("weights_in")
        xn_ready, max_ready, order = st.sem("xn_ready"), st.sem("max_ready"), st.sem("vector_order")
        act_ratio, ident_made, pool_max = st.sem("act_ratio"), st.sem("ident_made"), st.sem("pool_max")
        own_ready = st.sem("own_max_ready")
        pe_w = Steps(st.sem("pe_weight_steps"), ["gate0", "gate1", "up0", "up1", "down0", "down1", "down_row"])
        ve_w = Steps(st.sem("vector_weight_steps"), ["gate", "up", "down", "gate0", "gate1", "up0", "up1", "down0", "down1",
                                                     "diag", "down_row"])
        xq_ready, xT_full, xT_ready = st.sem("xq_ready"), st.sem("xT_full"), st.sem("xT_ready")
        both_full, silu_ready, hidden_ready = st.sem("gate_up_full"), st.sem("silu_ready"), st.sem("hidden_ready")
        hq_ready, down_full, rows_out = st.sem("hq_ready"), st.sem("down_full"), st.sem("rows_out")
        ve_x = st.sem("quantise_x_order")
        ve_h = st.sem("quantise_h_order")
        ve_r = st.sem("row_order")
        block = st.block()

        @block.sync
        def _(sp):
            for n in ("gate", "up"):
                sp.dma_start(wraw[n][:, 0:FT - 1, :], dram[f"l1f_{n}"][0:(FT - 1) * P, :].rearrange("(f p) d -> p f d", p=P)
                             ).then_inc(weights_in, 16)
                sp.dma_start(wraw[n][0:rows[-1], FT - 1, :], dram[f"l1f_{n}"][(FT - 1) * P:F, :]).then_inc(weights_in, 16)
            sp.dma_start(wraw["down"][:], dram["l1f_down"].rearrange("(c p) n -> p c n", p=P)).then_inc(weights_in, 16)
            for i, n in enumerate(("l1f_clip_x", "l1f_clip_down")):
                sp.dma_start(clip[:, i:i + 1], dram[n].to_broadcast([P, 1])).then_inc(small_in, 16)

        @block.gpsimd
        def _(pool):
            nc.gpsimd.memset(ones[:], 1.0)
            nc.gpsimd.tensor_copy(ident[:], core.ident[:]).then_inc(ident_made, 1)
            with pool.Fori(0, B) as b:
                norm.pool(pool, b)
            for i in range(2):
                pool.wait_ge(own_ready, i + 1)
                nc.gpsimd.partition_all_reduce(whole[:, i:i + 1], own[:, i:i + 1], P, bass.bass_isa.ReduceOp.max
                                               ).then_inc(pool_max, 1)

        @block.scalar
        def _(act):
            act.wait_ge(small_in, 32)
            nc.scalar.activation(ratio[:], clip[:], ACT.Sigmoid).then_inc(act_ratio, 1)
            with act.Fori(0, B) as b:
                for f, m in enumerate(rows):
                    act.wait_ge(both_full, b * FT + f + 1)
                    act.wait_ge(hidden_ready, b * FT + max(f + 1, SLOTS))
                    nc.scalar.activation(silu[0:m, f % SLOTS, :], core.ps[0:m, 2 * (f % SLOTS), :], ACT.Silu,
                                         scale=gate_scale[0:m, f:f + 1]).then_inc(silu_ready, 1)

        @block.tensor
        def _(pe):
            ps = core.ps
            pe.wait_ge(ident_made, 1)
            for n in ("gate", "up"):
                ve_w.wait(pe, n)
                for c in range(DC):
                    for f, m in enumerate(rows):
                        last = nc.tensor.transpose(ps[:, c, :].bitcast(BF16)[:, f * P:f * P + m],
                                                   wlev[n][0:m, f, c * P:(c + 1) * P], ident[0:m, 0:m])
                    pe_w.done(last, f"{n}{c}")
                    ve_w.wait(pe, f"{n}{c}")
            ve_w.wait(pe, "down")
            for c in range(DC):
                for f, m in enumerate(rows):
                    last = nc.tensor.transpose(ps[0:m, c, :].bitcast(BF16)[:, f * P:(f + 1) * P],
                                               wlev["down"][:, c, f * P:f * P + m], ident[:])
                pe_w.done(last, f"down{c}")
            ve_w.wait(pe, "diag")
            pe_w.done(nc.tensor.matmul(ps[:, 2, 0:D], ones[:], diag[:], start=True, stop=True), "down_row")
            ve_w.wait(pe, "down_row")
            with pe.Fori(0, B) as b:
                pe.wait_ge(xq_ready, b + 1)
                for c in range(DC):
                    for j in range(TT):
                        last = nc.tensor.transpose(ps[:, 6, :].bitcast(BF16)[:, (c * TT + j) * P:(c * TT + j + 1) * P],
                                                   xq[:, j, c * P:(c + 1) * P], ident[:])
                last.then_inc(xT_full, 1)
                pe.wait_ge(xT_ready, b + 1)
                for f, m in enumerate(rows):
                    pe.wait_ge(hidden_ready, b * FT + max(f + 1, SLOTS))
                    for i, n in enumerate(("gate", "up")):
                        for c in range(DC):
                            last = nc.tensor.matmul(ps[0:m, 2 * (f % SLOTS) + i, :], wT[n][:, c, f * P:f * P + m],
                                                    xqT[:, c, :], start=(c == 0), stop=(c == DC - 1))
                    last.then_inc(both_full, 1)
            with pe.Fori(0, B) as b:
                pe.wait_ge(hq_ready, b + 1)
                for j in range(TT):
                    pe.wait_ge(rows_out, b * TT + max(j + 1, 2))
                    for f, m in enumerate(rows):
                        last = nc.tensor.matmul(ps[:, 6 + j % 2, 0:D], hq[0:m, f, j * P:(j + 1) * P], wT["down"][0:m, f, :],
                                                start=(f == 0), stop=(f == FT - 1))
                    last.then_inc(down_full, 1)

        @block.vector
        def _(dve):
            ps, V = core.ps, nc.vector
            dve.sem_inc(hidden_ready, SLOTS)
            dve.sem_inc(rows_out, 2)
            with dve.Fori(0, B) as b:
                norm.vector(dve, b, lambda j: core.x[:, b * TT + j, :], lambda j: xn[:, b * TT + j, :], xn_ready)
                dve.wait_ge(xn_ready, b + 1)
                V.tensor_reduce(xmax[:, bass.ds(b * TT, TT)], xn[:, bass.ds(b * TT, TT), :], AX, ALU.max,
                                apply_absolute_value=True).then_inc(max_ready, 1)
            link = Chain(dve, order)

            def levels(link, dst, src, inv, tmp):
                link(V.tensor_scalar(tmp, src, inv, QMAX, ALU.mult, ALU.min))
                link(V.tensor_scalar(tmp, tmp, -QMAX - 1.0, ROUND, ALU.max, ALU.add))
                return V.tensor_scalar(dst, tmp, ROUND, None, ALU.subtract)

            def global_scale(i, maxima):
                link(V.tensor_reduce(own[:, i:i + 1], maxima, AX, ALU.max))
                V.tensor_copy(own[:, i:i + 1], own[:, i:i + 1]).then_inc(own_ready, 1)
                dve.wait_ge(pool_max, i + 1)
                link(V.tensor_tensor(scale[:, i:i + 1], whole[:, i:i + 1], ratio[:, i:i + 1], ALU.mult))
                link(V.tensor_scalar(scale[:, i:i + 1], scale[:, i:i + 1], 1.0 / QMAX, None, ALU.mult))
                link(V.reciprocal(inv[:, i:i + 1], scale[:, i:i + 1]))

            dve.wait_ge(max_ready, B)
            dve.wait_ge(act_ratio, 1)
            global_scale(0, xmax[:])
            dve.wait_ge(weights_in, 16 * 5)
            for n in ("gate", "up", "down"):
                tiles = [(c, P) for c in range(DC)] if n == "down" else list(enumerate(rows))
                for f, m in tiles:
                    link(V.tensor_reduce(wmax[n][0:m, f:f + 1], wraw[n][0:m, f, :], AX, ALU.max, apply_absolute_value=True))
                    link(V.tensor_scalar(wmax[n][0:m, f:f + 1], wmax[n][0:m, f:f + 1], 1.0 / QMAX, None, ALU.mult))
                    link(V.reciprocal(winv[n][0:m, f:f + 1], wmax[n][0:m, f:f + 1]))
                    last = levels(link, wlev[n][0:m, f, :], wraw[n][0:m, f, :], winv[n][0:m, f:f + 1], wraw[n][0:m, f, :])
                    if n != "down":
                        dst = gate_scale if n == "gate" else up_scale
                        V.tensor_scalar(dst[0:m, f:f + 1], wmax[n][0:m, f:f + 1], scale[0:m, 0:1], None, ALU.mult)
                ve_w.done(last, n)
            for n in ("gate", "up"):
                for c in range(DC):
                    pe_w.wait(dve, f"{n}{c}")
                    ve_w.done(V.tensor_copy(wT[n][:, c, :], ps[:, c, :].bitcast(BF16)[:, 0:F]), f"{n}{c}")
            for c in range(DC):
                pe_w.wait(dve, f"down{c}")
                turned = ps[:, c, :].bitcast(BF16)
                V.tensor_copy(wT["down"][:, 0:FT - 1, c * P:(c + 1) * P], turned[:, 0:(FT - 1) * P].rearrange("p (f n) -> p f n", n=P))
                ve_w.done(V.tensor_copy(wT["down"][0:rows[-1], FT - 1, c * P:(c + 1) * P], turned[0:rows[-1], (FT - 1) * P:FT * P]),
                          f"down{c}")
            for c in range(DC):
                last = V.tensor_scalar(diag[:, c * P:(c + 1) * P], core.ident[:], wmax["down"][:, c:c + 1], None, ALU.mult)
            ve_w.done(last, "diag")
            pe_w.wait(dve, "down_row")
            ve_w.done(V.tensor_copy(down_row[:], ps[:, 2, 0:D]), "down_row")
            V.memset(hT[rows[-1]:P, FT - 1, :], 0.0)
            with dve.Fori(0, B) as b:
                chain = Chain(dve, ve_x, b * 2)
                levels(chain, xq[:], xn[:, bass.ds(b * TT, TT), :], inv[:, 0:1], xr[:]).then_inc(xq_ready, 1)
                dve.wait_ge(xT_full, b + 1)
                V.tensor_copy(xqT[:], ps[:, 6, :].bitcast(BF16).rearrange("p (c s) -> p c s", c=DC)).then_inc(xT_ready, 1)
                for f, m in enumerate(rows):
                    dve.wait_ge(silu_ready, b * FT + f + 1)
                    V.scalar_tensor_tensor(out=hT[0:m, f, bass.ds(b * S, S)], in0=ps[0:m, 2 * (f % SLOTS) + 1, :],
                                           scalar=up_scale[0:m, f:f + 1], in1=silu[0:m, f % SLOTS, :],
                                           op0=ALU.mult, op1=ALU.mult).then_inc(hidden_ready, 1)
                dve.wait_ge(hidden_ready, (b + 1) * FT + SLOTS)
                V.tensor_reduce(hmax[:, bass.ds(b, 1)], hT[:, :, bass.ds(b * S, S)], mybir.AxisListType.XY, ALU.max,
                                apply_absolute_value=True).then_inc(max_ready, 1)
            dve.wait_ge(max_ready, 2 * B)
            global_scale(1, hmax[:])
            link(V.tensor_scalar(out_row[:], down_row[:], scale[:, 1:2], None, ALU.mult))
            with dve.Fori(0, B) as b:
                chain = Chain(dve, ve_h, b * 2)
                levels(chain, hq[:], hT[:, :, bass.ds(b * S, S)], inv[:, 1:2], hr[:]).then_inc(hq_ready, 1)
                for j in range(TT):
                    dve.wait_ge(down_full, b * TT + j + 1)
                    V.tensor_tensor(part[:, j, :], ps[:, 6 + j % 2, 0:D], out_row[:], ALU.mult).then_inc(rows_out, 1)
                    dve.wait_ge(rows_out, b * TT + j + 3)
                    row = core.x[:, b * TT + j, :]
                    last = V.tensor_tensor(row, row, part[:, j, :], ALU.add)
                last.then_inc(ve_r, 1)
                dve.wait_ge(ve_r, b + 1)


def autocorrelation_stage(core):
    nc, dram = core.nc, core.dram
    BEST = 12
    with Stage(core, "l2x") as st:
        norm = Norm(st)
        xn = st.sb("xn", [P, TT, D])
        xnT = st.sb("xnT", [P, DC, S])
        ctxT = st.sb("ctxT", [P, DC, S])
        wq, wk, wv, wo = (st.sb(n, [P, DC, D]) for n in ("wq", "wk", "wv", "wo"))
        bq, bk, bv, bo = (st.sb(n, [P, D]) for n in ("bq", "bk", "bv", "bo"))
        basis, inverse = st.sb("basis", [P, TT, S]), st.sb("inverse", [P, TT, S])
        qk = st.sb("qk", [P, TT, 2, D])
        qhat, junk = st.sb("qhat", [P, TT, D]), st.sb("junk", [P, TT, D])
        power = st.sb("power", [P, B, TT])
        power_b = st.sb("power_b", [P, TT, B])
        mean, work, chosen, gain = (st.sb(n, [B, S]) for n in ("mean", "work", "chosen", "gain"))
        eight, four = st.sb("eight", [B, 8]), st.sb("four", [B, 8])
        shift, total, inv = (st.sb(n, [B, 1]) for n in ("shift", "total", "inv"))
        circulant = st.sb("circulant", [P, B, TT, S])
        v = st.sb("v", [P, TT, D])
        aggT = st.sb("aggT", [P, DC, S])
        part = st.sb("part", [P, TT, D])
        rows = dram["delay_rows"]
        weights_in, bias_in, ctx_in, ctx_used = (st.sem(n) for n in ("weights_in", "bias_in", "ctx_in", "ctx_used"))
        xn_ready, order, rows_out, circulant_in = (st.sem(n) for n in ("xn_ready", "order", "rows_out", "circulant_in"))
        exp_done, summed = st.sem("exp_done"), st.sem("rows_summed")
        pe_a = Steps(st.sem("pe_spectrum_steps"), ["xT"] + [f"q{j}" for j in range(TT)] + [f"k{j}" for j in range(TT)]
                     + [f"hat{r}" for r in range(TT)])
        ve_a = Steps(st.sem("vector_spectrum_steps"), ["xT"] + [f"q{j}" for j in range(TT)] + [f"k{j}" for j in range(TT)]
                     + [f"power{r}" for r in range(TT)])
        act_a = Steps(st.sem("act_spectrum_steps"), [f"qhat{r}" for r in range(TT)])
        one = Steps(st.sem("pe_mean"), ["mean"])
        ve_m = Steps(st.sem("vector_mean_steps"), ["power", "shift", "gain"])
        pe_b = Steps(st.sem("pe_shift_steps"), [f"v{j}" for j in range(TT)] + [f"agg{c}" for c in range(DC)]
                     + [f"out{j}" for j in range(TT)])
        ve_b = Steps(st.sem("vector_shift_steps"), [f"v{j}" for j in range(TT)] + [f"agg{c}" for c in range(DC)]
                     + [f"out{j}" for j in range(TT)])
        block = st.block()

        @block.sync
        def _(sp):
            for dst, name in ((wq, "l2x_Wq"), (wk, "l2x_Wk"), (wv, "l2x_Wv"), (wo, "l2x_Wo"),
                              (basis, "dft_basis"), (inverse, "dft_inverse")):
                sp.dma_start(dst[:], dram[name].rearrange("(c p) n -> p c n", p=P)).then_inc(weights_in, 16)
            for dst, name in ((bq, "l2x_bq"), (bk, "l2x_bk"), (bv, "l2x_bv"), (bo, "l2x_bo")):
                sp.dma_start(dst[:], dram[name].to_broadcast([P, D])).then_inc(bias_in, 16)
            with sp.Fori(0, B) as b:
                sp.wait_ge(ctx_used, b + 1)
                sp.dma_start(ctxT[:], dram["ctxT"][b].rearrange("(c p) s -> p c s", p=P)).then_inc(ctx_in, 16)
            ve_m.wait(sp, "gain")
            for i in range(2):
                sp.dma_start(rows[:, i * S:(i + 1) * S], gain[:]).then_inc(rows_out, 16)
            sp.wait_ge(rows_out, 32)
            for b in range(B):
                for j in range(TT):
                    src = bass.AP(tensor=rows.tensor, offset=b * 2 * S + S - j * P - (P - 1), ap=[[1, P], [1, S]])
                    sp.dma_start(circulant[:, b, j, :], src).then_inc(circulant_in, 16)
            with sp.Fori(0, B) as b:
                sp.wait_ge(ctx_used, b + 1 + B)
                sp.dma_start(ctxT[:], dram["ctxT_back"][b].rearrange("(c p) s -> p c s", p=P)).then_inc(ctx_in, 16)

        @block.gpsimd
        def _(pool):
            with pool.Fori(0, B) as b:
                norm.pool(pool, b)

        @block.scalar
        def _(act):
            with act.Fori(0, B) as b:
                for r in range(TT):
                    pe_a.wait(act, f"hat{r}", b)
                    act_a.done(nc.scalar.activation(qhat[:, r, :], core.ps[:, r, 0:D], ACT.Copy), f"qhat{r}")
            ve_m.wait(act, "shift")
            nc.scalar.activation(gain[:], mean[:], ACT.Exp, bias=shift[:, 0:1]).then_inc(exp_done, 1)

        @block.tensor
        def _(pe):
            ps = core.ps
            pe.sem_inc(ctx_used, 1)
            pe.wait_ge(weights_in, 16 * 6)
            with pe.Fori(0, B) as b:
                pe.wait_ge(xn_ready, b + 1)
                for c in range(DC):
                    for j in range(TT):
                        last = nc.tensor.transpose(ps[:, 4 + c, j * P:(j + 1) * P], xn[:, j, c * P:(c + 1) * P], core.ident[:])
                pe_a.done(last, "xT")
                pe.wait_ge(ctx_in, b * 16 + 16)
                ve_a.wait(pe, "xT", b)
                for i, (src, w, name) in enumerate(((xnT, wq, "q"), (ctxT, wk, "k"))):
                    for j in range(TT):
                        n = i * TT + j
                        if n >= 2:
                            ve_a.wait(pe, f"{'qk'[(n - 2) // TT]}{(n - 2) % TT}", b)
                        for c in range(DC):
                            last = nc.tensor.matmul(ps[:, 6 + n % 2, 0:D], src[:, c, j * P:(j + 1) * P], w[:, c, :],
                                                    start=(c == 0), stop=(c == DC - 1))
                        pe_a.done(last, f"{name}{j}")
                ve_a.wait(pe, f"k{TT - 1}", b)
                pe.sem_inc(ctx_used, 1)
                for r in range(TT):
                    for j in range(TT):
                        last = nc.tensor.matmul(ps[:, r, :], basis[:, j, r * P:(r + 1) * P], qk[:, j, :, :],
                                                start=(j == 0), stop=(j == TT - 1))
                    pe_a.done(last, f"hat{r}")
                ve_a.wait(pe, f"power{TT - 1}", b)
            ve_m.wait(pe, "power")
            for r in range(TT):
                last = nc.tensor.matmul(ps[0:B, 0, :], power_b[:, r, :], inverse[:, r, :], start=(r == 0), stop=(r == TT - 1))
            one.done(last, "mean")
            pe.wait_ge(circulant_in, 16 * B * TT)
            with pe.Fori(0, B) as b:
                pe.wait_ge(ctx_in, b * 16 + 16 + B * 16)
                for j in range(TT):
                    if j >= 2:
                        ve_b.wait(pe, f"v{j - 2}", b)
                    for c in range(DC):
                        last = nc.tensor.matmul(ps[:, 6 + j % 2, 0:D], ctxT[:, c, j * P:(j + 1) * P], wv[:, c, :],
                                                start=(c == 0), stop=(c == DC - 1))
                    pe_b.done(last, f"v{j}")
                ve_b.wait(pe, f"v{TT - 1}", b)
                pe.sem_inc(ctx_used, 1)
                for c in range(DC):
                    for j in range(TT):
                        last = nc.tensor.matmul(ps[:, 4 + c, :], v[:, j, c * P:(c + 1) * P], circulant[:, b, j, :],
                                                start=(j == 0), stop=(j == TT - 1))
                    pe_b.done(last, f"agg{c}")
                ve_b.wait(pe, f"agg{DC - 1}", b)
                for j in range(TT):
                    for c in range(DC):
                        last = nc.tensor.matmul(ps[:, j, 0:D], aggT[:, c, j * P:(j + 1) * P], wo[:, c, :],
                                                start=(c == 0), stop=(c == DC - 1))
                    pe_b.done(last, f"out{j}")
                ve_b.wait(pe, f"out{TT - 1}", b)

        @block.vector
        def _(dve):
            ps, V = core.ps, nc.vector
            dve.wait_ge(bias_in, 16 * 4)
            with dve.Fori(0, B) as b:
                norm.vector(dve, b, lambda j: core.x[:, b * TT + j, :], lambda j: xn[:, j, :], xn_ready)
                pe_a.wait(dve, "xT", b)
                ve_a.done(V.tensor_copy(xnT[:], ps[:, 4:6, :]), "xT")
                for i, (name, bias) in enumerate((("q", bq), ("k", bk))):
                    for j in range(TT):
                        pe_a.wait(dve, f"{name}{j}", b)
                        ve_a.done(V.tensor_tensor(qk[:, j, i, :], ps[:, 6 + j % 2, 0:D], bias[:], ALU.add), f"{name}{j}")
                for r in range(TT):
                    act_a.wait(dve, f"qhat{r}", b)
                    ve_a.done(V.scalar_tensor_tensor(out=junk[:, r, :], in0=ps[:, r, D:2 * D], scalar=1.0, in1=qhat[:, r, :],
                                                     op0=ALU.mult, op1=ALU.mult, accum_out=power[:, b, r:r + 1]), f"power{r}")
                ve_a.wait(dve, f"power{TT - 1}", b)
            ve_m.done(V.tensor_copy(power_b[:].rearrange("p r b -> p b r"), power[:]), "power")
            one.wait(dve, "mean")
            link = Chain(dve, order)
            link(V.tensor_copy(mean[:], ps[0:B, 0, :]))
            link(V.max(eight[:], mean[:]))
            ve_m.done(V.tensor_scalar(shift[:], eight[:, 0:1], -1.0, None, ALU.mult), "shift")
            link(V.match_replace(work[:], eight[:], mean[:], NEG))
            link(V.max(four[:], work[:]))
            link(V.memset(four[:, BEST - 8:8], NEG))
            link(V.match_replace(work[:], four[:], work[:], NEG))
            link(V.tensor_tensor(chosen[:], work[:], mean[:], ALU.not_equal))
            dve.wait_ge(exp_done, 1)
            link(V.tensor_tensor(gain[:], gain[:], chosen[:], ALU.mult))
            link(V.tensor_reduce(total[:], gain[:], AX, ALU.add))
            link(V.reciprocal(inv[:], total[:]))
            ve_m.done(V.tensor_scalar(gain[:], gain[:], inv[:, 0:1], None, ALU.mult), "gain")
            with dve.Fori(0, B) as b:
                for j in range(TT):
                    pe_b.wait(dve, f"v{j}", b)
                    ve_b.done(V.tensor_tensor(v[:, j, :], ps[:, 6 + j % 2, 0:D], bv[:], ALU.add), f"v{j}")
                for c in range(DC):
                    pe_b.wait(dve, f"agg{c}", b)
                    ve_b.done(V.tensor_copy(aggT[:, c, :], ps[:, 4 + c, :]), f"agg{c}")
                for j in range(TT):
                    pe_b.wait(dve, f"out{j}", b)
                    ve_b.done(V.tensor_tensor(part[:, j, :], ps[:, j, 0:D], bo[:], ALU.add), f"out{j}")
                ve_b.wait(dve, f"out{TT - 1}", b)
                rows_now = core.x[:, bass.ds(b * TT, TT), :]
                V.tensor_tensor(rows_now, rows_now, part[:], ALU.add).then_inc(summed, 1)
                dve.wait_ge(summed, b + 1)


class Router:

    def __init__(self, st, name, keep_turned):
        self.st, self.nc, self.core, self.w_name, self.keep_turned = st, st.nc, st.core, name, keep_turned
        self.norm = Norm(st)
        self.xn = st.sb("xn", [P, TT, D])
        self.xnT = st.sb("xnT", [P, DC, S])
        if keep_turned:
            self.xT = st.sb("xT", [P, B, DC, S])
        else:
            self.kept_rows = st.sb("kept_rows", [P, B * TT, D])
        self.w = st.sb("w_router", [P, DC, 8])
        self.logits = st.sb("logits", [P, B * TT, 8])
        self.probs = st.sb("probs", [P, B * TT, 16])
        self.marked = st.sb("marked", [P, B * TT, 16])
        self.best = st.sb("best", [P, B * TT, 8])
        self.chosen = st.sb("chosen", [P, B * TT, 8])
        self.top, self.total, self.inv = (st.sb(n, [P, B * TT]) for n in ("top", "total", "inv"))
        self.w_in, self.xn_ready, self.order = st.sem("router_in"), st.sem("xn_ready"), st.sem("router_order")
        self.pe = Steps(st.sem("pe_router_steps"), ["xT", "logits"])
        self.ve = Steps(st.sem("vector_router_steps"), ["xT", "logits"])
        self.kept = st.sem("kept")
        self.centred, self.exp_done = st.sem("centred"), st.sem("exp_done")

    def sync(self, sp):
        sp.dma_start(self.w[:], self.core.dram[self.w_name].rearrange("(c p) n -> p c n", p=P)).then_inc(self.w_in, 16)

    def pool(self, pool):
        with pool.Fori(0, B) as b:
            self.norm.pool(pool, b)

    def tensor(self, pe):
        nc, ps = self.nc, self.core.ps
        pe.wait_ge(self.w_in, 16)
        with pe.Fori(0, B) as b:
            pe.wait_ge(self.xn_ready, b + 1)
            for c in range(DC):
                for j in range(TT):
                    last = nc.tensor.transpose(ps[:, c, j * P:(j + 1) * P], self.xn[:, j, c * P:(c + 1) * P], self.core.ident[:])
            self.pe.done(last, "xT")
            self.ve.wait(pe, "xT", b)
            for j in range(TT):
                for c in range(DC):
                    last = nc.tensor.matmul(ps[:, 2, j * 8:(j + 1) * 8], self.xnT[:, c, j * P:(j + 1) * P], self.w[:, c, :],
                                            start=(c == 0), stop=(c == DC - 1))
            self.pe.done(last, "logits")
            self.ve.wait(pe, "logits", b)

    def scalar(self, act):
        nc = self.nc
        with act.Fori(0, B) as b:
            if self.keep_turned:
                self.ve.wait(act, "xT", b)
                nc.scalar.activation(self.xT[:, b, :, :], self.xnT[:], ACT.Copy).then_inc(self.kept, 1)
            else:
                act.wait_ge(self.xn_ready, b + 1)
                nc.scalar.activation(self.kept_rows[:, bass.ds(b * TT, TT), :], self.xn[:], ACT.Copy).then_inc(self.kept, 1)
        act.wait_ge(self.centred, 1)
        nc.scalar.activation(self.logits[:], self.logits[:], ACT.Exp).then_inc(self.exp_done, 1)

    def vector(self, dve):
        V, ps = self.nc.vector, self.core.ps
        with dve.Fori(0, B) as b:
            self.norm.vector(dve, b, lambda j: self.core.x[:, b * TT + j, :], lambda j: self.xn[:, j, :],
                             self.xn_ready)
            self.pe.wait(dve, "xT", b)
            dve.wait_ge(self.xn_ready, b + 1)
            self.ve.done(V.tensor_copy(self.xnT[:], ps[:, 0:2, :]), "xT")
            self.pe.wait(dve, "logits", b)
            dve.wait_ge(self.kept, b + 1)
            self.ve.done(V.tensor_copy(self.logits[:, bass.ds(b * TT, TT), :],
                                       ps[:, 2, 0:TT * 8].rearrange("p (j e) -> p j e", e=8)), "logits")
        self.ve.wait(dve, "logits", B - 1)
        link = Chain(dve, self.order)
        shape = [P, B * TT, 8]
        link(V.tensor_reduce(self.top[:], self.logits[:], AX, ALU.max))
        V.tensor_tensor(self.logits[:], self.logits[:], self.top[:].unsqueeze(2).to_broadcast(shape), ALU.subtract
                        ).then_inc(self.centred, 1)
        dve.wait_ge(self.exp_done, 1)
        link(V.tensor_reduce(self.total[:], self.logits[:], AX, ALU.add))
        link(V.reciprocal(self.inv[:], self.total[:]))
        link(V.memset(self.probs[:, :, 8:16], -1.0))
        link(V.tensor_tensor(self.probs[:, :, 0:8], self.logits[:], self.inv[:].unsqueeze(2).to_broadcast(shape), ALU.mult))
        for t in range(B * TT):
            last = V.max(self.best[:, t, :], self.probs[:, t, :])
        link(last)
        link(V.tensor_tensor(self.total[:], self.best[:, :, 0], self.best[:, :, 1], ALU.add))
        link(V.memset(self.best[:, :, 2:8], -1.0))
        for t in range(B * TT):
            last = V.match_replace(self.marked[:, t, :], self.best[:, t, :], self.probs[:, t, :], 2.0)
        link(last)
        link(V.tensor_tensor(self.chosen[:], self.marked[:, :, 0:8], self.probs[:, :, 0:8], ALU.not_equal))
        return link


def relu_experts_stage(core):
    nc, dram = core.nc, core.dram
    E, FT = 10, 2
    ROUND_E = 2
    UNITS = ROUND_E * B
    with Stage(core, "l2f") as st:
        router = Router(st, "l2f_router", keep_turned=True)
        w1 = st.sb("w1", [P, ROUND_E, DC, FT * P])
        w2 = st.sb("w2", [P, ROUND_E, FT, D])
        weight = st.sb("weight", [P, B * TT, E])
        relu = st.sb("relu", [P, 2, FT, S])
        hT = st.sb("hT", [P, 2, FT, S])
        weights_in = [st.sem(f"weights_in{i}") for i in range(ROUND_E)]
        weights_used = [st.sem(f"weights_used{i}") for i in range(ROUND_E)]
        up_full, relu_ready, hidden_ready = st.sem("up_full"), st.sem("relu_ready"), st.sem("hidden_ready")
        down_full, rows_done, weighed = st.sem("down_full"), st.sem("rows_done"), st.sem("weighed")
        block = st.block()

        @block.sync
        def _(sp):
            router.sync(sp)
            with sp.Fori(0, E // ROUND_E) as r:
                for i in range(ROUND_E):
                    sp.wait_ge(weights_used[i], r + 1)
                    sp.dma_start(w1[:, i, :, :], dram["l2f_w1"][r * ROUND_E + i].rearrange("(c p) f -> p c f", p=P)
                                 ).then_inc(weights_in[i], 16)
                    sp.dma_start(w2[:, i, :, :], dram["l2f_w2"][r * ROUND_E + i].rearrange("(c p) f -> p c f", p=P)
                                 ).then_inc(weights_in[i], 16)

        @block.gpsimd
        def _(pool):
            router.pool(pool)

        @block.tensor
        def _(pe):
            ps = core.ps
            for i in range(ROUND_E):
                pe.sem_inc(weights_used[i], 1)
            router.tensor(pe)
            with pe.Fori(0, E // ROUND_E) as r:
                def up(u):
                    i, b = divmod(u, B)
                    if b == 0:
                        pe.wait_ge(weights_in[i], r * 32 + 32)
                    for f in range(FT):
                        n = u * FT + f
                        pe.wait_ge(relu_ready, (r * UNITS) * FT + n + 1)
                        for c in range(DC):
                            last = nc.tensor.matmul(ps[:, n % 4, :], w1[:, i, c, f * P:(f + 1) * P], router.xT[:, b, c, :],
                                                    start=(c == 0), stop=(c == DC - 1))
                        last.then_inc(up_full, 1)

                def down(u):
                    i, b = divmod(u, B)
                    pe.wait_ge(hidden_ready, (r * UNITS + u + 1) * FT + 4)
                    for j in range(TT):
                        pe.wait_ge(rows_done, (r * UNITS + u) * TT + j + 1)
                        for f in range(FT):
                            last = nc.tensor.matmul(ps[:, 4 + j, 0:D], hT[:, u % 2, f, j * P:(j + 1) * P], w2[:, i, f, :],
                                                    start=(f == 0), stop=(f == FT - 1))
                        last.then_inc(down_full, 1)
                    if b == B - 1:
                        pe.wait_ge(rows_done, (r * UNITS + u) * TT + TT + 4)
                        pe.sem_inc(weights_used[i], 1)

                up(0)
                for u in range(UNITS):
                    if u + 1 < UNITS:
                        up(u + 1)
                    down(u)

        @block.scalar
        def _(act):
            act.sem_inc(relu_ready, 4)
            router.scalar(act)
            with act.Fori(0, E // ROUND_E) as r:
                for u in range(UNITS):
                    for f in range(FT):
                        n = u * FT + f
                        act.wait_ge(up_full, r * UNITS * FT + n + 1)
                        act.wait_ge(hidden_ready, r * UNITS * FT + n + 1)
                        nc.scalar.activation(relu[:, u % 2, f, :], core.ps[:, n % 4, :], ACT.Relu).then_inc(relu_ready, 1)

        @block.vector
        def _(dve):
            ps, V = core.ps, nc.vector
            dve.sem_inc(hidden_ready, 4)
            dve.sem_inc(rows_done, 4)
            link = router.vector(dve)
            link(V.reciprocal(router.inv[:], router.total[:]))
            link(V.tensor_tensor(router.chosen[:], router.chosen[:], router.probs[:, :, 0:8], ALU.mult))
            link(V.memset(weight[:, :, 8:E], 1.0))
            link(V.tensor_tensor(weight[:, :, 0:8], router.chosen[:],
                                 router.inv[:].unsqueeze(2).to_broadcast([P, B * TT, 8]), ALU.mult))
            with dve.Fori(0, E // ROUND_E) as r:
                def square(u):
                    for f in range(FT):
                        n = u * FT + f
                        dve.wait_ge(relu_ready, r * UNITS * FT + n + 1 + 4)
                        if u >= 2:
                            dve.wait_ge(down_full, (r * UNITS + u - 1) * TT)
                        V.tensor_tensor(hT[:, u % 2, f, :], relu[:, u % 2, f, :], relu[:, u % 2, f, :], ALU.mult
                                        ).then_inc(hidden_ready, 1)

                def add(u):
                    i, b = divmod(u, B)
                    for j in range(TT):
                        t = b * TT + j
                        dve.wait_ge(down_full, (r * UNITS + u) * TT + j + 1)
                        dve.wait_ge(rows_done, (r * UNITS + u) * TT + j + 1)
                        V.scalar_tensor_tensor(out=core.x[:, t, :], in0=ps[:, 4 + j, 0:D],
                                               scalar=weight[:, t, bass.ds(r * ROUND_E + i, 1)], in1=core.x[:, t, :],
                                               op0=ALU.mult, op1=ALU.add).then_inc(rows_done, 1)

                square(0)
                for u in range(UNITS):
                    if u + 1 < UNITS:
                        square(u + 1)
                    add(u)


def gated_experts_stage(core):
    nc, dram = core.nc, core.dram
    E, F = 8, 704
    FT = -(-F // P)
    rows = [min(P, F - f * P) for f in range(FT)]
    T = B * TT
    N = 2 * P
    K = (2 * T * P + E * (N - 1)) // N
    W = D + 1
    LOOPED = (K - 2) // 2
    RING = 3
    U32 = mybir.dt.uint32
    with Stage(core, "l3f") as st:
        router = Router(st, "l3f_router", keep_turned=False)
        w1, w3 = (st.sb(n, [P, 2, DC, F]) for n in ("w1", "w3"))
        w2 = st.sb("w2", [P, 2, FT, D])
        earlier, ones = st.sb("earlier", [P, P]), st.sb("ones", [P, P])
        numbers = st.sb("numbers", [P, T, 2])
        starts = st.sb("starts", [P, E])
        block_no = st.sb("block_no", [P, K])
        spare_no = st.sb("spare_no", [P, 2 * K])
        blank = st.sb("blank", [P, 2 * K, W])
        y_in = blank[:, 0:2 * T, 0:D].rearrange("p (c t) d -> p c t d", c=2)
        score, slot, is_second = (st.sb(n, [P, T, E]) for n in ("score", "slot", "is_second"))
        sums = st.sb("sums", [P, 2, T, E])
        filled = st.sb("filled", [P, E, E])
        blocks, ends, counts = st.sb("blocks", [P, E]), st.sb("ends", [P, 2, E]), st.sb("counts", [P, E])
        ended = st.sb("ended", [P, K, E])
        expert, expert_no = st.sb("expert", [P, K]), st.sb("expert_no", [P, K], I32)
        slots, slot_no = st.sb("slots", [P, T, 2]), st.sb("slot_no", [P, T, 2], U32)
        slot_sum = st.sb("slot_sum", [P, T])
        choice_score = st.sb("choice_score", [P, T, 2])
        scaled = st.sb("scaled", [P, T, 2, W])
        xs = st.sb("xs", [P, 2, 2, W])
        xT = st.sb("xT_block", [P, 2, DC, N])
        silu = st.sb("silu", [P, RING, N])
        hT = st.sb("hT", [P, 2, FT, N])
        y = st.sb("y", [P, 2, 2, D])
        numbers_of = st.sb("numbers_of", [P, K, 2])
        row_no = st.sb("row_no", [P, 2, 2], U32)
        const_in, cleared, blank_ready = st.sem("const_in"), st.sem("cleared"), st.sem("blank_ready")
        placed, ranks_full, experts_known = st.sem("placed"), st.sem("ranks_full"), st.sem("experts_known")
        scaled_ready, scattered = st.sem("scaled_ready"), st.sem("scattered")
        xs_in = [st.sem(f"xs_in{i}") for i in range(2)]
        w13_in = [st.sem(f"w13_in{i}") for i in range(2)]
        w2_in = [st.sem(f"w2_in{i}") for i in range(2)]
        turned, xT_ready, both_full, silu_ready, hidden_ready = (
            st.sem(n) for n in ("turned", "xT_ready", "both_full", "silu_ready", "hidden_ready"))
        down_full, y_ready, row_no_ready = st.sem("down_full"), st.sem("y_ready"), st.sem("row_no_ready")
        y_out = [st.sem(f"y_out{i}") for i in range(2)]
        y_back = [st.sem(f"y_back{b}") for b in range(B)]
        added = st.sem("added")
        block = st.block()


        @block.sync
        def _(sp):
            router.sync(sp)
            for dst, name in ((earlier, "earlier"), (numbers, "choice_numbers"), (spare_no, "spare_numbers")):
                sp.dma_start(dst[:], dram[name]).then_inc(const_in, 16)
            sp.dma_start(starts[:], dram["block_starts"].to_broadcast([P, E])).then_inc(const_in, 16)
            sp.dma_start(block_no[:], dram["block_numbers"].to_broadcast([P, K])).then_inc(const_in, 16)
            sp.wait_ge(blank_ready, 2)
            sp.dma_start(dram["xs_rows"].rearrange("(k p) d -> p k d", p=P), blank[:]).then_inc(cleared, 16)

            def tokens(r, i):
                sp.dma_start(xs[:, i, :, :], dram["xs_rows"][bass.ds((r * 2 + i) * N, N), :].rearrange("(j p) d -> p j d", p=P)
                             ).then_inc(xs_in[i], 16)

            def gates(e, i):
                for dst, name in ((w1, "l3f_w1"), (w3, "l3f_w3")):
                    sp.dma_start(dst[:, i, :, :], dram[name][e].rearrange("(c p) f -> p c f", p=P)
                                 ).then_inc(w13_in[i], 16)

            def downs(e, i):
                sp.dma_start(w2[:, i, 0:FT - 1, :], dram["l3f_w2"][e, 0:(FT - 1) * P, :].rearrange("(f p) d -> p f d", p=P)
                             ).then_inc(w2_in[i], 16)
                sp.dma_start(w2[0:rows[-1], i, FT - 1, :], dram["l3f_w2"][e, (FT - 1) * P:F, :]
                             ).then_inc(w2_in[i], 16)

            def expert_of(k):
                return sp.value_load(expert_no[0:1, bass.ds(k, 1)], min_val=0, max_val=E - 1)

            def load(r, i):
                k = r * 2 + i
                e = expert_of(k)
                sp.wait_ge(xT_ready, k - 1)
                tokens(r, i)
                sp.wait_ge(both_full, (k - 1) * FT)
                gates(e, i)
                sp.wait_ge(down_full, k + 1)
                downs(e, i)

            sp.wait_ge(experts_known, 1)
            for i in range(2):
                e = expert_of(i)
                gates(e, i)
                downs(e, i)
            sp.wait_ge(scattered, 2 * T * 16)
            for i in range(2):
                tokens(0, i)
            with sp.Fori(1, K // 2) as r:
                for i in range(2):
                    load(r, i)
            for k in range(K // 2 * 2, K):
                load(k // 2, k % 2)
            for i in range(2):
                sp.wait_ge(y_out[i], 32 * ((K + 1 - i) // 2))
            for b in range(B):
                for c in range(2):
                    at = (c * B + b) * S
                    sp.dma_start(y_in[:, c, b * TT:(b + 1) * TT, :], dram["y_rows"][at:at + S, :].rearrange("(j p) d -> p j d", p=P)
                                 ).then_inc(y_back[b], 16)

        @block.gpsimd
        def _(pool):
            nc.gpsimd.memset(ones[:], 1.0)
            nc.gpsimd.memset(blank[:, :, 0:D], 0.0).then_inc(blank_ready, 1)
            pool.wait_ge(const_in, 80)
            nc.gpsimd.tensor_copy(blank[:, :, D], spare_no[:]).then_inc(blank_ready, 1)
            router.pool(pool)
            pool.wait_ge(cleared, 16)
            for t in range(T):
                pool.wait_ge(scaled_ready, t + 1)
                for c in range(2):
                    nc.gpsimd.indirect_dma_start(dram["xs_rows"], bass.IndirectOffsetOnAxis(ap=slot_no[:, t, c:c + 1], axis=0),
                                                 scaled[:, t, c, :], None).then_inc(scattered, 16)

            def scatter(r, i):
                k = r * 2 + i
                pool.wait_ge(y_ready, k + 1 + 2)
                nc.gpsimd.tensor_copy(row_no[:, i, :], numbers_of[:, bass.ds(k, 1), :].rearrange("p o j -> p (o j)")
                                      ).then_inc(row_no_ready, 1)
                pool.wait_ge(row_no_ready, k + 1)
                pool.nop(nofuse=True)
                for c in range(2):
                    nc.gpsimd.indirect_dma_start(dram["y_rows"], bass.IndirectOffsetOnAxis(ap=row_no[:, i, c:c + 1], axis=0),
                                                 y[:, i, c, :], None).then_inc(y_out[i], 16)

            with pool.Fori(0, K // 2) as r:
                for i in range(2):
                    scatter(r, i)
            for k in range(K // 2 * 2, K):
                scatter(k // 2, k % 2)

        @block.tensor
        def _(pe):
            ps = core.ps
            pe.sem_inc(down_full, 2)
            router.tensor(pe)
            pe.wait_ge(const_in, 80)
            pe.wait_ge(placed, 1)
            every = lambda a: a.rearrange("p t e -> p (t e)")
            nc.tensor.matmul(ps[:, 3, 0:T * E], earlier[:], every(router.chosen[:]), start=True, stop=False)
            nc.tensor.matmul(ps[:, 3, 0:T * E], ones[:], every(sums[:, 1]), start=False, stop=True)
            nc.tensor.matmul(ps[:, 4, 0:E], ones[:], sums[:, 0, T - 1, :], start=True, stop=True).then_inc(ranks_full, 1)

            def turn(r, i):
                pe.wait_ge(xs_in[i], (r + 1) * 16)
                for c in range(DC):
                    for j in range(2):
                        last = nc.tensor.transpose(ps[:, 6 + i, (c * 2 + j) * P:(c * 2 + j + 1) * P],
                                                   xs[:, i, j, c * P:(c + 1) * P], core.ident[:])
                last.then_inc(turned, 1)

            def up(r, i):
                k = r * 2 + i
                pe.wait_ge(w13_in[i], (r + 1) * 32)
                pe.wait_ge(xT_ready, k + 1)
                for f, m in enumerate(rows):
                    pe.wait_ge(hidden_ready, k * FT + f + 1)
                    for g, w in enumerate((w1, w3)):
                        for c in range(DC):
                            last = nc.tensor.matmul(ps[0:m, f % RING, g * N:(g + 1) * N], w[:, i, c, f * P:f * P + m],
                                                    xT[:, i, c, :], start=(c == 0), stop=(c == DC - 1))
                    last.then_inc(both_full, 1)

            def down(r, i):
                k = r * 2 + i
                pe.wait_ge(w2_in[i], (r + 1) * 32)
                pe.wait_ge(hidden_ready, (k + 1) * FT + RING)
                pe.wait_ge(y_ready, k + 1)
                for j in range(2):
                    for f, m in enumerate(rows):
                        last = nc.tensor.matmul(ps[:, 4 + i, j * D:(j + 1) * D], hT[0:m, i, f, j * P:(j + 1) * P],
                                                w2[0:m, i, f, :], start=(f == 0), stop=(f == FT - 1))
                last.then_inc(down_full, 1)

            turn(0, 0)
            up(0, 0)
            turn(0, 1)
            with pe.Fori(0, LOOPED) as r:
                for i in range(2):
                    up(r + i, 1 - i)
                    turn(r + 1, i)
                    down(r, i)
            for k in range(2 * LOOPED, K):
                if k + 1 < K:
                    up((k + 1) // 2, (k + 1) % 2)
                if k + 2 < K:
                    turn((k + 2) // 2, k % 2)
                down(k // 2, k % 2)

        @block.scalar
        def _(act):
            ps = core.ps
            act.sem_inc(y_ready, 2)
            router.scalar(act)

            def gate(r, i):
                k = r * 2 + i
                for f, m in enumerate(rows):
                    act.wait_ge(both_full, k * FT + f + 1)
                    act.wait_ge(hidden_ready, k * FT + f + 1)
                    nc.scalar.activation(silu[0:m, f % RING, :], ps[0:m, f % RING, 0:N], ACT.Silu).then_inc(silu_ready, 1)

            def out(r, i, wait=True):
                act.wait_ge(down_full, r * 2 + i + 1 + 2)
                if wait:
                    act.wait_ge(y_out[i], r * 32)
                nc.scalar.activation(y[:, i, :, :], ps[:, 4 + i, :], ACT.Copy).then_inc(y_ready, 1)

            gate(0, 0)
            for i in range(2):
                gate(i, 1 - i)
                out(0, i, wait=False)
            with act.Fori(1, (K - 1) // 2) as r:
                for i in range(2):
                    gate(r + i, 1 - i)
                    out(r, i)
            for k in range((K - 1) // 2 * 2, K):
                if k + 1 < K:
                    gate((k + 1) // 2, (k + 1) % 2)
                out(k // 2, k % 2)

        @block.vector
        def _(dve):
            ps, V = core.ps, nc.vector
            dve.sem_inc(hidden_ready, RING)
            link = router.vector(dve)
            chosen, probs = router.chosen[:], router.probs[:, :, 0:8]
            per_choice = [P, T, E]
            link(V.tensor_copy(sums[:, 0], chosen))
            n, at = 1, 0
            while n < T:
                V.tensor_copy(sums[:, 1 - at, 0:n, :], sums[:, at, 0:n, :])
                link(V.tensor_tensor(sums[:, 1 - at, n:T, :], sums[:, at, n:T, :], sums[:, at, 0:T - n, :], ALU.add))
                n, at = 2 * n, 1 - at
            assert at == 0
            V.tensor_tensor(sums[:, 1], sums[:, 0], chosen, ALU.subtract).then_inc(placed, 1)
            link(V.tensor_tensor(score[:], chosen, probs, ALU.mult))
            dve.wait_ge(const_in, 80)
            dve.wait_ge(ranks_full, 1)
            link(V.tensor_copy(counts[:], ps[:, 4, 0:E]))
            link(V.tensor_tensor(filled[:], counts[:].unsqueeze(2).to_broadcast([P, E, E]),
                                 starts[:].unsqueeze(1).to_broadcast([P, E, E]), ALU.is_gt))
            link(V.tensor_reduce(blocks[:], filled[:], AX, ALU.add))
            link(V.tensor_copy(ends[:, 0, :], blocks[:]))
            n, at = 1, 0
            while n < E:
                V.tensor_copy(ends[:, 1 - at, 0:n], ends[:, at, 0:n])
                link(V.tensor_tensor(ends[:, 1 - at, n:E], ends[:, at, n:E], ends[:, at, 0:E - n], ALU.add))
                n, at = 2 * n, 1 - at
            link(V.tensor_tensor(ended[:], block_no[:].unsqueeze(2).to_broadcast([P, K, E]),
                                 ends[:, at, :].unsqueeze(1).to_broadcast([P, K, E]), ALU.is_ge))
            link(V.tensor_reduce(expert[:], ended[:], AX, ALU.add))
            V.tensor_scalar(expert_no[:], expert[:], float(E - 1), None, ALU.min).then_inc(experts_known, 1)
            link(V.tensor_tensor(counts[:], ends[:, at, :], blocks[:], ALU.subtract))
            link(V.tensor_scalar(counts[:], counts[:], float(N), 1.0, ALU.mult, ALU.add))
            link(V.tensor_tensor(slot[:], ps[:, 3, 0:T * E].rearrange("p (t e) -> p t e", e=E),
                                 counts[:].unsqueeze(1).to_broadcast(per_choice), ALU.add))
            link(V.tensor_tensor(slot[:], slot[:], chosen, ALU.mult))
            V.tensor_reduce(slots[:, :, 1], slot[:], AX, ALU.max)
            link(V.tensor_reduce(slot_sum[:], slot[:], AX, ALU.add))
            link(V.tensor_tensor(slots[:, :, 0], slot_sum[:], slots[:, :, 1], ALU.subtract))
            V.tensor_scalar(slot_no[:], slots[:], -1.0, None, ALU.add)
            link(V.tensor_tensor(is_second[:], slot[:], slots[:, :, 1:2].to_broadcast(per_choice), ALU.is_equal))
            link(V.tensor_tensor(is_second[:], is_second[:], score[:], ALU.mult))
            V.tensor_reduce(choice_score[:, :, 1], is_second[:], AX, ALU.add)
            link(V.tensor_tensor(score[:], score[:], is_second[:], ALU.subtract))
            V.tensor_copy(scaled[:, :, :, D], numbers[:])
            link(V.tensor_reduce(choice_score[:, :, 0], score[:], AX, ALU.add))
            for t in range(T):
                for c in range(2):
                    last = V.tensor_scalar(scaled[:, t, c, 0:D], router.kept_rows[:, t, :], choice_score[:, t, c:c + 1], None, ALU.mult)
                last.then_inc(scaled_ready, 1)

            def take(r, i):
                k = r * 2 + i
                dve.wait_ge(turned, k + 1)
                V.tensor_copy(numbers_of[:, bass.ds(k, 1), :], xs[:, i, :, D:W].rearrange("p j o -> p o j"))
                V.tensor_copy(xT[:, i, :, :], ps[:, 6 + i, :].rearrange("p (c n) -> p c n", c=DC)).then_inc(xT_ready, 1)

            def product(r, i):
                k = r * 2 + i
                dve.wait_ge(down_full, k + 1)
                for f, m in enumerate(rows):
                    dve.wait_ge(silu_ready, k * FT + f + 1)
                    V.tensor_tensor(hT[0:m, i, f, :], silu[0:m, f % RING, :], ps[0:m, f % RING, N:2 * N], ALU.mult
                                    ).then_inc(hidden_ready, 1)

            take(0, 0)
            product(0, 0)
            take(0, 1)
            with dve.Fori(0, LOOPED) as r:
                for i in range(2):
                    product(r + i, 1 - i)
                    take(r + 1, i)
            for k in range(2 * LOOPED, K - 1):
                product((k + 1) // 2, (k + 1) % 2)
                if k + 2 < K:
                    take((k + 2) // 2, k % 2)
            for b in range(B):
                dve.wait_ge(y_back[b], 32)
                for c in range(2):
                    V.tensor_tensor(core.x[:, b * TT:(b + 1) * TT, :], core.x[:, b * TT:(b + 1) * TT, :], y_in[:, c, b * TT:(b + 1) * TT, :],
                                    ALU.add).then_inc(added, 1)
                    dve.wait_ge(added, 2 * b + c + 1)
def parallel_attention_stage(core):
    nc, dram = core.nc, core.dram
    H, HD = 16, 64
    HP = H // 2
    FT = 8
    UNITS = H * TT
    LAG_T, LAG_O = 3, 4
    RING = 2 * DC + 2 + HP + HP + HP + TT
    with Stage(core, "l3x") as st:
        norm1, norm2, normc = Norm(st), Norm(st, "_again"), Norm(st, "_ctx")
        wq, w1 = st.sb("wq", [P, DC, H * HD]), st.sb("w1", [P, DC, 2 * FT * P])
        wk, wv = st.sb("wk", [P, DC, P]), st.sb("wv", [P, DC, HD])
        wout, w2 = st.sb("wout", [P, HP, D]), st.sb("w2", [P, FT, D])
        gains = st.sb("gains", [P, 4, DC])
        xn = st.sb("xn", [P, TT, D])
        xn2 = st.sb("xn2", [P, TT, D])
        xnT, cnT = st.sb("xnT", [P, DC, S]), st.sb("cnT", [P, DC, S])
        ctx, mask = st.sb("ctx", [P, TT, D]), st.sb("mask", [P, TT, S])
        k_hi, k_lo = st.sb("k_hi", [P, S], F16), st.sb("k_lo", [P, S], F16)
        v = st.sb("v", [P, TT, HD])
        q2 = st.sb("q2", [P, H, S], F16)
        oT = st.sb("oT", [P, HP, S])
        silu = st.sb("silu", [P, 3, S])
        hT = st.sb("hT", [P, FT, S])
        biased = st.sb("biased", [P, 4, S])
        prob, probT = st.sb("prob", [P, 4, S]), st.sb("probT", [P, 4, S])
        neg_max, total, inv = (st.sb(n, [P, H, TT]) for n in ("neg_max", "total", "inv"))
        o = st.sb("o", [P, TT, H, HD])
        weights_in, small_in, ctx_in, mask_in = (st.sem(n) for n in ("weights_in", "small_in", "ctx_in", "mask_in"))
        batch_done = st.sem("batch_done")
        xn_ready, xn2_ready, cn_ready = st.sem("xn_ready"), st.sem("xn2_ready"), st.sem("cn_ready")
        ring_full, ring_free, hi_ready = st.sem("ring_full"), st.sem("ring_free"), st.sem("hi_ready")
        both_full, silu_ready, hidden_ready = st.sem("both_full"), st.sem("silu_ready"), st.sem("hidden_ready")
        scores_full, biased_ready, exp_done = st.sem("scores_full"), st.sem("biased_ready"), st.sem("exp_done")
        turned, out_done, inv_ready = st.sem("turned"), st.sem("out_done"), st.sem("inv_ready")
        copied = [st.sem("probT_by_act"), st.sem("probT_by_vector")]
        block = st.block()

        @block.sync
        def _(sp):
            for dst, name in ((wq, "l3x_wq"), (wk, "l3x_wk"), (wv, "l3x_wv"), (w1, "l3x_w1"), (wout, "l3x_wout"), (w2, "l3x_w2")):
                sp.dma_start(dst[:], dram[name].rearrange("(c p) n -> p c n", p=P)).then_inc(weights_in, 16)
            sp.dma_start(gains[:], dram["l3x_gains"]).then_inc(small_in, 16)
            with sp.Fori(0, B) as b:
                sp.wait_ge(batch_done, b + 1)
                sp.dma_start(ctx[:], dram["ctx"][b].rearrange("(j p) d -> p j d", p=P)).then_inc(ctx_in, 16)
                sp.dma_start(mask[:], dram["mask"][b].rearrange("(j p) s -> p j s", p=P)).then_inc(mask_in, 16)

        @block.gpsimd
        def _(pool):
            with pool.Fori(0, B) as b:
                norm1.pool(pool, b)
                norm2.pool(pool, b)
                normc.pool(pool, b)

        @block.tensor
        def _(pe):
            ps = core.ps
            pe.sem_inc(batch_done, 1)
            pe.sem_inc(turned, 4)
            pe.sem_inc(out_done, 4)
            pe.wait_ge(weights_in, 16 * 6)
            with pe.Fori(0, B) as b:
                ring = [0]

                def claim():
                    n = ring[0]
                    ring[0] += 1
                    pe.wait_ge(ring_free, b * RING + n + 1)
                    return 6 + n % 2

                def emptied():
                    pe.wait_ge(ring_free, b * RING + ring[0] + 2)

                for src, ready in ((xn2, xn2_ready), (ctx, cn_ready)):
                    pe.wait_ge(ready, b + 1)
                    for c in range(DC):
                        transpose_tokens(nc, core, src, claim(), c, ring_full)
                emptied()
                bank = claim()
                for c in range(DC):
                    last = nc.tensor.matmul(ps[:, bank, :], wk[:, c, :], cnT[:, c, :], start=(c == 0), stop=(c == DC - 1))
                last.then_inc(ring_full, 1)
                bank = claim()
                for j in range(TT):
                    for c in range(DC):
                        last = nc.tensor.matmul(ps[:, bank, j * HD:(j + 1) * HD], cnT[:, c, j * P:(j + 1) * P], wv[:, c, :],
                                                start=(c == 0), stop=(c == DC - 1))
                last.then_inc(ring_full, 1)
                for g in range(HP):
                    bank = claim()
                    for c in range(DC):
                        last = nc.tensor.matmul(ps[:, bank, :], wq[:, c, g * P:(g + 1) * P], xnT[:, c, :],
                                                start=(c == 0), stop=(c == DC - 1))
                    last.then_inc(ring_full, 1)
                for f in range(FT):
                    pe.wait_ge(hidden_ready, b * FT + max(f + 1, 3))
                    for i in range(2):
                        for c in range(DC):
                            last = nc.tensor.matmul(ps[:, 2 * (f % 3) + i, :], w1[:, c, (i * FT + f) * P:(i * FT + f + 1) * P],
                                                    xnT[:, c, :], start=(c == 0), stop=(c == DC - 1))
                    last.then_inc(both_full, 1)
                emptied()
                pe.wait_ge(hidden_ready, (b + 1) * FT + 3)

                for u in range(UNITS + LAG_O):
                    if u < UNITS:
                        h, j = divmod(u, TT)
                        pe.wait_ge(biased_ready, b * UNITS + u + 1)
                        for part, k in enumerate((k_hi, k_lo)):
                            last = nc.tensor.matmul(ps[:, u % 2, :], q2[:, h, j * P:(j + 1) * P], k[:],
                                                    start=(part == 0), stop=(part == 1))
                        last.then_inc(scores_full, 1)
                    t = u - LAG_T
                    if 0 <= t < UNITS:
                        pe.wait_ge(exp_done, b * UNITS + t + 1 + 4)
                        pe.wait_ge(copied[t % 2], b * (UNITS // 2) + t // 2 + 1)
                        for s in range(TT):
                            last = nc.tensor.transpose(ps[:, 2 + t % 4, s * P:(s + 1) * P], prob[:, t % 4, s * P:(s + 1) * P],
                                                       core.ident[:])
                        last.then_inc(turned, 1)
                    n = u - LAG_O
                    if n >= 0:
                        h, j = divmod(n, TT)
                        if n % (2 * TT) == 0:
                            bank = claim()
                        pe.wait_ge(copied[n % 2], b * (UNITS // 2) + n // 2 + 1 + 2)
                        at = ((h % 2) * TT + j) * HD
                        for s in range(TT):
                            last = nc.tensor.matmul(ps[:, bank, at:at + HD], probT[:, n % 4, s * P:(s + 1) * P], v[:, s, :],
                                                    start=(s == 0), stop=(s == TT - 1))
                        last.then_inc(out_done, 1)
                emptied()
                for g in range(HP):
                    bank = claim()
                    for j in range(TT):
                        last = nc.tensor.transpose(ps[:, bank, j * P:(j + 1) * P], o[:, j, 2 * g:2 * g + 2, :], core.ident[:])
                    last.then_inc(ring_full, 1)
                emptied()
                for j in range(TT):
                    bank = claim()
                    for g in range(HP):
                        nc.tensor.matmul(ps[:, bank, 0:D], oT[:, g, j * P:(j + 1) * P], wout[:, g, :], start=(g == 0), stop=False)
                    for f in range(FT):
                        last = nc.tensor.matmul(ps[:, bank, 0:D], hT[:, f, j * P:(j + 1) * P], w2[:, f, :],
                                                start=False, stop=(f == FT - 1))
                    last.then_inc(ring_full, 1)
                emptied()
                pe.sem_inc(batch_done, 1)
                assert ring[0] == RING

        @block.scalar
        def _(act):
            ps = core.ps
            act.sem_inc(exp_done, 4)
            act.sem_inc(copied[0], 2)
            with act.Fori(0, B) as b:
                act.wait_ge(ring_full, b * (RING - HP) + 2 * DC + 1)
                nc.scalar.activation(k_hi[:], ps[:, 6 + 2 * DC % 2, :], ACT.Copy).then_inc(hi_ready, 1)
                for g in range(HP):
                    n = 2 * DC + 2 + g
                    act.wait_ge(ring_full, b * (RING - HP) + n + 1)
                    for i in range(2):
                        last = nc.scalar.activation(q2[0:HD, 2 * g + i, :], ps[i * HD:(i + 1) * HD, 6 + n % 2, :], ACT.Copy,
                                                    scale=HD ** -0.5)
                    last.then_inc(hi_ready, 1)
                for f in range(FT):
                    act.wait_ge(both_full, b * FT + f + 1)
                    act.wait_ge(hidden_ready, b * FT + max(f + 1, 3))
                    nc.scalar.activation(silu[:, f % 3, :], ps[:, 2 * (f % 3) + 1, :], ACT.Silu).then_inc(silu_ready, 1)
                for u in range(UNITS + LAG_T):
                    if u < UNITS:
                        act.wait_ge(biased_ready, b * UNITS + u + 1 + 2)
                        act.wait_ge(turned, b * UNITS + u + 1)
                        nc.scalar.activation(prob[:, u % 4, :], biased[:, u % 4, :], ACT.Exp, scale=-1.0,
                                             bias=neg_max[:, u // TT, u % TT:u % TT + 1],
                                             accum_out=total[:, u // TT, u % TT:u % TT + 1]).then_inc(exp_done, 1)
                    t = u - LAG_T
                    if t >= 0 and t % 2 == 0:
                        act.wait_ge(turned, b * UNITS + t + 1 + 4)
                        act.wait_ge(out_done, b * UNITS + t + 1)
                        nc.scalar.activation(probT[:, t % 4, :], ps[:, 2 + t % 4, :], ACT.Copy).then_inc(copied[0], 1)

        @block.vector
        def _(dve):
            ps, V = core.ps, nc.vector
            dve.sem_inc(ring_free, 2)
            dve.sem_inc(hidden_ready, 3)
            dve.sem_inc(biased_ready, 2)
            dve.sem_inc(copied[1], 2)
            dve.wait_ge(small_in, 16)
            with dve.Fori(0, B) as b:
                ring, full = [0], [0]

                def take():
                    ring[0] += 1
                    full[0] += 1
                    dve.wait_ge(ring_full, b * (RING - HP) + full[0])
                    return 6 + (ring[0] - 1) % 2

                norm1.vector(dve, b, lambda j: core.x[:, b * TT + j, :], lambda j: xn[:, j, :], xn_ready)
                dve.wait_ge(xn_ready, b + 1)
                norm2.vector(dve, b, lambda j: xn[:, j, :], lambda j: xn2[:, j, :], xn2_ready)
                dve.wait_ge(ctx_in, b * 16 + 16)
                normc.vector(dve, b, lambda j: ctx[:, j, :], lambda j: ctx[:, j, :], cn_ready)
                for k, dst in enumerate((xnT, cnT)):
                    for c in range(DC):
                        V.tensor_scalar(dst[:, c, :], ps[:, take(), :], gains[:, 2 * k, c:c + 1], gains[:, 2 * k + 1, c:c + 1],
                                        ALU.mult, ALU.add).then_inc(ring_free, 1)
                bank = take()
                dve.wait_ge(hi_ready, b * (HP + 1) + 1)
                V.tensor_tensor(k_lo[:], ps[:, bank, :], k_hi[:], ALU.subtract).then_inc(ring_free, 1)
                V.tensor_copy(v[:], ps[:, take(), 0:TT * HD].rearrange("p (j d) -> p j d", j=TT)).then_inc(ring_free, 1)
                for g in range(HP):
                    bank = take()
                    dve.wait_ge(hi_ready, b * (HP + 1) + g + 2)
                    for i in range(2):
                        last = V.scalar_tensor_tensor(out=q2[HD:P, 2 * g + i, :], in0=ps[i * HD:(i + 1) * HD, bank, :],
                                                      scalar=HD ** -0.5, in1=q2[0:HD, 2 * g + i, :],
                                                      op0=ALU.mult, op1=ALU.subtract)
                    last.then_inc(ring_free, 1)
                for f in range(FT):
                    dve.wait_ge(silu_ready, b * FT + f + 1)
                    V.tensor_tensor(hT[:, f, :], silu[:, f % 3, :], ps[:, 2 * (f % 3), :], ALU.mult).then_inc(hidden_ready, 1)
                dve.wait_ge(mask_in, b * 16 + 16)

                def rows(g):
                    ring[0] += 1
                    bank = 6 + (ring[0] - 1) % 2
                    dve.wait_ge(out_done, b * UNITS + 2 * TT * (g + 1) + 4)
                    V.reciprocal(inv[:, 2 * g:2 * g + 2, :], total[:, 2 * g:2 * g + 2, :]).then_inc(inv_ready, 1)
                    dve.wait_ge(inv_ready, b * HP + g + 1)
                    for i in range(2):
                        last = V.tensor_tensor(o[:, :, 2 * g + i, :],
                                               ps[:, bank, i * TT * HD:(i + 1) * TT * HD].rearrange("p (j d) -> p j d", d=HD),
                                               inv[:, 2 * g + i, :].unsqueeze(2).to_broadcast([P, TT, HD]), ALU.mult)
                    last.then_inc(ring_free, 1)

                for u in range(UNITS + LAG_T):
                    if u < UNITS:
                        h, j = divmod(u, TT)
                        dve.wait_ge(scores_full, b * UNITS + u + 1)
                        dve.wait_ge(exp_done, b * UNITS + u + 1)
                        dve.nop(nofuse=True)
                        V.tensor_tensor_reduce(out=biased[:, u % 4, :], in0=ps[:, u % 2, :], in1=mask[:, j, :], scale=-1.0,
                                               scalar=3.0e38, op0=ALU.add, op1=ALU.min,
                                               accum_out=neg_max[:, h, j:j + 1]).then_inc(biased_ready, 1)
                    t = u - LAG_T
                    if t >= 0 and t % 2 == 1:
                        dve.wait_ge(turned, b * UNITS + t + 1 + 4)
                        dve.wait_ge(out_done, b * UNITS + t + 1)
                        V.tensor_copy(probT[:, t % 4, :], ps[:, 2 + t % 4, :]).then_inc(copied[1], 1)
                    n = u - LAG_T - 3
                    if n >= 0 and n % (2 * TT) == 2 * TT - 1:
                        rows(n // (2 * TT))
                rows(HP - 1)
                for g in range(HP):
                    V.tensor_copy(oT[:, g, :], ps[:, take(), :]).then_inc(ring_free, 1)
                for j in range(TT):
                    V.tensor_tensor(core.x[:, b * TT + j, :], core.x[:, b * TT + j, :], ps[:, take(), 0:D], ALU.add
                                    ).then_inc(ring_free, 1)


def build(nc, dram, out):
    with ExitStack() as ctx:
        core = Core(nc, ctx, dram)
        load_stage(core)
        sigmoid_attention_stage(core)
        mixture_of_depths_stage(core)
        causal_attention_stage(core)
        quantised_ffn_stage(core)
        autocorrelation_stage(core)
        relu_experts_stage(core)
        parallel_attention_stage(core)
        gated_experts_stage(core)
        store_stage(core, out)


def lay_out(inputs):
    import numpy as np
    a = {k: np.asarray(v) for k, v in inputs.items()}

    def strips(w):
        return np.repeat(w.reshape(D, 16, 1, 16), 2, 2).reshape(D, 512)

    arrays = {
        "x": a["x"],
        "ctx": a["ctx_1024"],
        "ctxT": a["ctx_1024"].transpose(0, 2, 1),
        "ctxT_back": a["ctx_1024"].transpose(0, 2, 1).reshape(B, D, TT, P)[:, :, :, ::-1].reshape(B, D, S),
        "lo_rows": np.where(np.arange(P) % 32 < 16, 0.0, -1.0).astype(np.float32)[:, None],
        "l0x_wq": strips(a["L0_xattn_Wq"].T),
        "l0x_wk": strips(a["L0_xattn_Wk"].T),
        "l0x_wv": strips(a["L0_xattn_Wv"].T),
        "l0x_wo": strips(a["L0_xattn_Wo"]).T,
    }
    arrays |= {
        "pos": a["L0_ffn_position_ids"][:, 0:S].reshape(B, TT, P).transpose(2, 0, 1).reshape(P, B * TT),
        "attention_mask": a["L0_ffn_attention_mask"][:, 0, 0:S, 0:S],
        "slot_base": np.array([[0], [64], [0], [64]], np.float32),
        "rope_freq": (np.float32(1) / np.float32(10000) ** (np.arange(0, 16, 2, dtype=np.float32) / np.float32(16)))[None],
        "l0f_rw": a["L0_ffn_router_w"].T,
        "l0f_rb": a["L0_ffn_router_b"][None],
        "l0f_ln1": a["L0_ffn_ln1"].reshape(DC, P).T,
        "l0f_ln2": a["L0_ffn_ln2"].reshape(DC, P).T,
        **{f"l0f_{n}": a[f"L0_ffn_{n}"] for n in ("wq", "wk", "wv", "wo", "w1", "w2")},
    }
    arrays |= {
        "l1f_gate": a["L1_ffn_w_gate"],
        "l1f_up": a["L1_ffn_w_up"],
        "l1f_down": a["L1_ffn_w_down"],
        "l1f_clip_x": a["L1_ffn_clip_x"][None],
        "l1f_clip_down": a["L1_ffn_clip_down"][None],
    }
    t, f = np.arange(S), np.arange(S // 2)
    angle = 2 * np.pi / S * ((t[:, None] * f[None, :]) % S)
    basis = np.concatenate([np.cos(angle), np.sin(angle)], 1)
    basis[:, S // 2] = np.where(t % 2, -1.0, 1.0)
    share = np.full(S, 2.0 / (S * D))
    share[0] = share[S // 2] = 1.0 / (S * D)
    inverse = (basis * share)[(-t) % S].T
    arrays |= {
        **{f"l2x_{n}": a[f"L2_xattn_{n}"] for n in ("Wq", "Wk", "Wv", "Wo")},
        **{f"l2x_{n}": a[f"L2_xattn_{n}"][None] for n in ("bq", "bk", "bv", "bo")},
        "dft_basis": basis.astype(np.float32),
        "dft_inverse": inverse.astype(np.float32),
        "l2f_router": a["L2_ffn_w_router"].T,
        "l2f_w1": np.concatenate([a["L2_ffn_w1_stack"], a["L2_ffn_ws1"].reshape(2, D, D)]).transpose(0, 2, 1),
        "l2f_w2": np.concatenate([a["L2_ffn_w2_stack"].transpose(0, 2, 1), a["L2_ffn_ws2"].T.reshape(2, D, D)]),
        "l3f_router": a["L3_ffn_gate_w"].T,
        **{f"l3f_{n}": a[f"L3_ffn_{n}"] for n in ("w1", "w2", "w3")},
    }
    token = np.arange(B * S).reshape(B * TT, P).T
    blocks = (2 * B * S + 8 * 255) // 256
    arrays |= {
        "earlier": np.triu(np.ones((P, P), np.float32), 1),
        "choice_numbers": np.stack([token, B * S + token], 2).astype(np.float32),
        "spare_numbers": (2 * B * S + np.arange(2 * blocks * P)).reshape(2 * blocks, P).T.astype(np.float32),
        "block_starts": np.arange(0, 8 * 256, 256, dtype=np.float32)[None],
        "block_numbers": np.arange(blocks, dtype=np.float32)[None],
    }
    kv = a["L3_xattn_Wkv"]
    arrays |= {
        "mask": a["mask_BxSxS2_ff0"],
        "l3x_wq": a["L3_xattn_Wq"],
        "l3x_wk": np.concatenate([kv[:, 0:64], kv[:, 0:64]], 1),
        "l3x_wv": kv[:, 64:128],
        "l3x_w1": a["L3_xattn_W1"],
        "l3x_wout": a["L3_xattn_Wout"],
        "l3x_w2": a["L3_xattn_W2"],
        "l3x_gains": np.stack([a[f"L3_xattn_{n}"].reshape(DC, P) for n in ("ln_g", "ln_b", "cln_g", "cln_b")]
                              ).transpose(2, 0, 1),
    }
    return {k: np.ascontiguousarray(v) for k, v in arrays.items()}


def kernel(**inputs):
    import concourse.bacc as bacc
    from concourse.bass_utils import run_bass_kernel_spmd

    nc = bacc.Bacc("TRN2", target_bir_lowering=False, num_devices=1)
    arrays = lay_out(inputs)
    dram = {k: nc.dram_tensor(f"in_{k}", v.shape, mybir.dt.from_np(v.dtype), kind="ExternalInput").ap()
            for k, v in arrays.items()}
    out = nc.dram_tensor("out_x", (B, S, D), F32, kind="ExternalOutput").ap()
    dram["delay_rows"] = nc.dram_tensor("delay_rows", (B, 2 * S), F32).ap()
    slots = arrays["spare_numbers"].size
    dram["xs_rows"] = nc.dram_tensor("xs_rows", (slots, D + 1), F32).ap()
    dram["y_rows"] = nc.dram_tensor("y_rows", (2 * B * S + slots, D), F32).ap()
    build(nc, dram, out)
    result = run_bass_kernel_spmd(nc, [{f"in_{k}": v for k, v in arrays.items()}], core_ids=[0])
    return result.results[0]["out_x"]
```

```python
from contextlib import ExitStack

import concourse.bass as bass
from concourse import mybir

ALU = mybir.AluOpType
ACT = mybir.ActivationFunctionType
AX = mybir.AxisListType.X
F32 = mybir.dt.float32
F16 = mybir.dt.float16
BF16 = mybir.dt.bfloat16
I32 = mybir.dt.int32
P = 128
B = 4
S = 512
D = 256
TT = S // P
DC = D // P
NEG = -3.0e38
ROUND = 12582912.0


class Stage:

    def __init__(self, core, name):
        self.core, self.nc, self.name, self.ctx = core, core.nc, name, ExitStack()
        self.sems = []

    def __enter__(self):
        return self

    def __exit__(self, *exc):
        done = self.ctx.__exit__(*exc)
        self.nc.clear_and_free_semaphores(self.sems)
        self.nc.all_engine_barrier()
        return done

    def sb(self, name, shape, dt=F32):
        return self.ctx.enter_context(self.nc.sbuf_tensor(f"{self.name}_{name}", shape, dt))

    def sem(self, name):
        self.sems.append(self.nc.alloc_semaphore(f"{self.name}_{name}"))
        return self.sems[-1]

    def block(self):
        return self.ctx.enter_context(self.nc.Block())


class Chain:

    def __init__(self, eng, sem, base=0):
        self.eng, self.sem, self.base, self.n = eng, sem, base, 0

    def __call__(self, ins):
        self.n += 1
        ins.then_inc(self.sem, 1)
        self.eng.wait_ge(self.sem, self.base + self.n)


class Steps:

    def __init__(self, sem, names):
        assert len(set(names)) == len(names)
        self.sem, self.names, self.next = sem, names, 0

    def done(self, ins, name):
        assert self.names[self.next % len(self.names)] == name, (name, self.next)
        self.next += 1
        ins.then_inc(self.sem, 1)

    def wait(self, eng, name, it=0):
        eng.wait_ge(self.sem, it * len(self.names) + self.names.index(name) + 1)


class Norm:

    LINKS = 4

    def __init__(self, st, tag="", eps=1e-5):
        self.st, self.nc, self.core, self.eps = st, st.nc, st.core, eps
        self.bn = st.sb(f"bn{tag}", [P, TT, 6])
        self.mv = st.sb(f"mv{tag}", [P, TT, 2])
        self.var = st.sb(f"var{tag}", [P, TT])
        self.rstd = st.sb(f"rstd{tag}", [P, TT])
        self.stats = st.sem(f"norm{tag}_stats")
        self.rstd_ready = st.sem(f"norm{tag}_rstd")

    def vector(self, dve, it, src, dst, done):
        for part in self.parts(dve, it, src, dst, done):
            part()

    def parts(self, dve, it, src, dst, done):
        link = Chain(dve, self.stats, it * self.LINKS)
        return [lambda: self.statistics(dve, link, src), lambda: self.apply(dve, it, link, src, dst, done)]

    def statistics(self, dve, link, src):
        nc = self.nc
        for j in range(TT):
            last = nc.vector.bn_stats(self.bn[:, j, :], src(j))
        link(last)
        dve.nop(nofuse=True)
        for j in range(TT):
            last = nc.vector.bn_aggr(self.mv[:, j, :], self.bn[:, j, :])
        link(last)
        link(nc.vector.tensor_scalar(self.var[:], self.mv[:, :, 1], self.eps, None, ALU.add))

    def apply(self, dve, it, link, src, dst, done):
        nc = self.nc
        dve.wait_ge(self.rstd_ready, it + 1)
        for j in range(TT):
            last = nc.vector.tensor_scalar(dst(j), src(j), self.mv[:, j, 0:1], self.rstd[:, j:j + 1],
                                           ALU.subtract, ALU.mult)
        last.then_inc(done, 1)
        link(self.nc.vector.tensor_copy(self.bn[:, 0, 0:1], self.mv[:, 0, 0:1]))

    def pool(self, pool, it):
        pool.wait_ge(self.stats, it * self.LINKS + 3)
        self.nc.gpsimd.tensor_tensor(self.rstd[:], self.var[:], self.core.neg_half[:, 0:TT],
                                     ALU.pow).then_inc(self.rstd_ready, 1)


class Core:

    def __init__(self, nc, ctx, dram):
        self.nc, self.dram = nc, dram
        self.x = ctx.enter_context(nc.sbuf_tensor("x_sb", [P, B * TT, D], F32))
        self.ident = ctx.enter_context(nc.sbuf_tensor("ident", [P, P], F32))
        self.neg_half = ctx.enter_context(nc.sbuf_tensor("neg_half", [P, 8], F32))
        self.ps = ctx.enter_context(nc.psum_tensor("ps", [P, 8, S], F32))


def load_stage(core):
    nc = core.nc
    with Stage(core, "load") as st:
        loaded, zeroed, made = st.sem("x_loaded"), st.sem("ident_zeroed"), st.sem("ident_made")
        block = st.block()

        @block.sync
        def _(sp):
            sp.dma_start(core.x[:], core.dram["x"].rearrange("b (j p) d -> p (b j) d", p=P)).then_inc(loaded, 16)
            sp.wait_ge(loaded, 16)

        @block.gpsimd
        def _(pool):
            nc.gpsimd.memset(core.neg_half[:], -0.5)
            nc.gpsimd.memset(core.ident[:], 0.0).then_inc(zeroed, 1)
            pool.wait_ge(zeroed, 1)
            nc.gpsimd.affine_select(out=core.ident[:], in_=core.ident[:], compare_op=ALU.not_equal, fill=1.0,
                                    base=0, pattern=[[-1, P]], channel_multiplier=1).then_inc(made, 1)


def transpose_tokens(nc, core, src, bank, c, inc):
    for j in range(TT):
        last = nc.tensor.transpose(core.ps[:, bank, j * P:(j + 1) * P], src[:, j, c * P:(c + 1) * P], core.ident[:])
    last.then_inc(inc, 1)


def sigmoid_attention_stage(core):
    nc, dram = core.nc, core.dram
    HG = 4
    UNITS = HG * TT * 2
    SLOTS = 3
    LATE = 2
    RING = DC + 3 * HG + HG + TT
    HALF = 16
    with Stage(core, "l0x") as st:
        norm = Norm(st)
        wq, wk, wv = (st.sb(n, [P, DC, HG * P]) for n in ("wq", "wk", "wv"))
        wo = st.sb("wo", [P, HG, D])
        lo_rows = st.sb("lo_rows", [P, 1])
        xn = st.sb("xn", [P, TT, D])
        xnT = st.sb("xnT", [P, DC, S])
        ctxT = st.sb("ctxT", [P, DC, S])
        k_hi, k_lo, q_hi, q2 = (st.sb(n, [P, HG, S], F16) for n in ("k_hi", "k_lo", "q_hi", "q2"))
        oT = st.sb("oT", [P, HG, S])
        v = st.sb("v", [P, TT, 4 * HG, 2, HALF], F16)
        prob = st.sb("prob", [P, SLOTS, 2, S])
        p_hi, p_lo = (st.sb(n, [P, SLOTS, 2, S], F16) for n in ("p_hi", "p_lo"))
        weights_in, ctx_in, ctx_used = st.sem("weights_in"), st.sem("ctx_in"), st.sem("ctx_used")
        xn_ready, ring_full, ring_free = st.sem("xn_ready"), st.sem("ring_full"), st.sem("ring_free")
        hi_ready = st.sem("hi_ready")
        scores_ready, probs_ready, probs_used = st.sem("scores_ready"), st.sem("probs_ready"), st.sem("probs_used")
        p_hi_ready, p_lo_ready = st.sem("p_hi_ready"), st.sem("p_lo_ready")
        block = st.block()

        def ring_bank(n):
            return 6 + n % 2

        @block.sync
        def _(sp):
            for dst, name in ((wk, "l0x_wk"), (wq, "l0x_wq"), (wv, "l0x_wv")):
                sp.dma_start(dst[:], dram[name].rearrange("(c p) n -> p c n", p=P)).then_inc(weights_in, 16)
            sp.dma_start(wo[:], dram["l0x_wo"].rearrange("(g p) n -> p g n", p=P)).then_inc(weights_in, 16)
            sp.dma_start(lo_rows[:], dram["lo_rows"]).then_inc(weights_in, 16)
            with sp.Fori(0, B) as b:
                sp.wait_ge(ctx_used, b + 1)
                sp.dma_start(ctxT[:], dram["ctxT"][b].rearrange("(c p) s -> p c s", p=P)).then_inc(ctx_in, 16)

        @block.gpsimd
        def _(pool):
            with pool.Fori(0, B) as b:
                norm.pool(pool, b)

        @block.tensor
        def _(pe):
            pe.sem_inc(ctx_used, 1)
            pe.sem_inc(probs_used, SLOTS)
            pe.wait_ge(weights_in, 80)
            with pe.Fori(0, B) as b:
                base = b * RING
                ring = [0]

                def claim():
                    n = ring[0]
                    ring[0] += 1
                    pe.wait_ge(ring_free, base + n + 1)
                    return ring_bank(n)

                def emptied():
                    pe.wait_ge(ring_free, base + ring[0] + 2)

                def project(w, g, rhs):
                    bank = claim()
                    for c in range(DC):
                        last = nc.tensor.matmul(core.ps[:, bank, :], w[:, c, g * P:(g + 1) * P], rhs[:, c, :],
                                                start=(c == 0), stop=(c == DC - 1))
                    last.then_inc(ring_full, 1)

                pe.wait_ge(ctx_in, b * 16 + 16)
                for g in range(HG):
                    project(wk, g, ctxT)
                for j in range(TT):
                    bank = claim()
                    for c in range(DC):
                        last = nc.tensor.matmul(core.ps[:, bank, :], ctxT[:, c, j * P:(j + 1) * P], wv[:, c, :],
                                                start=(c == 0), stop=(c == DC - 1))
                    last.then_inc(ring_full, 1)
                pe.wait_ge(xn_ready, b + 1)
                for c in range(DC):
                    transpose_tokens(nc, core, xn, claim(), c, ring_full)
                emptied()
                pe.sem_inc(ctx_used, 1)
                for g in range(HG):
                    project(wq, g, xnT)
                emptied()

                units = [(g, j, h) for g in range(HG) for j in range(TT) for h in range(2)]

                def score(u):
                    g, j, h = units[u]
                    pe.wait_ge(probs_ready, b * UNITS + max(u + 1, SLOTS))
                    for i in range(2):
                        r = 32 * (2 * h + i)
                        for part, k in enumerate((k_hi, k_lo)):
                            last = nc.tensor.matmul(core.ps[:, 2 * (u % SLOTS) + i, :], k[r:r + 32, g, j * P:(j + 1) * P],
                                                    q2[r:r + 32, g, :], start=(part == 0), stop=(part == 1))
                    last.then_inc(scores_ready, 1)

                for u in range(SLOTS):
                    score(u)
                for u, (g, j, h) in enumerate(units):
                    if u + SLOTS < UNITS:
                        score(u + SLOTS)
                    if (j, h) == (0, 0):
                        bank = claim()
                    pe.wait_ge(p_lo_ready, b * UNITS + u + 1 + SLOTS)
                    for part, probs in enumerate((p_hi, p_lo)):
                        for i in range(2):
                            head = 2 * h + i
                            r = 32 * head
                            last = nc.tensor.matmul(core.ps[r:r + 32, bank, :], v[:, j, 4 * g + head, :, :],
                                                    probs[:, u % SLOTS, i, :], start=(j == 0 and part == 0),
                                                    stop=(j == TT - 1 and part == 1), tile_position=(0, r))
                    last.then_inc(probs_used, 1)
                emptied()
                for j in range(TT):
                    bank = claim()
                    for g in range(HG):
                        last = nc.tensor.matmul(core.ps[:, bank, 0:D], oT[:, g, j * P:(j + 1) * P], wo[:, g, :],
                                                start=(g == 0), stop=(g == HG - 1))
                    last.then_inc(ring_full, 1)
                assert ring[0] == RING

        @block.scalar
        def _(act):
            act.sem_inc(probs_ready, SLOTS)
            with act.Fori(0, B) as b:
                def hi(n, dst, src):
                    act.wait_ge(ring_full, b * (RING - HG) + n + 1)
                    nc.scalar.activation(dst, src(core.ps[:, ring_bank(n), :]), ACT.Copy).then_inc(hi_ready, 1)

                for g in range(HG):
                    hi(g, k_hi[:, g, :], lambda full: full)
                for j in range(TT):
                    hi(HG + j, v[:, j, :, 0, :], lambda full: full.rearrange("p (h a d) -> p h a d", a=2, d=HALF)[:, :, 0, :])
                for g in range(HG):
                    hi(HG + TT + DC + g, q_hi[:, g, :], lambda full: full)
                for u in range(UNITS):
                    act.wait_ge(scores_ready, b * UNITS + u + 1)
                    act.wait_ge(p_lo_ready, b * UNITS + max(u + 1, SLOTS))
                    nc.scalar.activation(prob[:, u % SLOTS, :, :], core.ps[:, 2 * (u % SLOTS):2 * (u % SLOTS) + 2, :],
                                         ACT.Sigmoid, scale=0.25).then_inc(probs_ready, 1)

        @block.vector
        def _(dve):
            V = nc.vector
            dve.sem_inc(ring_free, 2)
            dve.sem_inc(p_lo_ready, SLOTS)
            dve.wait_ge(weights_in, 80)
            with dve.Fori(0, B) as b:
                ring, full, his = [0], [0], [0]

                def take():
                    ring[0] += 1
                    full[0] += 1
                    dve.wait_ge(ring_full, b * (RING - HG) + full[0])
                    return ring_bank(ring[0] - 1)

                def take_split():
                    his[0] += 1
                    bank = take()
                    dve.wait_ge(hi_ready, b * (2 * HG + TT) + his[0])
                    return bank

                norm.vector(dve, b, lambda j: core.x[:, b * TT + j, :], lambda j: xn[:, j, :], xn_ready)
                for g in range(HG):
                    V.tensor_tensor(k_lo[:, g, :], core.ps[:, take_split(), :], k_hi[:, g, :], ALU.subtract
                                    ).then_inc(ring_free, 1)
                for j in range(TT):
                    own = core.ps[:, take_split(), :].rearrange("p (h a d) -> p h a d", a=2, d=HALF)[:, :, 1, :]
                    V.tensor_tensor(v[:, j, :, 1, :], own, v[:, j, :, 0, :], ALU.subtract).then_inc(ring_free, 1)
                for c in range(DC):
                    V.tensor_copy(xnT[:, c, :], core.ps[:, take(), :]).then_inc(ring_free, 1)
                for g in range(HG):
                    V.scalar_tensor_tensor(out=q2[:, g, :], in0=q_hi[:, g, :], scalar=lo_rows[:, 0:1],
                                           in1=core.ps[:, take_split(), :], op0=ALU.mult, op1=ALU.add).then_inc(ring_free, 1)

                def rows(g):
                    ring[0] += 1
                    dve.wait_ge(probs_used, b * UNITS + SLOTS + (g + 1) * UNITS // HG)
                    V.tensor_copy(oT[:, g, :], core.ps[:, ring_bank(ring[0] - 1), :]).then_inc(ring_free, 1)

                for u in range(UNITS + 1):
                    if u < UNITS:
                        dve.wait_ge(probs_ready, b * UNITS + u + 1 + SLOTS)
                        dve.wait_ge(probs_used, b * UNITS + max(u + 1, SLOTS))
                        V.tensor_copy(p_hi[:, u % SLOTS, :, :], prob[:, u % SLOTS, :, :]).then_inc(p_hi_ready, 1)
                    if u >= 1:
                        n = u - 1
                        dve.wait_ge(p_hi_ready, b * UNITS + n + 1)
                        V.tensor_tensor(p_lo[:, n % SLOTS, :, :], prob[:, n % SLOTS, :, :], p_hi[:, n % SLOTS, :, :],
                                        ALU.subtract).then_inc(p_lo_ready, 1)
                        if n % (UNITS // HG) == LATE and n > LATE:
                            rows(n // (UNITS // HG) - 1)
                rows(HG - 1)
                for j in range(TT):
                    V.tensor_tensor(core.x[:, b * TT + j, :], core.x[:, b * TT + j, :],
                                    core.ps[:, take(), 0:D], ALU.add).then_inc(ring_free, 1)


def mixture_of_depths_stage(core):
    nc, dram = core.nc, core.dram
    K = S // 8
    HALF = 64
    T2 = 2
    H, HD = 16, 16
    HG, STRIP = 4, 32
    F = 1024
    FT = F // P
    NA = D + 2
    with Stage(core, "l0f") as st:
        norm = Norm(st)
        xa = st.sb("xa", [P, B * TT, NA])
        rw, rb = st.sb("rw", [P, D]), st.sb("rb", [P, 1])
        junk = st.sb("junk", [P, TT, D])
        pos = st.sb("pos", [P, B * TT], I32)
        wcol = st.sb("wcol", [P, TT, B])
        wrow, work, chosen, above, ones = (st.sb(n, [B, S]) for n in ("wrow", "work", "chosen", "above", "ones"))
        top = st.sb("top", [B, K])
        last8 = st.sb("last8", [B, 8])
        base = st.sb("slot_base", [B, 1])
        slot, keep = st.sb("slot", [P, B, TT]), st.sb("keep", [P, B, TT])
        iota = st.sb("iota", [P, P])
        pick = st.sb("pick", [P, B * TT, P])
        pickT = st.sb("pickT", [P, B * TT, P])
        mask = st.sb("mask", [P, TT, S])
        half_mask = st.sb("half_mask", [P, B * TT, P])
        bar = st.sb("bar", [P, P])
        bias = st.sb("bias", [P, T2, P])
        xs = st.sb("xs", [P, T2, NA])
        ss, rms = st.sb("ss", [P, T2]), st.sb("rms", [P, T2])
        hn = st.sb("hn", [P, T2, D])
        hT = st.sb("hT", [P, DC, T2 * P])
        ln1, ln2 = st.sb("ln1", [P, DC]), st.sb("ln2", [P, DC])
        wq, wk, wv, wo = (st.sb(n, [P, DC, D]) for n in ("wq", "wk", "wv", "wo"))
        w1 = st.sb("w1", [P, DC, F])
        w2 = st.sb("w2", [P, FT, D])
        freq = st.sb("freq", [P, HD // 2])
        ang, turns, sin, cos = (st.sb(n, [P, T2, HD]) for n in ("ang", "turns", "sin", "cos"))
        q, k = (st.sb(n, [P, T2, H, STRIP]) for n in ("q", "k"))
        rot = st.sb("rot", [P, H, HD])
        v = st.sb("v", [P, T2, D])
        qT, kT = (st.sb(n, [P, HG, T2 * P]) for n in ("qT", "kT"))
        prob = st.sb("prob", [P, H, P])
        probT = st.sb("probT", [P, H, P])
        mx, total, inv = (st.sb(n, [P, H]) for n in ("mx", "total", "inv"))
        o = st.sb("o", [P, T2, D])
        oT = st.sb("oT", [P, DC, T2 * P])
        x1 = st.sb("x1", [P, T2, D])
        gT = st.sb("gT", [P, FT, T2 * P])
        y = st.sb("y", [P, T2, D])
        small_in, weights_in, mask_in = st.sem("small_in"), st.sem("weights_in"), st.sem("mask_in")
        mask_used, xn_ready, weighed = st.sem("mask_used"), st.sem("xn_ready"), st.sem("weighed")
        order = st.sem("vector_order")
        half_full, half_free = st.sem("half_mask_full"), st.sem("half_mask_free")
        pool_s = Steps(st.sem("pool_steps"), ["consts", "rms1", "rms2"])
        act_s = Steps(st.sem("act_steps"), ["sincos", "exp0", "exp1"] + [f"gelu{f}" for f in range(FT)])
        PE = (["w_rows", "slot_cols"] + [f"pickT{t}" for t in range(4)] + ["gather", "bias", "hT", "q", "k", "v", "qT", "kT"]
              + sum([[f"scores{t}", *[f"probT{t}{r}" for r in range(4)], f"av{t}"] for t in range(T2)], [])
              + ["oT", "proj", "h2T"] + [f"up{f}" for f in range(FT)] + ["down"] + [f"scatter{t}" for t in range(B * TT)])
        pe_s = Steps(st.sem("pe_steps"), PE)
        ve_s = Steps(st.sem("vector_steps"), [
            n for n in ["wcol", "wrow", "slots", "cols", "pick", *[f"pickT{t}" for t in range(4)], "xs", "bias",
                        "sq1", "hn", "hT", "angles", "q", "k", "v", "qT", "kT"]
            + sum([[f"biased{t}", f"probs{t}", *[f"probT{t}{r}" for r in range(4)], f"o{t}"] for t in range(T2)], [])
            + ["oT", "x1", "sq2", "h2", "h2T", "y"] + [f"row{t}" for t in range(B * TT)]])
        block = st.block()

        @block.sync
        def _(sp):
            sp.dma_start(rw[:], dram["l0f_rw"].to_broadcast([P, D])).then_inc(small_in, 16)
            sp.dma_start(rb[:], dram["l0f_rb"].to_broadcast([P, 1])).then_inc(small_in, 16)
            sp.dma_start(freq[:], dram["rope_freq"].to_broadcast([P, HD // 2])).then_inc(small_in, 16)
            sp.dma_start(pos[:], dram["pos"]).then_inc(small_in, 16)
            sp.dma_start(base[:], dram["slot_base"]).then_inc(small_in, 16)
            sp.dma_start(ln1[:], dram["l0f_ln1"]).then_inc(small_in, 16)
            sp.dma_start(ln2[:], dram["l0f_ln2"]).then_inc(small_in, 16)
            for dst, name in ((wq, "l0f_wq"), (wk, "l0f_wk"), (wv, "l0f_wv"), (wo, "l0f_wo"), (w1, "l0f_w1"), (w2, "l0f_w2")):
                sp.dma_start(dst[:], dram[name].rearrange("(c p) n -> p c n", p=P)).then_inc(weights_in, 16)
            with sp.Fori(0, B) as b:
                sp.wait_ge(mask_used, b + 1)
                sp.dma_start(mask[:], dram["attention_mask"][b].rearrange("(j p) s -> p j s", p=P)).then_inc(mask_in, 16)

        @block.gpsimd
        def _(pool):
            nc.gpsimd.memset(ones[:], 1.0)
            nc.gpsimd.iota(iota[:], [[1, P]], base=0, channel_multiplier=0, allow_small_or_imprecise_dtypes=True)
            nc.gpsimd.memset(q[:], 0.0)
            pool_s.done(nc.gpsimd.memset(k[:], 0.0), "consts")
            with pool.Fori(0, B) as b:
                norm.pool(pool, b)
            for n in (1, 2):
                ve_s.wait(pool, f"sq{n}")
                pool_s.done(nc.gpsimd.tensor_tensor(rms[:], ss[:], core.neg_half[:, 0:T2], ALU.pow), f"rms{n}")

        @block.scalar
        def _(act):
            ve_s.wait(act, "angles")
            nc.scalar.activation(sin[:], ang[:], ACT.Sin)
            act_s.done(nc.scalar.activation(cos[:], ang[:], ACT.Sin, scale=0.5), "sincos")
            for t in range(T2):
                ve_s.wait(act, f"biased{t}")
                act_s.done(nc.scalar.activation(prob[:], prob[:], ACT.Exp), f"exp{t}")
            for f in range(FT):
                pe_s.wait(act, f"up{f}")
                act_s.done(nc.scalar.activation(gT[:, f, :], core.ps[:, f % 4, 0:T2 * P], ACT.Gelu_apprx_tanh), f"gelu{f}")

        @block.tensor
        def _(pe):
            ident = core.ident
            ps = core.ps
            pe.sem_inc(mask_used, 1)
            ve_s.wait(pe, "wcol")
            for j in range(TT):
                last = nc.tensor.transpose(ps[0:B, 0, j * P:(j + 1) * P], wcol[:, j, :], ident[:])
            pe_s.done(last, "w_rows")
            ve_s.wait(pe, "slots")
            for n, rows in enumerate((work, above)):
                for j in range(TT):
                    last = nc.tensor.transpose(ps[:, 1, n * 16 + j * B:n * 16 + (j + 1) * B], rows[:, j * P:(j + 1) * P],
                                               ident[0:B, 0:B])
            pe_s.done(last, "slot_cols")
            ve_s.wait(pe, "pick")
            for b in range(B):
                for j in range(TT):
                    last = nc.tensor.transpose(ps[:, 2 + b, j * P:(j + 1) * P], pick[:, b * TT + j, :], ident[:])
                pe_s.done(last, f"pickT{b}")
            for t in range(T2):
                for n in range(2 * TT):
                    last = nc.tensor.matmul(ps[:, 6 + t, 0:NA], pick[:, t * 2 * TT + n, :], xa[:, t * 2 * TT + n, :],
                                            start=(n == 0), stop=(n == 2 * TT - 1))
            pe_s.done(last, "gather")
            with pe.Fori(0, B) as b:
                pe.wait_ge(mask_in, b * 16 + 16)
                pe.wait_ge(half_free, b + 1)
                for kt in range(TT):
                    for j in range(TT):
                        last = nc.tensor.matmul(ps[:, 0, kt * P:(kt + 1) * P], mask[:, j, kt * P:(kt + 1) * P],
                                                pick[:, b * TT + j, :], start=(j == 0), stop=(j == TT - 1))
                last.then_inc(half_full, 1)
                pe.wait_ge(half_free, b + 2)
                pe.sem_inc(mask_used, 1)
            for t in range(T2):
                for n in range(2 * TT):
                    last = nc.tensor.matmul(ps[:, 1, t * P:(t + 1) * P], half_mask[:, t * 2 * TT + n, :],
                                            pick[:, t * 2 * TT + n, :], start=(n == 0), stop=(n == 2 * TT - 1))
            pe_s.done(last, "bias")
            ve_s.wait(pe, "hn")

            def turn(src, bank, name):
                for c in range(DC):
                    for t in range(T2):
                        last = nc.tensor.transpose(ps[:, bank, (c * T2 + t) * P:(c * T2 + t + 1) * P],
                                                   src[:, t, c * P:(c + 1) * P], ident[:])
                pe_s.done(last, name)

            turn(hn, 2, "hT")
            ve_s.wait(pe, "hT")
            pe.wait_ge(weights_in, 16 * 6)
            for bank, w, name in ((3, wq, "q"), (4, wk, "k"), (5, wv, "v")):
                for t in range(T2):
                    for c in range(DC):
                        last = nc.tensor.matmul(ps[:, bank, t * D:(t + 1) * D], hT[:, c, t * P:(t + 1) * P], w[:, c, :],
                                                start=(c == 0), stop=(c == DC - 1))
                pe_s.done(last, name)
            for src, bank, name in ((q, 6, "q"), (k, 0, "k")):
                ve_s.wait(pe, name)
                if name == "k":
                    ve_s.wait(pe, "bias")
                    pe.wait_ge(half_free, B + 1)
                for t in range(T2):
                    for g in range(HG):
                        last = nc.tensor.transpose(ps[:, bank + t, g * P:(g + 1) * P],
                                                   src[:, t, g * HG:(g + 1) * HG, :], ident[:])
                pe_s.done(last, name + "T")
            ve_s.wait(pe, "v")
            for t in range(T2):
                ve_s.wait(pe, "kT")
                if t:
                    ve_s.wait(pe, "o0")
                for r in range(4):
                    for g in range(HG):
                        last = nc.tensor.matmul(ps[:, 2 + r, g * P:(g + 1) * P],
                                                qT[r * STRIP:(r + 1) * STRIP, g, t * P:(t + 1) * P],
                                                kT[r * STRIP:(r + 1) * STRIP, g, t * P:(t + 1) * P], start=True, stop=True,
                                                tile_position=(r * STRIP, 0))
                pe_s.done(last, f"scores{t}")
                ve_s.wait(pe, f"probs{t}")
                for r in range(4):
                    for n in range(4):
                        last = nc.tensor.transpose(ps[:, 2 + r, n * P:(n + 1) * P], prob[:, r * 4 + n, :], ident[:])
                    pe_s.done(last, f"probT{t}{r}")
                ve_s.wait(pe, f"probT{t}3")
                for h in range(H):
                    n = (h % HG) * 4 + h // HG
                    last = nc.tensor.matmul(ps[:, 6, h * HD:(h + 1) * HD], probT[:, n, :], v[:, t, h * HD:(h + 1) * HD],
                                            start=True, stop=True)
                pe_s.done(last, f"av{t}")
            ve_s.wait(pe, "o1")
            turn(o, 7, "oT")
            ve_s.wait(pe, "oT")
            for t in range(T2):
                for c in range(DC):
                    last = nc.tensor.matmul(ps[:, 0, t * D:(t + 1) * D], oT[:, c, t * P:(t + 1) * P], wo[:, c, :],
                                            start=(c == 0), stop=(c == DC - 1))
            pe_s.done(last, "proj")
            ve_s.wait(pe, "h2")
            turn(hn, 1, "h2T")
            ve_s.wait(pe, "h2T")
            for f in range(FT):
                if f >= 4:
                    act_s.wait(pe, f"gelu{f - 4}")
                for c in range(DC):
                    last = nc.tensor.matmul(ps[:, f % 4, 0:T2 * P], w1[:, c, f * P:(f + 1) * P], hT[:, c, :],
                                            start=(c == 0), stop=(c == DC - 1))
                pe_s.done(last, f"up{f}")
            act_s.wait(pe, f"gelu{FT - 1}")
            for t in range(T2):
                for f in range(FT):
                    last = nc.tensor.matmul(ps[:, 4, t * D:(t + 1) * D], gT[:, f, t * P:(t + 1) * P], w2[:, f, :],
                                            start=(f == 0), stop=(f == FT - 1))
            pe_s.done(last, "down")
            ve_s.wait(pe, "y")
            for t in range(B * TT):
                if t >= 4:
                    ve_s.wait(pe, f"row{t - 4}")
                pe_s.done(nc.tensor.matmul(ps[:, t % 4, 0:D], pickT[:, t, :], y[:, t // (2 * TT), :], start=True, stop=True),
                          f"scatter{t}")

        @block.vector
        def _(dve):
            ps = core.ps
            V = nc.vector
            dve.sem_inc(half_free, 1)
            V.memset(bar[0:HALF, 0:HALF - 1], 0.0)
            V.memset(bar[0:HALF, HALF - 1:P], NEG)
            V.memset(bar[HALF:P, 0:HALF], NEG)
            V.memset(bar[HALF:P, HALF:P - 1], 0.0)
            V.memset(bar[HALF:P, P - 1:P], NEG)
            dve.wait_ge(small_in, 16 * 7)
            with dve.Fori(0, B) as b:
                norm.vector(dve, b, lambda j: core.x[:, b * TT + j, :], lambda j: xa[:, b * TT + j, 0:D], xn_ready)
                dve.wait_ge(xn_ready, b + 1)
                for j in range(TT):
                    last = V.scalar_tensor_tensor(out=junk[:, j, :], in0=xa[:, b * TT + j, 0:D], scalar=1.0, in1=rw[:],
                                                  op0=ALU.mult, op1=ALU.mult, accum_out=xa[:, b * TT + j, D:D + 1])
                last.then_inc(weighed, 1)
                dve.wait_ge(weighed, b + 1)
            link = Chain(dve, order)
            link(V.tensor_copy(xa[:, :, D + 1], pos[:]))
            link(V.tensor_scalar(xa[:, :, D], xa[:, :, D], rb[:, 0:1], None, ALU.add))
            ve_s.done(V.tensor_copy(wcol[:].rearrange("p j b -> p b j"), xa[:, :, D].rearrange("p (b j) -> p b j", b=B)),
                      "wcol")
            pe_s.wait(dve, "w_rows")
            link(V.tensor_copy(wrow[:], ps[0:B, 0, :]))
            ve_s.done(V.tensor_copy(work[:], ps[0:B, 0, :]), "wrow")
            ve_s.wait(dve, "wrow")
            for n in range(K // 8 - 1):
                eight = top[:, n * 8:n * 8 + 8]
                link(V.max(eight, work[:]))
                link(V.match_replace(work[:], eight, work[:], NEG))
            link(V.max(top[:, K - 8:K], work[:]))
            link(V.tensor_copy(last8[:], top[:, K - 8:K]))
            link(V.memset(last8[:, 7:8], NEG))
            link(V.match_replace(work[:], last8[:], work[:], NEG))
            link(V.tensor_tensor(chosen[:], work[:], wrow[:], ALU.not_equal))
            link(V.tensor_scalar(above[:], wrow[:], top[:, K - 1:K], None, ALU.is_gt))
            pool_s.wait(dve, "consts")
            link(V.tensor_tensor_scan(work[:], ones[:], chosen[:], 0.0, ALU.mult, ALU.add))
            link(V.scalar_tensor_tensor(out=work[:], in0=work[:], scalar=base[:, 0:1], in1=chosen[:],
                                        op0=ALU.add, op1=ALU.mult))
            ve_s.done(V.tensor_scalar(work[:], work[:], -1.0, None, ALU.add), "slots")
            pe_s.wait(dve, "slot_cols")
            V.tensor_copy(slot[:].rearrange("p b j -> p j b"), ps[:, 1, 0:16].rearrange("p (j b) -> p j b", b=B))
            ve_s.done(V.tensor_scalar(keep[:].rearrange("p b j -> p j b"), ps[:, 1, 16:32].rearrange("p (j b) -> p j b", b=B),
                                      -1.0, 1.0, ALU.mult, ALU.add), "cols")
            ve_s.wait(dve, "cols")
            for t in range(B * TT):
                last = V.tensor_scalar(pick[:, t, :], iota[:], slot[:, t // TT, t % TT:t % TT + 1], None, ALU.is_equal)
            ve_s.done(last, "pick")
            for b in range(B):
                pe_s.wait(dve, f"pickT{b}")
                ve_s.done(V.tensor_copy(pickT[:, b * TT:(b + 1) * TT, :], ps[:, 2 + b, :]), f"pickT{b}")
            pe_s.wait(dve, "gather")
            ve_s.done(V.tensor_copy(xs[:], ps[:, 6:8, 0:NA]), "xs")
            with dve.Fori(0, B) as b:
                dve.wait_ge(half_full, b + 1)
                V.tensor_copy(half_mask[:, bass.ds(b * TT, TT), :], ps[:, 0, :].rearrange("p (k s) -> p k s", s=P)
                              ).then_inc(half_free, 1)
            pe_s.wait(dve, "bias")
            ve_s.done(V.tensor_tensor(bias[:], ps[:, 1, 0:T2 * P].rearrange("p (t s) -> p t s", s=P),
                                      bar[:].unsqueeze(1).to_broadcast([P, T2, P]), ALU.add), "bias")

            def rms_norm(src, n, name):
                for t in range(T2):
                    last = V.scalar_tensor_tensor(out=junk[:, t, :], in0=src[:, t, 0:D], scalar=1.0, in1=src[:, t, 0:D],
                                                  op0=ALU.mult, op1=ALU.mult, accum_out=ss[:, t:t + 1])
                link(last)
                ve_s.done(V.tensor_scalar(ss[:], ss[:], 1.0 / D, 1e-6, ALU.mult, ALU.add), f"sq{n}")
                pool_s.wait(dve, f"rms{n}")
                for t in range(T2):
                    last = V.tensor_scalar(hn[:, t, :], src[:, t, 0:D], rms[:, t:t + 1], None, ALU.mult)
                ve_s.done(last, name)

            def gained(bank, gain, name):
                for c in range(DC):
                    last = V.tensor_scalar(hT[:, c, :], ps[:, bank, c * T2 * P:(c + 1) * T2 * P], gain[:, c:c + 1],
                                           None, ALU.mult)
                ve_s.done(last, name)

            ve_s.wait(dve, "xs")
            rms_norm(xs, 1, "hn")
            pe_s.wait(dve, "hT")
            gained(2, ln1, "hT")
            for t in range(T2):
                last = V.tensor_scalar(ang[:, t, 0:8], freq[:], xs[:, t, D + 1:D + 2], None, ALU.mult)
            link(last)
            link(V.tensor_scalar(turns[:, :, 0:8], ang[:, :, 0:8], 0.15915494309189535, ROUND, ALU.mult, ALU.add))
            link(V.tensor_scalar(turns[:, :, 0:8], turns[:, :, 0:8], ROUND, None, ALU.subtract))
            for part in (6.28125, 0.0019350051879882812, 3.019916050e-07):
                link(V.scalar_tensor_tensor(out=ang[:, :, 0:8], in0=turns[:, :, 0:8], scalar=-part, in1=ang[:, :, 0:8],
                                            op0=ALU.mult, op1=ALU.add))
            link(V.tensor_scalar(ang[:, :, 0:8], ang[:, :, 0:8], 3.1415925, -3.1415925, ALU.min, ALU.max))
            ve_s.done(V.tensor_copy(ang[:, :, 8:16], ang[:, :, 0:8]), "angles")
            act_s.wait(dve, "sincos")
            link(V.tensor_scalar(sin[:, :, 0:8], sin[:, :, 0:8], -1.0, None, ALU.mult))
            link(V.tensor_tensor(cos[:], cos[:], cos[:], ALU.mult))
            link(V.tensor_scalar(cos[:], cos[:], -2.0, 1.0, ALU.mult, ALU.add))
            for bank, dst, name in ((3, q, "q"), (4, k, "k")):
                pe_s.wait(dve, name)
                for t in range(T2):
                    src = ps[:, bank, t * D:(t + 1) * D].rearrange("p (h d) -> p h d", h=H)
                    for lo, hi in ((0, 8), (8, 0)):
                        last = V.tensor_tensor(rot[:, :, lo:lo + 8], src[:, :, hi:hi + 8],
                                               sin[:, t, lo:lo + 8].unsqueeze(1).to_broadcast([P, H, 8]), ALU.mult)
                    last = V.tensor_tensor(dst[:, t, :, 0:HD], src, cos[:, t, :].unsqueeze(1).to_broadcast([P, H, HD]),
                                           ALU.mult)
                    link(last)
                    last = V.tensor_tensor(dst[:, t, :, 0:HD], dst[:, t, :, 0:HD], rot[:], ALU.add)
                    if t == 0:
                        link(last)
                ve_s.done(last, name)
                ve_s.wait(dve, name)
            pe_s.wait(dve, "v")
            ve_s.done(V.tensor_copy(v[:], ps[:, 5, :].rearrange("p (t d) -> p t d", t=T2)), "v")
            for bank, dst, name in ((6, qT, "qT"), (0, kT, "kT")):
                pe_s.wait(dve, name)
                for t in range(T2):
                    last = V.tensor_copy(dst[:, :, t * P:(t + 1) * P], ps[:, bank + t, :].rearrange("p (g s) -> p g s", g=HG))
                ve_s.done(last, name)
            for t in range(T2):
                pe_s.wait(dve, f"scores{t}")
                for r in range(4):
                    last = V.scalar_tensor_tensor(out=prob[:, r * 4:r * 4 + 4, :],
                                                  in0=ps[:, 2 + r, :].rearrange("p (g s) -> p g s", g=HG), scalar=HD ** -0.5,
                                                  in1=bias[:, t, :].unsqueeze(1).to_broadcast([P, HG, P]),
                                                  op0=ALU.mult, op1=ALU.add)
                link(last)
                link(V.tensor_reduce(mx[:], prob[:], AX, ALU.max))
                ve_s.done(V.tensor_tensor(prob[:], prob[:], mx[:].unsqueeze(2).to_broadcast([P, H, P]), ALU.subtract),
                          f"biased{t}")
                act_s.wait(dve, f"exp{t}")
                link(V.tensor_reduce(total[:], prob[:], AX, ALU.add))
                link(V.reciprocal(inv[:], total[:]))
                ve_s.done(V.tensor_tensor(prob[:], prob[:], inv[:].unsqueeze(2).to_broadcast([P, H, P]), ALU.mult),
                          f"probs{t}")
                for r in range(4):
                    pe_s.wait(dve, f"probT{t}{r}")
                    ve_s.done(V.tensor_copy(probT[:, r * 4:r * 4 + 4, :], ps[:, 2 + r, :].rearrange("p (g s) -> p g s", g=4)),
                              f"probT{t}{r}")
                pe_s.wait(dve, f"av{t}")
                ve_s.done(V.tensor_copy(o[:, t, :], ps[:, 6, 0:D]), f"o{t}")
            pe_s.wait(dve, "oT")
            ve_s.done(V.tensor_copy(oT[:], ps[:, 7, :].rearrange("p (c s) -> p c s", c=DC)), "oT")
            pe_s.wait(dve, "proj")
            ve_s.done(V.tensor_tensor(x1[:], xs[:, :, 0:D], ps[:, 0, :].rearrange("p (t d) -> p t d", t=T2), ALU.add), "x1")
            ve_s.wait(dve, "x1")
            rms_norm(x1, 2, "h2")
            pe_s.wait(dve, "h2T")
            gained(1, ln2, "h2T")
            pe_s.wait(dve, "down")
            link(V.tensor_tensor(x1[:], x1[:], ps[:, 4, :].rearrange("p (t d) -> p t d", t=T2), ALU.add))
            for t in range(T2):
                last = V.tensor_scalar(y[:, t, :], x1[:, t, :], xs[:, t, D:D + 1], None, ALU.mult)
            ve_s.done(last, "y")
            for t in range(B * TT):
                link(V.scalar_tensor_tensor(out=junk[:, t % TT, :], in0=xa[:, t, 0:D], scalar=keep[:, t // TT, t % TT:t % TT + 1],
                                            in1=core.x[:, t, :], op0=ALU.mult, op1=ALU.add))
                pe_s.wait(dve, f"scatter{t}")
                ve_s.done(V.tensor_tensor(core.x[:, t, :], junk[:, t % TT, :], ps[:, t % 4, 0:D], ALU.add), f"row{t}")


def causal_attention_stage(core):
    nc, dram = core.nc, core.dram
    SCALE = D ** -0.5
    with Stage(core, "l1x") as st:
        norm = Norm(st)
        xn = st.sb("xn", [P, TT, D])
        xnT = st.sb("xnT", [P, DC, S])
        ctx = st.sb("ctx", [P, 2, TT, D])
        ctxT = st.sb("ctxT", [P, 2, DC, S])
        future = st.sb("future", [P, P])
        prob = st.sb("prob", [P, TT, S])
        probT = st.sb("probT", [P, 2, S])
        top, shift, total, inv = (st.sb(n, [P, TT]) for n in ("top", "shift", "total", "inv"))
        ctx_in = [st.sem(f"ctx_in{i}") for i in range(2)]
        xn_ready, zeroed, future_made = st.sem("xn_ready"), st.sem("zeroed"), st.sem("future_made")
        row_used = st.sem("rows_done")
        pe_s = Steps(st.sem("pe_steps"), ["xT"] + [f"scores{q}" for q in range(TT)]
                     + sum([[f"turned{q}", f"out{q}"] for q in range(TT)], []))
        ve_s = Steps(st.sem("vector_steps"), ["xT"] + sum([[f"masked{q}", f"max{q}", f"shift{q}"] for q in range(TT)], [])
                     + sum([[f"probT{q}", f"inv{q}", f"row{q}"] for q in range(TT)], []))
        act_s = Steps(st.sem("act_steps"), [f"exp{q}" for q in range(TT)])
        block = st.block()

        @block.sync
        def _(sp):
            with sp.Fori(0, B // 2) as pair:
                for i in range(2):
                    sp.wait_ge(row_used, pair * 2 + i + 1)
                    sp.dma_start(ctx[:, i, :, :], dram["ctx"][pair * 2 + i].rearrange("(j p) d -> p j d", p=P)).then_inc(ctx_in[i], 16)
                    sp.dma_start(ctxT[:, i, :, :], dram["ctxT"][pair * 2 + i].rearrange("(c p) s -> p c s", p=P)).then_inc(ctx_in[i], 16)

        @block.gpsimd
        def _(pool):
            nc.gpsimd.memset(future[:], 0.0).then_inc(zeroed, 1)
            pool.wait_ge(zeroed, 1)
            nc.gpsimd.affine_select(out=future[:], in_=future[:], compare_op=ALU.is_ge, fill=NEG,
                                    base=0, pattern=[[-1, P]], channel_multiplier=1).then_inc(future_made, 1)
            with pool.Fori(0, B) as b:
                norm.pool(pool, b)

        @block.tensor
        def _(pe):
            ps = core.ps
            pe.sem_inc(row_used, 2)
            with pe.Fori(0, B // 2) as pair:
                for i in range(2):
                    b = pair * 2 + i
                    pe.wait_ge(xn_ready, b + 1)
                    for c in range(DC):
                        for j in range(TT):
                            last = nc.tensor.transpose(ps[:, 6 + c, j * P:(j + 1) * P], xn[:, j, c * P:(c + 1) * P], core.ident[:])
                    pe_s.done(last, "xT")
                    pe.wait_ge(ctx_in[i], pair * 32 + 32)
                    ve_s.wait(pe, "xT", b)
                    for q in range(TT):
                        for c in range(DC):
                            last = nc.tensor.matmul(ps[:, q, 0:(q + 1) * P], xnT[:, c, q * P:(q + 1) * P],
                                                    ctxT[:, i, c, 0:(q + 1) * P], start=(c == 0), stop=(c == DC - 1))
                        pe_s.done(last, f"scores{q}")
                    for q in range(TT):
                        act_s.wait(pe, f"exp{q}", b)
                        if q >= 2:
                            ve_s.wait(pe, f"probT{q - 2}", b)
                        for k in range(q + 1):
                            last = nc.tensor.transpose(ps[:, 4 + q % 2, k * P:(k + 1) * P], prob[:, q, k * P:(k + 1) * P],
                                                       core.ident[:])
                        pe_s.done(last, f"turned{q}")
                        ve_s.wait(pe, f"probT{q}", b)
                        if q >= 2:
                            ve_s.wait(pe, f"row{q - 2}", b)
                        for k in range(q + 1):
                            last = nc.tensor.matmul(ps[:, 6 + q % 2, 0:D], probT[:, q % 2, k * P:(k + 1) * P],
                                                    ctx[:, i, k, :], start=(k == 0), stop=(k == q))
                        pe_s.done(last, f"out{q}")
                    ve_s.wait(pe, f"row{TT - 1}", b)
                    pe.sem_inc(row_used, 1)

        @block.scalar
        def _(act):
            with act.Fori(0, B) as b:
                for q in range(TT):
                    ve_s.wait(act, f"shift{q}", b)
                    act_s.done(nc.scalar.activation(prob[:, q, 0:(q + 1) * P], core.ps[:, q, 0:(q + 1) * P], ACT.Exp,
                                                    bias=shift[:, q:q + 1], scale=SCALE, accum_out=total[:, q:q + 1]),
                               f"exp{q}")

        @block.vector
        def _(dve):
            ps, V = core.ps, nc.vector
            dve.wait_ge(future_made, 1)
            with dve.Fori(0, B) as b:
                norm.vector(dve, b, lambda j: core.x[:, b * TT + j, :], lambda j: xn[:, j, :], xn_ready)
                pe_s.wait(dve, "xT", b)
                ve_s.done(V.tensor_copy(xnT[:], ps[:, 6:8, :]), "xT")
                for q in range(TT):
                    pe_s.wait(dve, f"scores{q}", b)
                    own = ps[:, q, q * P:(q + 1) * P]
                    ve_s.done(V.tensor_tensor(own, own, future[:], ALU.add), f"masked{q}")
                    ve_s.wait(dve, f"masked{q}", b)
                    ve_s.done(V.tensor_reduce(top[:, q:q + 1], ps[:, q, 0:(q + 1) * P], AX, ALU.max), f"max{q}")
                    ve_s.wait(dve, f"max{q}", b)
                    ve_s.done(V.tensor_scalar(shift[:, q:q + 1], top[:, q:q + 1], -SCALE, None, ALU.mult), f"shift{q}")
                for q in range(TT):
                    pe_s.wait(dve, f"turned{q}", b)
                    ve_s.done(V.tensor_copy(probT[:, q % 2, 0:(q + 1) * P], ps[:, 4 + q % 2, 0:(q + 1) * P]), f"probT{q}")
                    act_s.wait(dve, f"exp{q}", b)
                    ve_s.done(V.reciprocal(inv[:, q:q + 1], total[:, q:q + 1]), f"inv{q}")
                    ve_s.wait(dve, f"inv{q}", b)
                    pe_s.wait(dve, f"out{q}", b)
                    row = core.x[:, b * TT + q, :]
                    ve_s.done(V.scalar_tensor_tensor(out=row, in0=ps[:, 6 + q % 2, 0:D], scalar=inv[:, q:q + 1], in1=row,
                                                     op0=ALU.mult, op1=ALU.add), f"row{q}")


def quantised_ffn_stage(core):
    nc, dram = core.nc, core.dram
    F = 704
    FT = -(-F // P)
    rows = [min(P, F - f * P) for f in range(FT)]
    QMAX = 127.0
    SLOTS = 3
    with Stage(core, "l1f") as st:
        norm = Norm(st)
        xn = st.sb("xn", [P, B * TT, D])
        hT = st.sb("hT", [P, FT, B * S])
        hq = st.sb("hq", [P, FT, S], BF16)
        silu = st.sb("silu", [P, SLOTS, S])
        xr = st.sb("xr", [P, TT, D])
        hr = st.sb("hr", [P, FT, S])
        xq = st.sb("xq", [P, TT, D], BF16)
        xqT = st.sb("xqT", [P, DC, S], BF16)
        ident = st.sb("ident16", [P, P], BF16)
        ones = st.sb("ones", [P, P])
        wraw = {n: st.sb(f"{n}_raw", [P, FT, D]) for n in ("gate", "up")}
        wraw["down"] = st.sb("down_raw", [P, DC, F])
        wmax = {n: st.sb(f"{n}_max", [P, DC if n == "down" else FT]) for n in wraw}
        winv = {n: st.sb(f"{n}_inv", [P, DC if n == "down" else FT]) for n in wraw}
        wlev = {n: st.sb(f"{n}_levels", list(wraw[n].shape), BF16) for n in wraw}
        wT = {n: st.sb(f"{n}T", [P, DC, F] if n != "down" else [P, FT, D], BF16) for n in wraw}
        gate_scale, up_scale = st.sb("gate_scale", [P, FT]), st.sb("up_scale", [P, FT])
        diag = st.sb("diag", [P, D])
        down_row, out_row = st.sb("down_row", [P, D]), st.sb("out_row", [P, D])
        clip = st.sb("clip", [P, 2])
        ratio = st.sb("ratio", [P, 2])
        xmax, hmax = st.sb("xmax", [P, B * TT]), st.sb("hmax", [P, B])
        own, whole, scale, inv = (st.sb(n, [P, 2]) for n in ("own", "whole", "scale", "inv"))
        part = st.sb("part", [P, TT, D])
        small_in, weights_in = st.sem("small_in"), st.sem("weights_in")
        xn_ready, max_ready, order = st.sem("xn_ready"), st.sem("max_ready"), st.sem("vector_order")
        act_ratio, ident_made, pool_max = st.sem("act_ratio"), st.sem("ident_made"), st.sem("pool_max")
        own_ready = st.sem("own_max_ready")
        pe_w = Steps(st.sem("pe_weight_steps"), ["gate0", "gate1", "up0", "up1", "down0", "down1", "down_row"])
        ve_w = Steps(st.sem("vector_weight_steps"), ["gate", "up", "down", "gate0", "gate1", "up0", "up1", "down0", "down1",
                                                     "diag", "down_row"])
        xq_ready, xT_full, xT_ready = st.sem("xq_ready"), st.sem("xT_full"), st.sem("xT_ready")
        both_full, silu_ready, hidden_ready = st.sem("gate_up_full"), st.sem("silu_ready"), st.sem("hidden_ready")
        hq_ready, down_full, rows_out = st.sem("hq_ready"), st.sem("down_full"), st.sem("rows_out")
        ve_x = st.sem("quantise_x_order")
        ve_h = st.sem("quantise_h_order")
        ve_r = st.sem("row_order")
        block = st.block()

        @block.sync
        def _(sp):
            for n in ("gate", "up"):
                sp.dma_start(wraw[n][:, 0:FT - 1, :], dram[f"l1f_{n}"][0:(FT - 1) * P, :].rearrange("(f p) d -> p f d", p=P)
                             ).then_inc(weights_in, 16)
                sp.dma_start(wraw[n][0:rows[-1], FT - 1, :], dram[f"l1f_{n}"][(FT - 1) * P:F, :]).then_inc(weights_in, 16)
            sp.dma_start(wraw["down"][:], dram["l1f_down"].rearrange("(c p) n -> p c n", p=P)).then_inc(weights_in, 16)
            for i, n in enumerate(("l1f_clip_x", "l1f_clip_down")):
                sp.dma_start(clip[:, i:i + 1], dram[n].to_broadcast([P, 1])).then_inc(small_in, 16)

        @block.gpsimd
        def _(pool):
            nc.gpsimd.memset(ones[:], 1.0)
            nc.gpsimd.tensor_copy(ident[:], core.ident[:]).then_inc(ident_made, 1)
            with pool.Fori(0, B) as b:
                norm.pool(pool, b)
            for i in range(2):
                pool.wait_ge(own_ready, i + 1)
                nc.gpsimd.partition_all_reduce(whole[:, i:i + 1], own[:, i:i + 1], P, bass.bass_isa.ReduceOp.max
                                               ).then_inc(pool_max, 1)

        @block.scalar
        def _(act):
            act.wait_ge(small_in, 32)
            nc.scalar.activation(ratio[:], clip[:], ACT.Sigmoid).then_inc(act_ratio, 1)
            with act.Fori(0, B) as b:
                for f, m in enumerate(rows):
                    act.wait_ge(both_full, b * FT + f + 1)
                    act.wait_ge(hidden_ready, b * FT + max(f + 1, SLOTS))
                    nc.scalar.activation(silu[0:m, f % SLOTS, :], core.ps[0:m, 2 * (f % SLOTS), :], ACT.Silu,
                                         scale=gate_scale[0:m, f:f + 1]).then_inc(silu_ready, 1)

        @block.tensor
        def _(pe):
            ps = core.ps
            pe.wait_ge(ident_made, 1)
            for n in ("gate", "up"):
                ve_w.wait(pe, n)
                for c in range(DC):
                    for f, m in enumerate(rows):
                        last = nc.tensor.transpose(ps[:, c, :].bitcast(BF16)[:, f * P:f * P + m],
                                                   wlev[n][0:m, f, c * P:(c + 1) * P], ident[0:m, 0:m])
                    pe_w.done(last, f"{n}{c}")
                    ve_w.wait(pe, f"{n}{c}")
            ve_w.wait(pe, "down")
            for c in range(DC):
                for f, m in enumerate(rows):
                    last = nc.tensor.transpose(ps[0:m, c, :].bitcast(BF16)[:, f * P:(f + 1) * P],
                                               wlev["down"][:, c, f * P:f * P + m], ident[:])
                pe_w.done(last, f"down{c}")
            ve_w.wait(pe, "diag")
            pe_w.done(nc.tensor.matmul(ps[:, 2, 0:D], ones[:], diag[:], start=True, stop=True), "down_row")
            ve_w.wait(pe, "down_row")
            with pe.Fori(0, B) as b:
                pe.wait_ge(xq_ready, b + 1)
                for c in range(DC):
                    for j in range(TT):
                        last = nc.tensor.transpose(ps[:, 6, :].bitcast(BF16)[:, (c * TT + j) * P:(c * TT + j + 1) * P],
                                                   xq[:, j, c * P:(c + 1) * P], ident[:])
                last.then_inc(xT_full, 1)
                pe.wait_ge(xT_ready, b + 1)
                for f, m in enumerate(rows):
                    pe.wait_ge(hidden_ready, b * FT + max(f + 1, SLOTS))
                    for i, n in enumerate(("gate", "up")):
                        for c in range(DC):
                            last = nc.tensor.matmul(ps[0:m, 2 * (f % SLOTS) + i, :], wT[n][:, c, f * P:f * P + m],
                                                    xqT[:, c, :], start=(c == 0), stop=(c == DC - 1))
                    last.then_inc(both_full, 1)
            with pe.Fori(0, B) as b:
                pe.wait_ge(hq_ready, b + 1)
                for j in range(TT):
                    pe.wait_ge(rows_out, b * TT + max(j + 1, 2))
                    for f, m in enumerate(rows):
                        last = nc.tensor.matmul(ps[:, 6 + j % 2, 0:D], hq[0:m, f, j * P:(j + 1) * P], wT["down"][0:m, f, :],
                                                start=(f == 0), stop=(f == FT - 1))
                    last.then_inc(down_full, 1)

        @block.vector
        def _(dve):
            ps, V = core.ps, nc.vector
            dve.sem_inc(hidden_ready, SLOTS)
            dve.sem_inc(rows_out, 2)
            with dve.Fori(0, B) as b:
                norm.vector(dve, b, lambda j: core.x[:, b * TT + j, :], lambda j: xn[:, b * TT + j, :], xn_ready)
                dve.wait_ge(xn_ready, b + 1)
                V.tensor_reduce(xmax[:, bass.ds(b * TT, TT)], xn[:, bass.ds(b * TT, TT), :], AX, ALU.max,
                                apply_absolute_value=True).then_inc(max_ready, 1)
            link = Chain(dve, order)

            def levels(link, dst, src, inv, tmp):
                link(V.tensor_scalar(tmp, src, inv, QMAX, ALU.mult, ALU.min))
                link(V.tensor_scalar(tmp, tmp, -QMAX - 1.0, ROUND, ALU.max, ALU.add))
                return V.tensor_scalar(dst, tmp, ROUND, None, ALU.subtract)

            def global_scale(i, maxima):
                link(V.tensor_reduce(own[:, i:i + 1], maxima, AX, ALU.max))
                V.tensor_copy(own[:, i:i + 1], own[:, i:i + 1]).then_inc(own_ready, 1)
                dve.wait_ge(pool_max, i + 1)
                link(V.tensor_tensor(scale[:, i:i + 1], whole[:, i:i + 1], ratio[:, i:i + 1], ALU.mult))
                link(V.tensor_scalar(scale[:, i:i + 1], scale[:, i:i + 1], 1.0 / QMAX, None, ALU.mult))
                link(V.reciprocal(inv[:, i:i + 1], scale[:, i:i + 1]))

            dve.wait_ge(max_ready, B)
            dve.wait_ge(act_ratio, 1)
            global_scale(0, xmax[:])
            dve.wait_ge(weights_in, 16 * 5)
            for n in ("gate", "up", "down"):
                tiles = [(c, P) for c in range(DC)] if n == "down" else list(enumerate(rows))
                for f, m in tiles:
                    link(V.tensor_reduce(wmax[n][0:m, f:f + 1], wraw[n][0:m, f, :], AX, ALU.max, apply_absolute_value=True))
                    link(V.tensor_scalar(wmax[n][0:m, f:f + 1], wmax[n][0:m, f:f + 1], 1.0 / QMAX, None, ALU.mult))
                    link(V.reciprocal(winv[n][0:m, f:f + 1], wmax[n][0:m, f:f + 1]))
                    last = levels(link, wlev[n][0:m, f, :], wraw[n][0:m, f, :], winv[n][0:m, f:f + 1], wraw[n][0:m, f, :])
                    if n != "down":
                        dst = gate_scale if n == "gate" else up_scale
                        V.tensor_scalar(dst[0:m, f:f + 1], wmax[n][0:m, f:f + 1], scale[0:m, 0:1], None, ALU.mult)
                ve_w.done(last, n)
            for n in ("gate", "up"):
                for c in range(DC):
                    pe_w.wait(dve, f"{n}{c}")
                    ve_w.done(V.tensor_copy(wT[n][:, c, :], ps[:, c, :].bitcast(BF16)[:, 0:F]), f"{n}{c}")
            for c in range(DC):
                pe_w.wait(dve, f"down{c}")
                turned = ps[:, c, :].bitcast(BF16)
                V.tensor_copy(wT["down"][:, 0:FT - 1, c * P:(c + 1) * P], turned[:, 0:(FT - 1) * P].rearrange("p (f n) -> p f n", n=P))
                ve_w.done(V.tensor_copy(wT["down"][0:rows[-1], FT - 1, c * P:(c + 1) * P], turned[0:rows[-1], (FT - 1) * P:FT * P]),
                          f"down{c}")
            for c in range(DC):
                last = V.tensor_scalar(diag[:, c * P:(c + 1) * P], core.ident[:], wmax["down"][:, c:c + 1], None, ALU.mult)
            ve_w.done(last, "diag")
            pe_w.wait(dve, "down_row")
            ve_w.done(V.tensor_copy(down_row[:], ps[:, 2, 0:D]), "down_row")
            V.memset(hT[rows[-1]:P, FT - 1, :], 0.0)
            with dve.Fori(0, B) as b:
                chain = Chain(dve, ve_x, b * 2)
                levels(chain, xq[:], xn[:, bass.ds(b * TT, TT), :], inv[:, 0:1], xr[:]).then_inc(xq_ready, 1)
                dve.wait_ge(xT_full, b + 1)
                V.tensor_copy(xqT[:], ps[:, 6, :].bitcast(BF16).rearrange("p (c s) -> p c s", c=DC)).then_inc(xT_ready, 1)
                for f, m in enumerate(rows):
                    dve.wait_ge(silu_ready, b * FT + f + 1)
                    V.scalar_tensor_tensor(out=hT[0:m, f, bass.ds(b * S, S)], in0=ps[0:m, 2 * (f % SLOTS) + 1, :],
                                           scalar=up_scale[0:m, f:f + 1], in1=silu[0:m, f % SLOTS, :],
                                           op0=ALU.mult, op1=ALU.mult).then_inc(hidden_ready, 1)
                dve.wait_ge(hidden_ready, (b + 1) * FT + SLOTS)
                V.tensor_reduce(hmax[:, bass.ds(b, 1)], hT[:, :, bass.ds(b * S, S)], mybir.AxisListType.XY, ALU.max,
                                apply_absolute_value=True).then_inc(max_ready, 1)
            dve.wait_ge(max_ready, 2 * B)
            global_scale(1, hmax[:])
            link(V.tensor_scalar(out_row[:], down_row[:], scale[:, 1:2], None, ALU.mult))
            with dve.Fori(0, B) as b:
                chain = Chain(dve, ve_h, b * 2)
                levels(chain, hq[:], hT[:, :, bass.ds(b * S, S)], inv[:, 1:2], hr[:]).then_inc(hq_ready, 1)
                for j in range(TT):
                    dve.wait_ge(down_full, b * TT + j + 1)
                    V.tensor_tensor(part[:, j, :], ps[:, 6 + j % 2, 0:D], out_row[:], ALU.mult).then_inc(rows_out, 1)
                    dve.wait_ge(rows_out, b * TT + j + 3)
                    row = core.x[:, b * TT + j, :]
                    last = V.tensor_tensor(row, row, part[:, j, :], ALU.add)
                last.then_inc(ve_r, 1)
                dve.wait_ge(ve_r, b + 1)


def autocorrelation_stage(core):
    nc, dram = core.nc, core.dram
    BEST = 12
    with Stage(core, "l2x") as st:
        norm = Norm(st)
        xn = st.sb("xn", [P, TT, D])
        xnT = st.sb("xnT", [P, DC, S])
        ctxT = st.sb("ctxT", [P, DC, S])
        wq, wk, wv, wo = (st.sb(n, [P, DC, D]) for n in ("wq", "wk", "wv", "wo"))
        bq, bk, bv, bo = (st.sb(n, [P, D]) for n in ("bq", "bk", "bv", "bo"))
        basis, inverse = st.sb("basis", [P, TT, S]), st.sb("inverse", [P, TT, S])
        qk = st.sb("qk", [P, TT, 2, D])
        qhat, junk = st.sb("qhat", [P, TT, D]), st.sb("junk", [P, TT, D])
        power = st.sb("power", [P, B, TT])
        power_b = st.sb("power_b", [P, TT, B])
        mean, work, chosen, gain = (st.sb(n, [B, S]) for n in ("mean", "work", "chosen", "gain"))
        eight, four = st.sb("eight", [B, 8]), st.sb("four", [B, 8])
        shift, total, inv = (st.sb(n, [B, 1]) for n in ("shift", "total", "inv"))
        circulant = st.sb("circulant", [P, B, TT, S])
        v = st.sb("v", [P, TT, D])
        aggT = st.sb("aggT", [P, DC, S])
        part = st.sb("part", [P, TT, D])
        rows = dram["delay_rows"]
        weights_in, bias_in, ctx_in, ctx_used = (st.sem(n) for n in ("weights_in", "bias_in", "ctx_in", "ctx_used"))
        xn_ready, order, rows_out, circulant_in = (st.sem(n) for n in ("xn_ready", "order", "rows_out", "circulant_in"))
        exp_done, summed = st.sem("exp_done"), st.sem("rows_summed")
        pe_a = Steps(st.sem("pe_spectrum_steps"), ["xT"] + [f"q{j}" for j in range(TT)] + [f"k{j}" for j in range(TT)]
                     + [f"hat{r}" for r in range(TT)])
        ve_a = Steps(st.sem("vector_spectrum_steps"), ["xT"] + [f"q{j}" for j in range(TT)] + [f"k{j}" for j in range(TT)]
                     + [f"power{r}" for r in range(TT)])
        act_a = Steps(st.sem("act_spectrum_steps"), [f"qhat{r}" for r in range(TT)])
        one = Steps(st.sem("pe_mean"), ["mean"])
        ve_m = Steps(st.sem("vector_mean_steps"), ["power", "shift", "gain"])
        pe_b = Steps(st.sem("pe_shift_steps"), [f"v{j}" for j in range(TT)] + [f"agg{c}" for c in range(DC)]
                     + [f"out{j}" for j in range(TT)])
        ve_b = Steps(st.sem("vector_shift_steps"), [f"v{j}" for j in range(TT)] + [f"agg{c}" for c in range(DC)]
                     + [f"out{j}" for j in range(TT)])
        block = st.block()

        @block.sync
        def _(sp):
            for dst, name in ((wq, "l2x_Wq"), (wk, "l2x_Wk"), (wv, "l2x_Wv"), (wo, "l2x_Wo"),
                              (basis, "dft_basis"), (inverse, "dft_inverse")):
                sp.dma_start(dst[:], dram[name].rearrange("(c p) n -> p c n", p=P)).then_inc(weights_in, 16)
            for dst, name in ((bq, "l2x_bq"), (bk, "l2x_bk"), (bv, "l2x_bv"), (bo, "l2x_bo")):
                sp.dma_start(dst[:], dram[name].to_broadcast([P, D])).then_inc(bias_in, 16)
            with sp.Fori(0, B) as b:
                sp.wait_ge(ctx_used, b + 1)
                sp.dma_start(ctxT[:], dram["ctxT"][b].rearrange("(c p) s -> p c s", p=P)).then_inc(ctx_in, 16)
            ve_m.wait(sp, "gain")
            for i in range(2):
                sp.dma_start(rows[:, i * S:(i + 1) * S], gain[:]).then_inc(rows_out, 16)
            sp.wait_ge(rows_out, 32)
            for b in range(B):
                for j in range(TT):
                    src = bass.AP(tensor=rows.tensor, offset=b * 2 * S + S - j * P - (P - 1), ap=[[1, P], [1, S]])
                    sp.dma_start(circulant[:, b, j, :], src).then_inc(circulant_in, 16)
            with sp.Fori(0, B) as b:
                sp.wait_ge(ctx_used, b + 1 + B)
                sp.dma_start(ctxT[:], dram["ctxT_back"][b].rearrange("(c p) s -> p c s", p=P)).then_inc(ctx_in, 16)

        @block.gpsimd
        def _(pool):
            with pool.Fori(0, B) as b:
                norm.pool(pool, b)

        @block.scalar
        def _(act):
            with act.Fori(0, B) as b:
                for r in range(TT):
                    pe_a.wait(act, f"hat{r}", b)
                    act_a.done(nc.scalar.activation(qhat[:, r, :], core.ps[:, r, 0:D], ACT.Copy), f"qhat{r}")
            ve_m.wait(act, "shift")
            nc.scalar.activation(gain[:], mean[:], ACT.Exp, bias=shift[:, 0:1]).then_inc(exp_done, 1)

        @block.tensor
        def _(pe):
            ps = core.ps
            pe.sem_inc(ctx_used, 1)
            pe.wait_ge(weights_in, 16 * 6)
            with pe.Fori(0, B) as b:
                pe.wait_ge(xn_ready, b + 1)
                for c in range(DC):
                    for j in range(TT):
                        last = nc.tensor.transpose(ps[:, 4 + c, j * P:(j + 1) * P], xn[:, j, c * P:(c + 1) * P], core.ident[:])
                pe_a.done(last, "xT")
                pe.wait_ge(ctx_in, b * 16 + 16)
                ve_a.wait(pe, "xT", b)
                for i, (src, w, name) in enumerate(((xnT, wq, "q"), (ctxT, wk, "k"))):
                    for j in range(TT):
                        n = i * TT + j
                        if n >= 2:
                            ve_a.wait(pe, f"{'qk'[(n - 2) // TT]}{(n - 2) % TT}", b)
                        for c in range(DC):
                            last = nc.tensor.matmul(ps[:, 6 + n % 2, 0:D], src[:, c, j * P:(j + 1) * P], w[:, c, :],
                                                    start=(c == 0), stop=(c == DC - 1))
                        pe_a.done(last, f"{name}{j}")
                ve_a.wait(pe, f"k{TT - 1}", b)
                pe.sem_inc(ctx_used, 1)
                for r in range(TT):
                    for j in range(TT):
                        last = nc.tensor.matmul(ps[:, r, :], basis[:, j, r * P:(r + 1) * P], qk[:, j, :, :],
                                                start=(j == 0), stop=(j == TT - 1))
                    pe_a.done(last, f"hat{r}")
                ve_a.wait(pe, f"power{TT - 1}", b)
            ve_m.wait(pe, "power")
            for r in range(TT):
                last = nc.tensor.matmul(ps[0:B, 0, :], power_b[:, r, :], inverse[:, r, :], start=(r == 0), stop=(r == TT - 1))
            one.done(last, "mean")
            pe.wait_ge(circulant_in, 16 * B * TT)
            with pe.Fori(0, B) as b:
                pe.wait_ge(ctx_in, b * 16 + 16 + B * 16)
                for j in range(TT):
                    if j >= 2:
                        ve_b.wait(pe, f"v{j - 2}", b)
                    for c in range(DC):
                        last = nc.tensor.matmul(ps[:, 6 + j % 2, 0:D], ctxT[:, c, j * P:(j + 1) * P], wv[:, c, :],
                                                start=(c == 0), stop=(c == DC - 1))
                    pe_b.done(last, f"v{j}")
                ve_b.wait(pe, f"v{TT - 1}", b)
                pe.sem_inc(ctx_used, 1)
                for c in range(DC):
                    for j in range(TT):
                        last = nc.tensor.matmul(ps[:, 4 + c, :], v[:, j, c * P:(c + 1) * P], circulant[:, b, j, :],
                                                start=(j == 0), stop=(j == TT - 1))
                    pe_b.done(last, f"agg{c}")
                ve_b.wait(pe, f"agg{DC - 1}", b)
                for j in range(TT):
                    for c in range(DC):
                        last = nc.tensor.matmul(ps[:, j, 0:D], aggT[:, c, j * P:(j + 1) * P], wo[:, c, :],
                                                start=(c == 0), stop=(c == DC - 1))
                    pe_b.done(last, f"out{j}")
                ve_b.wait(pe, f"out{TT - 1}", b)

        @block.vector
        def _(dve):
            ps, V = core.ps, nc.vector
            dve.wait_ge(bias_in, 16 * 4)
            with dve.Fori(0, B) as b:
                norm.vector(dve, b, lambda j: core.x[:, b * TT + j, :], lambda j: xn[:, j, :], xn_ready)
                pe_a.wait(dve, "xT", b)
                ve_a.done(V.tensor_copy(xnT[:], ps[:, 4:6, :]), "xT")
                for i, (name, bias) in enumerate((("q", bq), ("k", bk))):
                    for j in range(TT):
                        pe_a.wait(dve, f"{name}{j}", b)
                        ve_a.done(V.tensor_tensor(qk[:, j, i, :], ps[:, 6 + j % 2, 0:D], bias[:], ALU.add), f"{name}{j}")
                for r in range(TT):
                    act_a.wait(dve, f"qhat{r}", b)
                    ve_a.done(V.scalar_tensor_tensor(out=junk[:, r, :], in0=ps[:, r, D:2 * D], scalar=1.0, in1=qhat[:, r, :],
                                                     op0=ALU.mult, op1=ALU.mult, accum_out=power[:, b, r:r + 1]), f"power{r}")
                ve_a.wait(dve, f"power{TT - 1}", b)
            ve_m.done(V.tensor_copy(power_b[:].rearrange("p r b -> p b r"), power[:]), "power")
            one.wait(dve, "mean")
            link = Chain(dve, order)
            link(V.tensor_copy(mean[:], ps[0:B, 0, :]))
            link(V.max(eight[:], mean[:]))
            ve_m.done(V.tensor_scalar(shift[:], eight[:, 0:1], -1.0, None, ALU.mult), "shift")
            link(V.match_replace(work[:], eight[:], mean[:], NEG))
            link(V.max(four[:], work[:]))
            link(V.memset(four[:, BEST - 8:8], NEG))
            link(V.match_replace(work[:], four[:], work[:], NEG))
            link(V.tensor_tensor(chosen[:], work[:], mean[:], ALU.not_equal))
            dve.wait_ge(exp_done, 1)
            link(V.tensor_tensor(gain[:], gain[:], chosen[:], ALU.mult))
            link(V.tensor_reduce(total[:], gain[:], AX, ALU.add))
            link(V.reciprocal(inv[:], total[:]))
            ve_m.done(V.tensor_scalar(gain[:], gain[:], inv[:, 0:1], None, ALU.mult), "gain")
            with dve.Fori(0, B) as b:
                for j in range(TT):
                    pe_b.wait(dve, f"v{j}", b)
                    ve_b.done(V.tensor_tensor(v[:, j, :], ps[:, 6 + j % 2, 0:D], bv[:], ALU.add), f"v{j}")
                for c in range(DC):
                    pe_b.wait(dve, f"agg{c}", b)
                    ve_b.done(V.tensor_copy(aggT[:, c, :], ps[:, 4 + c, :]), f"agg{c}")
                for j in range(TT):
                    pe_b.wait(dve, f"out{j}", b)
                    ve_b.done(V.tensor_tensor(part[:, j, :], ps[:, j, 0:D], bo[:], ALU.add), f"out{j}")
                ve_b.wait(dve, f"out{TT - 1}", b)
                rows_now = core.x[:, bass.ds(b * TT, TT), :]
                V.tensor_tensor(rows_now, rows_now, part[:], ALU.add).then_inc(summed, 1)
                dve.wait_ge(summed, b + 1)


class Router:

    def __init__(self, st, name, keep_turned):
        self.st, self.nc, self.core, self.w_name, self.keep_turned = st, st.nc, st.core, name, keep_turned
        self.norm = Norm(st)
        self.xn = st.sb("xn", [P, TT, D])
        self.xnT = st.sb("xnT", [P, DC, S])
        if keep_turned:
            self.xT = st.sb("xT", [P, B, DC, S])
        self.kept_rows = st.sb("kept_rows", [P, B * TT, D])
        self.w = st.sb("w_router", [P, DC, 8])
        self.logits = st.sb("logits", [P, B * TT, 8])
        self.probs = st.sb("probs", [P, B * TT, 16])
        self.marked = st.sb("marked", [P, B * TT, 16])
        self.best = st.sb("best", [P, B * TT, 8])
        self.chosen = st.sb("chosen", [P, B * TT, 8])
        self.top, self.total, self.inv = (st.sb(n, [P, B * TT]) for n in ("top", "total", "inv"))
        self.w_in, self.xn_ready, self.order = st.sem("router_in"), st.sem("xn_ready"), st.sem("router_order")
        self.pe = Steps(st.sem("pe_router_steps"), ["xT", "logits"])
        self.ve = Steps(st.sem("vector_router_steps"), ["xT", "logits"])
        self.kept = st.sem("kept")
        self.centred, self.exp_done = st.sem("centred"), st.sem("exp_done")

    def sync(self, sp):
        sp.dma_start(self.w[:], self.core.dram[self.w_name].rearrange("(c p) n -> p c n", p=P)).then_inc(self.w_in, 16)

    def pool(self, pool):
        with pool.Fori(0, B) as b:
            self.norm.pool(pool, b)

    def tensor(self, pe):
        nc, ps = self.nc, self.core.ps
        pe.wait_ge(self.w_in, 16)
        with pe.Fori(0, B) as b:
            pe.wait_ge(self.xn_ready, b + 1)
            for c in range(DC):
                for j in range(TT):
                    last = nc.tensor.transpose(ps[:, c, j * P:(j + 1) * P], self.xn[:, j, c * P:(c + 1) * P], self.core.ident[:])
            self.pe.done(last, "xT")
            self.ve.wait(pe, "xT", b)
            for j in range(TT):
                for c in range(DC):
                    last = nc.tensor.matmul(ps[:, 2, j * 8:(j + 1) * 8], self.xnT[:, c, j * P:(j + 1) * P], self.w[:, c, :],
                                            start=(c == 0), stop=(c == DC - 1))
            self.pe.done(last, "logits")
            self.ve.wait(pe, "logits", b)

    def scalar(self, act):
        nc = self.nc
        with act.Fori(0, B) as b:
            act.wait_ge(self.xn_ready, b + 1)
            rows = nc.scalar.activation(self.kept_rows[:, bass.ds(b * TT, TT), :], self.xn[:], ACT.Copy)
            if self.keep_turned:
                self.ve.wait(act, "xT", b)
                rows = nc.scalar.activation(self.xT[:, b, :, :], self.xnT[:], ACT.Copy)
            rows.then_inc(self.kept, 1)
        act.wait_ge(self.centred, 1)
        nc.scalar.activation(self.logits[:], self.logits[:], ACT.Exp).then_inc(self.exp_done, 1)

    def vector(self, dve):
        V, ps = self.nc.vector, self.core.ps

        def norm(b):
            self.norm.vector(dve, b, lambda j: self.core.x[:, b * TT + j, :], lambda j: self.xn[:, j, :], self.xn_ready)

        def batch(b, last):
            self.pe.wait(dve, "xT", b)
            dve.wait_ge(self.xn_ready, b + 1)
            self.ve.done(V.tensor_copy(self.xnT[:], ps[:, 0:2, :]), "xT")
            dve.wait_ge(self.kept, b + 1)
            if not last:
                norm(b + 1)
            self.pe.wait(dve, "logits", b)
            self.ve.done(V.tensor_copy(self.logits[:, bass.ds(b * TT, TT), :],
                                       ps[:, 2, 0:TT * 8].rearrange("p (j e) -> p j e", e=8)), "logits")

        norm(0)
        with dve.Fori(0, B - 1) as b:
            batch(b, last=False)
        batch(B - 1, last=True)
        self.ve.wait(dve, "logits", B - 1)
        link = Chain(dve, self.order)
        shape = [P, B * TT, 8]
        link(V.tensor_reduce(self.top[:], self.logits[:], AX, ALU.max))
        V.tensor_tensor(self.logits[:], self.logits[:], self.top[:].unsqueeze(2).to_broadcast(shape), ALU.subtract
                        ).then_inc(self.centred, 1)
        dve.wait_ge(self.exp_done, 1)
        link(V.tensor_reduce(self.total[:], self.logits[:], AX, ALU.add))
        link(V.reciprocal(self.inv[:], self.total[:]))
        link(V.memset(self.probs[:, :, 8:16], -1.0))
        link(V.tensor_tensor(self.probs[:, :, 0:8], self.logits[:], self.inv[:].unsqueeze(2).to_broadcast(shape), ALU.mult))
        for t in range(B * TT):
            last = V.max(self.best[:, t, :], self.probs[:, t, :])
        link(last)
        link(V.tensor_tensor(self.total[:], self.best[:, :, 0], self.best[:, :, 1], ALU.add))
        link(V.memset(self.best[:, :, 2:8], -1.0))
        for t in range(B * TT):
            last = V.match_replace(self.marked[:, t, :], self.best[:, t, :], self.probs[:, t, :], 2.0)
        link(last)
        link(V.tensor_tensor(self.chosen[:], self.marked[:, :, 0:8], self.probs[:, :, 0:8], ALU.not_equal))
        return link


class Slots:

    E = 8
    T = B * TT
    N = 2 * P
    K = (2 * T * P + E * (N - 1)) // N
    W = D + 2
    LOOPED = (K - 2) // 2

    def __init__(self, st, router, scaled):
        T, E, K, W, N = self.T, self.E, self.K, self.W, self.N
        U32 = mybir.dt.uint32
        self.nc, self.core, self.router, self.scaled, self.dram = st.nc, st.core, router, scaled, st.core.dram
        self.earlier, self.ones = st.sb("earlier", [P, P]), st.sb("ones", [P, P])
        self.numbers = st.sb("numbers", [P, T, 2])
        self.starts = st.sb("starts", [P, E])
        self.block_no = st.sb("block_no", [P, K])
        self.spare_no = st.sb("spare_no", [P, 2 * K])
        self.blank = st.sb("blank", [P, 2 * K, W])
        self.y_in = self.blank[:, 0:2 * T, 0:D].rearrange("p (c t) d -> p c t d", c=2)
        self.slot, self.is_second = (st.sb(n, [P, T, E]) for n in ("slot", "is_second"))
        self.sums = st.sb("sums", [P, 2, T, E])
        self.filled = st.sb("filled", [P, E, E])
        self.blocks, self.ends, self.counts = st.sb("blocks", [P, E]), st.sb("ends", [P, 2, E]), st.sb("counts", [P, E])
        self.ended = st.sb("ended", [P, K, E])
        self.expert, self.expert_no = st.sb("expert", [P, K]), st.sb("expert_no", [P, K], I32)
        self.slots, self.slot_no = st.sb("slots", [P, T, 2]), st.sb("slot_no", [P, T, 2], U32)
        self.slot_sum = st.sb("slot_sum", [P, T])
        self.weight = st.sb("weight", [P, T, 2])
        self.out_rows = st.sb("out_rows", [P, T, 2, W])
        self.xs = st.sb("xs", [P, 2, 2, W])
        if not scaled:
            self.xT = st.sb("xT_block", [P, 2, DC, N])
        self.y = st.sb("y", [P, 2, 2, D])
        self.numbers_of, self.weight_of = st.sb("numbers_of", [P, K, 2]), st.sb("weight_of", [P, 2, 2])
        self.row_no = st.sb("row_no", [P, 2, 2], U32)
        self.const_in, self.cleared, self.blank_ready = st.sem("const_in"), st.sem("cleared"), st.sem("blank_ready")
        self.placed, self.ranks_full, self.experts_known = st.sem("placed"), st.sem("ranks_full"), st.sem("experts_known")
        self.rows_ready, self.scattered = st.sem("rows_ready"), st.sem("scattered")
        self.xs_in = [st.sem(f"xs_in{i}") for i in range(2)]
        self.turned, self.xT_ready = st.sem("turned"), st.sem("xT_ready")
        self.y_ready, self.row_no_ready = st.sem("y_ready"), st.sem("row_no_ready")
        self.y_out = [st.sem(f"y_out{i}") for i in range(2)]
        self.y_back = [st.sem(f"y_back{b}") for b in range(B)]
        self.added = st.sem("added")


    def sync_constants(self, sp):
        dram = self.dram
        for dst, name in ((self.earlier, "earlier"), (self.numbers, "choice_numbers"), (self.spare_no, "spare_numbers")):
            sp.dma_start(dst[:], dram[name]).then_inc(self.const_in, 16)
        sp.dma_start(self.starts[:], dram["block_starts"].to_broadcast([P, self.E])).then_inc(self.const_in, 16)
        sp.dma_start(self.block_no[:], dram["block_numbers"].to_broadcast([P, self.K])).then_inc(self.const_in, 16)
        sp.wait_ge(self.blank_ready, 2)
        sp.dma_start(dram["xs_rows"].rearrange("(k p) d -> p k d", p=P), self.blank[:]).then_inc(self.cleared, 16)

    def sync_expert(self, sp, k):
        return sp.value_load(self.expert_no[0:1, bass.ds(k, 1)], min_val=0, max_val=self.E - 1)

    def sync_tokens(self, sp, r, i):
        sp.dma_start(self.xs[:, i, :, :],
                     self.dram["xs_rows"][bass.ds((r * 2 + i) * self.N, self.N), :].rearrange("(j p) d -> p j d", p=P)
                     ).then_inc(self.xs_in[i], 16)

    def sync_blocks(self, sp, first, second):
        K = self.K

        def second_of(r, i):
            second(self.sync_expert(sp, r * 2 + i), r, i)

        def step(r, i, left=3):
            first(self.sync_expert(sp, r * 2 + i), r, i)
            if left > 1:
                sp.wait_ge(self.xT_ready, r * 2 + i)
                self.sync_tokens(sp, r + i, 1 - i)
            second_of(r - 1 + i, 1 - i)

        sp.wait_ge(self.experts_known, 1)
        first(self.sync_expert(sp, 0), 0, 0)
        second_of(0, 0)
        first(self.sync_expert(sp, 1), 0, 1)
        sp.wait_ge(self.scattered, 2 * self.T * 16)
        for i in range(2):
            self.sync_tokens(sp, 0, i)
        sp.wait_ge(self.xT_ready, 1)
        self.sync_tokens(sp, 1, 0)
        with sp.Fori(1, (K - 1) // 2) as r:
            for i in range(2):
                step(r, i)
        for k in range((K - 1) // 2 * 2, K):
            step(k // 2, k % 2, left=K - k)
        second_of((K - 1) // 2, (K - 1) % 2)

    def sync_collect(self, sp):
        for i in range(2):
            sp.wait_ge(self.y_out[i], 32 * ((self.K + 1 - i) // 2))
        for b in range(B):
            for c in range(2):
                at = (c * B + b) * S
                sp.dma_start(self.y_in[:, c, b * TT:(b + 1) * TT, :],
                             self.dram["y_rows"][at:at + S, :].rearrange("(j p) d -> p j d", p=P)).then_inc(self.y_back[b], 16)


    def pool_blank(self, pool):
        nc = self.nc
        nc.gpsimd.memset(self.ones[:], 1.0)
        nc.gpsimd.memset(self.blank[:], 0.0).then_inc(self.blank_ready, 1)
        pool.wait_ge(self.blank_ready, 1)
        pool.wait_ge(self.const_in, 80)
        nc.gpsimd.tensor_copy(self.blank[:, :, D], self.spare_no[:]).then_inc(self.blank_ready, 1)

    def pool_send(self, pool):
        pool.wait_ge(self.cleared, 16)
        for t in range(self.T):
            pool.wait_ge(self.rows_ready, t + 1)
            for c in range(2):
                self.nc.gpsimd.indirect_dma_start(
                    self.dram["xs_rows"], bass.IndirectOffsetOnAxis(ap=self.slot_no[:, t, c:c + 1], axis=0),
                    self.out_rows[:, t, c, :], None).then_inc(self.scattered, 16)

    def pool_return(self, pool, r, i):
        k = r * 2 + i
        pool.wait_ge(self.y_ready, k + 1 + 2)
        self.nc.gpsimd.tensor_copy(self.row_no[:, i, :], self.numbers_of[:, bass.ds(k, 1), :].rearrange("p o j -> p (o j)")
                                   ).then_inc(self.row_no_ready, 1)
        pool.wait_ge(self.row_no_ready, k + 1)
        pool.nop(nofuse=True)
        for c in range(2):
            self.nc.gpsimd.indirect_dma_start(
                self.dram["y_rows"], bass.IndirectOffsetOnAxis(ap=self.row_no[:, i, c:c + 1], axis=0),
                self.y[:, i, c, :], None).then_inc(self.y_out[i], 16)

    def pool_return_all(self, pool):
        with pool.Fori(0, self.K // 2) as r:
            for i in range(2):
                self.pool_return(pool, r, i)
        for k in range(self.K // 2 * 2, self.K):
            self.pool_return(pool, k // 2, k % 2)


    def tensor_ranks(self, pe):
        nc, ps, TE = self.nc, self.core.ps, self.T * self.E
        pe.wait_ge(self.const_in, 80)
        pe.wait_ge(self.placed, 1)
        nc.tensor.matmul(ps[:, 3, 0:TE], self.earlier[:], self.router.chosen[:].rearrange("p t e -> p (t e)"),
                         start=True, stop=False)
        nc.tensor.matmul(ps[:, 3, 0:TE], self.ones[:], self.sums[:, 1].rearrange("p t e -> p (t e)"), start=False, stop=True)
        nc.tensor.matmul(ps[:, 4, 0:self.E], self.ones[:], self.sums[:, 0, self.T - 1, :], start=True, stop=True
                         ).then_inc(self.ranks_full, 1)

    def tensor_turn(self, pe, r, i):
        pe.wait_ge(self.xs_in[i], (r + 1) * 16)
        for c in range(DC):
            for j in range(2):
                last = self.nc.tensor.transpose(self.core.ps[:, 6 + i, (c * 2 + j) * P:(c * 2 + j + 1) * P],
                                                self.xs[:, i, j, c * P:(c + 1) * P], self.core.ident[:])
        last.then_inc(self.turned, 1)

    def tensor_blocks(self, pe, up, down):
        K, turn = self.K, self.tensor_turn
        turn(pe, 0, 0)
        up(0, 0)
        turn(pe, 0, 1)
        with pe.Fori(0, self.LOOPED) as r:
            for i in range(2):
                up(r + i, 1 - i)
                turn(pe, r + 1, i)
                down(r, i)
        for k in range(2 * self.LOOPED, K):
            if k + 1 < K:
                up((k + 1) // 2, (k + 1) % 2)
            if k + 2 < K:
                turn(pe, (k + 2) // 2, k % 2)
            down(k // 2, k % 2)


    def scalar_blocks(self, act, gate, out, take=lambda r, i: None):
        K = self.K
        take(0, 0)
        gate(0, 0)
        take(0, 1)
        for i in range(2):
            gate(i, 1 - i)
            take(1, i)
            out(0, i, wait=False)
        with act.Fori(1, self.LOOPED) as r:
            for i in range(2):
                gate(r + i, 1 - i)
                take(r + 1, i)
                out(r, i, wait=True)
        for k in range(2 * self.LOOPED, K):
            if k + 1 < K:
                gate((k + 1) // 2, (k + 1) % 2)
            if k + 2 < K:
                take((k + 2) // 2, k % 2)
            out(k // 2, k % 2, wait=True)


    def vector_places(self, dve, link, score):
        V, ps, T, E, K, N = self.nc.vector, self.core.ps, self.T, self.E, self.K, self.N
        sums, ends, counts, blocks, slot, slots, is_second = (
            self.sums, self.ends, self.counts, self.blocks, self.slot, self.slots, self.is_second)
        chosen = self.router.chosen[:]
        per_choice = [P, T, E]
        link(V.tensor_copy(sums[:, 0], chosen))
        n, at = 1, 0
        while n < T:
            V.tensor_copy(sums[:, 1 - at, 0:n, :], sums[:, at, 0:n, :])
            link(V.tensor_tensor(sums[:, 1 - at, n:T, :], sums[:, at, n:T, :], sums[:, at, 0:T - n, :], ALU.add))
            n, at = 2 * n, 1 - at
        assert at == 0
        V.tensor_tensor(sums[:, 1], sums[:, 0], chosen, ALU.subtract).then_inc(self.placed, 1)
        dve.wait_ge(self.const_in, 80)
        dve.wait_ge(self.ranks_full, 1)
        link(V.tensor_copy(counts[:], ps[:, 4, 0:E]))
        link(V.tensor_tensor(self.filled[:], counts[:].unsqueeze(2).to_broadcast([P, E, E]),
                             self.starts[:].unsqueeze(1).to_broadcast([P, E, E]), ALU.is_gt))
        link(V.tensor_reduce(blocks[:], self.filled[:], AX, ALU.add))
        link(V.tensor_copy(ends[:, 0, :], blocks[:]))
        n, at = 1, 0
        while n < E:
            V.tensor_copy(ends[:, 1 - at, 0:n], ends[:, at, 0:n])
            link(V.tensor_tensor(ends[:, 1 - at, n:E], ends[:, at, n:E], ends[:, at, 0:E - n], ALU.add))
            n, at = 2 * n, 1 - at
        V.tensor_tensor(self.ended[:], self.block_no[:].unsqueeze(2).to_broadcast([P, K, E]),
                        ends[:, at, :].unsqueeze(1).to_broadcast([P, K, E]), ALU.is_ge)
        link(V.tensor_tensor(counts[:], ends[:, at, :], blocks[:], ALU.subtract))
        V.tensor_reduce(self.expert[:], self.ended[:], AX, ALU.add)
        link(V.tensor_scalar(counts[:], counts[:], float(N), 1.0, ALU.mult, ALU.add))
        V.tensor_scalar(self.expert_no[:], self.expert[:], float(E - 1), None, ALU.min).then_inc(self.experts_known, 1)
        link(V.tensor_tensor(slot[:], ps[:, 3, 0:T * E].rearrange("p (t e) -> p t e", e=E),
                             counts[:].unsqueeze(1).to_broadcast(per_choice), ALU.add))
        link(V.tensor_tensor(slot[:], slot[:], chosen, ALU.mult))
        V.tensor_reduce(slots[:, :, 1], slot[:], AX, ALU.max)
        link(V.tensor_reduce(self.slot_sum[:], slot[:], AX, ALU.add))
        link(V.tensor_tensor(slots[:, :, 0], self.slot_sum[:], slots[:, :, 1], ALU.subtract))
        V.tensor_scalar(self.slot_no[:], slots[:], -1.0, None, ALU.add)
        link(V.tensor_tensor(is_second[:], slot[:], slots[:, :, 1:2].to_broadcast(per_choice), ALU.is_equal))
        link(V.tensor_tensor(is_second[:], is_second[:], score, ALU.mult))
        V.tensor_reduce(self.weight[:, :, 1], is_second[:], AX, ALU.add)
        link(V.tensor_tensor(slot[:], score, is_second[:], ALU.subtract))
        V.tensor_copy(self.out_rows[:, :, :, D], self.numbers[:])
        link(V.tensor_reduce(self.weight[:, :, 0], slot[:], AX, ALU.add))
        V.tensor_copy(self.out_rows[:, :, :, D + 1], self.weight[:])
        for t in range(T):
            for c in range(2):
                weight = self.weight[:, t, c:c + 1] if self.scaled else 1.0
                last = V.tensor_scalar(self.out_rows[:, t, c, 0:D], self.router.kept_rows[:, t, :], weight, None, ALU.mult)
            last.then_inc(self.rows_ready, 1)

    def vector_take(self, dve, r, i, tokens):
        V, k, xs = self.nc.vector, r * 2 + i, self.xs
        dve.wait_ge(self.turned, k + 1)
        V.tensor_copy(self.numbers_of[:, bass.ds(k, 1), :], xs[:, i, :, D:D + 1].rearrange("p j o -> p o j"))
        if not self.scaled:
            dve.wait_ge(self.y_ready, k + 1)
            V.tensor_copy(self.weight_of[:, i, :], xs[:, i, :, D + 1])
        tokens(r, i).then_inc(self.xT_ready, 1)

    def vector_blocks(self, dve, product, tokens):
        K, take = self.K, lambda dve, r, i: self.vector_take(dve, r, i, tokens)
        take(dve, 0, 0)
        product(0, 0)
        take(dve, 0, 1)
        with dve.Fori(0, self.LOOPED) as r:
            for i in range(2):
                product(r + i, 1 - i)
                take(dve, r + 1, i)
        for k in range(2 * self.LOOPED, K - 1):
            product((k + 1) // 2, (k + 1) % 2)
            if k + 2 < K:
                take(dve, (k + 2) // 2, k % 2)

    def vector_collect(self, dve):
        for b in range(B):
            dve.wait_ge(self.y_back[b], 32)
            for c in range(2):
                rows = self.core.x[:, b * TT:(b + 1) * TT, :]
                self.nc.vector.tensor_tensor(rows, rows, self.y_in[:, c, b * TT:(b + 1) * TT, :], ALU.add
                                             ).then_inc(self.added, 1)
                dve.wait_ge(self.added, 2 * b + c + 1)


def relu_experts_stage(core):
    nc, dram = core.nc, core.dram
    FT = 2
    UNITS = 2 * B
    with Stage(core, "l2f") as st:
        router = Router(st, "l2f_router", keep_turned=True)
        slots = Slots(st, router, scaled=False)
        K, N = slots.K, slots.N
        ws1, ws2 = st.sb("ws1", [P, 2, DC, FT * P]), st.sb("ws2", [P, 2, FT, D])
        w1, w2 = st.sb("w1", [P, 2, DC, FT * P]), st.sb("w2", [P, 2, FT, D])
        relu, hT = st.sb("relu_shared", [P, 2, FT, S]), st.sb("hT_shared", [P, 2, FT, S])
        relu_b, hT_b = st.sb("relu", [P, 2, FT, N]), st.sb("hT", [P, 2, FT, N])
        shared_in = st.sem("shared_in")
        shared_up, shared_relu, shared_hidden = st.sem("shared_up"), st.sem("shared_relu"), st.sem("shared_hidden")
        shared_down, shared_done = st.sem("shared_down"), st.sem("shared_done")
        w1_in, w2_in = [st.sem(f"w1_in{i}") for i in range(2)], [st.sem(f"w2_in{i}") for i in range(2)]
        up_full, relu_ready, hidden_ready, down_full = (
            st.sem(n) for n in ("up_full", "relu_ready", "hidden_ready", "down_full"))
        block = st.block()

        @block.sync
        def _(sp):
            router.sync(sp)
            slots.sync_constants(sp)
            sp.dma_start(ws1[:], dram["l2f_ws1"].rearrange("i (c p) f -> p i c f", p=P)).then_inc(shared_in, 16)
            sp.dma_start(ws2[:], dram["l2f_ws2"].rearrange("i (c p) f -> p i c f", p=P)).then_inc(shared_in, 16)

            def first(e, r, i):
                if not (isinstance(r, int) and r == 0):
                    sp.wait_ge(up_full, r * 2 + i - 1)
                sp.dma_start(w1[:, i, :, :], dram["l2f_w1"][e].rearrange("(c p) f -> p c f", p=P)).then_inc(w1_in[i], 16)

            def second(e, r, i):
                sp.wait_ge(down_full, r * 2 + i + 1)
                sp.dma_start(w2[:, i, :, :], dram["l2f_w2"][e].rearrange("(c p) f -> p c f", p=P)).then_inc(w2_in[i], 16)

            slots.sync_blocks(sp, first, second)
            slots.sync_collect(sp)

        @block.gpsimd
        def _(pool):
            slots.pool_blank(pool)
            router.pool(pool)
            slots.pool_send(pool)
            slots.pool_return_all(pool)

        @block.tensor
        def _(pe):
            ps = core.ps
            pe.sem_inc(down_full, 2)
            router.tensor(pe)
            slots.tensor_ranks(pe)
            pe.wait_ge(shared_in, 32)

            def shared_first(u):
                i, b = divmod(u, B)
                for f in range(FT):
                    n = u * FT + f
                    if n >= 2:
                        pe.wait_ge(shared_relu, n - 1)
                    for c in range(DC):
                        last = nc.tensor.matmul(ps[:, n % 2, :], ws1[:, i, c, f * P:(f + 1) * P], router.xT[:, b, c, :],
                                                start=(c == 0), stop=(c == DC - 1))
                    last.then_inc(shared_up, 1)

            def shared_second(u):
                i, b = divmod(u, B)
                pe.wait_ge(shared_hidden, (u + 1) * FT)
                for j in range(TT):
                    if u:
                        pe.wait_ge(shared_done, (u - 1) * TT + j + 1)
                    for f in range(FT):
                        last = nc.tensor.matmul(ps[:, 4 + j, 0:D], hT[:, u % 2, f, j * P:(j + 1) * P], ws2[:, i, f, :],
                                                start=(f == 0), stop=(f == FT - 1))
                    last.then_inc(shared_down, 1)

            shared_first(0)
            pe.wait_ge(slots.experts_known, 1)
            for u in range(UNITS):
                if u + 1 < UNITS:
                    shared_first(u + 1)
                shared_second(u)
            pe.wait_ge(shared_done, UNITS * TT)

            def up(r, i):
                k = r * 2 + i
                pe.wait_ge(w1_in[i], (r + 1) * 16)
                pe.wait_ge(slots.xT_ready, k + 1)
                pe.wait_ge(relu_ready, k + 1)
                for f in range(FT):
                    for c in range(DC):
                        last = nc.tensor.matmul(ps[:, i, f * N:(f + 1) * N], w1[:, i, c, f * P:(f + 1) * P],
                                                slots.xT[:, i, c, :], start=(c == 0), stop=(c == DC - 1))
                last.then_inc(up_full, 1)

            def down(r, i):
                k = r * 2 + i
                pe.wait_ge(w2_in[i], (r + 1) * 16)
                pe.wait_ge(hidden_ready, k + 1 + 2)
                pe.wait_ge(slots.y_ready, k + 1)
                for j in range(2):
                    for f in range(FT):
                        last = nc.tensor.matmul(ps[:, 4 + i, j * D:(j + 1) * D], hT_b[:, i, f, j * P:(j + 1) * P],
                                                w2[:, i, f, :], start=(f == 0), stop=(f == FT - 1))
                last.then_inc(down_full, 1)

            slots.tensor_blocks(pe, up, down)

        @block.scalar
        def _(act):
            act.sem_inc(slots.y_ready, 2)
            act.sem_inc(relu_ready, 2)
            router.scalar(act)
            for u in range(UNITS):
                for f in range(FT):
                    n = u * FT + f
                    act.wait_ge(shared_up, n + 1)
                    if u >= 2:
                        act.wait_ge(shared_hidden, n - 3)
                    nc.scalar.activation(relu[:, u % 2, f, :], core.ps[:, n % 2, :], ACT.Relu).then_inc(shared_relu, 1)

            def gate(r, i):
                k = r * 2 + i
                act.wait_ge(up_full, k + 1)
                act.wait_ge(hidden_ready, k + 1)
                nc.scalar.activation(relu_b[:, i, :, :], core.ps[:, i, :].rearrange("p (f n) -> p f n", f=FT), ACT.Relu
                                     ).then_inc(relu_ready, 1)

            def out(r, i, wait):
                act.wait_ge(down_full, r * 2 + i + 1 + 2)
                if wait:
                    act.wait_ge(slots.y_out[i], r * 32)
                for j in range(2):
                    last = nc.scalar.activation(slots.y[:, i, j, :], core.ps[:, 4 + i, j * D:(j + 1) * D], ACT.Copy,
                                                scale=slots.weight_of[:, i, j:j + 1])
                last.then_inc(slots.y_ready, 1)

            slots.scalar_blocks(act, gate, out)

        @block.vector
        def _(dve):
            ps, V = core.ps, nc.vector
            dve.sem_inc(hidden_ready, 2)
            link = router.vector(dve)
            link(V.reciprocal(router.inv[:], router.total[:]))
            link(V.tensor_tensor(router.logits[:], router.chosen[:], router.probs[:, :, 0:8], ALU.mult))
            link(V.tensor_tensor(router.logits[:], router.logits[:],
                                 router.inv[:].unsqueeze(2).to_broadcast([P, B * TT, 8]), ALU.mult))
            slots.vector_places(dve, link, router.logits[:])

            def square(u):
                for f in range(FT):
                    n = u * FT + f
                    dve.wait_ge(shared_relu, n + 1)
                    if u >= 2:
                        dve.wait_ge(shared_down, (u - 1) * TT)
                    V.tensor_tensor(hT[:, u % 2, f, :], relu[:, u % 2, f, :], relu[:, u % 2, f, :], ALU.mult
                                    ).then_inc(shared_hidden, 1)

            def add(u):
                b = u % B
                for j in range(TT):
                    rows = core.x[:, b * TT + j, :]
                    dve.wait_ge(shared_down, u * TT + j + 1)
                    if u >= B:
                        dve.wait_ge(shared_done, (u - B) * TT + j + 1)
                    V.tensor_tensor(rows, rows, ps[:, 4 + j, 0:D], ALU.add).then_inc(shared_done, 1)

            square(0)
            for u in range(UNITS):
                if u + 1 < UNITS:
                    square(u + 1)
                add(u)

            def product(r, i):
                k = r * 2 + i
                dve.wait_ge(relu_ready, k + 1 + 2)
                dve.wait_ge(down_full, k + 1)
                V.tensor_tensor(hT_b[:, i, :, :], relu_b[:, i, :, :], relu_b[:, i, :, :], ALU.mult).then_inc(hidden_ready, 1)

            def tokens(r, i):
                return V.tensor_copy(slots.xT[:, i, :, :], ps[:, 6 + i, :].rearrange("p (c n) -> p c n", c=DC))

            slots.vector_blocks(dve, product, tokens)
            slots.vector_collect(dve)


def gated_experts_stage(core, out):
    nc, dram = core.nc, core.dram
    F = 704
    FT = -(-F // P)
    LAST = F - (FT - 1) * P
    COLS = DC * 2 * F
    RING = 3
    with Stage(core, "l3f") as st:
        router = Router(st, "l3f_router", keep_turned=False)
        slots = Slots(st, router, scaled=True)
        K, N = slots.K, slots.N
        w13 = st.sb("w13", [P, 2, 2, COLS], F16)
        w2 = st.sb("w2", [P, 2, 2, FT * D], F16)
        x_hi, x_lo = (st.sb(n, [P, 2, DC, N], F16) for n in ("x_hi", "x_lo"))
        silu = st.sb("silu", [P, RING, N])
        h = st.sb("h", [P, RING, N])
        h_hi, h_lo = (st.sb(n, [P, 2, FT, N], F16) for n in ("h_hi", "h_lo"))
        x_hi_ready = st.sem("x_hi_ready")
        w13_in, w2_in = [st.sem(f"w13_in{i}") for i in range(2)], [st.sem(f"w2_in{i}") for i in range(2)]
        both_full, silu_ready, hidden_ready, h_hi_ready, h_lo_ready, down_full = (
            st.sem(n) for n in ("both_full", "silu_ready", "hidden_ready", "h_hi_ready", "h_lo_ready", "down_full"))
        stored = st.sem("stored")
        block = st.block()

        @block.sync
        def _(sp):
            router.sync(sp)
            slots.sync_constants(sp)

            def gates(e, r, i):
                if not (isinstance(r, int) and r == 0):
                    sp.wait_ge(both_full, (r * 2 + i - 1) * FT)
                sp.dma_start(w13[:, i, :, :], dram["l3f_parts"][e, :, :, 0:COLS]).then_inc(w13_in[i], 16)

            def downs(e, r, i):
                sp.wait_ge(down_full, r * 2 + i + 1)
                sp.dma_start(w2[:, i, :, :], dram["l3f_parts"][e, :, :, COLS:COLS + FT * D]).then_inc(w2_in[i], 16)

            slots.sync_blocks(sp, gates, downs)
            slots.sync_collect(sp)
            for b in range(B):
                sp.wait_ge(slots.added, 2 * b + 2)
                sp.dma_start(out[b].rearrange("(j p) d -> p j d", p=P), core.x[:, b * TT:(b + 1) * TT, :]).then_inc(stored, 16)
            sp.wait_ge(stored, 16 * B)

        @block.gpsimd
        def _(pool):
            slots.pool_blank(pool)
            router.pool(pool)
            slots.pool_send(pool)
            slots.pool_return_all(pool)

        @block.tensor
        def _(pe):
            ps = core.ps
            pe.sem_inc(down_full, 2)
            router.tensor(pe)
            slots.tensor_ranks(pe)

            def up(r, i):
                k = r * 2 + i
                pe.wait_ge(w13_in[i], (r + 1) * 16)
                pe.wait_ge(slots.xT_ready, k + 1)
                for f in range(FT):
                    pe.wait_ge(hidden_ready, k * FT + f + 1)
                    for g in range(2 if f < FT - 1 else 1):
                        at = (2 * f + g) * P
                        passes = [(c, part, x) for c in range(DC) for part, x in ((0, x_hi), (0, x_lo), (1, x_hi))]
                        for n, (c, part, x) in enumerate(passes):
                            last = nc.tensor.matmul(ps[:, f % RING, g * N:(g + 1) * N],
                                                    w13[:, i, part, c * 2 * F + at:c * 2 * F + at + P], x[:, i, c, :],
                                                    start=(n == 0), stop=(n == len(passes) - 1))
                    last.then_inc(both_full, 1)

            def down(r, i):
                k = r * 2 + i
                pe.wait_ge(w2_in[i], (r + 1) * 16)
                pe.wait_ge(h_lo_ready, (k + 1) * FT + RING)
                pe.wait_ge(slots.y_ready, k + 1)
                for j in range(2):
                    passes = [(f, part, hT, P) for f in range(FT - 1) for part, hT in ((0, h_hi), (0, h_lo), (1, h_hi))]
                    passes += [(FT - 1, 0, h_hi, P), (FT - 1, 1, h_hi, LAST)]
                    for n, (f, part, hT, m) in enumerate(passes):
                        last = nc.tensor.matmul(ps[:, 4 + i, j * D:(j + 1) * D], hT[0:m, i, f, j * P:(j + 1) * P],
                                                w2[0:m, i, part, f * D:(f + 1) * D], start=(n == 0), stop=(n == len(passes) - 1))
                last.then_inc(down_full, 1)

            slots.tensor_blocks(pe, up, down)

        @block.scalar
        def _(act):
            ps = core.ps
            act.sem_inc(slots.y_ready, 2)
            router.scalar(act)

            def high_tokens(r, i):
                act.wait_ge(slots.turned, r * 2 + i + 1)
                nc.scalar.activation(x_hi[:, i, :, :], ps[:, 6 + i, :].rearrange("p (c n) -> p c n", c=DC), ACT.Copy
                                     ).then_inc(x_hi_ready, 1)

            def high(k, i, f):
                m = P if f < FT - 1 else LAST
                act.wait_ge(hidden_ready, k * FT + f + 1 + RING)
                nc.scalar.activation(h_hi[0:m, i, f, :], h[0:m, f % RING, :], ACT.Copy).then_inc(h_hi_ready, 1)

            def gate(r, i):
                k = r * 2 + i
                act.wait_ge(down_full, k + 1)
                for f in range(FT):
                    m = P if f < FT - 1 else LAST
                    act.wait_ge(both_full, k * FT + f + 1)
                    act.wait_ge(hidden_ready, k * FT + f + 1)
                    nc.scalar.activation(silu[0:m, f % RING, :], ps[0:m, f % RING, 0:N], ACT.Silu).then_inc(silu_ready, 1)
                    if f:
                        high(k, i, f - 1)
                high(k, i, FT - 1)

            def out(r, i, wait):
                act.wait_ge(down_full, r * 2 + i + 1 + 2)
                if wait:
                    act.wait_ge(slots.y_out[i], r * 32)
                nc.scalar.activation(slots.y[:, i, :, :], ps[:, 4 + i, :], ACT.Copy).then_inc(slots.y_ready, 1)

            slots.scalar_blocks(act, gate, out, high_tokens)

        @block.vector
        def _(dve):
            ps, V = core.ps, nc.vector
            dve.sem_inc(hidden_ready, RING)
            dve.sem_inc(h_lo_ready, RING)
            link = router.vector(dve)
            link(V.tensor_tensor(router.logits[:], router.chosen[:], router.probs[:, :, 0:8], ALU.mult))
            slots.vector_places(dve, link, router.logits[:])

            def low(k, i, f):
                dve.wait_ge(h_hi_ready, k * FT + f + 1)
                if f < FT - 1:
                    V.tensor_tensor(h_lo[:, i, f, :], h[:, f % RING, :], h_hi[:, i, f, :], ALU.subtract).then_inc(h_lo_ready, 1)
                else:
                    V.tensor_tensor(h_hi[LAST:P, i, f, :], h[0:LAST, f % RING, :], h_hi[0:LAST, i, f, :], ALU.subtract
                                    ).then_inc(h_lo_ready, 1)

            def product(r, i):
                k = r * 2 + i
                dve.wait_ge(down_full, k + 1)
                for f in range(FT):
                    dve.wait_ge(silu_ready, k * FT + f + 1)
                    dve.wait_ge(h_lo_ready, k * FT + f + 1)
                    if f < FT - 1:
                        V.tensor_tensor(h[:, f % RING, :], silu[:, f % RING, :], ps[:, f % RING, N:2 * N], ALU.mult
                                        ).then_inc(hidden_ready, 1)
                    else:
                        V.tensor_tensor(h[0:LAST, f % RING, :], silu[0:LAST, f % RING, :], ps[LAST:P, f % RING, 0:N], ALU.mult
                                        ).then_inc(hidden_ready, 1)
                    if f:
                        low(k, i, f - 1)
                low(k, i, FT - 1)

            def low_tokens(r, i):
                dve.wait_ge(x_hi_ready, r * 2 + i + 1)
                return V.tensor_tensor(x_lo[:, i, :, :], ps[:, 6 + i, :].rearrange("p (c n) -> p c n", c=DC),
                                       x_hi[:, i, :, :], ALU.subtract)

            slots.vector_blocks(dve, product, low_tokens)
            slots.vector_collect(dve)


class WeightSplit:

    E, COLS = 8, 4352
    CUTS = 4
    M = COLS // CUTS
    PER = E * CUTS // B

    def __init__(self, st):
        self.nc, self.dram = st.nc, st.core.dram
        self.raw, self.parts = st.sb("raw", [P, 2, self.M]), st.sb("raw_parts", [P, 2, 2, self.M], F16)
        self.raw_in = [st.sem(f"raw_in{i}") for i in range(2)]
        self.parts_out = [st.sem(f"parts_out{i}") for i in range(2)]
        self.order = st.sem("split_order")

    def load(self, pool, b, c):
        pool.dma_start(self.raw[:, c % 2, :], self.dram["l3f_weights"][b * (self.E // B) + c // self.CUTS, :,
                                                                       (c % self.CUTS) * self.M:(c % self.CUTS + 1) * self.M]
                       ).then_inc(self.raw_in[c % 2], 16)

    def batch(self, pool, b, first=False, last=False):
        G = self.nc.gpsimd
        link = Chain(pool, self.order, b * self.PER * 2)
        for c in range(self.PER):
            i = c % 2
            if c + 1 < self.PER:
                self.load(pool, b, c + 1)
            elif not last:
                self.load(pool, b + 1, 0)
            raw, hi, lo = self.raw[:, i, :], self.parts[:, i, 0, :], self.parts[:, i, 1, :]
            pool.wait_ge(self.raw_in[i], (b * self.PER + c - i) * 8 + 16)
            if not (first and c < 2):
                pool.wait_ge(self.parts_out[i], (b * self.PER + c - i) * 8)
            pool.nop(nofuse=True)
            link(G.tensor_copy(hi, raw))
            link(G.tensor_tensor(lo, raw, hi, ALU.subtract))
            pool.dma_start(self.dram["l3f_parts"][b * (self.E // B) + c // self.CUTS, :, :,
                                                  (c % self.CUTS) * self.M:(c % self.CUTS + 1) * self.M],
                           self.parts[:, i, :, :]).then_inc(self.parts_out[i], 16)

    def finish(self, pool):
        for i in range(2):
            pool.wait_ge(self.parts_out[i], self.E * self.CUTS * 8)


def parallel_attention_stage(core):
    nc, dram = core.nc, core.dram
    H, HD = 16, 64
    HP = H // 2
    FT = 8
    assert FT == HP == 2 * TT
    UNITS = H * TT
    LAG_T, LAG_C, LAG_O, LAG_R = 2, 3, 5, 7
    RING = 2 * DC + 2 + HP + HP + HP
    with Stage(core, "l3x") as st:
        norm1, norm2, normc = Norm(st), Norm(st, "_again"), Norm(st, "_ctx")
        wq, w1, wout, w2 = (st.sb(n, [P, 2, cols], F16) for n, cols in
                            (("wq", DC * H * HD), ("w1", DC * 2 * FT * P), ("wout", HP * D), ("w2", FT * D)))
        wk, wv = st.sb("wk", [P, DC, P]), st.sb("wv", [P, DC, HD])
        split = WeightSplit(st)
        gains = st.sb("gains", [P, 4, DC])
        xn = st.sb("xn", [P, TT, D])
        xn2 = st.sb("xn2", [P, TT, D])
        xnT, cnT = st.sb("xnT", [P, DC, S]), st.sb("cnT", [P, DC, S])
        x_hi, x_lo = st.sb("x_hi", [P, DC, S], F16), st.sb("x_lo", [P, DC, S], F16)
        ctx, mask = st.sb("ctx", [P, TT, D]), st.sb("mask", [P, TT, S])
        k_hi, k_lo = st.sb("k_hi", [P, S], F16), st.sb("k_lo", [P, S], F16)
        v = st.sb("v", [P, TT, HD])
        q2 = st.sb("q2", [P, H, S], F16)
        o_hi, o_lo = st.sb("o_hi", [P, HP, S], F16), st.sb("o_lo", [P, HP, S], F16)
        silu = st.sb("silu", [P, 3, S])
        h_hi, h_lo = st.sb("h_hi", [P, FT, S], F16), st.sb("h_lo", [P, FT, S], F16)
        biased = st.sb("biased", [P, 4, S])
        hidden = biased[:, 0:3, :]
        prob, probT = st.sb("prob", [P, 4, S]), st.sb("probT", [P, 4, S])
        neg_max, total, inv = (st.sb(n, [P, H, TT]) for n in ("neg_max", "total", "inv"))
        o = st.sb("o", [P, TT, H, HD])
        raws = {"wq": (wq, biased[:].rearrange("p a b -> p (a b)")), "w1": (w1, o[:].rearrange("p a b c -> p (a b c)")),
                "wout": (wout, prob[:].rearrange("p a b -> p (a b)")), "w2": (w2, probT[:].rearrange("p a b -> p (a b)"))}
        raw_in = {n: st.sem(f"{n}_in") for n in raws}
        raw_hi, weights_split = st.sem("weights_hi"), st.sem("weights_split")
        x_hi_ready, x_lo_ready = st.sem("x_hi_ready"), st.sem("x_lo_ready")
        h_hi_ready, h_lo_ready, o_hi_ready = st.sem("h_hi_ready"), st.sem("h_lo_ready"), st.sem("o_hi_ready")
        rows_full, rows_added = st.sem("rows_full"), st.sem("rows_added")
        kv_in, small_in, ctx_in, mask_in = (st.sem(n) for n in ("kv_in", "small_in", "ctx_in", "mask_in"))
        batch_done, ctx_used = st.sem("batch_done"), st.sem("ctx_used")
        xn_ready, xn2_ready, cn_ready = st.sem("xn_ready"), st.sem("xn2_ready"), st.sem("cn_ready")
        ring_full, ring_free, hi_ready = st.sem("ring_full"), st.sem("ring_free"), st.sem("hi_ready")
        both_full, silu_ready, hidden_ready = st.sem("both_full"), st.sem("silu_ready"), st.sem("hidden_ready")
        scores_full, biased_ready, exp_done = st.sem("scores_full"), st.sem("biased_ready"), st.sem("exp_done")
        turned, out_done, inv_ready = st.sem("turned"), st.sem("out_done"), st.sem("inv_ready")
        copied = [st.sem("probT_by_act"), st.sem("probT_by_vector")]
        block = st.block()

        @block.sync
        def _(sp):
            def context(b):
                sp.dma_start(ctx[:], dram["ctx"][b].rearrange("(j p) d -> p j d", p=P)).then_inc(ctx_in, 16)

            def masks(b):
                sp.dma_start(mask[:], dram["mask"][b].rearrange("(j p) s -> p j s", p=P)).then_inc(mask_in, 16)

            sp.dma_start(gains[:], dram["l3x_gains"]).then_inc(small_in, 16)
            context(0)
            for dst, name in ((wk, "l3x_wk"), (wv, "l3x_wv")):
                sp.dma_start(dst[:], dram[name].rearrange("(c p) n -> p c n", p=P)).then_inc(kv_in, 16)
            for n, (_, raw) in raws.items():
                source = dram[f"l3x_{n}"].rearrange("(c p) n -> p c n", p=P)
                sp.dma_start(raw.rearrange("p (c n) -> p c n", c=source.shape[1]), source).then_inc(raw_in[n], 16)
            masks(0)
            with sp.Fori(1, B) as b:
                sp.wait_ge(ctx_used, b)
                context(b)
                sp.wait_ge(batch_done, b)
                masks(b)

        @block.gpsimd
        def _(pool):
            def norms(b):
                norm1.pool(pool, b)
                norm2.pool(pool, b)
                normc.pool(pool, b)

            norms(0)
            split.load(pool, 0, 0)
            norms(1)
            split.batch(pool, 0, first=True)
            with pool.Fori(1, B - 1) as b:
                norms(b + 1)
                split.batch(pool, b)
            split.batch(pool, B - 1, last=True)
            split.finish(pool)

        @block.tensor
        def _(pe):
            ps = core.ps
            pe.sem_inc(turned, 4)
            pe.sem_inc(out_done, 4)
            pe.wait_ge(kv_in, 32)

            def three(out, *pairs, begin=True, end=True):
                passes = [(a, b) for (a_hi, a_lo), (b_hi, b_lo) in pairs for a, b in ((a_hi, b_hi), (a_hi, b_lo), (a_lo, b_hi))]
                for n, (a, b) in enumerate(passes):
                    last = nc.tensor.matmul(out, a, b, start=(begin and n == 0), stop=(end and n == len(passes) - 1))
                return last

            def parts_of(hi, lo, f, j):
                return hi[:, f, j * P:(j + 1) * P], lo[:, f, j * P:(j + 1) * P]

            def cut(w, at, size):
                return w[:, 0, at:at + size], w[:, 1, at:at + size]

            def tokens(c):
                return x_hi[:, c, :], x_lo[:, c, :]

            with pe.Fori(0, B) as b:
                ring = [0]

                def claim():
                    n = ring[0]
                    ring[0] += 1
                    pe.wait_ge(ring_free, b * RING + n + 1)
                    return 6 + n % 2

                def emptied():
                    pe.wait_ge(ring_free, b * RING + ring[0] + 2)

                for src, ready in ((xn2, xn2_ready), (ctx, cn_ready)):
                    pe.wait_ge(ready, b + 1)
                    for c in range(DC):
                        transpose_tokens(nc, core, src, claim(), c, ring_full)
                emptied()
                pe.sem_inc(ctx_used, 1)
                bank = claim()
                for c in range(DC):
                    last = nc.tensor.matmul(ps[:, bank, :], wk[:, c, :], cnT[:, c, :], start=(c == 0), stop=(c == DC - 1))
                last.then_inc(ring_full, 1)
                bank = claim()
                for j in range(TT):
                    for c in range(DC):
                        last = nc.tensor.matmul(ps[:, bank, j * HD:(j + 1) * HD], cnT[:, c, j * P:(j + 1) * P], wv[:, c, :],
                                                start=(c == 0), stop=(c == DC - 1))
                last.then_inc(ring_full, 1)
                pe.wait_ge(weights_split, 1)
                pe.wait_ge(x_lo_ready, b + 1)
                pe.wait_ge(rows_added, (b + 1) * TT)
                for f in range(FT):
                    bank = claim()
                    three(ps[:, bank, :], *((cut(wq, c * H * HD + f * P, P), tokens(c)) for c in range(DC))).then_inc(ring_full, 1)
                    if f == 0:
                        pe.wait_ge(weights_split, 4)
                    pe.wait_ge(hidden_ready, b * FT + max(f + 1, 3))
                    for i in range(2):
                        last = three(ps[:, 2 * (f % 3) + i, :],
                                     *((cut(w1, (c * 2 * FT + i * FT + f) * P, P), tokens(c)) for c in range(DC)))
                    last.then_inc(both_full, 1)
                emptied()
                pe.wait_ge(hidden_ready, (b + 1) * FT + 3)

                for u in range(UNITS + LAG_O):
                    if u < UNITS:
                        h, j = divmod(u, TT)
                        pe.wait_ge(biased_ready, b * UNITS + u + 1)
                        for part, k in enumerate((k_hi, k_lo)):
                            last = nc.tensor.matmul(ps[:, u % 2, :], q2[:, h, j * P:(j + 1) * P], k[:],
                                                    start=(part == 0), stop=(part == 1))
                        last.then_inc(scores_full, 1)
                    t = u - LAG_T
                    if 0 <= t < UNITS:
                        pe.wait_ge(exp_done, b * UNITS + t + 1 + 4)
                        pe.wait_ge(copied[t % 2], b * (UNITS // 2) + t // 2 + 1)
                        for s in range(TT):
                            last = nc.tensor.transpose(ps[:, 2 + t % 4, s * P:(s + 1) * P], prob[:, t % 4, s * P:(s + 1) * P],
                                                       core.ident[:])
                        last.then_inc(turned, 1)
                    n = u - LAG_O
                    if n >= 0:
                        h, j = divmod(n, TT)
                        if n % (2 * TT) == 0:
                            bank = claim()
                        pe.wait_ge(copied[n % 2], b * (UNITS // 2) + n // 2 + 1 + 2)
                        at = ((h % 2) * TT + j) * HD
                        for s in range(TT):
                            last = nc.tensor.matmul(ps[:, bank, at:at + HD], probT[:, n % 4, s * P:(s + 1) * P], v[:, s, :],
                                                    start=(s == 0), stop=(s == TT - 1))
                        last.then_inc(out_done, 1)
                pe.wait_ge(h_lo_ready, (b + 1) * FT + 3)
                for j in range(TT):
                    for f in range(FT):
                        three(ps[:, j, 0:D], (parts_of(h_hi, h_lo, f, j), cut(w2, f * D, D)), begin=(f == 0), end=False)
                    if j == 0:
                        emptied()
                    for g in (2 * j, 2 * j + 1):
                        bank = claim()
                        for t in range(TT):
                            last = nc.tensor.transpose(ps[:, bank, t * P:(t + 1) * P], o[:, t, 2 * g:2 * g + 2, :], core.ident[:])
                        last.then_inc(ring_full, 1)
                emptied()
                for j in range(TT):
                    for g in range(HP):
                        last = three(ps[:, j, 0:D], (parts_of(o_hi, o_lo, g, j), cut(wout, g * D, D)), begin=False, end=(g == HP - 1))
                    last.then_inc(rows_full, 1)
                pe.sem_inc(batch_done, 1)
                assert ring[0] == RING

        @block.scalar
        def _(act):
            ps = core.ps
            act.sem_inc(exp_done, 4)
            act.sem_inc(copied[0], 2)
            for n, (w, raw) in raws.items():
                act.wait_ge(raw_in[n], 16)
                nc.scalar.activation(w[:, 0, :], raw, ACT.Copy).then_inc(raw_hi, 1)

            def high(b, f):
                act.wait_ge(hidden_ready, b * FT + f + 1 + 3)
                nc.scalar.activation(h_hi[:, f, :], hidden[:, f % 3, :], ACT.Copy).then_inc(h_hi_ready, 1)

            with act.Fori(0, B) as b:
                act.wait_ge(ring_free, b * RING + DC + 2)
                nc.scalar.activation(x_hi[:], xnT[:], ACT.Copy).then_inc(x_hi_ready, 1)
                act.wait_ge(ring_full, b * (RING - HP) + 2 * DC + 1)
                nc.scalar.activation(k_hi[:], ps[:, 6 + 2 * DC % 2, :], ACT.Copy).then_inc(hi_ready, 1)
                for f in range(FT):
                    n = 2 * DC + 2 + f
                    act.wait_ge(ring_full, b * (RING - HP) + n + 1)
                    for i in range(2):
                        last = nc.scalar.activation(q2[0:HD, 2 * f + i, :], ps[i * HD:(i + 1) * HD, 6 + n % 2, :], ACT.Copy,
                                                    scale=HD ** -0.5)
                    last.then_inc(hi_ready, 1)
                    act.wait_ge(both_full, b * FT + f + 1)
                    act.wait_ge(hidden_ready, b * FT + max(f + 1, 3))
                    nc.scalar.activation(silu[:, f % 3, :], ps[:, 2 * (f % 3) + 1, :], ACT.Silu).then_inc(silu_ready, 1)
                    if f:
                        high(b, f - 1)
                high(b, FT - 1)
                for u in range(UNITS + LAG_C):
                    if u < UNITS:
                        act.wait_ge(biased_ready, b * UNITS + u + 1 + 2)
                        act.wait_ge(turned, b * UNITS + u + 1)
                        nc.scalar.activation(prob[:, u % 4, :], biased[:, u % 4, :], ACT.Exp, scale=-1.0,
                                             bias=neg_max[:, u // TT, u % TT:u % TT + 1],
                                             accum_out=total[:, u // TT, u % TT:u % TT + 1]).then_inc(exp_done, 1)
                    t = u - LAG_C
                    if t >= 0 and t % 2 == 0:
                        act.wait_ge(turned, b * UNITS + t + 1 + 4)
                        act.wait_ge(out_done, b * UNITS + t + 1)
                        nc.scalar.activation(probT[:, t % 4, :], ps[:, 2 + t % 4, :], ACT.Copy).then_inc(copied[0], 1)
                for g in range(HP):
                    act.wait_ge(ring_full, b * (RING - HP) + 2 * DC + 2 + HP + g + 1)
                    nc.scalar.activation(o_hi[:, g, :], ps[:, 6 + (2 * DC + 2 + 2 * HP + g) % 2, :], ACT.Copy
                                         ).then_inc(o_hi_ready, 1)

        @block.vector
        def _(dve):
            ps, V = core.ps, nc.vector
            dve.sem_inc(ring_free, 2)
            dve.sem_inc(rows_added, TT)
            dve.sem_inc(hidden_ready, 3)
            dve.sem_inc(h_lo_ready, 3)
            dve.sem_inc(biased_ready, 2)
            dve.sem_inc(copied[1], 2)
            dve.wait_ge(small_in, 16)

            def norms(b):
                first = norm1.parts(dve, b, lambda j: core.x[:, b * TT + j, :], lambda j: xn[:, j, :], xn_ready)
                again = norm2.parts(dve, b, lambda j: xn[:, j, :], lambda j: xn2[:, j, :], xn2_ready)
                context = normc.parts(dve, b, lambda j: ctx[:, j, :], lambda j: ctx[:, j, :], cn_ready)
                return [*first, lambda: dve.wait_ge(xn_ready, b + 1), *again,
                        lambda: dve.wait_ge(ctx_in, b * 16 + 16), *context]

            def batch(b, following):
                ring, full = [0], [0]

                def take():
                    ring[0] += 1
                    full[0] += 1
                    dve.wait_ge(ring_full, b * (RING - HP) + full[0])
                    return 6 + (ring[0] - 1) % 2

                def low(f):
                    dve.wait_ge(h_hi_ready, b * FT + f + 1)
                    V.tensor_tensor(h_lo[:, f, :], hidden[:, f % 3, :], h_hi[:, f, :], ALU.subtract).then_inc(h_lo_ready, 1)

                for k, dst in enumerate((xnT, cnT)):
                    for c in range(DC):
                        V.tensor_scalar(dst[:, c, :], ps[:, take(), :], gains[:, 2 * k, c:c + 1], gains[:, 2 * k + 1, c:c + 1],
                                        ALU.mult, ALU.add).then_inc(ring_free, 1)
                dve.wait_ge(x_hi_ready, b + 1)
                V.tensor_tensor(x_lo[:], xnT[:], x_hi[:], ALU.subtract).then_inc(x_lo_ready, 1)
                bank = take()
                dve.wait_ge(hi_ready, b * (HP + 1) + 1)
                V.tensor_tensor(k_lo[:], ps[:, bank, :], k_hi[:], ALU.subtract).then_inc(ring_free, 1)
                V.tensor_copy(v[:], ps[:, take(), 0:TT * HD].rearrange("p (j d) -> p j d", j=TT)).then_inc(ring_free, 1)
                for f in range(FT):
                    bank = take()
                    dve.wait_ge(hi_ready, b * (HP + 1) + f + 2)
                    for i in range(2):
                        last = V.scalar_tensor_tensor(out=q2[HD:P, 2 * f + i, :], in0=ps[i * HD:(i + 1) * HD, bank, :],
                                                      scalar=HD ** -0.5, in1=q2[0:HD, 2 * f + i, :],
                                                      op0=ALU.mult, op1=ALU.subtract)
                    last.then_inc(ring_free, 1)
                    dve.wait_ge(silu_ready, b * FT + f + 1)
                    dve.wait_ge(h_lo_ready, b * FT + f + 1)
                    V.tensor_tensor(hidden[:, f % 3, :], silu[:, f % 3, :], ps[:, 2 * (f % 3), :], ALU.mult).then_inc(hidden_ready, 1)
                    if f:
                        low(f - 1)
                low(FT - 1)
                dve.wait_ge(h_lo_ready, (b + 1) * FT + 3)
                dve.wait_ge(mask_in, b * 16 + 16)

                def rows(g):
                    ring[0] += 1
                    bank = 6 + (ring[0] - 1) % 2
                    dve.wait_ge(out_done, b * UNITS + 2 * TT * (g + 1) + 4)
                    V.reciprocal(inv[:, 2 * g:2 * g + 2, :], total[:, 2 * g:2 * g + 2, :]).then_inc(inv_ready, 1)
                    dve.wait_ge(inv_ready, b * HP + g + 1)
                    for i in range(2):
                        last = V.tensor_tensor(o[:, :, 2 * g + i, :],
                                               ps[:, bank, i * TT * HD:(i + 1) * TT * HD].rearrange("p (j d) -> p j d", d=HD),
                                               inv[:, 2 * g + i, :].unsqueeze(2).to_broadcast([P, TT, HD]), ALU.mult)
                    last.then_inc(ring_free, 1)

                for u in range(UNITS + LAG_C):
                    if u % 4 == 0 and following:
                        following.pop(0)()
                    if u < UNITS:
                        h, j = divmod(u, TT)
                        dve.wait_ge(scores_full, b * UNITS + u + 1)
                        dve.wait_ge(exp_done, b * UNITS + u + 1)
                        dve.nop(nofuse=True)
                        V.tensor_tensor_reduce(out=biased[:, u % 4, :], in0=ps[:, u % 2, :], in1=mask[:, j, :], scale=-1.0,
                                               scalar=3.0e38, op0=ALU.add, op1=ALU.min,
                                               accum_out=neg_max[:, h, j:j + 1]).then_inc(biased_ready, 1)
                    t = u - LAG_C
                    if t >= 0 and t % 2 == 1:
                        dve.wait_ge(turned, b * UNITS + t + 1 + 4)
                        dve.wait_ge(out_done, b * UNITS + t + 1)
                        V.tensor_copy(probT[:, t % 4, :], ps[:, 2 + t % 4, :]).then_inc(copied[1], 1)
                    n = u - LAG_R
                    if n >= 0 and n % (2 * TT) == 2 * TT - 1:
                        rows(n // (2 * TT))
                rows(HP - 1)
                for g in range(HP):
                    bank = take()
                    dve.wait_ge(o_hi_ready, b * HP + g + 1)
                    V.tensor_tensor(o_lo[:, g, :], ps[:, bank, :], o_hi[:, g, :], ALU.subtract).then_inc(ring_free, 1)
                for j in range(TT):
                    dve.wait_ge(rows_full, b * TT + j + 1)
                    V.tensor_tensor(core.x[:, b * TT + j, :], core.x[:, b * TT + j, :], ps[:, j, 0:D], ALU.add
                                    ).then_inc(rows_added, 1)

            for part in norms(0):
                part()
            for n, (w, raw) in enumerate(raws.values()):
                dve.wait_ge(raw_hi, n + 1)
                V.tensor_tensor(w[:, 1, :], raw, w[:, 0, :], ALU.subtract).then_inc(weights_split, 1)
            with dve.Fori(0, B - 1) as b:
                batch(b, norms(b + 1))
            batch(B - 1, [])


def build(nc, dram, out):
    with ExitStack() as ctx:
        core = Core(nc, ctx, dram)
        load_stage(core)
        sigmoid_attention_stage(core)
        mixture_of_depths_stage(core)
        causal_attention_stage(core)
        quantised_ffn_stage(core)
        autocorrelation_stage(core)
        relu_experts_stage(core)
        parallel_attention_stage(core)
        gated_experts_stage(core, out)


def lay_out(inputs):
    import numpy as np
    a = {k: np.asarray(v) for k, v in inputs.items()}

    def strips(w):
        return np.repeat(w.reshape(D, 16, 1, 16), 2, 2).reshape(D, 512)

    def expert_columns(gate, up, down):
        E, F = gate.shape[0], gate.shape[2]
        cuts = [*range(0, F, P), F]
        up_proj = np.concatenate([w[:, :, s:e] for s, e in zip(cuts, cuts[1:]) for w in (gate, up)], 2)
        down = np.concatenate([down, down[:, cuts[-2]:]], 1)
        return np.concatenate([up_proj.reshape(E, DC, P, 2 * F).transpose(0, 2, 1, 3).reshape(E, P, -1),
                               down.reshape(E, -1, P, D).transpose(0, 2, 1, 3).reshape(E, P, -1)], 2)

    arrays = {
        "x": a["x"],
        "ctx": a["ctx_1024"],
        "ctxT": a["ctx_1024"].transpose(0, 2, 1),
        "ctxT_back": a["ctx_1024"].transpose(0, 2, 1).reshape(B, D, TT, P)[:, :, :, ::-1].reshape(B, D, S),
        "lo_rows": np.where(np.arange(P) % 32 < 16, 0.0, -1.0).astype(np.float32)[:, None],
        "l0x_wq": strips(a["L0_xattn_Wq"].T),
        "l0x_wk": strips(a["L0_xattn_Wk"].T),
        "l0x_wv": strips(a["L0_xattn_Wv"].T),
        "l0x_wo": strips(a["L0_xattn_Wo"]).T,
    }
    arrays |= {
        "pos": a["L0_ffn_position_ids"][:, 0:S].reshape(B, TT, P).transpose(2, 0, 1).reshape(P, B * TT),
        "attention_mask": a["L0_ffn_attention_mask"][:, 0, 0:S, 0:S],
        "slot_base": np.array([[0], [64], [0], [64]], np.float32),
        "rope_freq": (np.float32(1) / np.float32(10000) ** (np.arange(0, 16, 2, dtype=np.float32) / np.float32(16)))[None],
        "l0f_rw": a["L0_ffn_router_w"].T,
        "l0f_rb": a["L0_ffn_router_b"][None],
        "l0f_ln1": a["L0_ffn_ln1"].reshape(DC, P).T,
        "l0f_ln2": a["L0_ffn_ln2"].reshape(DC, P).T,
        **{f"l0f_{n}": a[f"L0_ffn_{n}"] for n in ("wq", "wk", "wv", "wo", "w1", "w2")},
    }
    arrays |= {
        "l1f_gate": a["L1_ffn_w_gate"],
        "l1f_up": a["L1_ffn_w_up"],
        "l1f_down": a["L1_ffn_w_down"],
        "l1f_clip_x": a["L1_ffn_clip_x"][None],
        "l1f_clip_down": a["L1_ffn_clip_down"][None],
    }
    t, f = np.arange(S), np.arange(S // 2)
    angle = 2 * np.pi / S * ((t[:, None] * f[None, :]) % S)
    basis = np.concatenate([np.cos(angle), np.sin(angle)], 1)
    basis[:, S // 2] = np.where(t % 2, -1.0, 1.0)
    share = np.full(S, 2.0 / (S * D))
    share[0] = share[S // 2] = 1.0 / (S * D)
    inverse = (basis * share)[(-t) % S].T
    arrays |= {
        **{f"l2x_{n}": a[f"L2_xattn_{n}"] for n in ("Wq", "Wk", "Wv", "Wo")},
        **{f"l2x_{n}": a[f"L2_xattn_{n}"][None] for n in ("bq", "bk", "bv", "bo")},
        "dft_basis": basis.astype(np.float32),
        "dft_inverse": inverse.astype(np.float32),
        "l2f_router": a["L2_ffn_w_router"].T,
        "l2f_w1": a["L2_ffn_w1_stack"].transpose(0, 2, 1),
        "l2f_w2": a["L2_ffn_w2_stack"].transpose(0, 2, 1),
        "l2f_ws1": a["L2_ffn_ws1"].reshape(2, D, D).transpose(0, 2, 1),
        "l2f_ws2": a["L2_ffn_ws2"].T.reshape(2, D, D),
        "l3f_router": a["L3_ffn_gate_w"].T,
        "l3f_weights": expert_columns(a["L3_ffn_w1"], a["L3_ffn_w3"], a["L3_ffn_w2"]),
    }
    token = np.arange(B * S).reshape(B * TT, P).T
    blocks = (2 * B * S + 8 * 255) // 256
    arrays |= {
        "earlier": np.triu(np.ones((P, P), np.float32), 1),
        "choice_numbers": np.stack([token, B * S + token], 2).astype(np.float32),
        "spare_numbers": (2 * B * S + np.arange(2 * blocks * P)).reshape(2 * blocks, P).T.astype(np.float32),
        "block_starts": np.arange(0, 8 * 256, 256, dtype=np.float32)[None],
        "block_numbers": np.arange(blocks, dtype=np.float32)[None],
    }
    kv = a["L3_xattn_Wkv"]
    arrays |= {
        "mask": a["mask_BxSxS2_ff0"],
        "l3x_wq": a["L3_xattn_Wq"],
        "l3x_wk": np.concatenate([kv[:, 0:64], kv[:, 0:64]], 1),
        "l3x_wv": kv[:, 64:128],
        "l3x_w1": a["L3_xattn_W1"],
        "l3x_wout": a["L3_xattn_Wout"],
        "l3x_w2": a["L3_xattn_W2"],
        "l3x_gains": np.stack([a[f"L3_xattn_{n}"].reshape(DC, P) for n in ("ln_g", "ln_b", "cln_g", "cln_b")]
                              ).transpose(2, 0, 1),
    }
    return {k: np.ascontiguousarray(v) for k, v in arrays.items()}


def kernel(**inputs):
    import concourse.bacc as bacc
    from concourse.bass_utils import run_bass_kernel_spmd

    nc = bacc.Bacc("TRN2", target_bir_lowering=False, num_devices=1)
    arrays = lay_out(inputs)
    dram = {k: nc.dram_tensor(f"in_{k}", v.shape, mybir.dt.from_np(v.dtype), kind="ExternalInput").ap()
            for k, v in arrays.items()}
    out = nc.dram_tensor("out_x", (B, S, D), F32, kind="ExternalOutput").ap()
    dram["delay_rows"] = nc.dram_tensor("delay_rows", (B, 2 * S), F32).ap()
    dram["l3f_parts"] = nc.dram_tensor("l3f_parts", (8, P, 2, arrays["l3f_weights"].shape[2]), F16).ap()
    slots = arrays["spare_numbers"].size
    dram["xs_rows"] = nc.dram_tensor("xs_rows", (slots, D + 2), F32).ap()
    dram["y_rows"] = nc.dram_tensor("y_rows", (2 * B * S + slots, D), F32).ap()
    build(nc, dram, out)
    result = run_bass_kernel_spmd(nc, [{f"in_{k}": v for k, v in arrays.items()}], core_ids=[0])
    return result.results[0]["out_x"]
```
